# Optimizing a Trainium2 kernel written in Bass

```python
import numpy as np
import jax
import jax.numpy as jnp

def _softmax(x, axis=-1):
    return jax.nn.softmax(x, axis=axis)

def _gelu(x):
    return jax.nn.gelu(x, approximate=True)

def _silu(x):
    return jax.nn.silu(x)

def _sigmoid(x):
    return jax.nn.sigmoid(x)

def _layernorm(x, axis=-1, eps=1e-05):
    m = jnp.mean(x, axis=axis, keepdims=True)
    v = jnp.var(x, axis=axis, keepdims=True)
    return (x - m) / jnp.sqrt(v + eps)

def _scatter_add(tgt, idx, src, axis=0):
    return tgt.at[idx].add(src)

def _segment_sum(src, seg, n):
    return jax.ops.segment_sum(src, seg, n)
kernel_name = 'mk_gps_d2_gnn_r32_23181b'

def setup_inputs(seed: int=0):
    np.random.seed(seed)
    _w = jnp.asarray

    def _rec_inputs():
        import jax
        import jax.numpy as jnp
        _gk = jax.random.key(seed)
        x = -0.0003713 + 1 * jax.random.normal(jax.random.fold_in(_gk, 1), (3125, 256), jnp.float32)
        src = jax.random.randint(jax.random.fold_in(_gk, 2), (50000,), 0, 3125, jnp.int32)
        dst = jax.random.randint(jax.random.fold_in(_gk, 3), (50000,), 0, 3125, jnp.int32)
        _o = jnp.argsort(dst, stable=True)
        src = src[_o]
        dst = dst[_o]
        return (x, src, dst)
    x, src, dst = _rec_inputs()

    def _L0_gnn_setup():
        import jax, jax.numpy as jnp
        import numpy as np
        N = 50000
        E = 25000
        D_IN = 256
        HID = 32
        HEADS = 8
        D_OUT = 64
        NEG_SLOPE = 0.2

        def _gat_conv(x, src, dst, W, att_src, att_dst, bias, heads, out_dim, concat):
            n = x.shape[0]
            h = (x @ W.T).reshape(n, heads, out_dim)
            a_s = jnp.sum(h * att_src, axis=-1)
            a_d = jnp.sum(h * att_dst, axis=-1)
            logits = jax.nn.leaky_relu(a_s[src] + a_d[dst], NEG_SLOPE)
            m = jax.ops.segment_max(logits, dst, num_segments=n)
            e = jnp.exp(logits - m[dst])
            den = jax.ops.segment_sum(e, dst, num_segments=n)
            alpha = e / (den[dst] + 1e-16)
            out = jax.ops.segment_sum(alpha[:, :, None] * h[src], dst, num_segments=n)
            out = out.reshape(n, heads * out_dim) if concat else out.mean(axis=1)
            return out + bias
        key = jax.random.key(seed)
        ks = jax.random.split(key, 12)
        x = jax.random.normal(ks[0], (N, D_IN), jnp.float32)
        edge_index = jax.random.randint(ks[1], (2, E), 0, N, dtype=jnp.int32)
        g = lambda k, shape, fan_in: jax.random.normal(k, shape, jnp.float32) / np.sqrt(fan_in)
        W0 = g(ks[2], (HEADS * HID, D_IN), D_IN)
        att_src0 = g(ks[3], (1, HEADS, HID), HID)
        att_dst0 = g(ks[4], (1, HEADS, HID), HID)
        b0 = jnp.zeros((HEADS * HID,), jnp.float32)
        W1 = g(ks[5], (1 * D_OUT, HEADS * HID), HEADS * HID)
        att_src1 = g(ks[6], (1, 1, D_OUT), D_OUT)
        att_dst1 = g(ks[7], (1, 1, D_OUT), D_OUT)
        b1 = jnp.zeros((D_OUT,), jnp.float32)
        return {'x': x, 'edge_index': edge_index, 'W0': W0, 'att_src0': att_src0, 'att_dst0': att_dst0, 'b0': b0, 'W1': W1, 'att_src1': att_src1, 'att_dst1': att_dst1, 'b1': b1}
    _L0_gnn_all = _L0_gnn_setup()
    _L0_gnn_in = {k: v for k, v in _L0_gnn_all.items() if k in ('W0', 'att_src0', 'att_dst0', 'b0', 'W1', 'att_src1', 'att_dst1', 'b1')}
    del _L0_gnn_all

    def _L0_mix_setup():
        import jax, jax.numpy as jnp
        import numpy as np
        EPS_NORM = 1e-06
        EPS_ATTN = 1e-06
        HEADS = 8

        def rmsnorm(x, w):
            ms = jnp.mean(x * x, axis=-1, keepdims=True)
            return w * (x * jax.lax.rsqrt(ms + EPS_NORM))

        def linear_attention(x, w_qkv, w_out, b_out):
            B, N, D = x.shape
            hd = D // HEADS
            qkv = (x @ w_qkv).reshape(B, N, 3, HEADS, hd)
            q, k, v = (qkv[:, :, 0], qkv[:, :, 1], qkv[:, :, 2])
            q = jax.nn.elu(q) + 1.0
            k = jax.nn.elu(k) + 1.0
            kv = jnp.einsum('bnhd,bnhm->bhdm', k, v)
            z = 1.0 / (jnp.einsum('bnhd,bhd->bnh', q, k.sum(axis=1)) + EPS_ATTN)
            out = jnp.einsum('bnhd,bhdm,bnh->bnhm', q, kv, z)
            out = out.reshape(B, N, D)
            return out @ w_out + b_out
        key = jax.random.key(seed)
        ks = jax.random.split(key, 4)
        B, N, D = (16, 256, 256)
        x = jax.random.normal(ks[0], (B, N, D), dtype=jnp.float32)
        w_norm1 = jnp.ones((D,), dtype=jnp.float32)
        w_qkv = jax.random.normal(ks[1], (D, 3 * D), dtype=jnp.float32) * 0.02
        w_out = jax.random.normal(ks[2], (D, D), dtype=jnp.float32) * 0.02
        b_out = jnp.zeros((D,), dtype=jnp.float32)
        w_norm2 = jnp.ones((D,), dtype=jnp.float32)
        return {'x': x, 'w_norm1': w_norm1, 'w_qkv': w_qkv, 'w_out': w_out, 'b_out': b_out, 'w_norm2': w_norm2}
    _L0_mix_all = _L0_mix_setup()
    _L0_mix_in = {k: v for k, v in _L0_mix_all.items() if k in ('w_norm1', 'w_qkv', 'w_out', 'b_out', 'w_norm2')}
    del _L0_mix_all

    def _L0_ffn_setup():
        import jax, jax.numpy as jnp
        import numpy as np
        B, S, D = (8, 128, 256)
        H = 4 * D
        CAPACITY = 0.5
        key = jax.random.key(seed)
        ks = jax.random.split(key, 6)
        x = jax.random.normal(ks[0], (B, S, D), dtype=jnp.float32)
        attention_mask = jnp.zeros((B, 1, 1, S), dtype=jnp.float32)
        wr = jax.random.normal(ks[1], (D, 1), dtype=jnp.float32) * 0.02
        br = jnp.zeros((1,), dtype=jnp.float32)
        w1 = jax.random.normal(ks[2], (D, H), dtype=jnp.float32) * 0.02
        b1 = jnp.zeros((H,), dtype=jnp.float32)
        w2 = jax.random.normal(ks[3], (H, D), dtype=jnp.float32) * 0.02
        b2 = jnp.zeros((D,), dtype=jnp.float32)
        return {'x': x, 'attention_mask': attention_mask, 'wr': wr, 'br': br, 'w1': w1, 'b1': b1, 'w2': w2, 'b2': b2}
    _L0_ffn_all = _L0_ffn_setup()
    _L0_ffn_in = {k: v for k, v in _L0_ffn_all.items() if k in ('attention_mask', 'wr', 'br', 'w1', 'b1', 'w2', 'b2')}
    del _L0_ffn_all

    def _L1_gnn_setup():
        import jax, jax.numpy as jnp
        import numpy as np
        N_NODES = 3125
        N_EDGES = 100000
        NFEAT = 256
        NHID = 256
        key = jax.random.key(seed)
        k_x, k_ws, k_wn, k_src, k_dst = jax.random.split(key, 5)
        x = jax.random.normal(k_x, (N_NODES, NFEAT), dtype=jnp.float32)
        W_self = jax.random.normal(k_ws, (NFEAT, NHID), dtype=jnp.float32) * (1.0 / np.sqrt(NFEAT))
        W_neigh = jax.random.normal(k_wn, (NFEAT, NHID), dtype=jnp.float32) * (1.0 / np.sqrt(NFEAT))
        b = jnp.zeros((NHID,), dtype=jnp.float32)
        edge_src = jax.random.randint(k_src, (N_EDGES,), 0, N_NODES, dtype=jnp.int32)
        edge_dst = jax.random.randint(k_dst, (N_EDGES,), 0, N_NODES, dtype=jnp.int32)
        return {'x': x, 'W_self': W_self, 'W_neigh': W_neigh, 'b': b, 'edge_src': edge_src, 'edge_dst': edge_dst}
    _L1_gnn_all = _L1_gnn_setup()
    _L1_gnn_in = {k: v for k, v in _L1_gnn_all.items() if k in ('W_self', 'W_neigh', 'b')}
    del _L1_gnn_all

    def _L1_mix_setup():
        import jax, jax.numpy as jnp
        import numpy as np
        B, L, D, H = (4, 512, 256, 8)
        DK = D // H

        def _heads(t):
            b, l, d = t.shape
            return t.reshape(b, l, H, DK).transpose(0, 2, 1, 3)
        key = jax.random.key(seed)
        ks = jax.random.split(key, 9)
        s = 0.02
        return {'x': jax.random.normal(ks[0], (B, L, D), dtype=jnp.float32), 'Wq': jax.random.normal(ks[1], (D, D), dtype=jnp.float32) * s, 'bq': jnp.zeros((D,), dtype=jnp.float32), 'Wk': jax.random.normal(ks[2], (D, D), dtype=jnp.float32) * s, 'bk': jnp.zeros((D,), dtype=jnp.float32), 'Wv': jax.random.normal(ks[3], (D, D), dtype=jnp.float32) * s, 'bv': jnp.zeros((D,), dtype=jnp.float32), 'Wfc': jax.random.normal(ks[4], (D, D), dtype=jnp.float32) * s, 'bfc': jnp.zeros((D,), dtype=jnp.float32)}
    _L1_mix_all = _L1_mix_setup()
    _L1_mix_in = {k: v for k, v in _L1_mix_all.items() if k in ('Wq', 'bq', 'Wk', 'bk', 'Wv', 'bv', 'Wfc', 'bfc')}
    del _L1_mix_all

    def _L1_ffn_setup():
        import jax, jax.numpy as jnp
        import numpy as np
        E = 8
        K = 2
        D = 256
        H = 512
        DOUT = 256
        EPS = 1e-05
        key = jax.random.key(seed)
        ks = jax.random.split(key, 9)
        s = 0.02
        return {'x': jax.random.normal(ks[0], (4, 256, D), jnp.float32), 'gamma': 1.0 + 0.05 * jax.random.normal(ks[1], (D,), jnp.float32), 'beta': 0.05 * jax.random.normal(ks[2], (D,), jnp.float32), 'Wr': 0.01 * jax.random.normal(ks[3], (D, E), jnp.float32), 'br': jnp.zeros((E,), jnp.float32), 'W1': s * jax.random.normal(ks[4], (E, D, H), jnp.float32), 'b1': s * jax.random.normal(ks[5], (E, H), jnp.float32), 'W2': s * jax.random.normal(ks[6], (E, H, DOUT), jnp.float32), 'b2': s * jax.random.normal(ks[7], (E, DOUT), jnp.float32)}
    _L1_ffn_all = _L1_ffn_setup()
    _L1_ffn_in = {k: v for k, v in _L1_ffn_all.items() if k in ('gamma', 'beta', 'Wr', 'br', 'W1', 'b1', 'W2', 'b2')}
    del _L1_ffn_all
    return {'x': x, 'src': src, 'dst': dst, 'L0_gnn_W0': _L0_gnn_in['W0'], 'L0_gnn_att_src0': _L0_gnn_in['att_src0'], 'L0_gnn_att_dst0': _L0_gnn_in['att_dst0'], 'L0_gnn_b0': _L0_gnn_in['b0'], 'L0_gnn_W1': _L0_gnn_in['W1'], 'L0_gnn_att_src1': _L0_gnn_in['att_src1'], 'L0_gnn_att_dst1': _L0_gnn_in['att_dst1'], 'L0_gnn_b1': _L0_gnn_in['b1'], 'L0_mix_w_norm1': _L0_mix_in['w_norm1'], 'L0_mix_w_qkv': _L0_mix_in['w_qkv'], 'L0_mix_w_out': _L0_mix_in['w_out'], 'L0_mix_b_out': _L0_mix_in['b_out'], 'L0_mix_w_norm2': _L0_mix_in['w_norm2'], 'L0_ffn_attention_mask': _L0_ffn_in['attention_mask'], 'L0_ffn_wr': _L0_ffn_in['wr'], 'L0_ffn_br': _L0_ffn_in['br'], 'L0_ffn_w1': _L0_ffn_in['w1'], 'L0_ffn_b1': _L0_ffn_in['b1'], 'L0_ffn_w2': _L0_ffn_in['w2'], 'L0_ffn_b2': _L0_ffn_in['b2'], 'L1_gnn_W_self': _L1_gnn_in['W_self'], 'L1_gnn_W_neigh': _L1_gnn_in['W_neigh'], 'L1_gnn_b': _L1_gnn_in['b'], 'L1_mix_Wq': _L1_mix_in['Wq'], 'L1_mix_bq': _L1_mix_in['bq'], 'L1_mix_Wk': _L1_mix_in['Wk'], 'L1_mix_bk': _L1_mix_in['bk'], 'L1_mix_Wv': _L1_mix_in['Wv'], 'L1_mix_bv': _L1_mix_in['bv'], 'L1_mix_Wfc': _L1_mix_in['Wfc'], 'L1_mix_bfc': _L1_mix_in['bfc'], 'L1_ffn_gamma': _L1_ffn_in['gamma'], 'L1_ffn_beta': _L1_ffn_in['beta'], 'L1_ffn_Wr': _L1_ffn_in['Wr'], 'L1_ffn_br': _L1_ffn_in['br'], 'L1_ffn_W1': _L1_ffn_in['W1'], 'L1_ffn_b1': _L1_ffn_in['b1'], 'L1_ffn_W2': _L1_ffn_in['W2'], 'L1_ffn_b2': _L1_ffn_in['b2']}

def reference(x, src, dst, L0_gnn_W0, L0_gnn_att_src0, L0_gnn_att_dst0, L0_gnn_b0, L0_gnn_W1, L0_gnn_att_src1, L0_gnn_att_dst1, L0_gnn_b1, L0_mix_w_norm1, L0_mix_w_qkv, L0_mix_w_out, L0_mix_b_out, L0_mix_w_norm2, L0_ffn_attention_mask, L0_ffn_wr, L0_ffn_br, L0_ffn_w1, L0_ffn_b1, L0_ffn_w2, L0_ffn_b2, L1_gnn_W_self, L1_gnn_W_neigh, L1_gnn_b, L1_mix_Wq, L1_mix_bq, L1_mix_Wk, L1_mix_bk, L1_mix_Wv, L1_mix_bv, L1_mix_Wfc, L1_mix_bfc, L1_ffn_gamma, L1_ffn_beta, L1_ffn_Wr, L1_ffn_br, L1_ffn_W1, L1_ffn_b1, L1_ffn_W2, L1_ffn_b2):
    import jax
    import jax.numpy as jnp

    def _L0_gnn_ref(x, edge_index, W0, att_src0, att_dst0, b0, W1, att_src1, att_dst1, b1):
        import jax, jax.numpy as jnp
        import numpy as np
        N = 50000
        E = 25000
        D_IN = 256
        HID = 32
        HEADS = 8
        D_OUT = 64
        NEG_SLOPE = 0.2

        def _gat_conv(x, src, dst, W, att_src, att_dst, bias, heads, out_dim, concat):
            n = x.shape[0]
            h = (x @ W.T).reshape(n, heads, out_dim)
            a_s = jnp.sum(h * att_src, axis=-1)
            a_d = jnp.sum(h * att_dst, axis=-1)
            logits = jax.nn.leaky_relu(a_s[src] + a_d[dst], NEG_SLOPE)
            m = jax.ops.segment_max(logits, dst, num_segments=n)
            e = jnp.exp(logits - m[dst])
            den = jax.ops.segment_sum(e, dst, num_segments=n)
            alpha = e / (den[dst] + 1e-16)
            out = jax.ops.segment_sum(alpha[:, :, None] * h[src], dst, num_segments=n)
            out = out.reshape(n, heads * out_dim) if concat else out.mean(axis=1)
            return out + bias
        n = x.shape[0]
        loop = jnp.arange(n, dtype=edge_index.dtype)
        ei = jnp.concatenate([edge_index, jnp.stack([loop, loop])], axis=1)
        src, dst = (ei[0], ei[1])
        out1 = jax.nn.elu(_gat_conv(x, src, dst, W0, att_src0, att_dst0, b0, HEADS, HID, True))
        _ = _gat_conv(out1, src, dst, W1, att_src1, att_dst1, b1, 1, D_OUT, False)
        return out1

    def _L0_mix_ref(x, w_norm1, w_qkv, w_out, b_out, w_norm2):
        import jax, jax.numpy as jnp
        import numpy as np
        EPS_NORM = 1e-06
        EPS_ATTN = 1e-06
        HEADS = 8

        def rmsnorm(x, w):
            ms = jnp.mean(x * x, axis=-1, keepdims=True)
            return w * (x * jax.lax.rsqrt(ms + EPS_NORM))

        def linear_attention(x, w_qkv, w_out, b_out):
            B, N, D = x.shape
            hd = D // HEADS
            qkv = (x @ w_qkv).reshape(B, N, 3, HEADS, hd)
            q, k, v = (qkv[:, :, 0], qkv[:, :, 1], qkv[:, :, 2])
            q = jax.nn.elu(q) + 1.0
            k = jax.nn.elu(k) + 1.0
            kv = jnp.einsum('bnhd,bnhm->bhdm', k, v)
            z = 1.0 / (jnp.einsum('bnhd,bhd->bnh', q, k.sum(axis=1)) + EPS_ATTN)
            out = jnp.einsum('bnhd,bhdm,bnh->bnhm', q, kv, z)
            out = out.reshape(B, N, D)
            return out @ w_out + b_out
        h = x + linear_attention(rmsnorm(x, w_norm1), w_qkv, w_out, b_out)
        return h + rmsnorm(h, w_norm2)

    def _L0_ffn_ref(x, attention_mask, wr, br, w1, b1, w2, b2):
        import jax, jax.numpy as jnp
        import numpy as np
        B, S, D = (8, 128, 256)
        H = 4 * D
        CAPACITY = 0.5
        b, s, d = x.shape
        weights = (jnp.einsum('bsd,do->bso', x, wr) + br)[..., 0]
        k = max(1, int(CAPACITY * s))
        kk = k - 1 if k > 1 else 1
        _, idx = jax.lax.top_k(weights, k)
        sel_idx = idx[:, :kk]
        sel = jnp.take_along_axis(x, sel_idx[:, :, None], axis=1)
        h = jax.nn.gelu(jnp.einsum('bkd,dh->bkh', sel, w1) + b1)
        y = jnp.einsum('bkh,hd->bkd', h, w2) + b2
        w_sel = jnp.take_along_axis(weights, sel_idx, axis=1)
        y = y * w_sel[..., None]
        batch_idx = jnp.arange(b)[:, None]
        processed = jnp.zeros_like(x).at[batch_idx, sel_idx].set(y)
        return processed + x

    def _L1_gnn_ref(x, W_self, W_neigh, b, edge_src, edge_dst):
        import jax, jax.numpy as jnp
        import numpy as np
        N_NODES = 3125
        N_EDGES = 100000
        NFEAT = 256
        NHID = 256
        n = x.shape[0]
        msg = x[edge_src]
        agg = jax.ops.segment_sum(msg, edge_dst, num_segments=n)
        deg = jax.ops.segment_sum(jnp.ones_like(edge_dst, dtype=x.dtype), edge_dst, num_segments=n)
        h_neigh = agg / jnp.maximum(deg, 1.0)[:, None]
        out = x @ W_self + h_neigh @ W_neigh + b
        return jax.nn.relu(out)

    def _L1_mix_ref(x, Wq, bq, Wk, bk, Wv, bv, Wfc, bfc):
        import jax, jax.numpy as jnp
        import numpy as np
        B, L, D, H = (4, 512, 256, 8)
        DK = D // H

        def _heads(t):
            b, l, d = t.shape
            return t.reshape(b, l, H, DK).transpose(0, 2, 1, 3)
        q = _heads(x @ Wq.T + bq)
        k = _heads(x @ Wk.T + bk)
        v = _heads(x @ Wv.T + bv)
        seq_len = q.shape[-2]
        p_attn = jnp.einsum('bhnd,bhne->bhde', k, v) / seq_len
        out = jnp.einsum('bhnd,bhde->bhne', q, p_attn)
        out = out.transpose(0, 2, 1, 3).reshape(x.shape[0], seq_len, H * DK)
        return out @ Wfc.T + bfc

    def _L1_ffn_ref(x, gamma, beta, Wr, br, W1, b1, W2, b2):
        import jax, jax.numpy as jnp
        import numpy as np
        E = 8
        K = 2
        D = 256
        H = 512
        DOUT = 256
        EPS = 1e-05
        mu = jnp.mean(x, axis=-1, keepdims=True)
        var = jnp.mean(jnp.square(x - mu), axis=-1, keepdims=True)
        xn = (x - mu) * jax.lax.rsqrt(var + EPS) * gamma + beta
        logits = jnp.einsum('bsd,de->bse', xn, Wr) + br
        top_vals, top_idx = jax.lax.top_k(logits, K)
        w = jax.nn.softmax(top_vals, axis=-1)
        w_full = jnp.einsum('bsk,bske->bse', w, jax.nn.one_hot(top_idx, E, dtype=w.dtype))
        y = jnp.zeros(x.shape[:-1] + (DOUT,), x.dtype)
        for e in range(E):
            h = jax.nn.gelu(jnp.einsum('bsd,dh->bsh', xn, W1[e]) + b1[e], approximate=False)
            y_e = jnp.einsum('bsh,hd->bsd', h, W2[e]) + b2[e]
            y = y + y_e * w_full[..., e, None]
        return y
    edge_index = jnp.stack([src, dst])
    xn = _layernorm(x, axis=-1)
    x = x + _L0_gnn_ref(xn, edge_index, L0_gnn_W0, L0_gnn_att_src0, L0_gnn_att_dst0, L0_gnn_b0, L0_gnn_W1, L0_gnn_att_src1, L0_gnn_att_dst1, L0_gnn_b1) + _L0_mix_ref(xn[None], L0_mix_w_norm1, L0_mix_w_qkv, L0_mix_w_out, L0_mix_b_out, L0_mix_w_norm2)[0]
    x = x + _L0_ffn_ref(_layernorm(x, axis=-1)[None], L0_ffn_attention_mask, L0_ffn_wr, L0_ffn_br, L0_ffn_w1, L0_ffn_b1, L0_ffn_w2, L0_ffn_b2)[0]
    xn = _layernorm(x, axis=-1)
    x = x + _L1_gnn_ref(xn, L1_gnn_W_self, L1_gnn_W_neigh, L1_gnn_b, src, dst) + _L1_mix_ref(xn[None], L1_mix_Wq, L1_mix_bq, L1_mix_Wk, L1_mix_bk, L1_mix_Wv, L1_mix_bv, L1_mix_Wfc, L1_mix_bfc)[0]
    x = x + _L1_ffn_ref(_layernorm(x, axis=-1)[None], L1_ffn_gamma, L1_ffn_beta, L1_ffn_Wr, L1_ffn_br, L1_ffn_W1, L1_ffn_b1, L1_ffn_W2, L1_ffn_b2)[0]
    return x

_drawn_inputs = setup_inputs


def setup_inputs(seed=0):
    import zlib

    import numpy as np

    out = dict(_drawn_inputs(seed))
    spreads = {'L0_gnn_b0': (0.0, 0.1),
     'L0_gnn_b1': (0.0, 0.1),
     'L0_mix_w_norm1': (1.0, 0.6),
     'L0_mix_b_out': (0.0, 0.1),
     'L0_mix_w_norm2': (1.0, 0.2),
     'L0_ffn_b1': (0.0, 0.8),
     'L0_ffn_b2': (0.0, 0.8),
     'L1_gnn_b': (0.0, 2.0),
     'L1_mix_bq': (0.0, 0.8),
     'L1_mix_bk': (0.0, 0.8),
     'L1_mix_bv': (0.0, 0.8),
     'L1_mix_bfc': (0.0, 2.0),
     'L1_ffn_br': (0.0, 0.8)}
    factors = {'L0_gnn_att_dst0': 2.833,
     'L0_mix_w_qkv': 8.0,
     'L0_mix_w_out': 8.0,
     'L0_ffn_wr': 7.366,
     'L0_ffn_w1': 8.0,
     'L0_ffn_w2': 8.0,
     'L1_mix_Wq': 8.0,
     'L1_mix_Wk': 8.0,
     'L1_mix_Wv': 8.0,
     'L1_mix_Wfc': 8.0,
     'L1_ffn_gamma': 8.0,
     'L1_ffn_beta': 8.0,
     'L1_ffn_Wr': 4.94,
     'L1_ffn_W1': 4.338,
     'L1_ffn_b1': 64.0,
     'L1_ffn_W2': 4.219,
     'L1_ffn_b2': 200.0,
     'L1_gnn_W_self': 4.296,
     'L1_gnn_W_neigh': 8.0}
    for name, (base, spread) in spreads.items():
        noise = np.random.default_rng([zlib.crc32(name.encode()), seed]).standard_normal(out[name].shape)
        drawn = base * np.exp(spread * noise) if base else spread * noise
        out[name] = jnp.asarray(drawn.astype(out[name].dtype))
    for name, factor in factors.items():
        out[name] = (out[name] * factor).astype(out[name].dtype)
    return out
```

```python
import concourse.bass as bass
from concourse import mybir
from contextlib import ExitStack

P = 128
N = 3125
D = 256
C = D // P
T = 26
HEADS = 8
HD = D // HEADS
E = 50000
ET = 391
EP = ET * P
SQ = 104
SG = 4
S = SQ * SG
HW = 272
TW = 264
BIG = 1.5e38
FF0 = 1024
KEEP = int(0.5 * N) - 1
NE = 8
FF1 = 512
HJ = 17
PART = [(0, 8), (8, HJ)]


def node_tiles(nc, K, eng, s, n):
    return nc.values_load_multi_w_load_instructions(
        K.ns[0:1, bass.ds(s, n)], [eng.engine], min_val=0, max_val=T - 1,
        skip_runtime_bounds_check_because="edge_tables counts at most T - 1 ends of node tiles")[1]


def setup(nc, I, K):
    fp32, ALU = mybir.dt.float32, mybir.AluOpType
    with ExitStack() as ctx:
        loaded = K.sem("x_loaded")
        made = K.sem("constants_made")
        with nc.Block() as block:
            @block.sync
            def _(sp):
                sp.dma_start(K.X[:, :, :], I["x"].rearrange("(t p) d -> p t d", p=P)).then_inc(loaded, 16)
                sp.dma_start(K.src_p[:, :], I["src"].rearrange("(p f) -> p f", p=P)).then_inc(loaded, 16)
                sp.wait_ge(loaded, 32)

            @block.gpsimd
            def _(pool):
                pool.memset(K.ident[:, :], 0.0)
                pool.memset(K.real[:, :], 1.0)
                pool.memset(K.upper[:, :], 1.0)
                pool.memset(K.ones[:, :], 1.0)
                pool.memset(K.blockmask[:, :, :], 1.0).then_inc(made, 1)
                pool.wait_ge(made, 1)
                pool.sem_inc(made, -1)
                pool.affine_select(out=K.ident[:, :], in_=K.ident[:, :], compare_op=ALU.not_equal, fill=1.0,
                                   base=0, pattern=[[-1, P]], channel_multiplier=1)
                pool.affine_select(out=K.real[:, :], in_=K.real[:, :], compare_op=ALU.is_ge, fill=0.0,
                                   base=N - 1, pattern=[[-P, T]], channel_multiplier=-1)
                pool.affine_select(out=K.upper[:, :], in_=K.upper[:, :], compare_op=ALU.is_ge, fill=0.0,
                                   base=0, pattern=[[1, P]], channel_multiplier=-1)
                pool.affine_select(out=K.blockmask[:, :, :], in_=K.blockmask[:, :, :], compare_op=ALU.is_ge,
                                   fill=0.0, base=0, pattern=[[P, C], [-HD, HEADS]],
                                   channel_multiplier=1).then_inc(made, 1)
                pool.wait_ge(made, 1)
                pool.sem_inc(made, -1)
                pool.affine_select(out=K.blockmask[:, :, :], in_=K.blockmask[:, :, :], compare_op=ALU.is_ge,
                                   fill=0.0, base=HD - 1, pattern=[[-P, C], [HD, HEADS]], channel_multiplier=-1)
                pool.iota(K.iotai[:, :], pattern=[[1, 512]], base=0, channel_multiplier=0).then_inc(made, 1)
                pool.wait_ge(made, 1)
                pool.sem_inc(made, -1)
                pool.tensor_copy(K.iota[:, :], K.iotai[:, :])


def row_stats(nc, K, name):
    fp32, ALU, ACT = mybir.dt.float32, mybir.AluOpType, mybir.ActivationFunctionType
    with ExitStack() as ctx:
        def sb(n, shape):
            return ctx.enter_context(nc.sbuf_tensor(f"{name}_{n}", shape, fp32))
        halves, mv = sb("halves", [P, T, 6]), sb("mv", [P, T])
        var, root, tmp = sb("var", [P, T]), sb("root", [P, T]), sb("tmp", [P, T])
        chain = K.sem(f"{name}_chain")
        var_ready = K.sem(f"{name}_var_ready")
        root_ready = K.sem(f"{name}_root_ready")
        with nc.Block() as block:
            @block.vector
            def _(dve):
                with dve.Fori(0, T // 2 - 1) as i:
                    for k in range(2):
                        nc.vector.bn_stats(halves[:, bass.ds(2 * i + k, 1), :], K.X[:, bass.ds(2 * i + k, 1), :])
                nc.vector.bn_stats(halves[:, T - 2, :], K.X[:, T - 2, :])
                nc.vector.bn_stats(halves[:, T - 1, :], K.X[:, T - 1, :]).then_inc(chain, 1)
                dve.wait_ge(chain, 1)
                dve.sem_inc(chain, -1)
                nc.vector.tensor_tensor(K.mean[:, :], halves[:, :, 1], halves[:, :, 4], ALU.add)
                nc.vector.tensor_tensor(tmp[:, :], halves[:, :, 1], halves[:, :, 4], ALU.subtract)
                nc.vector.tensor_tensor(mv[:, :], halves[:, :, 2], halves[:, :, 5], ALU.add).then_inc(chain, 1)
                dve.wait_ge(chain, 1)
                dve.sem_inc(chain, -1)
                nc.vector.tensor_scalar(K.mean[:, :], K.mean[:, :], 0.5, None, ALU.mult)
                nc.vector.tensor_tensor(tmp[:, :], tmp[:, :], tmp[:, :], ALU.mult).then_inc(chain, 1)
                dve.wait_ge(chain, 1)
                dve.sem_inc(chain, -1)
                nc.vector.tensor_scalar(tmp[:, :], tmp[:, :], 0.25 * D, None, ALU.mult).then_inc(chain, 1)
                dve.wait_ge(chain, 1)
                dve.sem_inc(chain, -1)
                nc.vector.tensor_tensor(mv[:, :], mv[:, :], tmp[:, :], ALU.add).then_inc(chain, 1)
                dve.wait_ge(chain, 1)
                dve.sem_inc(chain, -1)
                nc.vector.tensor_scalar(mv[:, :], mv[:, :], 1.0 / D, None, ALU.mult).then_inc(chain, 1)
                dve.wait_ge(chain, 1)
                dve.sem_inc(chain, -1)
                nc.vector.tensor_scalar(var[:, :], mv[:, :], 1e-5, None, ALU.add).then_inc(var_ready, 1)
                dve.wait_ge(root_ready, 1)
                dve.sem_inc(root_ready, -1)
                nc.vector.reciprocal(root[:, :], root[:, :]).then_inc(chain, 1)
                dve.wait_ge(chain, 1)
                dve.sem_inc(chain, -1)
                nc.vector.tensor_tensor(tmp[:, :], root[:, :], root[:, :], ALU.mult).then_inc(chain, 1)
                dve.wait_ge(chain, 1)
                dve.sem_inc(chain, -1)
                nc.vector.tensor_tensor(tmp[:, :], tmp[:, :], var[:, :], ALU.mult).then_inc(chain, 1)
                dve.wait_ge(chain, 1)
                dve.sem_inc(chain, -1)
                nc.vector.tensor_scalar(tmp[:, :], tmp[:, :], -0.5, 1.5, ALU.mult, ALU.add).then_inc(chain, 1)
                dve.wait_ge(chain, 1)
                dve.sem_inc(chain, -1)
                nc.vector.tensor_tensor(K.rstd[:, :], root[:, :], tmp[:, :], ALU.mult).then_inc(chain, 1)
                dve.wait_ge(chain, 1)
                dve.sem_inc(chain, -1)
                nc.vector.tensor_tensor(tmp[:, :], K.rstd[:, :], K.rstd[:, :], ALU.mult).then_inc(chain, 1)
                dve.wait_ge(chain, 1)
                dve.sem_inc(chain, -1)
                nc.vector.tensor_tensor(K.meansq[:, :], tmp[:, :], mv[:, :], ALU.mult)

            @block.scalar
            def _(act):
                act.wait_ge(var_ready, 1)
                act.sem_inc(var_ready, -1)
                nc.scalar.activation(root[:, :], var[:, :], ACT.Sqrt).then_inc(root_ready, 1)


def source_terms(nc, I, K, atab):
    fp32, ALU, ACT = mybir.dt.float32, mybir.AluOpType, mybir.ActivationFunctionType
    with ExitStack() as ctx:
        def sb(n, shape):
            return ctx.enter_context(nc.sbuf_tensor(f"st_{n}", shape, fp32))

        def ps(n):
            return ctx.enter_context(nc.psum_tensor(f"st_{n}", [P, 512], fp32))

        def sem(n):
            return K.sem(f"st_{n}")
        w0, att, attbd, terms = sb("w0", [P, C, D]), sb("att", [P, C, 2]), sb("attbd", [P, C, 2 * HEADS]), sb("terms", [P, T, HEADS])
        xs, xT = sb("xs", [P, 2, D]), sb("xT", [P, 2, C, P])
        psW, psT, psL = ps("psW"), [ps("psT0"), ps("psT1")], [ps("psL0"), ps("psL1")]
        loaded, stored, att_ready, wa_full, wa_ready = (sem(n) for n in ("loaded", "stored", "att_ready", "wa_full", "wa_ready"))
        xs_ready, xt_full, xt_ready, l_full, l_free, chain = (sem(n) for n in ("xs_ready", "xt_full", "xt_ready", "l_full", "l_free", "chain"))
        terms_ready = sem("terms_ready")
        with nc.Block() as block:
            @block.sync
            def _(sp):
                sp.dma_start(w0[:, :, :], I["W0"].rearrange("(c p) n -> p c n", p=P)).then_inc(loaded, 16)
                sp.dma_start(att[:, :, :], I["att"].rearrange("(c p) n -> p c n", p=P)).then_inc(loaded, 16)
                sp.wait_ge(terms_ready, 1)
                sp.sem_inc(terms_ready, -1)
                sp.dma_start(atab.rearrange("(t p) n -> p t n", p=P), terms[:, :, :]).then_inc(stored, 16)
                sp.wait_ge(stored, 16)

            @block.vector
            def _(dve):
                def norm(t, k):
                    nc.vector.tensor_scalar(xs[:, k, :].unsqueeze(1), K.X[:, bass.ds(t, 1), :],
                                            K.mean[:, bass.ds(t, 1)], K.rstd[:, bass.ds(t, 1)],
                                            ALU.subtract, ALU.mult).then_inc(xs_ready, 1)

                def body(t, k, final):
                    dve.wait_ge(l_full, 1)
                    dve.sem_inc(l_full, -1)
                    copy = nc.vector.tensor_copy(terms[:, bass.ds(t, 1), :], psL[k][:, 0:HEADS].unsqueeze(1))
                    if final:
                        copy.then_inc(chain, 1)
                        dve.wait_ge(chain, 1)
                        dve.sem_inc(chain, -1)
                    else:
                        copy.then_inc(l_free, 1)
                        norm(t + 2, k)
                norm(0, 0)
                norm(1, 1)
                dve.wait_ge(loaded, 32)
                for c in range(C):
                    for s in range(2):
                        last = nc.vector.tensor_scalar(attbd[:, c, s * HEADS:(s + 1) * HEADS], K.blockmask[:, c, :],
                                                       att[:, c, s:s + 1], None, ALU.mult)
                last.then_inc(att_ready, 1)
                dve.wait_ge(wa_full, 1)
                dve.sem_inc(wa_full, -1)
                nc.vector.tensor_copy(K.wa[:, :, :], psW[:, 0:C * 16].rearrange("p (c n) -> p c n", c=C)).then_inc(wa_ready, 1)
                with dve.Fori(0, T // 2 - 1) as i:
                    for k in range(2):
                        body(2 * i + k, k, False)
                body(T - 2, 0, True)
                body(T - 1, 1, True)
                dve.sem_inc(terms_ready, 1)

            @block.scalar
            def _(act):
                with act.Fori(0, T // 2) as i:
                    for k in range(2):
                        act.wait_ge(xt_full, 1)
                        act.sem_inc(xt_full, -1)
                        nc.scalar.activation(xT[:, k, :, :], psT[k][:, 0:D].rearrange("p (c n) -> p c n", c=C),
                                             ACT.Copy).then_inc(xt_ready, 1)

            @block.tensor
            def _(pe):
                def transposes(k):
                    pe.wait_ge(xs_ready, 1)
                    pe.sem_inc(xs_ready, -1)
                    for c in range(C):
                        last = nc.tensor.transpose(psT[k][:, c * P:(c + 1) * P], xs[:, k, c * P:(c + 1) * P], K.ident[:, :])
                    last.then_inc(xt_full, 1)

                def terms_of(k, final):
                    pe.wait_ge(xt_ready, 1)
                    pe.sem_inc(xt_ready, -1)
                    if not final:
                        transposes(1 - k)
                    pe.wait_ge(l_free, 1)
                    pe.sem_inc(l_free, -1)
                    for c in range(C):
                        last = nc.tensor.matmul(psL[k][:, 0:HEADS], xT[:, k, c, :], K.wa[:, c, 0:HEADS], start=(c == 0), stop=(c == C - 1))
                    last.then_inc(l_full, 1)
                pe.sem_inc(l_free, 2)
                transposes(0)
                pe.wait_ge(att_ready, 1)
                pe.sem_inc(att_ready, -1)
                for m in range(C):
                    for c in range(C):
                        last = nc.tensor.matmul(psW[:, m * 16:(m + 1) * 16], w0[:, c, m * P:(m + 1) * P],
                                                attbd[:, c, :], start=(c == 0), stop=(c == C - 1))
                last.then_inc(wa_full, 1)
                pe.wait_ge(wa_ready, 1)
                pe.sem_inc(wa_ready, -1)
                with pe.Fori(0, T // 2 - 1) as i:
                    for k in range(2):
                        terms_of(k, False)
                terms_of(0, False)
                terms_of(1, True)


def gather_terms(nc, K, pool, atab, first, last):
    def issue(i, h):
        a, b = PART[h]
        nc.gpsimd.tensor_copy(K.cur[:, a:b], K.src_p[:, bass.ds(i * HJ + a, b - a)]).then_inc(K.cur_set, 1)
        pool.wait_ge(K.cur_set, 1)
        pool.sem_inc(K.cur_set, -1)
        for k in range(a, b):
            nc.gpsimd.indirect_dma_start(
                out=K.got[:, k, :], out_offset=None, in_=atab,
                in_offset=bass.IndirectOffsetOnAxis(ap=K.cur[:, k:k + 1].bitcast(mybir.dt.uint32), axis=0)
            ).then_inc(K.got_in[h], 16)

    def collect(i, h):
        a, b = PART[h]
        pool.wait_ge(K.got_in[h], (i + 1) * (16 * (b - a)))
        pool.sem_inc(K.passed, 1)
        nc.gpsimd.tensor_copy(K.term[:, bass.ds(i * HJ + a, b - a), :], K.got[:, a:b, :]).then_inc(K.cur_set, 1)
        pool.wait_ge(K.cur_set, 1)
        pool.sem_inc(K.cur_set, -1)
    issue(first, 0)
    if last - first > 1:
        with pool.Fori(first, last - 1) as i:
            issue(i, 1)
            collect(i, 0)
            issue(i + 1, 0)
            collect(i, 1)
    issue(last - 1, 1)
    collect(last - 1, 0)
    collect(last - 1, 1)


def project(nc, I, K, htab, atab):
    fp32, ALU, ACT = mybir.dt.float32, mybir.AluOpType, mybir.ActivationFunctionType
    with ExitStack() as ctx:
        def sb(n, shape):
            return ctx.enter_context(nc.sbuf_tensor(f"pj_{n}", shape, fp32))

        def ps(n):
            return ctx.enter_context(nc.psum_tensor(f"pj_{n}", [P, 512], fp32))

        def sem(n):
            return K.sem(f"pj_{n}")
        w0t, wqkv, wn1 = sb("w0t", [P, C, HW]), sb("wqkv", [P, C, 3 * D]), sb("wn1", [P, C])
        root, scale, tmp = sb("root", [P, T]), sb("scale", [P, T]), sb("tmp", [P, T])
        xs, xT = sb("xs", [P, 2, D]), sb("xT", [P, 2, C, P])
        low, pos = sb("low", [P, 2, 2 * D]), sb("pos", [P, 2, 2 * D])
        kb, vb = sb("kb", [P, 2, D]), sb("vb", [P, 2, C, P + 1])
        psT, psKV = ps("psT"), ps("psKV")
        psH, psQ, psV = ([ps(f"ps{x}{j}") for j in range(2)] for x in "HQV")
        loaded, stored, chain = sem("weights_loaded"), sem("tables_stored"), sem("chain")
        ms_ready, root_ready = sem("ms_ready"), sem("root_ready")
        w_ready = sem("w_ready")
        xs_ready, xt_full, xt_ready = sem("xs_ready"), sem("xt_full"), sem("xt_ready")
        h_full, q_full, v_full = sem("h_full"), sem("q_full"), sem("v_full")
        h_free, q_free, v_free = sem("h_free"), sem("q_free"), sem("v_free")
        low_ready, exp_ready, k_ready, v_ready = sem("low_ready"), sem("exp_ready"), sem("k_ready"), sem("v_ready")
        kv_used, kv_done, h_done = sem("kv_used"), sem("kv_done"), sem("h_done")
        with nc.Block() as block:
            @block.sync
            def _(sp):
                sp.dma_start(w0t[:, :, 0:D], I["W0T"].rearrange("(c p) n -> p c n", p=P)).then_inc(loaded, 16)
                sp.dma_start(wqkv[:, :, :], I["w_qkv"].rearrange("(c p) n -> p c n", p=P)).then_inc(loaded, 16)
                sp.dma_start(wn1[:, :], I["w_norm1"]).then_inc(loaded, 16)
                sp.wait_ge(h_done, 1)
                sp.sem_inc(h_done, -1)
                sp.dma_start(htab.rearrange("(t p) n -> p t n", p=P), K.H[:, :, 0:TW]).then_inc(stored, 16)
                sp.wait_ge(stored, 16)

            @block.vector
            def _(dve):
                nc.vector.memset(kb[:, :, :], 0.0)
                nc.vector.memset(vb[:, :, :, :], 0.0)
                nc.vector.tensor_scalar(tmp[:, :], K.meansq[:, :], 1e-6, None, ALU.add).then_inc(chain, 1)
                dve.wait_ge(chain, 1)
                dve.sem_inc(chain, -1)
                nc.vector.tensor_copy(root[:, :], tmp[:, :]).then_inc(ms_ready, 1)
                dve.wait_ge(root_ready, 1)
                dve.sem_inc(root_ready, -1)
                nc.vector.reciprocal(scale[:, :], root[:, :]).then_inc(chain, 1)
                dve.wait_ge(chain, 1)
                dve.sem_inc(chain, -1)
                nc.vector.tensor_tensor(scale[:, :], scale[:, :], K.rstd[:, :], ALU.mult).then_inc(chain, 1)
                dve.wait_ge(chain, 1)
                dve.sem_inc(chain, -1)
                dve.wait_ge(loaded, 48)
                nc.vector.tensor_copy(w0t[:, :, D:HW], K.wa[:, :, :])
                for c in range(C):
                    last = nc.vector.tensor_scalar(wqkv[:, c, :], wqkv[:, c, :], wn1[:, c:c + 1], None, ALU.mult)
                last.then_inc(w_ready, 1)

                def norm(t, k):
                    nc.vector.tensor_scalar(xs[:, k, :].unsqueeze(1), K.X[:, bass.ds(t, 1), :],
                                            K.mean[:, bass.ds(t, 1)], scale[:, bass.ds(t, 1)],
                                            ALU.subtract, ALU.mult).then_inc(xs_ready, 1)

                def body(i, final):
                    for k in range(2):
                        t = 2 * i + k
                        dve.wait_ge(h_full, 1)
                        dve.sem_inc(h_full, -1)
                        nc.vector.tensor_scalar(K.H[:, bass.ds(t, 1), :], psH[k][:, 0:HW].unsqueeze(1),
                                                root[:, bass.ds(t, 1)], None, ALU.mult).then_inc(h_free, 1)
                        dve.wait_ge(kv_used, 1)
                        dve.sem_inc(kv_used, -1)
                        dve.wait_ge(q_full, 1)
                        dve.sem_inc(q_full, -1)
                        nc.vector.tensor_scalar(low[:, k, :], psQ[k][:, :], 0.0, None, ALU.min).then_inc(low_ready, 1)
                        nc.vector.tensor_copy(vb[:, k, :, P:P + 1],
                                              K.real[:, bass.ds(t, 1)].unsqueeze(1).broadcast_to([P, C, 1]))
                        dve.wait_ge(v_full, 1)
                        dve.sem_inc(v_full, -1)
                        nc.vector.tensor_copy(vb[:, k, :, 0:P],
                                              psV[k][:, 0:D].rearrange("p (c n) -> p c n", c=C)).then_inc(v_ready, 1)
                        if not final:
                            norm(t + 2, k)
                        dve.wait_ge(exp_ready, 1)
                        dve.sem_inc(exp_ready, -1)
                        nc.vector.tensor_tensor(kb[:, k, :], pos[:, k, D:2 * D], low[:, k, D:2 * D],
                                                ALU.add).then_inc(k_ready, 1)
                        nc.vector.tensor_tensor(K.Q[:, bass.ds(t, 1), :], pos[:, k, 0:D].unsqueeze(1),
                                                low[:, k, 0:D].unsqueeze(1), ALU.add)
                norm(0, 0)
                norm(1, 1)
                with dve.Fori(0, T // 2 - 1) as i:
                    body(i, False)
                body(T // 2 - 1, True)
                nc.vector.memset(K.kvbd[:, :, :, :], 0.0).then_inc(chain, 1)
                dve.wait_ge(chain, 1)
                dve.sem_inc(chain, -1)
                dve.wait_ge(kv_done, 1)
                dve.sem_inc(kv_done, -1)
                for c in range(C):
                    psk = psKV[:, c * (P + 1):(c + 1) * (P + 1)]
                    mask = K.blockmask[:, c, 4 * c:4 * c + 4].unsqueeze(2).broadcast_to([P, 4, HD])
                    nc.vector.tensor_tensor(K.kvbd[:, c, 0, :].rearrange("p (h m) -> p h m", m=HD),
                                            psk[:, 0:P].rearrange("p (h m) -> p h m", m=HD), mask, ALU.mult)
                    last = nc.vector.tensor_tensor(K.kvbd[:, c, 1, :].rearrange("p (h m) -> p h m", m=HD),
                                                   psk[:, P:P + 1].unsqueeze(2).broadcast_to([P, 4, HD]), mask, ALU.mult)
                last.then_inc(h_done, 1)

            @block.scalar
            def _(act):
                act.wait_ge(ms_ready, 1)
                act.sem_inc(ms_ready, -1)
                nc.scalar.activation(root[:, :], root[:, :], ACT.Sqrt).then_inc(root_ready, 1)
                with act.Fori(0, T // 2) as i:
                    for k in range(2):
                        act.wait_ge(xt_full, 1)
                        act.sem_inc(xt_full, -1)
                        nc.scalar.activation(xT[:, k, :, :], psT[:, 0:D].rearrange("p (c n) -> p c n", c=C),
                                             ACT.Copy).then_inc(xt_ready, 1)
                        act.wait_ge(low_ready, 1)
                        act.sem_inc(low_ready, -1)
                        nc.scalar.activation(pos[:, k, :], psQ[k][:, :], ACT.Relu).then_inc(q_free, 1)
                        nc.scalar.activation(low[:, k, :], low[:, k, :], ACT.Exp).then_inc(exp_ready, 1)

            @block.gpsimd
            def _(pool):
                gather_terms(nc, K, pool, atab, 0, 11)

            @block.tensor
            def _(pe):
                pe.wait_ge(w_ready, 1)
                pe.sem_inc(w_ready, -1)
                nc.tensor.matmul(psKV[:, 0:C * (P + 1)], kb[:, 0, 0:P], vb[:, 0, :, :].rearrange("p c n -> p (c n)"),
                                 start=True, stop=False, skip_group_check=True)
                pe.sem_inc(k_ready, 1)
                pe.sem_inc(v_ready, 1)
                pe.sem_inc(kv_used, 1)
                pe.sem_inc(h_free, 2)
                pe.sem_inc(q_free, 2)

                def transposes(k):
                    pe.wait_ge(xs_ready, 1)
                    pe.sem_inc(xs_ready, -1)
                    for c in range(C):
                        last = nc.tensor.transpose(psT[:, c * P:(c + 1) * P], xs[:, k, c * P:(c + 1) * P], K.ident[:, :])
                    last.then_inc(xt_full, 1)

                def kv(k, stop=False):
                    pe.wait_ge(k_ready, 1)
                    pe.sem_inc(k_ready, -1)
                    pe.wait_ge(v_ready, 1)
                    pe.sem_inc(v_ready, -1)
                    for c in range(C):
                        last = nc.tensor.matmul(psKV[:, c * (P + 1):(c + 1) * (P + 1)], kb[:, k, c * P:(c + 1) * P],
                                                vb[:, k, c, :], start=False, stop=stop, skip_group_check=True)
                    return last

                def body(i, final):
                    for k in range(2):
                        pe.wait_ge(xt_ready, 1)
                        pe.sem_inc(xt_ready, -1)
                        pe.wait_ge(h_free, 1)
                        pe.sem_inc(h_free, -1)
                        for c in range(C):
                            last = nc.tensor.matmul(psH[k][:, 0:HW], xT[:, k, c, :], w0t[:, c, :],
                                                    start=(c == 0), stop=(c == C - 1))
                        last.then_inc(h_full, 1)
                        pe.wait_ge(q_free, 1)
                        pe.sem_inc(q_free, -1)
                        for m in range(C):
                            for c in range(C):
                                nc.tensor.matmul(psQ[k][:, m * P:(m + 1) * P], wqkv[:, c, m * P:(m + 1) * P],
                                                 xT[:, k, c, :], start=(c == 0), stop=(c == C - 1))
                        for c in range(C):
                            last = nc.tensor.matmul(psQ[k][:, D:2 * D], xT[:, k, c, :], wqkv[:, c, D:2 * D],
                                                    start=(c == 0), stop=(c == C - 1))
                        last.then_inc(q_full, 1)
                        for c in range(C):
                            last = nc.tensor.matmul(psV[k][:, 0:D], xT[:, k, c, :], wqkv[:, c, 2 * D:3 * D],
                                                    start=(c == 0), stop=(c == C - 1))
                        last.then_inc(v_full, 1)
                        if not (final and k == 1):
                            transposes(1 - k)
                        kv(1 - k).then_inc(kv_used, 1)
                transposes(0)
                with pe.Fori(0, T // 2 - 1) as i:
                    body(i, False)
                body(T // 2 - 1, True)
                kv(1, stop=True).then_inc(kv_done, 1)


def mix0(nc, I, K, atab):
    fp32, ALU, ACT = mybir.dt.float32, mybir.AluOpType, mybir.ActivationFunctionType
    with ExitStack() as ctx:
        def sb(n, shape):
            return ctx.enter_context(nc.sbuf_tensor(f"mx_{n}", shape, fp32))

        def ps(n):
            return ctx.enter_context(nc.psum_tensor(f"mx_{n}", [P, 512], fp32))

        def sem(n):
            return K.sem(f"mx_{n}")
        wout, bout, wn2, h0 = sb("wout", [P, C, D]), sb("bout", [1, D]), sb("wn2", [P, D]), sb("h0", [P, T, D])
        den, oT, junk = sb("den", [P, 2, 2 * D]), sb("oT", [P, 2, C, D]), sb("sq", [P, 2, D])
        nmr, xn, ssq, tmp, gain = sb("nmr", [P, T]), sb("xn", [P, 2, D]), sb("ssq", [P, T]), sb("tmp", [P, T]), sb("gain", [P, 2, D])
        psN, psD = [ps("psN0"), ps("psN1")], [ps("psD0"), ps("psD1")]
        psO = [ps("psO0"), ps("psO1")]
        loaded, chain = sem("weights_loaded"), sem("chain")
        n_full, d_full, nd_free, o_ready = sem("num_full"), sem("den_full"), sem("numden_free"), sem("o_ready")
        out_full, out_free, xn_ready, xn_free = sem("out_full"), sem("out_free"), sem("xn_ready"), sem("xn_free")
        nmr_ready, h0_ready, root_ready, ms_ready = sem("nmr_ready"), sem("h0_ready"), sem("root_ready"), sem("ms_ready")
        gain_ready, gain_free, wn2_loaded, sq_done = sem("gain_ready"), sem("gain_free"), sem("wn2_loaded"), sem("sq_done")
        with nc.Block() as block:
            @block.sync
            def _(sp):
                sp.dma_start(wout[:, :, :], I["w_out"].rearrange("(c p) n -> p c n", p=P)).then_inc(loaded, 16)
                sp.dma_start(bout[:, :], I["b_out"].rearrange("(a n) -> a n", a=1)).then_inc(loaded, 16)
                sp.dma_start(wn2[:, :], I["w_norm2"].partition_broadcast(P)).then_inc(wn2_loaded, 16)
                sp.wait_ge(wn2_loaded, 16)

            @block.gpsimd
            def _(pool):
                gather_terms(nc, K, pool, atab, 11, 21)

            @block.tensor
            def _(pe):
                pe.sem_inc(nd_free, 2)
                pe.sem_inc(out_free, 2)
                pe.wait_ge(loaded, 32)
                Qv = K.Q[:, :, :].rearrange("p t (c r) -> p c t r", c=C)

                def numden(i, k):
                    pe.wait_ge(nd_free, 1)
                    pe.sem_inc(nd_free, -1)
                    for ps, j, full in ((psN, 0, n_full), (psD, 1, d_full)):
                        for c in range(C):
                            last = nc.tensor.matmul(ps[k][:, c * D:(c + 1) * D].rearrange("p (t r) -> p t r", t=2),
                                                    K.kvbd[:, c, j, :], Qv[:, c, bass.ds(2 * i, 2), :], start=True, stop=True)
                        last.then_inc(full, 1)

                def out(k):
                    pe.wait_ge(o_ready, 1)
                    pe.sem_inc(o_ready, -1)
                    for r in range(2):
                        pe.wait_ge(out_free, 1)
                        pe.sem_inc(out_free, -1)
                        nc.tensor.matmul(psO[r][:, 0:D], K.ones[0:1, :], bout[:, :], start=True, stop=False)
                        for c in range(C):
                            last = nc.tensor.matmul(psO[r][:, 0:D], oT[:, k, c, r * P:(r + 1) * P], wout[:, c, :],
                                                    start=False, stop=(c == C - 1))
                        last.then_inc(out_full, 1)
                numden(0, 0)
                with pe.Fori(0, T // 4) as i:
                    numden(2 * i + 1, 1)
                    out(0)
                    numden(2 * i + 2, 0)
                    out(1)
                out(0)

            @block.vector
            def _(dve):
                nc.vector.tensor_scalar(nmr[:, :], K.mean[:, :], -1.0, None, ALU.mult).then_inc(chain, 1)
                dve.wait_ge(chain, 1)
                dve.sem_inc(chain, -1)
                nc.vector.tensor_tensor(nmr[:, :], nmr[:, :], K.rstd[:, :], ALU.mult).then_inc(nmr_ready, 1)

                def pair(i, k):
                    dve.wait_ge(n_full, 1)
                    dve.sem_inc(n_full, -1)
                    dve.wait_ge(d_full, 1)
                    dve.sem_inc(d_full, -1)
                    nc.vector.tensor_scalar(den[:, k, :], psD[k][:, :], 1e-6, None, ALU.add).then_inc(chain, 1)
                    dve.wait_ge(chain, 1)
                    dve.sem_inc(chain, -1)
                    nc.vector.reciprocal(den[:, k, :], den[:, k, :]).then_inc(chain, 1)
                    dve.wait_ge(chain, 1)
                    dve.sem_inc(chain, -1)
                    nc.vector.tensor_tensor(oT[:, k, :, :].rearrange("p c n -> p (c n)"), psN[k][:, :],
                                            den[:, k, :], ALU.mult).then_inc(chain, 1)
                    dve.wait_ge(chain, 1)
                    dve.sem_inc(chain, -1)
                    dve.sem_inc(nd_free, 1)
                    dve.sem_inc(o_ready, 1)
                    for r in range(2):
                        t = 2 * i + r
                        dve.wait_ge(out_full, 1)
                        dve.sem_inc(out_full, -1)
                        dve.wait_ge(xn_ready, 1)
                        dve.sem_inc(xn_ready, -1)
                        nc.vector.tensor_tensor(h0[:, bass.ds(t, 1), :], psO[r][:, 0:D].unsqueeze(1),
                                                xn[:, r, :].unsqueeze(1), ALU.add).then_inc(h0_ready, 1)
                with dve.Fori(0, T // 4) as i:
                    pair(2 * i, 0)
                    pair(2 * i + 1, 1)
                pair(T // 2 - 1, 0)
                dve.wait_ge(sq_done, 1)
                dve.sem_inc(sq_done, -1)
                nc.vector.tensor_scalar(tmp[:, :], ssq[:, :], 1.0 / D, 1e-6, ALU.mult, ALU.add).then_inc(chain, 1)
                dve.wait_ge(chain, 1)
                dve.sem_inc(chain, -1)
                nc.vector.tensor_copy(ssq[:, :], tmp[:, :]).then_inc(ms_ready, 1)
                dve.wait_ge(root_ready, 1)
                dve.sem_inc(root_ready, -1)
                nc.vector.reciprocal(tmp[:, :], ssq[:, :]).then_inc(chain, 1)
                dve.wait_ge(chain, 1)
                dve.sem_inc(chain, -1)
                dve.sem_inc(gain_free, 2)
                dve.wait_ge(wn2_loaded, 16)
                with dve.Fori(0, T // 2) as i:
                    for r in range(2):
                        t = 2 * i + r
                        nc.vector.tensor_scalar(gain[:, r, :], wn2[:, :], tmp[:, bass.ds(t, 1)], 1.0,
                                                ALU.mult, ALU.add).then_inc(chain, 1)
                        dve.wait_ge(chain, 1)
                        dve.sem_inc(chain, -1)
                        nc.vector.tensor_tensor(gain[:, r, :].unsqueeze(1), gain[:, r, :].unsqueeze(1),
                                                h0[:, bass.ds(t, 1), :], ALU.mult).then_inc(chain, 1)
                        dve.wait_ge(chain, 1)
                        dve.sem_inc(chain, -1)
                        nc.vector.tensor_tensor(K.X[:, bass.ds(t, 1), :], K.X[:, bass.ds(t, 1), :],
                                                gain[:, r, :].unsqueeze(1), ALU.add)

            @block.scalar
            def _(act):
                act.wait_ge(nmr_ready, 1)
                act.sem_inc(nmr_ready, -1)
                act.sem_inc(xn_free, 2)

                def normal(t, r):
                    nc.scalar.activation(xn[:, r, :].unsqueeze(1), K.X[:, bass.ds(t, 1), :], ACT.Identity,
                                         bias=nmr[:, bass.ds(t, 1)], scale=K.rstd[:, bass.ds(t, 1)]).then_inc(xn_ready, 1)

                def square(t, r):
                    act.wait_ge(h0_ready, 1)
                    act.sem_inc(h0_ready, -1)
                    nc.scalar.activation(junk[:, r, :].unsqueeze(1), h0[:, bass.ds(t, 1), :], ACT.Square,
                                         accum_out=ssq[:, bass.ds(t, 1)]).then_inc(out_free, 1)
                normal(0, 0)
                normal(1, 1)
                with act.Fori(0, T // 2 - 1) as i:
                    for r in range(2):
                        square(2 * i + r, r)
                        normal(2 * i + 2 + r, r)
                square(T - 2, 0)
                square(T - 1, 1)
                act.drain().then_inc(sq_done, 1)
                act.wait_ge(ms_ready, 1)
                act.sem_inc(ms_ready, -1)
                nc.scalar.activation(ssq[:, :], ssq[:, :], ACT.Sqrt).then_inc(root_ready, 1)


def edge_tables(nc, I, K, atab):
    fp32, i32, bf16, ALU = mybir.dt.float32, mybir.dt.int32, mybir.dt.bfloat16, mybir.AluOpType
    with ExitStack() as ctx:
        def sb(n, shape, dt=fp32):
            return ctx.enter_context(nc.sbuf_tensor(f"et_{n}", shape, dt))

        def ps(n):
            return ctx.enter_context(nc.psum_tensor(f"et_{n}", [P, 512], fp32))

        def sem(n):
            return K.sem(f"et_{n}")
        dst_i, lo_i, hi_i = sb("dst_i", [P, ET], i32), sb("lo_i", [P, ET], i32), sb("hi_i", [P, ET], i32)
        prev_i, prev = sb("prev_i", [P, 1], i32), sb("prev", [P, 1])
        dstf, lo, hi, hits = sb("dstf", [P, ET]), sb("lo", [P, ET]), sb("hi", [P, ET]), sb("hits", [P, ET])
        bound, cnt, ends, ends_i, rank = sb("bound", [P, T]), sb("cnt", [P, T]), sb("ends", [P, T]), sb("ends_i", [P, T], i32), sb("rank", [P, T])
        ns, cs_i, cs, es = sb("ns", [P, S]), sb("cs_i", [SQ, SG], i32), sb("cs", [SQ, SG]), sb("es", [SQ, SG])
        es_i = sb("es_i", [SQ, SG], i32)
        rows_i, rows = sb("rows_i", [SQ, 2, SG, P], i32), sb("rows", [SQ, 2, SG, P])
        onelo, onehi = sb("onelo", [P, HJ, P], bf16), sb("onehi", [P, HJ, T], bf16)
        zero = sb("zero", [P, P], bf16)
        last_e = sb("last_e", [P, T])
        psC, psH, psU, psR = ps("psC"), ps("psH"), ps("psU"), [ps("psR0"), ps("psR1")]
        prev_set, loaded, chain, cs_ready = sem("prev_set"), sem("loaded"), sem("chain"), sem("cs_ready")
        cnt_ready, ends_full, es_ready, rows_in, rows_ready, rows_full = (
            sem("cnt_ready"), sem("ends_full"), sem("es_ready"), sem("rows_in"), sem("rows_ready"), sem("rows_full"))
        hot_ready, hot_free = [sem("hot_ready0"), sem("hot_ready1")], [sem("hot_free0"), sem("hot_free1")]
        hist_full, deg_ready, cum_full = sem("hist_full"), sem("deg_ready"), sem("cum_full")
        zero_set = sem("zero_set")
        with nc.Block() as block:
            @block.sync
            def _(sp):
                sp.dma_start(dst_i[:, :], I["dst"].rearrange("(p f) -> p f", p=P)).then_inc(loaded, 16)
                sp.wait_ge(prev_set, 1)
                sp.sem_inc(prev_set, -1)
                sp.dma_start(prev_i[1:P, :], I["dst"].rearrange("(p f) -> p f", p=P)[0:P - 1, ET - 1:ET],
                             allow_slow_non_contiguous=True).then_inc(loaded, 16)

            @block.gpsimd
            def _(pool):
                pool.iota(cs_i[:, :], pattern=[[SQ, SG]], base=0, channel_multiplier=1).then_inc(cs_ready, 1)
                pool.wait_ge(es_ready, 1)
                pool.sem_inc(es_ready, -1)
                for g in range(SG):
                    for j, table in enumerate(("src", "dst")):
                        nc.gpsimd.indirect_dma_start(
                            out=rows_i[:, j, g, :], out_offset=None, in_=I[table].rearrange("(t e) -> t e", e=P),
                            in_offset=bass.IndirectOffsetOnAxis(ap=es_i[:, g:g + 1].bitcast(mybir.dt.uint32), axis=0)
                        ).then_inc(rows_in, 16)
                gather_terms(nc, K, pool, atab, 21, ET // HJ)

            @block.vector
            def _(dve):
                nc.vector.memset(prev_i[:, :], -1).then_inc(prev_set, 1)
                nc.vector.memset(zero[:, :], 0.0).then_inc(zero_set, 1)
                nc.vector.memset(ns[:, :], 0.0)
                nc.vector.memset(es[:, :], 0.0)
                nc.vector.memset(K.base[:, S:S + 8], 0.0)
                nc.vector.memset(K.ns[:, 0:4], T - 1)
                nc.vector.memset(K.ns[:, 4 + S:], 0)
                dve.wait_ge(loaded, 32)
                nc.vector.tensor_copy(dstf[:, :], dst_i[:, :])
                nc.vector.tensor_copy(prev[:, :], prev_i[:, :])
                nc.vector.tensor_scalar(lo_i[:, :], dst_i[:, :], P - 1, None, ALU.bitwise_and)
                nc.vector.tensor_scalar(hi_i[:, :], dst_i[:, :], 7, None, ALU.arith_shift_right)
                nc.vector.tensor_scalar(bound[:, :], K.iota[:, 0:T], float(P), float(P), ALU.mult, ALU.add).then_inc(chain, 1)
                dve.wait_ge(chain, 1)
                dve.sem_inc(chain, -1)
                nc.vector.tensor_copy(lo[:, :], lo_i[:, :])
                nc.vector.tensor_copy(hi[:, :], hi_i[:, :])
                nc.vector.tensor_tensor(K.cap[:, 1:ET], dstf[:, 1:ET], dstf[:, 0:ET - 1], ALU.is_equal)
                nc.vector.tensor_tensor(K.cap[:, 0:1], dstf[:, 0:1], prev[:, :], ALU.is_equal).then_inc(chain, 1)
                dve.wait_ge(chain, 1)
                dve.sem_inc(chain, -1)
                nc.vector.tensor_reduce(K.capall[:, :], K.cap[:, :], mybir.AxisListType.X, ALU.min).then_inc(chain, 1)
                dve.wait_ge(chain, 1)
                dve.sem_inc(chain, -1)
                nc.vector.tensor_scalar(K.cap[:, :], K.cap[:, :], 2 * BIG, -BIG, ALU.mult, ALU.add)
                nc.vector.tensor_scalar(K.capall[:, :], K.capall[:, :], 2 * BIG, -BIG, ALU.mult, ALU.add).then_inc(chain, 1)
                dve.wait_ge(chain, 1)
                dve.sem_inc(chain, -1)
                with dve.Fori(0, T) as n:
                    nc.vector.tensor_scalar(hits[:, :], dstf[:, :], bound[:, bass.ds(n, 1)], None,
                                            ALU.is_lt, ALU.add, accum_out=cnt[:, bass.ds(n, 1)]).then_inc(chain, 1)
                    dve.wait_ge(chain, 1)
                    dve.sem_inc(chain, -1)
                nc.vector.tensor_copy(bound[:, 0:1], cnt[:, 0:1]).then_inc(cnt_ready, 1)
                dve.wait_ge(ends_full, 1)
                dve.sem_inc(ends_full, -1)
                nc.vector.tensor_copy(ends[:, :], psC[:, 0:T])
                nc.vector.tensor_copy(ends_i[:, :], psC[:, 0:T]).then_inc(chain, 1)
                dve.wait_ge(chain, 1)
                dve.sem_inc(chain, -1)
                nc.vector.tensor_scalar(ends_i[:, :], ends_i[:, :], 7, None, ALU.arith_shift_right).then_inc(chain, 1)
                dve.wait_ge(chain, 1)
                dve.sem_inc(chain, -1)
                nc.vector.tensor_tensor(rank[:, :], ends_i[:, :], K.iota[:, 0:T], ALU.add).then_inc(chain, 1)
                dve.wait_ge(chain, 1)
                dve.sem_inc(chain, -1)
                dve.wait_ge(cs_ready, 1)
                dve.sem_inc(cs_ready, -1)
                nc.vector.tensor_copy(cs[:, :], cs_i[:, :]).then_inc(chain, 1)
                dve.wait_ge(chain, 1)
                dve.sem_inc(chain, -1)
                with dve.Fori(0, T - 1) as n:
                    nc.vector.scalar_tensor_tensor(ns[:, :], K.iota[:, 0:S], rank[:, bass.ds(n, 1)], ns[:, :],
                                                   ALU.is_gt, ALU.add)
                    nc.vector.scalar_tensor_tensor(es[:, :], cs[:, :], rank[0:SQ, bass.ds(n, 1)], es[:, :],
                                                   ALU.is_gt, ALU.add).then_inc(chain, 1)
                    dve.wait_ge(chain, 1)
                    dve.sem_inc(chain, -1)
                nc.vector.tensor_tensor(es[:, :], cs[:, :], es[:, :], ALU.subtract).then_inc(chain, 1)
                dve.wait_ge(chain, 1)
                dve.sem_inc(chain, -1)
                nc.vector.tensor_copy(K.ns[:, 4:4 + S], ns[:, :])
                nc.vector.tensor_copy(es_i[:, :], es[:, :]).then_inc(es_ready, 1)

                with dve.Fori(0, ET // HJ) as i:
                    for h, (a, b) in enumerate(PART):
                        n = b - a
                        dve.wait_ge(hot_free[h], 1)
                        dve.sem_inc(hot_free[h], -1)
                        nc.vector.tensor_tensor(onehi[:, a:b, :], hi[:, bass.ds(i * HJ + a, n)].unsqueeze(2).broadcast_to([P, n, T]),
                                                K.iota[:, 0:T].unsqueeze(1).broadcast_to([P, n, T]), ALU.is_equal)
                        nc.vector.tensor_tensor(onelo[:, a:b, :], lo[:, bass.ds(i * HJ + a, n)].unsqueeze(2).broadcast_to([P, n, P]),
                                                K.iota[:, 0:P].unsqueeze(1).broadcast_to([P, n, P]), ALU.is_equal).then_inc(hot_ready[h], 1)
                dve.wait_ge(rows_in, 16 * 2 * SG)
                nc.vector.tensor_copy(rows[:, :, :, :], rows_i[:, :, :, :]).then_inc(rows_ready, 1)
                dve.wait_ge(hist_full, 1)
                dve.sem_inc(hist_full, -1)
                nc.vector.tensor_copy(K.deg[:, :], psH[:, 0:T]).then_inc(deg_ready, 1)
                dve.wait_ge(rows_full, 1)
                dve.sem_inc(rows_full, -1)
                nc.vector.tensor_copy(K.src_s[:, :], psR[0][:, 0:S])
                nc.vector.scalar_tensor_tensor(K.base[:, 0:S], ns[:, :], float(P), psR[1][:, 0:S], ALU.mult, ALU.subtract)
                dve.wait_ge(cum_full, 1)
                dve.sem_inc(cum_full, -1)
                nc.vector.tensor_scalar(last_e[:, 0:1], psU[:, 0:1], -1.0, None, ALU.add)
                nc.vector.scalar_tensor_tensor(last_e[:, 1:T], psU[:, 1:T], -1.0, ends[:, 0:T - 1],
                                               ALU.add, ALU.add).then_inc(chain, 1)
                dve.wait_ge(chain, 1)
                dve.sem_inc(chain, -1)
                nc.vector.tensor_scalar(last_e[:, :], last_e[:, :], 0.0, None, ALU.max).then_inc(chain, 1)
                dve.wait_ge(chain, 1)
                dve.sem_inc(chain, -1)
                nc.vector.tensor_copy(K.last_edge[:, :], last_e[:, :])

            @block.tensor
            def _(pe):
                pe.wait_ge(zero_set, 1)
                pe.sem_inc(zero_set, -1)
                nc.tensor.matmul(psH[:, 0:T], zero[:, :], zero[:, 0:T], start=True, stop=False)
                pe.sem_inc(hot_free[0], 1)
                pe.sem_inc(hot_free[1], 1)
                pe.wait_ge(cnt_ready, 1)
                pe.sem_inc(cnt_ready, -1)
                nc.tensor.matmul(psC[:, 0:T], K.ones[:, :], cnt[:, :], start=True, stop=True).then_inc(ends_full, 1)
                with pe.Fori(0, ET // HJ) as i:
                    for h, (a, b) in enumerate(PART):
                        pe.wait_ge(hot_ready[h], 1)
                        pe.sem_inc(hot_ready[h], -1)
                        for k in range(a, b):
                            last = nc.tensor.matmul(psH[:, 0:T], onelo[:, k, :], onehi[:, k, :], start=False, stop=False)
                        last.then_inc(hot_free[h], 1)
                nc.tensor.matmul(psH[:, 0:T], zero[:, :], zero[:, 0:T], start=False, stop=True).then_inc(hist_full, 1)
                pe.wait_ge(rows_ready, 1)
                pe.sem_inc(rows_ready, -1)
                for j in range(2):
                    for g in range(SG):
                        last = nc.tensor.transpose(psR[j][:, g * SQ:(g + 1) * SQ], rows[:, j, g, :], K.ident[0:SQ, 0:SQ])
                last.then_inc(rows_full, 1)
                pe.wait_ge(deg_ready, 1)
                pe.sem_inc(deg_ready, -1)
                nc.tensor.matmul(psU[:, 0:T], K.upper[:, :], K.deg[:, :], start=True, stop=True).then_inc(cum_full, 1)


def softmax_maxima(nc, K, ftab):
    fp32, i32, ALU, ACT = mybir.dt.float32, mybir.dt.int32, mybir.AluOpType, mybir.ActivationFunctionType
    with ExitStack() as ctx:
        def sb(n, shape, dt=fp32):
            return ctx.enter_context(nc.sbuf_tensor(f"sm_{n}", shape, dt))

        def sem(n):
            return K.sem(f"sm_{n}")
        run = sb("run", [P, ET, HEADS])
        part, partT, capT = sb("part", [P, 2, HEADS]), sb("partT", [HEADS, P]), sb("capT", [HEADS, P])
        carryT, carry = sb("carryT", [HEADS, P + 1]), sb("carry", [P, HEADS])
        top, has = sb("top", [P, T, HEADS]), sb("has", [P, T, 2])
        tmp = sb("tmp", [P, T, HEADS])
        psT = ctx.enter_context(nc.psum_tensor("sm_psT", [P, 512], fp32))
        psB = ctx.enter_context(nc.psum_tensor("sm_psB", [P, 512], fp32))
        chain = sem("chain")
        part_ready, partT_full, carry_ready, carry_full = sem("part_ready"), sem("partT_full"), sem("carry_ready"), sem("carry_full")
        run_ready, stored, top_in, self_ready = sem("run_ready"), sem("stored"), sem("top_in"), sem("self_ready")
        with nc.Block() as block:
            @block.gpsimd
            def _(pool):
                pool.wait_ge(stored, 16)
                for t in range(T):
                    nc.gpsimd.indirect_dma_start(
                        out=top[:, t, :], out_offset=None, in_=ftab,
                        in_offset=bass.IndirectOffsetOnAxis(ap=K.last_edge[:, t:t + 1].bitcast(mybir.dt.uint32), axis=0)
                    ).then_inc(top_in, 16)

            @block.sync
            def _(sp):
                sp.wait_ge(run_ready, 1)
                sp.sem_inc(run_ready, -1)
                sp.dma_start(ftab.rearrange("(p f) h -> p (f h)", p=P), run[:, :, :].rearrange("p f h -> p (f h)")).then_inc(stored, 16)

            @block.vector
            def _(dve):
                nc.vector.memset(carryT[:, 0:1], -BIG).then_inc(chain, 1)
                dve.wait_ge(chain, 1)
                dve.sem_inc(chain, -1)
                for h in range(HEADS):
                    last = nc.vector.tensor_tensor_scan(run[:, :, h], K.cap[:, :], K.term[:, :, h], -BIG, ALU.min, ALU.max)
                last.then_inc(chain, 1)
                dve.wait_ge(chain, 1)
                dve.sem_inc(chain, -1)
                nc.vector.tensor_copy(part[:, 0, :], run[:, ET - 1, :])
                nc.vector.tensor_copy(part[:, 1, :], K.capall[:, 0:1].broadcast_to([P, HEADS])).then_inc(part_ready, 1)
                dve.wait_ge(partT_full, 1)
                dve.sem_inc(partT_full, -1)
                nc.vector.tensor_copy(partT[:, :], psT[0:HEADS, 0:P])
                nc.vector.tensor_copy(capT[:, :], psT[0:HEADS, P:2 * P]).then_inc(chain, 1)
                dve.wait_ge(chain, 1)
                dve.sem_inc(chain, -1)
                nc.vector.tensor_tensor_scan(carryT[:, 1:P + 1], capT[:, :], partT[:, :], -BIG, ALU.min, ALU.max).then_inc(carry_ready, 1)
                dve.wait_ge(carry_full, 1)
                dve.sem_inc(carry_full, -1)
                nc.vector.tensor_copy(carry[:, :], psB[:, 0:HEADS]).then_inc(chain, 1)
                dve.wait_ge(chain, 1)
                dve.sem_inc(chain, -1)
                for h in range(HEADS):
                    last = nc.vector.tensor_tensor_scan(run[:, :, h], K.cap[:, :], K.term[:, :, h], carry[:, h:h + 1], ALU.min, ALU.max)
                last.then_inc(run_ready, 1)
                nc.vector.tensor_scalar(has[:, :, 0], K.deg[:, :], 1.0, None, ALU.min).then_inc(chain, 1)
                dve.wait_ge(chain, 1)
                dve.sem_inc(chain, -1)
                nc.vector.tensor_scalar(has[:, :, 1], has[:, :, 0], BIG, -BIG, ALU.mult, ALU.add).then_inc(chain, 1)
                dve.wait_ge(chain, 1)
                dve.sem_inc(chain, -1)
                dve.wait_ge(top_in, 16 * T)
                a_s, a_d = K.H[:, :, D:TW], K.H[:, :, TW:HW]
                nc.vector.tensor_tensor(top[:, :, :], top[:, :, :], has[:, :, 0:1].broadcast_to([P, T, HEADS]), ALU.mult).then_inc(chain, 1)
                dve.wait_ge(chain, 1)
                dve.sem_inc(chain, -1)
                nc.vector.tensor_tensor(top[:, :, :], top[:, :, :], has[:, :, 1:2].broadcast_to([P, T, HEADS]), ALU.add).then_inc(chain, 1)
                dve.wait_ge(chain, 1)
                dve.sem_inc(chain, -1)
                nc.vector.tensor_tensor(top[:, :, :], top[:, :, :], a_s, ALU.max).then_inc(chain, 1)
                dve.wait_ge(chain, 1)
                dve.sem_inc(chain, -1)
                nc.vector.tensor_tensor(top[:, :, :], top[:, :, :], a_d, ALU.add).then_inc(chain, 1)
                dve.wait_ge(chain, 1)
                dve.sem_inc(chain, -1)
                nc.vector.scalar_tensor_tensor(K.node[:, :, HEADS:], top[:, :, :], 0.2, top[:, :, :], ALU.mult, ALU.max)
                nc.vector.tensor_copy(K.node[:, :, 0:HEADS], a_d)
                nc.vector.tensor_tensor(tmp[:, :, :], a_s, a_d, ALU.add).then_inc(chain, 1)
                dve.wait_ge(chain, 1)
                dve.sem_inc(chain, -1)
                nc.vector.scalar_tensor_tensor(tmp[:, :, :], tmp[:, :, :], 0.2, tmp[:, :, :], ALU.mult, ALU.max).then_inc(chain, 1)
                dve.wait_ge(chain, 1)
                dve.sem_inc(chain, -1)
                nc.vector.tensor_tensor(tmp[:, :, :], tmp[:, :, :], K.node[:, :, HEADS:], ALU.subtract).then_inc(self_ready, 1)

            @block.scalar
            def _(act):
                act.wait_ge(self_ready, 1)
                act.sem_inc(self_ready, -1)
                nc.scalar.activation(K.selfw[:, :, :], tmp[:, :, :], ACT.Exp)

            @block.tensor
            def _(pe):
                pe.wait_ge(part_ready, 1)
                pe.sem_inc(part_ready, -1)
                nc.tensor.transpose(psT[0:HEADS, 0:P], part[:, 0, :], K.ident[:, :])
                nc.tensor.transpose(psT[0:HEADS, P:2 * P], part[:, 1, :], K.ident[:, :]).then_inc(partT_full, 1)
                pe.wait_ge(carry_ready, 1)
                pe.sem_inc(carry_ready, -1)
                nc.tensor.transpose(psB[:, 0:HEADS], carryT[:, 0:P], K.ident[0:HEADS, 0:HEADS]).then_inc(carry_full, 1)


def gat(nc, I, K, htab):
    fp32, i32, ALU, ACT = mybir.dt.float32, mybir.dt.int32, mybir.AluOpType, mybir.ActivationFunctionType
    G = 4
    R = 4
    with ExitStack() as ctx:
        def sb(n, shape, dt=fp32):
            return ctx.enter_context(nc.sbuf_tensor(f"ga_{n}", shape, dt))

        def ps(n):
            return ctx.enter_context(nc.psum_tensor(f"ga_{n}", [P, 512], fp32))

        def sem(n):
            return K.sem(f"ga_{n}")
        cur, rows, wrows = sb("cur", [P, R, G], i32), sb("rows", [P, R, G, TW]), sb("wrows", [P, 2, G, TW])
        hot, hotT, z = sb("hot", [P, R, G, P]), sb("hotT", [P, 2, G, P]), sb("z", [P, 2, G, HEADS])
        acc, zero, b0 = sb("acc", [P, T, TW]), sb("zero", [P, P]), sb("b0", [P, D])
        off = sb("off", [P, 2, G, P])
        psT, psN, psA = ps("psT"), [ps("psN0"), ps("psN1")], [ps(f"psA{k}") for k in range(G)]
        chain, pchain, achain, passed = sem("chain"), sem("pchain"), sem("achain"), sem("passed")
        rows_in, rows_free = [sem(f"rows_in{h}") for h in range(R)], sem("rows_free")
        hot_ready, hotT_full, hotT_ready, node_full = sem("hot_ready"), sem("hotT_full"), sem("hotT_ready"), sem("node_full")
        z_ready, w_ready, wrows_ready, acc_full, acc_free = sem("z_ready"), sem("w_ready"), sem("wrows_ready"), sem("acc_full"), sem("acc_free")
        zero_set, b0_in, low_ready, exp_ready = sem("zero_set"), sem("b0_in"), sem("low_ready"), sem("exp_ready")
        STAGES = S // G
        with nc.Block() as block:
            @block.gpsimd
            def _(pool):
                pool.sem_inc(rows_free, R)
                with pool.Fori(0, STAGES // R) as i:
                    for h in range(R):
                        pool.wait_ge(rows_free, 1)
                        pool.sem_inc(rows_free, -1)
                        nc.gpsimd.tensor_copy(cur[:, h, :], K.src_s[:, bass.ds((R * i + h) * G, G)]).then_inc(pchain, 1)
                        pool.wait_ge(pchain, 1)
                        pool.sem_inc(pchain, -1)
                        for k in range(G):
                            nc.gpsimd.indirect_dma_start(
                                out=rows[:, h, k, :], out_offset=None, in_=htab,
                                in_offset=bass.IndirectOffsetOnAxis(ap=cur[:, h, k:k + 1].bitcast(mybir.dt.uint32), axis=0)
                            ).then_inc(rows_in[h], 16)

            @block.sync
            def _(sp):
                sp.dma_start(b0[:, :], I["b0"].partition_broadcast(P)).then_inc(b0_in, 16)

            @block.vector
            def _(dve):
                nc.vector.memset(zero[:, :], 0.0).then_inc(zero_set, 1)
                nc.vector.memset(acc[:, :, :], 0.0).then_inc(chain, 1)
                dve.wait_ge(chain, 1)
                dve.sem_inc(chain, -1)

                def add(q):
                    ns = node_tiles(nc, K, dve, q * G, G)
                    for k in range(G):
                        dve.wait_ge(acc_full, 1)
                        dve.sem_inc(acc_full, -1)
                        n = ns[k]
                        nc.vector.tensor_tensor(acc[:, bass.ds(n, 1), :], acc[:, bass.ds(n, 1), :],
                                                psA[k][:, 0:TW].unsqueeze(1), ALU.add).then_inc(chain, 1)
                        dve.wait_ge(chain, 1)
                        dve.sem_inc(chain, -1)
                        dve.sem_inc(acc_free, 1)

                with dve.Fori(0, STAGES // R) as i:
                    for h in range(R):
                        q, w2 = R * i + h, h % 2
                        dve.wait_ge(node_full, 1)
                        dve.sem_inc(node_full, -1)
                        dve.wait_ge(rows_in[h], (i + 1) * (16 * G))
                        dve.sem_inc(passed, 1)
                        nd = psN[w2][:, 0:G * 16].rearrange("p (k n) -> p k n", k=G)
                        nc.vector.tensor_tensor(z[:, w2, :, :], rows[:, h, :, D:TW], nd[:, :, 0:HEADS], ALU.add).then_inc(chain, 1)
                        dve.wait_ge(chain, 1)
                        dve.sem_inc(chain, -1)
                        nc.vector.scalar_tensor_tensor(z[:, w2, :, :], z[:, w2, :, :], 0.2, z[:, w2, :, :], ALU.mult, ALU.max).then_inc(chain, 1)
                        dve.wait_ge(chain, 1)
                        dve.sem_inc(chain, -1)
                        nc.vector.tensor_tensor(z[:, w2, :, :], z[:, w2, :, :], nd[:, :, HEADS:], ALU.subtract).then_inc(chain, 1)
                        dve.wait_ge(chain, 1)
                        dve.sem_inc(chain, -1)
                        nc.vector.tensor_scalar(z[:, w2, :, :], z[:, w2, :, :], 0.0, None, ALU.min).then_inc(z_ready, 1)
                        add(q)
                        dve.wait_ge(w_ready, 1)
                        dve.sem_inc(w_ready, -1)
                        nc.vector.tensor_tensor(
                            wrows[:, w2, :, 0:D].rearrange("p k (a d) -> p k a d", d=HD),
                            rows[:, h, :, 0:D].rearrange("p k (a d) -> p k a d", d=HD),
                            wrows[:, w2, :, D:TW].unsqueeze(3).broadcast_to([P, G, HEADS, HD]), ALU.mult).then_inc(chain, 1)
                        dve.wait_ge(chain, 1)
                        dve.sem_inc(chain, -1)
                        dve.sem_inc(wrows_ready, 1)
                        dve.sem_inc(rows_free, 1)
                add(STAGES)
                a_den = acc[:, :, D:TW]
                by_head = lambda x: x.rearrange("p t (a d) -> p t a d", d=HD)
                nc.vector.tensor_tensor(a_den, a_den, K.selfw[:, :, :], ALU.add).then_inc(chain, 1)
                dve.wait_ge(chain, 1)
                dve.sem_inc(chain, -1)
                nc.vector.tensor_scalar(a_den, a_den, 1e-16, None, ALU.add).then_inc(chain, 1)
                dve.wait_ge(chain, 1)
                dve.sem_inc(chain, -1)
                nc.vector.reciprocal(a_den, a_den).then_inc(chain, 1)
                dve.wait_ge(chain, 1)
                dve.sem_inc(chain, -1)
                dve.wait_ge(b0_in, 16)
                for t0, t1 in ((0, T // 2), (T // 2, T)):
                    n = t1 - t0
                    hs, a = K.H[:, t0:t1, 0:D], acc[:, t0:t1, 0:D]
                    for t in range(t0, t1):
                        last = nc.vector.tensor_tensor(K.H[:, t, 0:D].rearrange("p (a d) -> p a d", d=HD), K.H[:, t, 0:D].rearrange("p (a d) -> p a d", d=HD),
                                                       K.selfw[:, t, :].unsqueeze(2).broadcast_to([P, HEADS, HD]), ALU.mult)
                    last.then_inc(chain, 1)
                    dve.wait_ge(chain, 1)
                    dve.sem_inc(chain, -1)
                    nc.vector.tensor_tensor(a, a, hs, ALU.add).then_inc(chain, 1)
                    dve.wait_ge(chain, 1)
                    dve.sem_inc(chain, -1)
                    for t in range(t0, t1):
                        last = nc.vector.tensor_tensor(acc[:, t, 0:D].rearrange("p (a d) -> p a d", d=HD), acc[:, t, 0:D].rearrange("p (a d) -> p a d", d=HD),
                                                       acc[:, t, D:TW].unsqueeze(2).broadcast_to([P, HEADS, HD]), ALU.mult)
                    last.then_inc(chain, 1)
                    dve.wait_ge(chain, 1)
                    dve.sem_inc(chain, -1)
                    nc.vector.tensor_tensor(a, a, b0[:, :].unsqueeze(1).broadcast_to([P, n, D]), ALU.add).then_inc(chain, 1)
                    dve.wait_ge(chain, 1)
                    dve.sem_inc(chain, -1)
                    nc.vector.tensor_scalar(hs, a, 0.0, None, ALU.min).then_inc(low_ready, 1)
                    nc.vector.tensor_scalar(a, a, 0.0, -1.0, ALU.max, ALU.add).then_inc(chain, 1)
                    dve.wait_ge(chain, 1)
                    dve.sem_inc(chain, -1)
                    nc.vector.tensor_tensor(K.X[:, t0:t1, :], K.X[:, t0:t1, :], a, ALU.add).then_inc(chain, 1)
                    dve.wait_ge(chain, 1)
                    dve.sem_inc(chain, -1)
                    dve.wait_ge(exp_ready, 1)
                    dve.sem_inc(exp_ready, -1)
                    nc.vector.tensor_tensor(K.X[:, t0:t1, :], K.X[:, t0:t1, :], hs, ALU.add)

            @block.scalar
            def _(act):
                def onehot(q, h):
                    for k in range(G):
                        last = nc.scalar.activation(off[:, h % 2, k, :], K.iota[:, 0:P], ACT.Abs, bias=K.base[:, bass.ds(q * G + k, 1)])
                    last.then_inc(achain, 1)
                    act.wait_ge(achain, 1)
                    act.sem_inc(achain, -1)
                    nc.scalar.activation(hot[:, h, :, :], off[:, h % 2, :, :], ACT.Relu, bias=K.ones[:, 0:1], scale=-1.0).then_inc(hot_ready, 1)

                def copy(h):
                    act.wait_ge(hotT_full, 1)
                    act.sem_inc(hotT_full, -1)
                    nc.scalar.activation(hotT[:, h, :, :].rearrange("p k n -> p (k n)"), psT[:, :], ACT.Copy).then_inc(hotT_ready, 1)
                onehot(0, 0)
                onehot(1, 1)
                copy(0)
                with act.Fori(0, STAGES // R) as i:
                    for h in range(R):
                        copy((h + 1) % 2)
                        onehot(R * i + h + 2, (h + 2) % R)
                        act.wait_ge(z_ready, 1)
                        act.sem_inc(z_ready, -1)
                        nc.scalar.activation(wrows[:, h % 2, :, D:TW], z[:, h % 2, :, :], ACT.Exp).then_inc(w_ready, 1)
                for t0, t1 in ((0, T // 2), (T // 2, T)):
                    act.wait_ge(low_ready, 1)
                    act.sem_inc(low_ready, -1)
                    nc.scalar.activation(K.H[:, t0:t1, 0:D], K.H[:, t0:t1, 0:D], ACT.Exp).then_inc(exp_ready, 1)

            @block.tensor
            def _(pe):
                def transposes(h):
                    pe.wait_ge(hot_ready, 1)
                    pe.sem_inc(hot_ready, -1)
                    for k in range(G):
                        last = nc.tensor.transpose(psT[:, k * P:(k + 1) * P], hot[:, h, k, :], K.ident[:, :])
                    last.then_inc(hotT_full, 1)

                def node_terms(q, h):
                    pe.wait_ge(hotT_ready, 1)
                    pe.sem_inc(hotT_ready, -1)
                    ns = node_tiles(nc, K, pe, (q + 1) * G, G)
                    for k in range(G):
                        last = nc.tensor.matmul(psN[h][:, k * 16:(k + 1) * 16], hotT[:, h, k, :],
                                                K.node[:, bass.ds(ns[k], 1), :].rearrange("p a b -> p (a b)"), start=True, stop=True)
                    last.then_inc(node_full, 1)
                pe.wait_ge(zero_set, 1)
                pe.sem_inc(zero_set, -1)
                for k in range(G):
                    nc.tensor.matmul(psA[k][:, 0:TW], zero[:, :], K.iota[:, 0:TW], start=True, stop=True).then_inc(acc_full, 1)
                transposes(0)
                node_terms(0, 0)
                transposes(1)
                with pe.Fori(0, STAGES // R) as i:
                    for h in range(R):
                        node_terms(R * i + h + 1, (h + 1) % 2)
                        transposes((h + 2) % R)
                        pe.wait_ge(wrows_ready, 1)
                        pe.sem_inc(wrows_ready, -1)
                        for k in range(G):
                            pe.wait_ge(acc_free, 1)
                            pe.sem_inc(acc_free, -1)
                            nc.tensor.matmul(psA[k][:, 0:TW], hot[:, h, k, :], wrows[:, h % 2, k, :],
                                             start=True, stop=True).then_inc(acc_full, 1)


def choose(nc, I, K, wtab):
    fp32, ALU = mybir.dt.float32, mybir.AluOpType
    AX = mybir.AxisListType.X
    with ExitStack() as ctx:
        def sb(n, shape):
            return ctx.enter_context(nc.sbuf_tensor(f"ch_{n}", shape, fp32))

        def sem(n):
            return K.sem(f"ch_{n}")
        wr, br, w, tmp = sb("wr", [P, D]), sb("br", [P, 1]), sb("w", [P, T]), sb("tmp", [P, T])
        prod, wT, every, above = sb("prod", [P, 2, D]), sb("wT", [T, P]), sb("every", [P, T * P]), sb("above", [P, 2, T * P])
        rank, least, leastT, edge = sb("rank", [P, T]), sb("least", [P, 1]), sb("leastT", [1, P]), sb("edge", [1, 1])
        gt, eq, cum, tot, both, need = sb("gt", [P, T]), sb("eq", [P, T]), sb("cum", [P, T]), sb("tot", [P, T + 1]), sb("both", [P, 2]), sb("need", [P, 1])
        zeros, tau = sb("zeros", [P, T]), sb("tau", [P, 1])
        ps = [ctx.enter_context(nc.psum_tensor(f"ch_ps{j}", [P, 512], fp32)) for j in range(4)]
        loaded, chain, w_ready, wT_full, wT_ready, stored, every_in = (
            sem("loaded"), sem("chain"), sem("w_ready"), sem("wT_full"), sem("wT_ready"), sem("stored"), sem("every_in"))
        least_ready, leastT_full, edge_ready, tau_full, marks_ready, marks_full = (
            sem("least_ready"), sem("leastT_full"), sem("edge_ready"), sem("tau_full"), sem("marks_ready"), sem("marks_full"))
        with nc.Block() as block:
            @block.sync
            def _(sp):
                sp.dma_start(wr[:, :], I["f0_wr"].partition_broadcast(P)).then_inc(loaded, 16)
                sp.dma_start(br[:, :], I["f0_br"].partition_broadcast(P)).then_inc(loaded, 16)
                sp.wait_ge(wT_ready, 1)
                sp.sem_inc(wT_ready, -1)
                sp.dma_start(wtab.rearrange("(t p) -> t p", p=P), wT[:, :]).then_inc(stored, 16)
                sp.wait_ge(stored, 16)
                sp.dma_start(every[:, :], wtab.partition_broadcast(P)).then_inc(every_in, 16)

            @block.vector
            def _(dve):
                nc.vector.memset(zeros[:, :], 0.0)
                nc.vector.memset(tot[:, 0:1], 0.0)
                dve.wait_ge(loaded, 32)
                with dve.Fori(0, T // 2) as i:
                    for k in range(2):
                        nc.vector.scalar_tensor_tensor(
                            prod[:, k, :].unsqueeze(1), K.X[:, bass.ds(2 * i + k, 1), :], K.mean[:, bass.ds(2 * i + k, 1)],
                            wr[:, :].unsqueeze(1), ALU.subtract, ALU.mult, accum_out=w[:, bass.ds(2 * i + k, 1)]).then_inc(chain, 1)
                        dve.wait_ge(chain, 1)
                        dve.sem_inc(chain, -1)
                nc.vector.tensor_tensor(w[:, :], w[:, :], K.rstd[:, :], ALU.mult).then_inc(chain, 1)
                dve.wait_ge(chain, 1)
                dve.sem_inc(chain, -1)
                nc.vector.tensor_scalar(w[:, :], w[:, :], br[:, 0:1], None, ALU.add).then_inc(chain, 1)
                dve.wait_ge(chain, 1)
                dve.sem_inc(chain, -1)
                nc.vector.tensor_tensor(w[:, :], w[:, :], K.real[:, :], ALU.mult).then_inc(chain, 1)
                dve.wait_ge(chain, 1)
                dve.sem_inc(chain, -1)
                nc.vector.tensor_scalar(tmp[:, :], K.real[:, :], BIG, -BIG, ALU.mult, ALU.add).then_inc(chain, 1)
                dve.wait_ge(chain, 1)
                dve.sem_inc(chain, -1)
                nc.vector.tensor_tensor(w[:, :], w[:, :], tmp[:, :], ALU.add).then_inc(w_ready, 1)
                dve.wait_ge(wT_full, 1)
                dve.sem_inc(wT_full, -1)
                nc.vector.tensor_copy(wT[:, :], ps[0][0:T, 0:P]).then_inc(wT_ready, 1)
                dve.wait_ge(every_in, 16)
                with dve.Fori(0, T // 2) as i:
                    for k in range(2):
                        nc.vector.tensor_scalar(above[:, k, :], every[:, :], w[:, bass.ds(2 * i + k, 1)], None,
                                                ALU.is_gt, ALU.add, accum_out=rank[:, bass.ds(2 * i + k, 1)]).then_inc(chain, 1)
                        dve.wait_ge(chain, 1)
                        dve.sem_inc(chain, -1)
                nc.vector.tensor_scalar(gt[:, :], rank[:, :], float(KEEP), None, ALU.is_lt).then_inc(chain, 1)
                dve.wait_ge(chain, 1)
                dve.sem_inc(chain, -1)
                nc.vector.tensor_tensor(cum[:, :], w[:, :], gt[:, :], ALU.mult).then_inc(chain, 1)
                dve.wait_ge(chain, 1)
                dve.sem_inc(chain, -1)
                nc.vector.tensor_scalar(gt[:, :], gt[:, :], -BIG, BIG, ALU.mult, ALU.add).then_inc(chain, 1)
                dve.wait_ge(chain, 1)
                dve.sem_inc(chain, -1)
                nc.vector.tensor_tensor(cum[:, :], cum[:, :], gt[:, :], ALU.add).then_inc(chain, 1)
                dve.wait_ge(chain, 1)
                dve.sem_inc(chain, -1)
                nc.vector.tensor_reduce(least[:, :], cum[:, :], AX, ALU.min).then_inc(least_ready, 1)
                dve.wait_ge(leastT_full, 1)
                dve.sem_inc(leastT_full, -1)
                nc.vector.tensor_reduce(edge[:, :], ps[1][0:1, 0:P], AX, ALU.min).then_inc(edge_ready, 1)
                dve.wait_ge(tau_full, 1)
                dve.sem_inc(tau_full, -1)
                nc.vector.tensor_copy(tau[:, :], ps[2][:, 0:1]).then_inc(chain, 1)
                dve.wait_ge(chain, 1)
                dve.sem_inc(chain, -1)
                nc.vector.tensor_scalar(gt[:, :], w[:, :], tau[:, 0:1], None, ALU.is_gt)
                nc.vector.tensor_scalar(eq[:, :], w[:, :], tau[:, 0:1], None, ALU.is_equal).then_inc(chain, 1)
                dve.wait_ge(chain, 1)
                dve.sem_inc(chain, -1)
                nc.vector.tensor_reduce(both[:, 0:1], gt[:, :], AX, ALU.add).then_inc(marks_ready, 1)
                dve.wait_ge(marks_full, 1)
                dve.sem_inc(marks_full, -1)
                nc.vector.tensor_scalar(need[:, :], ps[3][:, 0:1], -1.0, float(KEEP), ALU.mult, ALU.add)
                nc.vector.tensor_copy(cum[:, :], ps[3][:, 64:64 + T])
                nc.vector.tensor_tensor_scan(tot[:, 1:T + 1], zeros[:, :], ps[3][:, 128:128 + T], 0.0, ALU.add, ALU.add).then_inc(chain, 1)
                dve.wait_ge(chain, 1)
                dve.sem_inc(chain, -1)
                nc.vector.tensor_tensor(cum[:, :], cum[:, :], tot[:, 0:T], ALU.add).then_inc(chain, 1)
                dve.wait_ge(chain, 1)
                dve.sem_inc(chain, -1)
                nc.vector.tensor_scalar(cum[:, :], cum[:, :], need[:, 0:1], None, ALU.is_le).then_inc(chain, 1)
                dve.wait_ge(chain, 1)
                dve.sem_inc(chain, -1)
                nc.vector.tensor_tensor(eq[:, :], eq[:, :], cum[:, :], ALU.mult).then_inc(chain, 1)
                dve.wait_ge(chain, 1)
                dve.sem_inc(chain, -1)
                nc.vector.tensor_tensor(gt[:, :], gt[:, :], eq[:, :], ALU.add).then_inc(chain, 1)
                dve.wait_ge(chain, 1)
                dve.sem_inc(chain, -1)
                nc.vector.tensor_tensor(K.coef[:, :], gt[:, :], w[:, :], ALU.mult)

            @block.tensor
            def _(pe):
                pe.wait_ge(w_ready, 1)
                pe.sem_inc(w_ready, -1)
                nc.tensor.transpose(ps[0][0:T, 0:P], w[:, :], K.ident[:, :]).then_inc(wT_full, 1)
                pe.wait_ge(least_ready, 1)
                pe.sem_inc(least_ready, -1)
                nc.tensor.transpose(ps[1][0:1, 0:P], least[:, :], K.ident[:, :]).then_inc(leastT_full, 1)
                pe.wait_ge(edge_ready, 1)
                pe.sem_inc(edge_ready, -1)
                nc.tensor.matmul(ps[2][:, 0:1], K.ones[0:1, :], edge[:, :], start=True, stop=True).then_inc(tau_full, 1)
                pe.wait_ge(marks_ready, 1)
                pe.sem_inc(marks_ready, -1)
                nc.tensor.matmul(ps[3][:, 0:1], K.ones[:, :], both[:, 0:1], start=True, stop=True)
                nc.tensor.matmul(ps[3][:, 64:64 + T], K.upper[:, :], eq[:, :], start=True, stop=True)
                nc.tensor.matmul(ps[3][:, 128:128 + T], K.ones[:, :], eq[:, :], start=True, stop=True).then_inc(marks_full, 1)


def ffn0(nc, I, K):
    fp32, ALU, ACT = mybir.dt.float32, mybir.AluOpType, mybir.ActivationFunctionType
    M = FF0 // P
    with ExitStack() as ctx:
        def sb(n, shape):
            return ctx.enter_context(nc.sbuf_tensor(f"f0_{n}", shape, fp32))

        def ps(n):
            return ctx.enter_context(nc.psum_tensor(f"f0_{n}", [P, 512], fp32))

        def sem(n):
            return K.sem(f"f0_{n}")
        w1, b1, w2, b2 = sb("w1", [P, C, FF0]), sb("b1", [P, M]), sb("w2", [P, M, D]), sb("b2", [1, D])
        xs, xT, hT = sb("xs", [P, 2, D]), sb("xT", [P, C, 2 * P]), sb("hT", [P, M, 2 * P])
        gain, shift = sb("gain", [P, T]), sb("shift", [P, T])
        psT, psU, psO = ps("psT"), [ps("psU0"), ps("psU1")], [ps("psO0"), ps("psO1")]
        loaded, chain = sem("loaded"), sem("chain")
        xs_ready, xT_full, xT_ready, up_full, up_free, hT_ready, out_full, out_free = (
            sem(n) for n in ("xs_ready", "xT_full", "xT_ready", "up_full", "up_free", "hT_ready", "out_full", "out_free"))
        xs_free = sem("xs_free")
        with nc.Block() as block:
            @block.sync
            def _(sp):
                sp.dma_start(w1[:, :, :], I["f0_w1"].rearrange("(c p) n -> p c n", p=P)).then_inc(loaded, 16)
                sp.dma_start(w2[:, :, :], I["f0_w2"].rearrange("(m p) n -> p m n", p=P)).then_inc(loaded, 16)
                sp.dma_start(b1[:, :], I["f0_b1"]).then_inc(loaded, 16)
                sp.dma_start(b2[:, :], I["f0_b2"].rearrange("(a n) -> a n", a=1)).then_inc(loaded, 16)

            @block.vector
            def _(dve):
                nc.vector.tensor_scalar(gain[:, :], K.rstd[:, :], 1.0, None, ALU.add)
                nc.vector.tensor_tensor(shift[:, :], K.mean[:, :], K.rstd[:, :], ALU.mult).then_inc(chain, 1)
                dve.wait_ge(chain, 1)
                dve.sem_inc(chain, -1)
                nc.vector.tensor_scalar(shift[:, :], shift[:, :], -1.0, None, ALU.mult).then_inc(chain, 1)
                dve.wait_ge(chain, 1)
                dve.sem_inc(chain, -1)

                def norm(i):
                    for r in range(2):
                        t = 2 * i + r
                        last = nc.vector.tensor_scalar(xs[:, r, :].unsqueeze(1), K.X[:, bass.ds(t, 1), :],
                                                       K.mean[:, bass.ds(t, 1)], K.rstd[:, bass.ds(t, 1)],
                                                       ALU.subtract, ALU.mult)
                    last.then_inc(xs_ready, 1)

                def finish(i):
                    for r in range(2):
                        t = 2 * i + r
                        x = K.X[:, bass.ds(t, 1), :]
                        nc.vector.tensor_scalar(x, x, gain[:, bass.ds(t, 1)], shift[:, bass.ds(t, 1)],
                                                ALU.mult, ALU.add).then_inc(chain, 1)
                        dve.wait_ge(chain, 1)
                        dve.sem_inc(chain, -1)
                        dve.wait_ge(out_full, 1)
                        dve.sem_inc(out_full, -1)
                        nc.vector.scalar_tensor_tensor(x, psO[r][:, 0:D].unsqueeze(1), K.coef[:, bass.ds(t, 1)], x,
                                                       ALU.mult, ALU.add).then_inc(out_free, 1)
                norm(0)
                with dve.Fori(0, T // 2 - 1) as i:
                    dve.wait_ge(xs_free, 1)
                    dve.sem_inc(xs_free, -1)
                    norm(i + 1)
                    finish(i)
                finish(T // 2 - 1)

            @block.scalar
            def _(act):
                with act.Fori(0, T // 2) as i:
                    act.wait_ge(xT_full, 1)
                    act.sem_inc(xT_full, -1)
                    nc.scalar.activation(xT[:, :, :].rearrange("p c n -> p (c n)"), psT[:, :], ACT.Copy).then_inc(xT_ready, 1)
                    for m in range(M):
                        act.wait_ge(up_full, 1)
                        act.sem_inc(up_full, -1)
                        nc.scalar.activation(hT[:, m, :], psU[m % 2][:, 0:2 * P], ACT.Gelu_apprx_tanh,
                                             bias=b1[:, m:m + 1]).then_inc(up_free, 1)

            @block.tensor
            def _(pe):
                pe.sem_inc(out_free, 2)
                pe.sem_inc(up_free, 2)
                pe.wait_ge(loaded, 64)

                def transposes():
                    pe.wait_ge(xs_ready, 1)
                    pe.sem_inc(xs_ready, -1)
                    for c in range(C):
                        for r in range(2):
                            last = nc.tensor.transpose(psT[:, (2 * c + r) * P:(2 * c + r + 1) * P],
                                                       xs[:, r, c * P:(c + 1) * P], K.ident[:, :])
                    last.then_inc(xT_full, 1)

                def body(final):
                    pe.wait_ge(xT_ready, 1)
                    pe.sem_inc(xT_ready, -1)
                    pe.sem_inc(xs_free, 1)
                    for m in range(M):
                        pe.wait_ge(up_free, 1)
                        pe.sem_inc(up_free, -1)
                        for c in range(C):
                            last = nc.tensor.matmul(psU[m % 2][:, 0:2 * P], w1[:, c, m * P:(m + 1) * P], xT[:, c, :],
                                                    start=(c == 0), stop=(c == C - 1))
                        last.then_inc(up_full, 1)
                    if not final:
                        transposes()
                    pe.wait_ge(up_free, 2)
                    pe.sem_inc(up_free, -2)
                    pe.sem_inc(up_free, 2)
                    for r in range(2):
                        pe.wait_ge(out_free, 1)
                        pe.sem_inc(out_free, -1)
                        nc.tensor.matmul(psO[r][:, 0:D], K.ones[0:1, :], b2[:, :], start=True, stop=False)
                        for m in range(M):
                            last = nc.tensor.matmul(psO[r][:, 0:D], hT[:, m, r * P:(r + 1) * P], w2[:, m, :],
                                                    start=False, stop=(m == M - 1))
                        last.then_inc(out_full, 1)
                transposes()
                with pe.Fori(0, T // 2 - 1) as i:
                    body(False)
                body(True)


def normalise(nc, K, ztab):
    fp32, ALU = mybir.dt.float32, mybir.AluOpType
    with ExitStack() as ctx:
        done, stored = K.sem("no_done"), K.sem("no_stored")
        with nc.Block() as block:
            @block.vector
            def _(dve):
                with dve.Fori(0, T // 2) as i:
                    for k in range(2):
                        t = 2 * i + k
                        nc.vector.tensor_scalar(K.Z[:, bass.ds(t, 1), :], K.X[:, bass.ds(t, 1), :], K.mean[:, bass.ds(t, 1)],
                                                K.rstd[:, bass.ds(t, 1)], ALU.subtract, ALU.mult).then_inc(done, 1)

            @block.sync
            def _(sp):
                sp.wait_ge(done, T)
                sp.sem_inc(done, -T)
                sp.dma_start(ztab.rearrange("(t p) n -> p t n", p=P), K.Z[:, :, :]).then_inc(stored, 16)
                sp.wait_ge(stored, 16)


def aggregate(nc, K, ztab):
    fp32, i32, ALU, ACT = mybir.dt.float32, mybir.dt.int32, mybir.AluOpType, mybir.ActivationFunctionType
    G = 4
    R = 4
    with ExitStack() as ctx:
        def sb(n, shape, dt=fp32):
            return ctx.enter_context(nc.sbuf_tensor(f"ag_{n}", shape, dt))

        def sem(n):
            return K.sem(f"ag_{n}")
        cur, rows, hot, zero = sb("cur", [P, R, G], i32), sb("rows", [P, R, G, D]), sb("hot", [P, 2, G, P]), sb("zero", [P, P])
        off = sb("off", [P, 2, G, P])
        psA = [ctx.enter_context(nc.psum_tensor(f"ag_psA{k}", [P, 512], fp32)) for k in range(G)]
        chain, pchain, achain, hot_free = sem("chain"), sem("pchain"), sem("achain"), sem("hot_free")
        rows_in, rows_free, passed = [sem(f"rows_in{h}") for h in range(R)], sem("rows_free"), sem("passed")
        hot_ready, acc_full, acc_free, zero_set = sem("hot_ready"), sem("acc_full"), sem("acc_free"), sem("zero_set")
        STAGES = S // G
        with nc.Block() as block:
            @block.gpsimd
            def _(pool):
                pool.sem_inc(rows_free, R - 1)
                with pool.Fori(0, STAGES // R) as i:
                    for h in range(R):
                        pool.wait_ge(rows_free, 1)
                        pool.sem_inc(rows_free, -1)
                        nc.gpsimd.tensor_copy(cur[:, h, :], K.src_s[:, bass.ds((R * i + h) * G, G)]).then_inc(pchain, 1)
                        pool.wait_ge(pchain, 1)
                        pool.sem_inc(pchain, -1)
                        for k in range(G):
                            nc.gpsimd.indirect_dma_start(
                                out=rows[:, h, k, :], out_offset=None, in_=ztab,
                                in_offset=bass.IndirectOffsetOnAxis(ap=cur[:, h, k:k + 1].bitcast(mybir.dt.uint32), axis=0)
                            ).then_inc(rows_in[h], 16)

            @block.vector
            def _(dve):
                nc.vector.memset(zero[:, :], 0.0).then_inc(zero_set, 1)
                nc.vector.memset(K.agg[:, :, :], 0.0).then_inc(chain, 1)
                dve.wait_ge(chain, 1)
                dve.sem_inc(chain, -1)

                def add(q):
                    ns = node_tiles(nc, K, dve, q * G, G)
                    for k in range(G):
                        dve.wait_ge(acc_full, 1)
                        dve.sem_inc(acc_full, -1)
                        n = ns[k]
                        nc.vector.tensor_tensor(K.agg[:, bass.ds(n, 1), :], K.agg[:, bass.ds(n, 1), :],
                                                psA[k][:, 0:D].unsqueeze(1), ALU.add).then_inc(chain, 1)
                        dve.wait_ge(chain, 1)
                        dve.sem_inc(chain, -1)
                        dve.sem_inc(acc_free, 1)
                    dve.sem_inc(rows_free, 1)
                    dve.sem_inc(hot_free, 1)
                with dve.Fori(0, STAGES // R) as i:
                    for h in range(R):
                        add(R * i + h)
                add(STAGES)

            @block.scalar
            def _(act):
                act.sem_inc(hot_free, 1)
                with act.Fori(0, STAGES // R) as i:
                    for h in range(R):
                        act.wait_ge(hot_free, 1)
                        act.sem_inc(hot_free, -1)
                        for k in range(G):
                            last = nc.scalar.activation(off[:, h % 2, k, :], K.iota[:, 0:P], ACT.Abs, bias=K.base[:, bass.ds((R * i + h) * G + k, 1)])
                        last.then_inc(achain, 1)
                        act.wait_ge(achain, 1)
                        act.sem_inc(achain, -1)
                        nc.scalar.activation(hot[:, h % 2, :, :], off[:, h % 2, :, :], ACT.Relu, bias=K.ones[:, 0:1], scale=-1.0).then_inc(hot_ready, 1)

            @block.tensor
            def _(pe):
                pe.wait_ge(zero_set, 1)
                pe.sem_inc(zero_set, -1)
                for k in range(G):
                    nc.tensor.matmul(psA[k][:, 0:D], zero[:, :], K.iota[:, 0:D], start=True, stop=True).then_inc(acc_full, 1)
                with pe.Fori(0, STAGES // R) as i:
                    for h in range(R):
                        pe.wait_ge(hot_ready, 1)
                        pe.sem_inc(hot_ready, -1)
                        pe.wait_ge(rows_in[h], (i + 1) * (16 * G))
                        pe.sem_inc(passed, 1)
                        for k in range(G):
                            pe.wait_ge(acc_free, 1)
                            pe.sem_inc(acc_free, -1)
                            nc.tensor.matmul(psA[k][:, 0:D], hot[:, h % 2, k, :], rows[:, h, k, :],
                                             start=True, stop=True).then_inc(acc_full, 1)


def combine1(nc, I, K):
    fp32, ALU, ACT = mybir.dt.float32, mybir.AluOpType, mybir.ActivationFunctionType
    with ExitStack() as ctx:
        def sb(n, shape):
            return ctx.enter_context(nc.sbuf_tensor(f"c1_{n}", shape, fp32))

        def sem(n):
            return K.sem(f"c1_{n}")
        wk, wv, wfc, wq = (sb(n, [P, C, D]) for n in ("wk", "wv", "wfc", "wq"))
        wself, wneigh = sb("wself", [P, C, D]), sb("wneigh", [P, C, D])
        bk, bv, bfc, bg, bq = sb("bk", [1, D]), sb("bv", [1, D]), sb("bfc", [1, D]), sb("bg", [1, D]), sb("bq", [P, C])
        xs, gram, col = sb("xs", [P, 2, D + 1]), sb("gram", [P, C, D + 1]), sb("col", [1, D + 1])
        t1, t1a, kvT, m2, m3, b3 = sb("t1", [P, C, D]), sb("t1a", [1, D]), sb("kvT", [P, C, P]), sb("m2", [P, C, D]), sb("m3", [P, C, D]), sb("b3", [1, D])
        rdeg, ys, xT, yT, g = sb("rdeg", [P, T]), sb("ys", [P, 2, 2, D]), sb("xT", [P, 2, C, P]), sb("yT", [P, 2, C, P]), sb("g", [P, 2, D])
        ps = [ctx.enter_context(nc.psum_tensor(f"c1_ps{j}", [P, 512], fp32)) for j in range(8)]
        loaded, chain, step = sem("loaded"), sem("chain"), sem("step")
        z_ready, z_free, ready, full, opened = sem("z_ready"), sem("z_free"), sem("ready"), sem("full"), sem("opened")
        ys_ready, yT_full, yT_ready, gm_full, gm_free, relu_ready, m_free = (
            sem(n) for n in ("ys_ready", "yT_full", "yT_ready", "gm_full", "gm_free", "relu_ready", "m_free"))
        with nc.Block() as block:
            @block.sync
            def _(sp):
                for a, n in ((wk, "WkT"), (wv, "WvT"), (wfc, "WfcT"), (wq, "Wq"), (wself, "Wself"), (wneigh, "Wneigh")):
                    sp.dma_start(a[:, :, :], I[n].rearrange("(c p) n -> p c n", p=P)).then_inc(loaded, 16)
                for a, n in ((bk, "bk"), (bv, "bv"), (bfc, "bfc"), (bg, "bgnn")):
                    sp.dma_start(a[:, :], I[n].rearrange("(a n) -> a n", a=1)).then_inc(loaded, 16)
                sp.dma_start(bq[:, :], I["bq"]).then_inc(loaded, 16)

            @block.vector
            def _(dve):
                dve.sem_inc(z_free, 2)
                with dve.Fori(0, T // 2) as i:
                    for k in range(2):
                        dve.wait_ge(z_free, 1)
                        dve.sem_inc(z_free, -1)
                        nc.vector.tensor_copy(xs[:, k, D:D + 1], K.real[:, bass.ds(2 * i + k, 1)])
                        nc.vector.tensor_scalar(xs[:, k, 0:D].unsqueeze(1), K.Z[:, bass.ds(2 * i + k, 1), :],
                                                K.real[:, bass.ds(2 * i + k, 1)], None, ALU.mult).then_inc(z_ready, 1)
                dve.wait_ge(full, 1)
                dve.sem_inc(full, -1)
                for c in range(C):
                    last = nc.vector.tensor_copy(gram[:, c, :], ps[c][:, 0:D + 1])
                nc.vector.memset(col[:, D:D + 1], float(N)).then_inc(ready, 1)
                dve.wait_ge(full, 1)
                dve.sem_inc(full, -1)
                nc.vector.tensor_copy(col[:, 0:D], ps[2][0:1, 0:D]).then_inc(ready, 1)
                dve.wait_ge(full, 1)
                dve.sem_inc(full, -1)
                for c in range(C):
                    nc.vector.tensor_copy(t1[:, c, :], ps[3 + c][:, 0:D])
                nc.vector.tensor_copy(t1a[:, :], ps[5][0:1, 0:D]).then_inc(ready, 1)
                dve.wait_ge(full, 1)
                dve.sem_inc(full, -1)
                for c in range(C):
                    mask = K.blockmask[:, c, 4 * c:4 * c + 4].unsqueeze(2).broadcast_to([P, 4, HD])
                    last = nc.vector.scalar_tensor_tensor(
                        kvT[:, c, :].rearrange("p (h m) -> p h m", m=HD),
                        ps[6 + c][:, c * P:(c + 1) * P].rearrange("p (h m) -> p h m", m=HD), 1.0 / N, mask, ALU.mult, ALU.mult)
                last.then_inc(ready, 1)
                dve.wait_ge(full, 1)
                dve.sem_inc(full, -1)
                for c in range(C):
                    last = nc.vector.tensor_copy(m2[:, c, :], ps[c][:, 0:D])
                last.then_inc(ready, 1)
                dve.wait_ge(full, 1)
                dve.sem_inc(full, -1)
                for c in range(C):
                    nc.vector.tensor_copy(m3[:, c, :], ps[2 + c][:, 0:D])
                nc.vector.tensor_copy(b3[:, :], ps[4][0:1, 0:D]).then_inc(ready, 1)

                nc.vector.tensor_scalar(rdeg[:, :], K.deg[:, :], 1.0, None, ALU.max).then_inc(chain, 1)
                dve.wait_ge(chain, 1)
                dve.sem_inc(chain, -1)
                nc.vector.reciprocal(rdeg[:, :], rdeg[:, :]).then_inc(chain, 1)
                dve.wait_ge(chain, 1)
                dve.sem_inc(chain, -1)

                def stage(t, k):
                    nc.vector.tensor_copy(ys[:, k, 0, :].unsqueeze(1), K.Z[:, bass.ds(t, 1), :])
                    nc.vector.tensor_scalar(ys[:, k, 1, :].unsqueeze(1), K.agg[:, bass.ds(t, 1), :], rdeg[:, bass.ds(t, 1)],
                                            None, ALU.mult).then_inc(ys_ready, 1)

                def finish(t, k):
                    x = K.X[:, bass.ds(t, 1), :]
                    dve.wait_ge(gm_full, 1)
                    dve.sem_inc(gm_full, -1)
                    nc.vector.tensor_tensor(x, x, ps[4 + k][:, 0:D].unsqueeze(1), ALU.add).then_inc(chain, 1)
                    dve.wait_ge(chain, 1)
                    dve.sem_inc(chain, -1)
                    dve.wait_ge(relu_ready, 1)
                    dve.sem_inc(relu_ready, -1)
                    nc.vector.tensor_tensor(x, x, g[:, k, :].unsqueeze(1), ALU.add).then_inc(m_free, 1)
                stage(0, 0)
                stage(1, 1)
                with dve.Fori(0, T // 2 - 1) as i:
                    for k in range(2):
                        finish(2 * i + k, k)
                        stage(2 * i + k + 2, k)
                finish(T - 2, 0)
                finish(T - 1, 1)

            @block.scalar
            def _(act):
                act.sem_inc(m_free, 2)
                with act.Fori(0, T // 2) as i:
                    for k in range(2):
                        act.wait_ge(yT_full, 1)
                        act.sem_inc(yT_full, -1)
                        nc.scalar.activation(xT[:, k, :, :].rearrange("p c n -> p (c n)"), ps[6 + k][:, 0:D], ACT.Copy)
                        nc.scalar.activation(yT[:, k, :, :].rearrange("p c n -> p (c n)"), ps[6 + k][:, D:2 * D],
                                             ACT.Copy).then_inc(yT_ready, 1)
                        act.wait_ge(m_free, 1)
                        act.sem_inc(m_free, -1)
                        act.wait_ge(gm_free, 1)
                        act.sem_inc(gm_free, -1)
                        nc.scalar.activation(g[:, k, :], ps[k][:, 0:D], ACT.Relu).then_inc(relu_ready, 1)

            @block.tensor
            def _(pe):
                pe.wait_ge(loaded, 16 * 11)
                for c in range(C):
                    nc.tensor.matmul(ps[c][:, 0:D + 1], K.ones[0:1, :], K.iota[0:1, 0:1].broadcast_to([1, D + 1]), start=True, stop=False)
                with pe.Fori(0, T // 2) as i:
                    for k in range(2):
                        pe.wait_ge(z_ready, 1)
                        pe.sem_inc(z_ready, -1)
                        for c in range(C):
                            last = nc.tensor.matmul(ps[c][:, 0:D + 1], xs[:, k, c * P:(c + 1) * P], xs[:, k, :], start=False, stop=False)
                        last.then_inc(z_free, 1)
                for c in range(C):
                    last = nc.tensor.matmul(ps[c][:, 0:D + 1], K.ones[0:1, :], K.iota[0:1, 0:1].broadcast_to([1, D + 1]), start=False, stop=True)
                last.then_inc(full, 1)
                pe.wait_ge(ready, 1)
                pe.sem_inc(ready, -1)
                for c in range(C):
                    last = nc.tensor.transpose(ps[2][0:1, c * P:(c + 1) * P], gram[:, c, D:D + 1], K.ident[:, :])
                last.then_inc(full, 1)
                pe.wait_ge(ready, 1)
                pe.sem_inc(ready, -1)
                for m in range(C):
                    for c in range(C):
                        nc.tensor.matmul(ps[3 + m][:, 0:D], gram[:, c, m * P:(m + 1) * P], wk[:, c, :], start=(c == 0), stop=False)
                    nc.tensor.matmul(ps[3 + m][:, 0:D], col[:, m * P:(m + 1) * P], bk[:, :], start=False, stop=True)
                for c in range(C):
                    nc.tensor.matmul(ps[5][0:1, 0:D], gram[:, c, D:D + 1], wk[:, c, :], start=(c == 0), stop=False)
                nc.tensor.matmul(ps[5][0:1, 0:D], col[:, D:D + 1], bk[:, :], start=False, stop=True).then_inc(full, 1)
                pe.wait_ge(ready, 1)
                pe.sem_inc(ready, -1)
                for m in range(C):
                    for c in range(C):
                        nc.tensor.matmul(ps[6 + m][:, 0:D], wv[:, c, m * P:(m + 1) * P], t1[:, c, :], start=(c == 0), stop=False)
                    last = nc.tensor.matmul(ps[6 + m][:, 0:D], bv[:, m * P:(m + 1) * P], t1a[:, :], start=False, stop=True)
                last.then_inc(full, 1)
                pe.wait_ge(ready, 1)
                pe.sem_inc(ready, -1)
                for c in range(C):
                    last = nc.tensor.matmul(ps[c][:, 0:D], kvT[:, c, :], wfc[:, c, :], start=True, stop=True)
                last.then_inc(full, 1)
                pe.wait_ge(ready, 1)
                pe.sem_inc(ready, -1)
                for m in range(C):
                    for c in range(C):
                        nc.tensor.matmul(ps[2 + m][:, 0:D], wq[:, c, m * P:(m + 1) * P], m2[:, c, :], start=(c == 0), stop=(c == C - 1))
                nc.tensor.matmul(ps[4][0:1, 0:D], K.ones[0:1, 0:1], bfc[:, :], start=True, stop=False)
                for c in range(C):
                    last = nc.tensor.matmul(ps[4][0:1, 0:D], bq[:, c:c + 1], m2[:, c, :], start=False, stop=(c == C - 1))
                last.then_inc(full, 1)
                pe.wait_ge(ready, 1)
                pe.sem_inc(ready, -1)

                def transposes(k):
                    pe.wait_ge(ys_ready, 1)
                    pe.sem_inc(ys_ready, -1)
                    for j in range(2):
                        for c in range(C):
                            last = nc.tensor.transpose(ps[6 + k][:, (2 * j + c) * P:(2 * j + c + 1) * P],
                                                       ys[:, k, j, c * P:(c + 1) * P], K.ident[:, :])
                    last.then_inc(yT_full, 1)

                def body(final):
                    for k in range(2):
                        pe.wait_ge(yT_ready, 1)
                        pe.sem_inc(yT_ready, -1)
                        if not (final and k == 1):
                            transposes(1 - k)
                        nc.tensor.matmul(ps[k][:, 0:D], K.ones[0:1, :], bg[:, :], start=True, stop=False)
                        for c in range(C):
                            nc.tensor.matmul(ps[k][:, 0:D], xT[:, k, c, :], wself[:, c, :], start=False, stop=False)
                        for c in range(C):
                            last = nc.tensor.matmul(ps[k][:, 0:D], yT[:, k, c, :], wneigh[:, c, :], start=False, stop=(c == C - 1))
                        last.then_inc(gm_free, 1)
                        nc.tensor.matmul(ps[4 + k][:, 0:D], K.ones[0:1, :], b3[:, :], start=True, stop=False)
                        for c in range(C):
                            last = nc.tensor.matmul(ps[4 + k][:, 0:D], xT[:, k, c, :], m3[:, c, :], start=False, stop=(c == C - 1))
                        last.then_inc(gm_full, 1)
                transposes(0)
                with pe.Fori(0, T // 2 - 1) as i:
                    body(False)
                body(True)


def route(nc, I, K):
    fp32, ALU, ACT = mybir.dt.float32, mybir.AluOpType, mybir.ActivationFunctionType
    AX = mybir.AxisListType.X
    with ExitStack() as ctx:
        def sb(n, shape):
            return ctx.enter_context(nc.sbuf_tensor(f"ro_{n}", shape, fp32))

        def sem(n):
            return K.sem(f"ro_{n}")
        wr, br, gamma, beta = sb("wr", [P, C, NE]), sb("br", [1, NE]), sb("gamma", [P, C]), sb("beta", [P, C])
        xs, xT, logit = sb("xs", [P, 2, D]), sb("xT", [P, 2, C, P]), sb("logit", [P, T, NE])
        eq, which, left, order = sb("eq", [P, T, NE]), sb("which", [P, T]), sb("left", [P, T, NE]), sb("order", [P, NE])
        one, two = sb("one", [P, T, NE]), sb("two", [P, T, NE])
        top, top2, e, w1, w2 = (sb(n, [P, T]) for n in ("top", "top2", "e", "w1", "w2"))
        psT = [ctx.enter_context(nc.psum_tensor(f"ro_psT{j}", [P, 512], fp32)) for j in range(2)]
        psL = [ctx.enter_context(nc.psum_tensor(f"ro_psL{j}", [P, 512], fp32)) for j in range(2)]
        loaded, chain, xs_ready, xT_full, xT_ready, l_full, gap_ready, e_ready = (
            sem(n) for n in ("loaded", "chain", "xs_ready", "xT_full", "xT_ready", "l_full", "gap_ready", "e_ready"))
        with nc.Block() as block:
            @block.sync
            def _(sp):
                sp.dma_start(wr[:, :, :], I["f1_Wr"].rearrange("(c p) n -> p c n", p=P)).then_inc(loaded, 16)
                sp.dma_start(br[:, :], I["f1_br"].rearrange("(a n) -> a n", a=1)).then_inc(loaded, 16)
                sp.dma_start(gamma[:, :], I["f1_gamma"]).then_inc(loaded, 16)
                sp.dma_start(beta[:, :], I["f1_beta"]).then_inc(loaded, 16)

            @block.vector
            def _(dve):
                def norm(t, k):
                    nc.vector.tensor_scalar(xs[:, k, :].unsqueeze(1), K.X[:, bass.ds(t, 1), :], K.mean[:, bass.ds(t, 1)],
                                            K.rstd[:, bass.ds(t, 1)], ALU.subtract, ALU.mult).then_inc(xs_ready, 1)

                def keep(t, k):
                    dve.wait_ge(l_full, 1)
                    dve.sem_inc(l_full, -1)
                    nc.vector.tensor_copy(logit[:, bass.ds(t, 1), :], psL[k][:, 0:NE].unsqueeze(1))
                norm(0, 0)
                norm(1, 1)
                with dve.Fori(0, T // 2 - 1) as i:
                    for k in range(2):
                        keep(2 * i + k, k)
                        norm(2 * i + k + 2, k)
                keep(T - 2, 0)
                dve.wait_ge(l_full, 1)
                dve.sem_inc(l_full, -1)
                nc.vector.tensor_copy(logit[:, T - 1, :], psL[1][:, 0:NE]).then_inc(chain, 1)
                dve.wait_ge(chain, 1)
                dve.sem_inc(chain, -1)
                wide = lambda a: a.unsqueeze(2).broadcast_to([P, T, NE])
                nc.vector.tensor_scalar(order[:, :], K.iota[:, 0:NE], -1.0, float(NE), ALU.mult, ALU.add).then_inc(chain, 1)
                dve.wait_ge(chain, 1)
                dve.sem_inc(chain, -1)

                def first(values, largest, hot):
                    nc.vector.tensor_reduce(largest, values, AX, ALU.max).then_inc(chain, 1)
                    dve.wait_ge(chain, 1)
                    dve.sem_inc(chain, -1)
                    nc.vector.tensor_tensor(eq[:, :, :], values, wide(largest), ALU.is_equal).then_inc(chain, 1)
                    dve.wait_ge(chain, 1)
                    dve.sem_inc(chain, -1)
                    nc.vector.tensor_tensor(eq[:, :, :], eq[:, :, :], order[:, :].unsqueeze(1).broadcast_to([P, T, NE]), ALU.mult).then_inc(chain, 1)
                    dve.wait_ge(chain, 1)
                    dve.sem_inc(chain, -1)
                    nc.vector.tensor_reduce(which[:, :], eq[:, :, :], AX, ALU.max).then_inc(chain, 1)
                    dve.wait_ge(chain, 1)
                    dve.sem_inc(chain, -1)
                    nc.vector.tensor_tensor(hot, eq[:, :, :], wide(which[:, :]), ALU.is_equal).then_inc(chain, 1)
                    dve.wait_ge(chain, 1)
                    dve.sem_inc(chain, -1)
                first(logit[:, :, :], top[:, :], one[:, :, :])
                nc.vector.scalar_tensor_tensor(left[:, :, :], one[:, :, :], -2 * BIG, logit[:, :, :], ALU.mult, ALU.add).then_inc(chain, 1)
                dve.wait_ge(chain, 1)
                dve.sem_inc(chain, -1)
                first(left[:, :, :], top2[:, :], two[:, :, :])
                nc.vector.tensor_tensor(e[:, :], top2[:, :], top[:, :], ALU.subtract).then_inc(gap_ready, 1)
                dve.wait_ge(e_ready, 1)
                dve.sem_inc(e_ready, -1)
                nc.vector.tensor_scalar(w1[:, :], e[:, :], 1.0, None, ALU.add).then_inc(chain, 1)
                dve.wait_ge(chain, 1)
                dve.sem_inc(chain, -1)
                nc.vector.reciprocal(w1[:, :], w1[:, :]).then_inc(chain, 1)
                dve.wait_ge(chain, 1)
                dve.sem_inc(chain, -1)
                nc.vector.tensor_tensor(w2[:, :], w1[:, :], e[:, :], ALU.mult).then_inc(chain, 1)
                dve.wait_ge(chain, 1)
                dve.sem_inc(chain, -1)
                nc.vector.tensor_tensor(one[:, :, :], one[:, :, :], wide(w1[:, :]), ALU.mult)
                nc.vector.tensor_tensor(two[:, :, :], two[:, :, :], wide(w2[:, :]), ALU.mult).then_inc(chain, 1)
                dve.wait_ge(chain, 1)
                dve.sem_inc(chain, -1)
                nc.vector.tensor_tensor(K.share[:, :, :], one[:, :, :], two[:, :, :], ALU.add)

            @block.scalar
            def _(act):
                act.wait_ge(loaded, 64)
                with act.Fori(0, T // 2) as i:
                    for k in range(2):
                        act.wait_ge(xT_full, 1)
                        act.sem_inc(xT_full, -1)
                        for c in range(C):
                            last = nc.scalar.activation(xT[:, k, c, :], psT[k][:, c * P:(c + 1) * P], ACT.Identity,
                                                        bias=beta[:, c:c + 1], scale=gamma[:, c:c + 1])
                        last.then_inc(xT_ready, 1)
                act.wait_ge(gap_ready, 1)
                act.sem_inc(gap_ready, -1)
                nc.scalar.activation(e[:, :], e[:, :], ACT.Exp).then_inc(e_ready, 1)

            @block.tensor
            def _(pe):
                pe.wait_ge(loaded, 64)

                def transposes(k):
                    pe.wait_ge(xs_ready, 1)
                    pe.sem_inc(xs_ready, -1)
                    for c in range(C):
                        last = nc.tensor.transpose(psT[k][:, c * P:(c + 1) * P], xs[:, k, c * P:(c + 1) * P], K.ident[:, :])
                    last.then_inc(xT_full, 1)

                def body(final):
                    for k in range(2):
                        pe.wait_ge(xT_ready, 1)
                        pe.sem_inc(xT_ready, -1)
                        if not (final and k == 1):
                            transposes(1 - k)
                        nc.tensor.matmul(psL[k][:, 0:NE], K.ones[0:1, :], br[:, :], start=True, stop=False)
                        for c in range(C):
                            last = nc.tensor.matmul(psL[k][:, 0:NE], xT[:, k, c, :], wr[:, c, :], start=False, stop=(c == C - 1))
                        last.then_inc(l_full, 1)
                transposes(0)
                with pe.Fori(0, T // 2 - 1) as i:
                    body(False)
                body(True)


def experts(nc, I, K):
    fp32, ALU, ACT = mybir.dt.float32, mybir.AluOpType, mybir.ActivationFunctionType
    M = FF1 // P
    with ExitStack() as ctx:
        def sb(n, shape):
            return ctx.enter_context(nc.sbuf_tensor(f"ex_{n}", shape, fp32))

        def ps(n):
            return ctx.enter_context(nc.psum_tensor(f"ex_{n}", [P, 512], fp32))

        def sem(n):
            return K.sem(f"ex_{n}")
        w1, b1, w2, b2 = sb("w1", [P, NE, C, FF1]), sb("b1", [P, NE, M]), sb("w2", [P, NE, M, D]), sb("b2", [NE, D])
        gamma, beta = sb("gamma", [P, C]), sb("beta", [P, C])
        xs, xT, hT = sb("xs", [P, 2, D]), sb("xT", [P, C, 2 * P]), sb("hT", [P, 2, M, 2 * P])
        sh, shT = sb("sh", [P, 2, NE]), sb("shT", [NE, 2 * P])
        psT, psU, psO, psS = ps("psT"), [ps("psU0"), ps("psU1")], [ps(f"psO{j}") for j in range(4)], ps("psS")
        loaded, chain = sem("loaded"), sem("chain")
        xs_ready, xT_full, xT_ready, up_full, up_free, out_full, out_free = (
            sem(n) for n in ("xs_ready", "xT_full", "xT_ready", "up_full", "up_free", "out_full", "out_free"))
        xs_free, bias_full, bias_free = sem("xs_free"), sem("bias_full"), sem("bias_free")
        with nc.Block() as block:
            @block.sync
            def _(sp):
                sp.dma_start(w1[:, :, :, :], I["f1_W1"].rearrange("e (c p) n -> p e c n", p=P)).then_inc(loaded, 16)
                sp.dma_start(w2[:, :, :, :], I["f1_W2"].rearrange("e (m p) n -> p e m n", p=P)).then_inc(loaded, 16)
                sp.dma_start(b1[:, :, :], I["f1_b1"]).then_inc(loaded, 16)
                sp.dma_start(b2[:, :], I["f1_b2"]).then_inc(loaded, 16)
                sp.dma_start(gamma[:, :], I["f1_gamma"]).then_inc(loaded, 16)
                sp.dma_start(beta[:, :], I["f1_beta"]).then_inc(loaded, 16)

            @block.vector
            def _(dve):
                def norm(i):
                    for r in range(2):
                        t = 2 * i + r
                        nc.vector.tensor_copy(sh[:, r, :].unsqueeze(1), K.share[:, bass.ds(t, 1), :])
                        last = nc.vector.tensor_scalar(xs[:, r, :].unsqueeze(1), K.X[:, bass.ds(t, 1), :],
                                                       K.mean[:, bass.ds(t, 1)], K.rstd[:, bass.ds(t, 1)],
                                                       ALU.subtract, ALU.mult)
                    last.then_inc(xs_ready, 1)

                def finish(i):
                    dve.wait_ge(bias_full, 1)
                    dve.sem_inc(bias_full, -1)
                    x = K.X[:, bass.ds(2 * i, 2), :]
                    nc.vector.tensor_tensor(x, psT[:, :].rearrange("p (r n) -> p r n", r=2), x, ALU.add).then_inc(chain, 1)
                    dve.wait_ge(chain, 1)
                    dve.sem_inc(chain, -1)
                    dve.sem_inc(bias_free, 1)
                    for e in range(NE):
                        for r in range(2):
                            t = 2 * i + r
                            x = K.X[:, bass.ds(t, 1), :]
                            dve.wait_ge(out_full, 1)
                            dve.sem_inc(out_full, -1)
                            nc.vector.scalar_tensor_tensor(
                                x, psO[2 * (e % 2) + r][:, 0:D].unsqueeze(1),
                                K.share[:, bass.ds(t, 1), e:e + 1].rearrange("p a b -> p (a b)"), x, ALU.mult, ALU.add).then_inc(chain, 1)
                            dve.wait_ge(chain, 1)
                            dve.sem_inc(chain, -1)
                            dve.sem_inc(out_free, 1)
                norm(0)
                with dve.Fori(0, T // 2 - 1) as i:
                    dve.wait_ge(xs_free, 1)
                    dve.sem_inc(xs_free, -1)
                    norm(i + 1)
                    finish(i)
                finish(T // 2 - 1)

            @block.scalar
            def _(act):
                act.wait_ge(loaded, 96)
                with act.Fori(0, T // 2) as i:
                    act.wait_ge(xT_full, 1)
                    act.sem_inc(xT_full, -1)
                    nc.scalar.activation(shT[:, :], psS[0:NE, 0:2 * P], ACT.Copy)
                    for c in range(C):
                        last = nc.scalar.activation(xT[:, c, :], psT[:, c * 2 * P:(c + 1) * 2 * P], ACT.Identity,
                                                    bias=beta[:, c:c + 1], scale=gamma[:, c:c + 1])
                    last.then_inc(xT_ready, 1)
                    for e in range(NE):
                        for m in range(M):
                            act.wait_ge(up_full, 1)
                            act.sem_inc(up_full, -1)
                            nc.scalar.activation(hT[:, e % 2, m, :], psU[m % 2][:, 0:2 * P], ACT.Gelu,
                                                 bias=b1[:, e, m:m + 1]).then_inc(up_free, 1)

            @block.tensor
            def _(pe):
                pe.sem_inc(out_free, 4)
                pe.sem_inc(up_free, 2)
                pe.sem_inc(bias_free, 1)
                pe.wait_ge(loaded, 96)

                def transposes():
                    pe.wait_ge(xs_ready, 1)
                    pe.sem_inc(xs_ready, -1)
                    pe.wait_ge(bias_free, 1)
                    pe.sem_inc(bias_free, -1)
                    for r in range(2):
                        nc.tensor.transpose(psS[0:NE, r * P:(r + 1) * P], sh[:, r, :], K.ident[:, :])
                    for c in range(C):
                        for r in range(2):
                            last = nc.tensor.transpose(psT[:, (2 * c + r) * P:(2 * c + r + 1) * P],
                                                       xs[:, r, c * P:(c + 1) * P], K.ident[:, :])
                    last.then_inc(xT_full, 1)

                def body(final):
                    pe.wait_ge(xT_ready, 1)
                    pe.sem_inc(xT_ready, -1)
                    pe.sem_inc(xs_free, 1)
                    for r in range(2):
                        last = nc.tensor.matmul(psT[:, r * D:(r + 1) * D], shT[:, r * P:(r + 1) * P], b2[:, :], start=True, stop=True)
                    last.then_inc(bias_full, 1)

                    def up(e):
                        for m in range(M):
                            pe.wait_ge(up_free, 1)
                            pe.sem_inc(up_free, -1)
                            for c in range(C):
                                last = nc.tensor.matmul(psU[m % 2][:, 0:2 * P], w1[:, e, c, m * P:(m + 1) * P], xT[:, c, :],
                                                        start=(c == 0), stop=(c == C - 1))
                            last.then_inc(up_full, 1)

                    def down(e):
                        for r in range(2):
                            pe.wait_ge(out_free, 1)
                            pe.sem_inc(out_free, -1)
                            for m in range(M):
                                last = nc.tensor.matmul(psO[2 * (e % 2) + r][:, 0:D], hT[:, e % 2, m, r * P:(r + 1) * P],
                                                        w2[:, e, m, :], start=(m == 0), stop=(m == M - 1))
                            last.then_inc(out_full, 1)
                    up(0)
                    for e in range(1, NE):
                        up(e)
                        down(e - 1)
                    pe.wait_ge(up_free, 2)
                    pe.sem_inc(up_free, -2)
                    pe.sem_inc(up_free, 2)
                    if not final:
                        transposes()
                    down(NE - 1)
                transposes()
                with pe.Fori(0, T // 2 - 1) as i:
                    body(False)
                body(True)


def store(nc, K, out):
    with ExitStack() as ctx:
        stored = K.sem("x_stored")
        full = N // P * P
        with nc.Block() as block:
            @block.sync
            def _(sp):
                sp.dma_start(out[0:full, :].rearrange("(t p) d -> p t d", p=P), K.X[:, 0:N // P, :]).then_inc(stored, 16)
                sp.dma_start(out[full:N, :], K.X[0:N - full, N // P, :]).then_inc(stored, 16)
                sp.wait_ge(stored, 32)


class Kept:

    def __init__(self, nc):
        self.nc, self.sems = nc, []

    def sem(self, name):
        self.sems.append(self.nc.alloc_semaphore(name))
        return self.sems[-1]

    def clear(self):
        self.nc.clear_and_free_semaphores(self.sems)
        self.nc.all_engine_barrier()
        self.sems = []


def program(nc, I, out):
    fp32, i32 = mybir.dt.float32, mybir.dt.int32
    htab = nc.dram_tensor("htab", (T * P, TW), fp32, kind="Internal").ap()
    atab = nc.dram_tensor("atab", (T * P, HEADS), fp32, kind="Internal").ap()
    ztab = nc.dram_tensor("ztab", (T * P, D), fp32, kind="Internal").ap()
    wtab = nc.dram_tensor("wtab", (T * P,), fp32, kind="Internal").ap()
    ftab = nc.dram_tensor("ftab", (EP, HEADS), fp32, kind="Internal").ap()
    with ExitStack() as ctx:
        def sb(n, shape, dt=fp32):
            return ctx.enter_context(nc.sbuf_tensor(n, shape, dt))
        K = Kept(nc)
        K.X = sb("X", [P, T, D])
        K.ident, K.upper, K.ones = sb("ident", [P, P]), sb("upper", [P, P]), sb("ones", [P, P])
        K.iota, K.iotai = sb("iota", [P, 512]), sb("iotai", [P, 512], i32)
        K.real, K.blockmask = sb("real", [P, T]), sb("blockmask", [P, C, HEADS])
        K.mean, K.rstd, K.meansq = sb("mean", [P, T]), sb("rstd", [P, T]), sb("meansq", [P, T])
        K.coef, K.share = sb("coef", [P, T]), sb("share", [P, T, NE])
        K.src_s, K.base, K.ns = sb("src_s", [P, S], i32), sb("base", [P, S + 8]), sb("node_tile", [P, S + 8], i32)
        K.src_p, K.cap, K.capall = sb("src_p", [P, ET], i32), sb("cap", [P, ET]), sb("capall", [P, 1])
        K.deg, K.last_edge = sb("deg", [P, T]), sb("last_edge", [P, T], i32)
        setup(nc, I, K)
        row_stats(nc, K, "ln0")
        K.got_in, K.cur_set, K.passed = [K.sem("got_in0"), K.sem("got_in1")], K.sem("cur_set"), K.sem("passed")
        with ExitStack() as layer:
            K.cur = layer.enter_context(nc.sbuf_tensor("cur", [P, HJ], i32))
            K.got = layer.enter_context(nc.sbuf_tensor("got", [P, HJ, HEADS], fp32))
            K.term = layer.enter_context(nc.sbuf_tensor("term", [P, ET, HEADS], fp32))
            K.wa = layer.enter_context(nc.sbuf_tensor("wa", [P, C, 2 * HEADS], fp32))
            source_terms(nc, I, K, atab)
            K.H = layer.enter_context(nc.sbuf_tensor("H", [P, T, HW], fp32))
            with ExitStack() as mixing:
                K.Q = mixing.enter_context(nc.sbuf_tensor("Q", [P, T, D], fp32))
                K.kvbd = mixing.enter_context(nc.sbuf_tensor("kvbd", [P, C, 2, P], fp32))
                project(nc, I, K, htab, atab)
                mix0(nc, I, K, atab)
            K.node = layer.enter_context(nc.sbuf_tensor("node", [P, T, 2 * HEADS], fp32))
            K.selfw = layer.enter_context(nc.sbuf_tensor("selfw", [P, T, HEADS], fp32))
            edge_tables(nc, I, K, atab)
            softmax_maxima(nc, K, ftab)
            gat(nc, I, K, htab)
        row_stats(nc, K, "ln1")
        choose(nc, I, K, wtab)
        ffn0(nc, I, K)
        K.clear()
        row_stats(nc, K, "ln2")
        with ExitStack() as layer:
            K.Z = layer.enter_context(nc.sbuf_tensor("Z", [P, T, D], fp32))
            K.agg = layer.enter_context(nc.sbuf_tensor("agg", [P, T, D], fp32))
            normalise(nc, K, ztab)
            aggregate(nc, K, ztab)
            combine1(nc, I, K)
        row_stats(nc, K, "ln3")
        route(nc, I, K)
        experts(nc, I, K)
        store(nc, K, out)


def laid_out(x, src, dst, **w):
    import numpy as np
    f = {k: np.asarray(v) for k, v in w.items()}
    x, src, dst = np.asarray(x), np.asarray(src), np.asarray(dst)
    o = {}
    o["x"] = np.concatenate([x, np.zeros((T * P - N, D), x.dtype)])
    o["src"] = np.concatenate([src, np.zeros(EP - E, src.dtype)])
    o["dst"] = np.concatenate([dst, np.full(EP - E, 4000, dst.dtype)])
    o["W0"], o["W0T"] = f["L0_gnn_W0"], f["L0_gnn_W0"].T
    o["att"] = np.stack([f["L0_gnn_att_src0"].reshape(D), f["L0_gnn_att_dst0"].reshape(D)], axis=1)
    o["b0"] = f["L0_gnn_b0"]
    for n in ("w_qkv", "w_out", "b_out", "w_norm2"):
        o[n] = f["L0_mix_" + n]
    o["w_norm1"] = f["L0_mix_w_norm1"].reshape(C, P).T
    for n in ("wr", "br", "w1", "b1", "w2", "b2"):
        o["f0_" + n] = f["L0_ffn_" + n]
    o["f0_wr"] = o["f0_wr"].reshape(D)
    o["f0_b1"] = o["f0_b1"].reshape(FF0 // P, P).T
    o["Wself"], o["Wneigh"], o["bgnn"] = f["L1_gnn_W_self"], f["L1_gnn_W_neigh"], f["L1_gnn_b"]
    o["Wq"], o["WkT"], o["WvT"], o["WfcT"] = f["L1_mix_Wq"], f["L1_mix_Wk"].T, f["L1_mix_Wv"].T, f["L1_mix_Wfc"].T
    for n in ("bk", "bv", "bfc"):
        o[n] = f["L1_mix_" + n]
    o["bq"] = f["L1_mix_bq"].reshape(C, P).T
    for n in ("gamma", "beta", "Wr", "br", "W1", "b1", "W2", "b2"):
        o["f1_" + n] = f["L1_ffn_" + n]
    o["f1_gamma"], o["f1_beta"] = (o["f1_" + n].reshape(C, P).T for n in ("gamma", "beta"))
    o["f1_b1"] = o["f1_b1"].reshape(NE, FF1 // P, P).transpose(2, 0, 1)
    return o


def kernel(**inputs):
    import numpy as _np
    import concourse.bacc as _bacc
    from concourse import mybir as _mybir
    from concourse.bass_utils import run_bass_kernel_spmd as _run

    nc = _bacc.Bacc("TRN2", target_bir_lowering=False, num_devices=1)
    arrays, args = {}, {}
    for name, a in laid_out(**inputs).items():
        a = _np.ascontiguousarray(a)
        arrays[f"in_{name}"] = a
        args[name] = nc.dram_tensor(f"in_{name}", a.shape, _mybir.dt.from_np(a.dtype), kind="ExternalInput").ap()
    out = nc.dram_tensor("out_x", (N, D), _mybir.dt.float32, kind="ExternalOutput").ap()
    program(nc, args, out)
    r = _run(nc, [arrays], core_ids=[0])
    return r.results[0]["out_x"]
```

```python
import concourse.bass as bass
from concourse import mybir
from contextlib import ExitStack

P = 128
N = 3125
D = 256
C = D // P
T = 26
HEADS = 8
HD = D // HEADS
E = 50000
ET = 391
EP = ET * P
SQ = 104
SG = 4
S = SQ * SG
HW = 272
TW = 264
BIG = 1.5e38
FF0 = 1024
KEEP = int(0.5 * N) - 1
NE = 8
TN = (N + P - 1) // P
ST = (2 * N + NE * (P - 1)) // P
FF1 = 512
HJ = 17
PART = [(0, 8), (8, HJ)]


def node_tiles(nc, K, eng, s, n):
    return nc.values_load_multi_w_load_instructions(
        K.ns[0:1, bass.ds(s, n)], [eng.engine], min_val=0, max_val=T - 1,
        skip_runtime_bounds_check_because="edge_tables counts at most T - 1 ends of node tiles")[1]


def setup(nc, I, K):
    fp32, ALU = mybir.dt.float32, mybir.AluOpType
    with ExitStack() as ctx:
        loaded = K.sem("x_loaded")
        made = K.sem("constants_made")
        with nc.Block() as block:
            @block.sync
            def _(sp):
                sp.dma_start(K.X[:, :, :], I["x"].rearrange("(t p) d -> p t d", p=P)).then_inc(loaded, 16)
                sp.dma_start(K.src_p[:, :], I["src"].rearrange("(p f) -> p f", p=P)).then_inc(loaded, 16)
                sp.wait_ge(loaded, 32)

            @block.gpsimd
            def _(pool):
                pool.memset(K.ident[:, :], 0.0)
                pool.memset(K.real[:, :], 1.0)
                pool.memset(K.upper[:, :], 1.0)
                pool.memset(K.ones[:, :], 1.0)
                pool.memset(K.blockmask[:, :, :], 1.0).then_inc(made, 1)
                pool.wait_ge(made, 1)
                pool.sem_inc(made, -1)
                pool.affine_select(out=K.ident[:, :], in_=K.ident[:, :], compare_op=ALU.not_equal, fill=1.0,
                                   base=0, pattern=[[-1, P]], channel_multiplier=1)
                pool.affine_select(out=K.real[:, :], in_=K.real[:, :], compare_op=ALU.is_ge, fill=0.0,
                                   base=N - 1, pattern=[[-P, T]], channel_multiplier=-1)
                pool.affine_select(out=K.upper[:, :], in_=K.upper[:, :], compare_op=ALU.is_ge, fill=0.0,
                                   base=0, pattern=[[1, P]], channel_multiplier=-1)
                pool.affine_select(out=K.blockmask[:, :, :], in_=K.blockmask[:, :, :], compare_op=ALU.is_ge,
                                   fill=0.0, base=0, pattern=[[P, C], [-HD, HEADS]],
                                   channel_multiplier=1).then_inc(made, 1)
                pool.wait_ge(made, 1)
                pool.sem_inc(made, -1)
                pool.affine_select(out=K.blockmask[:, :, :], in_=K.blockmask[:, :, :], compare_op=ALU.is_ge,
                                   fill=0.0, base=HD - 1, pattern=[[-P, C], [HD, HEADS]], channel_multiplier=-1)
                pool.iota(K.iotai[:, :], pattern=[[1, 512]], base=0, channel_multiplier=0).then_inc(made, 1)
                pool.wait_ge(made, 1)
                pool.sem_inc(made, -1)
                pool.tensor_copy(K.iota[:, :], K.iotai[:, :])


def row_stats(nc, K, name):
    fp32, ALU, ACT = mybir.dt.float32, mybir.AluOpType, mybir.ActivationFunctionType
    with ExitStack() as ctx:
        def sb(n, shape):
            return ctx.enter_context(nc.sbuf_tensor(f"{name}_{n}", shape, fp32))
        halves, mv = sb("halves", [P, T, 6]), sb("mv", [P, T])
        var, root, tmp = sb("var", [P, T]), sb("root", [P, T]), sb("tmp", [P, T])
        chain = K.sem(f"{name}_chain")
        var_ready = K.sem(f"{name}_var_ready")
        root_ready = K.sem(f"{name}_root_ready")
        with nc.Block() as block:
            @block.vector
            def _(dve):
                with dve.Fori(0, T // 2 - 1) as i:
                    for k in range(2):
                        nc.vector.bn_stats(halves[:, bass.ds(2 * i + k, 1), :], K.X[:, bass.ds(2 * i + k, 1), :])
                nc.vector.bn_stats(halves[:, T - 2, :], K.X[:, T - 2, :])
                nc.vector.bn_stats(halves[:, T - 1, :], K.X[:, T - 1, :]).then_inc(chain, 1)
                dve.wait_ge(chain, 1)
                dve.sem_inc(chain, -1)
                nc.vector.tensor_tensor(K.mean[:, :], halves[:, :, 1], halves[:, :, 4], ALU.add)
                nc.vector.tensor_tensor(tmp[:, :], halves[:, :, 1], halves[:, :, 4], ALU.subtract)
                nc.vector.tensor_tensor(mv[:, :], halves[:, :, 2], halves[:, :, 5], ALU.add).then_inc(chain, 1)
                dve.wait_ge(chain, 1)
                dve.sem_inc(chain, -1)
                nc.vector.tensor_scalar(K.mean[:, :], K.mean[:, :], 0.5, None, ALU.mult)
                nc.vector.tensor_tensor(tmp[:, :], tmp[:, :], tmp[:, :], ALU.mult).then_inc(chain, 1)
                dve.wait_ge(chain, 1)
                dve.sem_inc(chain, -1)
                nc.vector.tensor_scalar(tmp[:, :], tmp[:, :], 0.25 * D, None, ALU.mult).then_inc(chain, 1)
                dve.wait_ge(chain, 1)
                dve.sem_inc(chain, -1)
                nc.vector.tensor_tensor(mv[:, :], mv[:, :], tmp[:, :], ALU.add).then_inc(chain, 1)
                dve.wait_ge(chain, 1)
                dve.sem_inc(chain, -1)
                nc.vector.tensor_scalar(mv[:, :], mv[:, :], 1.0 / D, None, ALU.mult).then_inc(chain, 1)
                dve.wait_ge(chain, 1)
                dve.sem_inc(chain, -1)
                nc.vector.tensor_scalar(var[:, :], mv[:, :], 1e-5, None, ALU.add).then_inc(var_ready, 1)
                dve.wait_ge(root_ready, 1)
                dve.sem_inc(root_ready, -1)
                nc.vector.reciprocal(root[:, :], root[:, :]).then_inc(chain, 1)
                dve.wait_ge(chain, 1)
                dve.sem_inc(chain, -1)
                nc.vector.tensor_tensor(tmp[:, :], root[:, :], root[:, :], ALU.mult).then_inc(chain, 1)
                dve.wait_ge(chain, 1)
                dve.sem_inc(chain, -1)
                nc.vector.tensor_tensor(tmp[:, :], tmp[:, :], var[:, :], ALU.mult).then_inc(chain, 1)
                dve.wait_ge(chain, 1)
                dve.sem_inc(chain, -1)
                nc.vector.tensor_scalar(tmp[:, :], tmp[:, :], -0.5, 1.5, ALU.mult, ALU.add).then_inc(chain, 1)
                dve.wait_ge(chain, 1)
                dve.sem_inc(chain, -1)
                nc.vector.tensor_tensor(K.rstd[:, :], root[:, :], tmp[:, :], ALU.mult).then_inc(chain, 1)
                dve.wait_ge(chain, 1)
                dve.sem_inc(chain, -1)
                nc.vector.tensor_tensor(tmp[:, :], K.rstd[:, :], K.rstd[:, :], ALU.mult).then_inc(chain, 1)
                dve.wait_ge(chain, 1)
                dve.sem_inc(chain, -1)
                nc.vector.tensor_tensor(K.meansq[:, :], tmp[:, :], mv[:, :], ALU.mult)

            @block.scalar
            def _(act):
                act.wait_ge(var_ready, 1)
                act.sem_inc(var_ready, -1)
                nc.scalar.activation(root[:, :], var[:, :], ACT.Sqrt).then_inc(root_ready, 1)


def source_terms(nc, I, K, atab):
    fp32, ALU, ACT = mybir.dt.float32, mybir.AluOpType, mybir.ActivationFunctionType
    with ExitStack() as ctx:
        def sb(n, shape):
            return ctx.enter_context(nc.sbuf_tensor(f"st_{n}", shape, fp32))

        def ps(n):
            return ctx.enter_context(nc.psum_tensor(f"st_{n}", [P, 512], fp32))

        def sem(n):
            return K.sem(f"st_{n}")
        w0, att, attbd, terms = sb("w0", [P, C, D]), sb("att", [P, C, 2]), sb("attbd", [P, C, 2 * HEADS]), sb("terms", [P, T, HEADS])
        xs, xT = sb("xs", [P, 2, D]), sb("xT", [P, 2, C, P])
        psW, psT, psL = ps("psW"), [ps("psT0"), ps("psT1")], [ps("psL0"), ps("psL1")]
        loaded, stored, att_ready, wa_full, wa_ready = (sem(n) for n in ("loaded", "stored", "att_ready", "wa_full", "wa_ready"))
        xs_ready, xt_full, xt_ready, l_full, l_free, chain = (sem(n) for n in ("xs_ready", "xt_full", "xt_ready", "l_full", "l_free", "chain"))
        terms_ready = sem("terms_ready")
        with nc.Block() as block:
            @block.sync
            def _(sp):
                sp.dma_start(w0[:, :, :], I["W0"].rearrange("(c p) n -> p c n", p=P)).then_inc(loaded, 16)
                sp.dma_start(att[:, :, :], I["att"].rearrange("(c p) n -> p c n", p=P)).then_inc(loaded, 16)
                sp.wait_ge(terms_ready, 1)
                sp.sem_inc(terms_ready, -1)
                sp.dma_start(atab.rearrange("(t p) n -> p t n", p=P), terms[:, :, :]).then_inc(stored, 16)
                sp.wait_ge(stored, 16)

            @block.vector
            def _(dve):
                def norm(t, k):
                    nc.vector.tensor_scalar(xs[:, k, :].unsqueeze(1), K.X[:, bass.ds(t, 1), :],
                                            K.mean[:, bass.ds(t, 1)], K.rstd[:, bass.ds(t, 1)],
                                            ALU.subtract, ALU.mult).then_inc(xs_ready, 1)

                def body(t, k, final):
                    dve.wait_ge(l_full, 1)
                    dve.sem_inc(l_full, -1)
                    copy = nc.vector.tensor_copy(terms[:, bass.ds(t, 1), :], psL[k][:, 0:HEADS].unsqueeze(1))
                    if final:
                        copy.then_inc(chain, 1)
                        dve.wait_ge(chain, 1)
                        dve.sem_inc(chain, -1)
                    else:
                        copy.then_inc(l_free, 1)
                        norm(t + 2, k)
                norm(0, 0)
                norm(1, 1)
                dve.wait_ge(loaded, 32)
                for c in range(C):
                    for s in range(2):
                        last = nc.vector.tensor_scalar(attbd[:, c, s * HEADS:(s + 1) * HEADS], K.blockmask[:, c, :],
                                                       att[:, c, s:s + 1], None, ALU.mult)
                last.then_inc(att_ready, 1)
                dve.wait_ge(wa_full, 1)
                dve.sem_inc(wa_full, -1)
                nc.vector.tensor_copy(K.wa[:, :, :], psW[:, 0:C * 16].rearrange("p (c n) -> p c n", c=C)).then_inc(wa_ready, 1)
                with dve.Fori(0, T // 2 - 1) as i:
                    for k in range(2):
                        body(2 * i + k, k, False)
                body(T - 2, 0, True)
                body(T - 1, 1, True)
                dve.sem_inc(terms_ready, 1)

            @block.scalar
            def _(act):
                with act.Fori(0, T // 2) as i:
                    for k in range(2):
                        act.wait_ge(xt_full, 1)
                        act.sem_inc(xt_full, -1)
                        nc.scalar.activation(xT[:, k, :, :], psT[k][:, 0:D].rearrange("p (c n) -> p c n", c=C),
                                             ACT.Copy).then_inc(xt_ready, 1)

            @block.tensor
            def _(pe):
                def transposes(k):
                    pe.wait_ge(xs_ready, 1)
                    pe.sem_inc(xs_ready, -1)
                    for c in range(C):
                        last = nc.tensor.transpose(psT[k][:, c * P:(c + 1) * P], xs[:, k, c * P:(c + 1) * P], K.ident[:, :])
                    last.then_inc(xt_full, 1)

                def terms_of(k, final):
                    pe.wait_ge(xt_ready, 1)
                    pe.sem_inc(xt_ready, -1)
                    if not final:
                        transposes(1 - k)
                    pe.wait_ge(l_free, 1)
                    pe.sem_inc(l_free, -1)
                    for c in range(C):
                        last = nc.tensor.matmul(psL[k][:, 0:HEADS], xT[:, k, c, :], K.wa[:, c, 0:HEADS], start=(c == 0), stop=(c == C - 1))
                    last.then_inc(l_full, 1)
                pe.sem_inc(l_free, 2)
                transposes(0)
                pe.wait_ge(att_ready, 1)
                pe.sem_inc(att_ready, -1)
                for m in range(C):
                    for c in range(C):
                        last = nc.tensor.matmul(psW[:, m * 16:(m + 1) * 16], w0[:, c, m * P:(m + 1) * P],
                                                attbd[:, c, :], start=(c == 0), stop=(c == C - 1))
                last.then_inc(wa_full, 1)
                pe.wait_ge(wa_ready, 1)
                pe.sem_inc(wa_ready, -1)
                with pe.Fori(0, T // 2 - 1) as i:
                    for k in range(2):
                        terms_of(k, False)
                terms_of(0, False)
                terms_of(1, True)


def gather_terms(nc, K, pool, atab, first, last):
    def issue(i, h):
        a, b = PART[h]
        nc.gpsimd.tensor_copy(K.cur[:, a:b], K.src_p[:, bass.ds(i * HJ + a, b - a)]).then_inc(K.cur_set, 1)
        pool.wait_ge(K.cur_set, 1)
        pool.sem_inc(K.cur_set, -1)
        for k in range(a, b):
            nc.gpsimd.indirect_dma_start(
                out=K.got[:, k, :], out_offset=None, in_=atab,
                in_offset=bass.IndirectOffsetOnAxis(ap=K.cur[:, k:k + 1].bitcast(mybir.dt.uint32), axis=0)
            ).then_inc(K.got_in[h], 16)

    def collect(i, h):
        a, b = PART[h]
        pool.wait_ge(K.got_in[h], (i + 1) * (16 * (b - a)))
        pool.sem_inc(K.passed, 1)
        nc.gpsimd.tensor_copy(K.term[:, bass.ds(i * HJ + a, b - a), :], K.got[:, a:b, :]).then_inc(K.cur_set, 1)
        pool.wait_ge(K.cur_set, 1)
        pool.sem_inc(K.cur_set, -1)
    issue(first, 0)
    if last - first > 1:
        with pool.Fori(first, last - 1) as i:
            issue(i, 1)
            collect(i, 0)
            issue(i + 1, 0)
            collect(i, 1)
    issue(last - 1, 1)
    collect(last - 1, 0)
    collect(last - 1, 1)


def project(nc, I, K, htab, atab):
    fp32, ALU, ACT = mybir.dt.float32, mybir.AluOpType, mybir.ActivationFunctionType
    with ExitStack() as ctx:
        def sb(n, shape):
            return ctx.enter_context(nc.sbuf_tensor(f"pj_{n}", shape, fp32))

        def ps(n):
            return ctx.enter_context(nc.psum_tensor(f"pj_{n}", [P, 512], fp32))

        def sem(n):
            return K.sem(f"pj_{n}")
        w0t, wqkv, wn1 = sb("w0t", [P, C, HW]), sb("wqkv", [P, C, 3 * D]), sb("wn1", [P, C])
        root, scale, tmp = sb("root", [P, T]), sb("scale", [P, T]), sb("tmp", [P, T])
        xs, xT = sb("xs", [P, 2, D]), sb("xT", [P, 2, C, P])
        low, pos = sb("low", [P, 2, 2 * D]), sb("pos", [P, 2, 2 * D])
        kb, vb = sb("kb", [P, 2, D]), sb("vb", [P, 2, C, P + 1])
        psT, psKV = ps("psT"), ps("psKV")
        psH, psQ, psV = ([ps(f"ps{x}{j}") for j in range(2)] for x in "HQV")
        loaded, stored, chain = sem("weights_loaded"), sem("tables_stored"), sem("chain")
        ms_ready, root_ready = sem("ms_ready"), sem("root_ready")
        w_ready = sem("w_ready")
        xs_ready, xt_full, xt_ready = sem("xs_ready"), sem("xt_full"), sem("xt_ready")
        h_full, q_full, v_full = sem("h_full"), sem("q_full"), sem("v_full")
        h_free, q_free, v_free = sem("h_free"), sem("q_free"), sem("v_free")
        low_ready, exp_ready, k_ready, v_ready = sem("low_ready"), sem("exp_ready"), sem("k_ready"), sem("v_ready")
        kv_used, kv_done, h_done = sem("kv_used"), sem("kv_done"), sem("h_done")
        with nc.Block() as block:
            @block.sync
            def _(sp):
                sp.dma_start(w0t[:, :, 0:D], I["W0T"].rearrange("(c p) n -> p c n", p=P)).then_inc(loaded, 16)
                sp.dma_start(wqkv[:, :, :], I["w_qkv"].rearrange("(c p) n -> p c n", p=P)).then_inc(loaded, 16)
                sp.dma_start(wn1[:, :], I["w_norm1"]).then_inc(loaded, 16)
                sp.wait_ge(h_done, 1)
                sp.sem_inc(h_done, -1)
                sp.dma_start(htab.rearrange("(t p) n -> p t n", p=P), K.H[:, :, 0:TW]).then_inc(stored, 16)
                sp.wait_ge(stored, 16)

            @block.vector
            def _(dve):
                nc.vector.memset(kb[:, :, :], 0.0)
                nc.vector.memset(vb[:, :, :, :], 0.0)
                nc.vector.tensor_scalar(tmp[:, :], K.meansq[:, :], 1e-6, None, ALU.add).then_inc(chain, 1)
                dve.wait_ge(chain, 1)
                dve.sem_inc(chain, -1)
                nc.vector.tensor_copy(root[:, :], tmp[:, :]).then_inc(ms_ready, 1)
                dve.wait_ge(root_ready, 1)
                dve.sem_inc(root_ready, -1)
                nc.vector.reciprocal(scale[:, :], root[:, :]).then_inc(chain, 1)
                dve.wait_ge(chain, 1)
                dve.sem_inc(chain, -1)
                nc.vector.tensor_tensor(scale[:, :], scale[:, :], K.rstd[:, :], ALU.mult).then_inc(chain, 1)
                dve.wait_ge(chain, 1)
                dve.sem_inc(chain, -1)
                dve.wait_ge(loaded, 48)
                nc.vector.tensor_copy(w0t[:, :, D:HW], K.wa[:, :, :])
                for c in range(C):
                    last = nc.vector.tensor_scalar(wqkv[:, c, :], wqkv[:, c, :], wn1[:, c:c + 1], None, ALU.mult)
                last.then_inc(w_ready, 1)

                def norm(t, k):
                    nc.vector.tensor_scalar(xs[:, k, :].unsqueeze(1), K.X[:, bass.ds(t, 1), :],
                                            K.mean[:, bass.ds(t, 1)], scale[:, bass.ds(t, 1)],
                                            ALU.subtract, ALU.mult).then_inc(xs_ready, 1)

                def body(i, final):
                    for k in range(2):
                        t = 2 * i + k
                        dve.wait_ge(h_full, 1)
                        dve.sem_inc(h_full, -1)
                        nc.vector.tensor_scalar(K.H[:, bass.ds(t, 1), :], psH[k][:, 0:HW].unsqueeze(1),
                                                root[:, bass.ds(t, 1)], None, ALU.mult).then_inc(h_free, 1)
                        dve.wait_ge(kv_used, 1)
                        dve.sem_inc(kv_used, -1)
                        dve.wait_ge(q_full, 1)
                        dve.sem_inc(q_full, -1)
                        nc.vector.tensor_scalar(low[:, k, :], psQ[k][:, :], 0.0, None, ALU.min).then_inc(low_ready, 1)
                        nc.vector.tensor_copy(vb[:, k, :, P:P + 1],
                                              K.real[:, bass.ds(t, 1)].unsqueeze(1).broadcast_to([P, C, 1]))
                        dve.wait_ge(v_full, 1)
                        dve.sem_inc(v_full, -1)
                        nc.vector.tensor_copy(vb[:, k, :, 0:P],
                                              psV[k][:, 0:D].rearrange("p (c n) -> p c n", c=C)).then_inc(v_ready, 1)
                        if not final:
                            norm(t + 2, k)
                        dve.wait_ge(exp_ready, 1)
                        dve.sem_inc(exp_ready, -1)
                        nc.vector.tensor_tensor(kb[:, k, :], pos[:, k, D:2 * D], low[:, k, D:2 * D],
                                                ALU.add).then_inc(k_ready, 1)
                        nc.vector.tensor_tensor(K.Q[:, bass.ds(t, 1), :], pos[:, k, 0:D].unsqueeze(1),
                                                low[:, k, 0:D].unsqueeze(1), ALU.add)
                norm(0, 0)
                norm(1, 1)
                with dve.Fori(0, T // 2 - 1) as i:
                    body(i, False)
                body(T // 2 - 1, True)
                nc.vector.memset(K.kvbd[:, :, :, :], 0.0).then_inc(chain, 1)
                dve.wait_ge(chain, 1)
                dve.sem_inc(chain, -1)
                dve.wait_ge(kv_done, 1)
                dve.sem_inc(kv_done, -1)
                for c in range(C):
                    psk = psKV[:, c * (P + 1):(c + 1) * (P + 1)]
                    mask = K.blockmask[:, c, 4 * c:4 * c + 4].unsqueeze(2).broadcast_to([P, 4, HD])
                    nc.vector.tensor_tensor(K.kvbd[:, c, 0, :].rearrange("p (h m) -> p h m", m=HD),
                                            psk[:, 0:P].rearrange("p (h m) -> p h m", m=HD), mask, ALU.mult)
                    last = nc.vector.tensor_tensor(K.kvbd[:, c, 1, :].rearrange("p (h m) -> p h m", m=HD),
                                                   psk[:, P:P + 1].unsqueeze(2).broadcast_to([P, 4, HD]), mask, ALU.mult)
                last.then_inc(h_done, 1)

            @block.scalar
            def _(act):
                act.wait_ge(ms_ready, 1)
                act.sem_inc(ms_ready, -1)
                nc.scalar.activation(root[:, :], root[:, :], ACT.Sqrt).then_inc(root_ready, 1)
                with act.Fori(0, T // 2) as i:
                    for k in range(2):
                        act.wait_ge(xt_full, 1)
                        act.sem_inc(xt_full, -1)
                        nc.scalar.activation(xT[:, k, :, :], psT[:, 0:D].rearrange("p (c n) -> p c n", c=C),
                                             ACT.Copy).then_inc(xt_ready, 1)
                        act.wait_ge(low_ready, 1)
                        act.sem_inc(low_ready, -1)
                        nc.scalar.activation(pos[:, k, :], psQ[k][:, :], ACT.Relu).then_inc(q_free, 1)
                        nc.scalar.activation(low[:, k, :], low[:, k, :], ACT.Exp).then_inc(exp_ready, 1)

            @block.gpsimd
            def _(pool):
                gather_terms(nc, K, pool, atab, 0, 11)

            @block.tensor
            def _(pe):
                pe.wait_ge(w_ready, 1)
                pe.sem_inc(w_ready, -1)
                nc.tensor.matmul(psKV[:, 0:C * (P + 1)], kb[:, 0, 0:P], vb[:, 0, :, :].rearrange("p c n -> p (c n)"),
                                 start=True, stop=False, skip_group_check=True)
                pe.sem_inc(k_ready, 1)
                pe.sem_inc(v_ready, 1)
                pe.sem_inc(kv_used, 1)
                pe.sem_inc(h_free, 2)
                pe.sem_inc(q_free, 2)

                def transposes(k):
                    pe.wait_ge(xs_ready, 1)
                    pe.sem_inc(xs_ready, -1)
                    for c in range(C):
                        last = nc.tensor.transpose(psT[:, c * P:(c + 1) * P], xs[:, k, c * P:(c + 1) * P], K.ident[:, :])
                    last.then_inc(xt_full, 1)

                def kv(k, stop=False):
                    pe.wait_ge(k_ready, 1)
                    pe.sem_inc(k_ready, -1)
                    pe.wait_ge(v_ready, 1)
                    pe.sem_inc(v_ready, -1)
                    for c in range(C):
                        last = nc.tensor.matmul(psKV[:, c * (P + 1):(c + 1) * (P + 1)], kb[:, k, c * P:(c + 1) * P],
                                                vb[:, k, c, :], start=False, stop=stop, skip_group_check=True)
                    return last

                def body(i, final):
                    for k in range(2):
                        pe.wait_ge(xt_ready, 1)
                        pe.sem_inc(xt_ready, -1)
                        pe.wait_ge(h_free, 1)
                        pe.sem_inc(h_free, -1)
                        for c in range(C):
                            last = nc.tensor.matmul(psH[k][:, 0:HW], xT[:, k, c, :], w0t[:, c, :],
                                                    start=(c == 0), stop=(c == C - 1))
                        last.then_inc(h_full, 1)
                        pe.wait_ge(q_free, 1)
                        pe.sem_inc(q_free, -1)
                        for m in range(C):
                            for c in range(C):
                                nc.tensor.matmul(psQ[k][:, m * P:(m + 1) * P], wqkv[:, c, m * P:(m + 1) * P],
                                                 xT[:, k, c, :], start=(c == 0), stop=(c == C - 1))
                        for c in range(C):
                            last = nc.tensor.matmul(psQ[k][:, D:2 * D], xT[:, k, c, :], wqkv[:, c, D:2 * D],
                                                    start=(c == 0), stop=(c == C - 1))
                        last.then_inc(q_full, 1)
                        for c in range(C):
                            last = nc.tensor.matmul(psV[k][:, 0:D], xT[:, k, c, :], wqkv[:, c, 2 * D:3 * D],
                                                    start=(c == 0), stop=(c == C - 1))
                        last.then_inc(v_full, 1)
                        if not (final and k == 1):
                            transposes(1 - k)
                        kv(1 - k).then_inc(kv_used, 1)
                transposes(0)
                with pe.Fori(0, T // 2 - 1) as i:
                    body(i, False)
                body(T // 2 - 1, True)
                kv(1, stop=True).then_inc(kv_done, 1)


def mix0(nc, I, K, atab):
    fp32, ALU, ACT = mybir.dt.float32, mybir.AluOpType, mybir.ActivationFunctionType
    with ExitStack() as ctx:
        def sb(n, shape):
            return ctx.enter_context(nc.sbuf_tensor(f"mx_{n}", shape, fp32))

        def ps(n):
            return ctx.enter_context(nc.psum_tensor(f"mx_{n}", [P, 512], fp32))

        def sem(n):
            return K.sem(f"mx_{n}")
        wout, bout, wn2, h0 = sb("wout", [P, C, D]), sb("bout", [1, D]), sb("wn2", [P, D]), sb("h0", [P, T, D])
        den, oT, junk = sb("den", [P, 2, 2 * D]), sb("oT", [P, 2, C, D]), sb("sq", [P, 2, D])
        nmr, xn, ssq, tmp, gain = sb("nmr", [P, T]), sb("xn", [P, 2, D]), sb("ssq", [P, T]), sb("tmp", [P, T]), sb("gain", [P, 2, D])
        psN, psD = [ps("psN0"), ps("psN1")], [ps("psD0"), ps("psD1")]
        psO = [ps("psO0"), ps("psO1")]
        loaded, chain = sem("weights_loaded"), sem("chain")
        n_full, d_full, nd_free, o_ready = sem("num_full"), sem("den_full"), sem("numden_free"), sem("o_ready")
        out_full, out_free, xn_ready, xn_free = sem("out_full"), sem("out_free"), sem("xn_ready"), sem("xn_free")
        nmr_ready, h0_ready, root_ready, ms_ready = sem("nmr_ready"), sem("h0_ready"), sem("root_ready"), sem("ms_ready")
        gain_ready, gain_free, wn2_loaded, sq_done = sem("gain_ready"), sem("gain_free"), sem("wn2_loaded"), sem("sq_done")
        with nc.Block() as block:
            @block.sync
            def _(sp):
                sp.dma_start(wout[:, :, :], I["w_out"].rearrange("(c p) n -> p c n", p=P)).then_inc(loaded, 16)
                sp.dma_start(bout[:, :], I["b_out"].rearrange("(a n) -> a n", a=1)).then_inc(loaded, 16)
                sp.dma_start(wn2[:, :], I["w_norm2"].partition_broadcast(P)).then_inc(wn2_loaded, 16)
                sp.wait_ge(wn2_loaded, 16)

            @block.gpsimd
            def _(pool):
                gather_terms(nc, K, pool, atab, 11, 21)

            @block.tensor
            def _(pe):
                pe.sem_inc(nd_free, 2)
                pe.sem_inc(out_free, 2)
                pe.wait_ge(loaded, 32)
                Qv = K.Q[:, :, :].rearrange("p t (c r) -> p c t r", c=C)

                def numden(i, k):
                    pe.wait_ge(nd_free, 1)
                    pe.sem_inc(nd_free, -1)
                    for ps, j, full in ((psN, 0, n_full), (psD, 1, d_full)):
                        for c in range(C):
                            last = nc.tensor.matmul(ps[k][:, c * D:(c + 1) * D].rearrange("p (t r) -> p t r", t=2),
                                                    K.kvbd[:, c, j, :], Qv[:, c, bass.ds(2 * i, 2), :], start=True, stop=True)
                        last.then_inc(full, 1)

                def out(k):
                    pe.wait_ge(o_ready, 1)
                    pe.sem_inc(o_ready, -1)
                    for r in range(2):
                        pe.wait_ge(out_free, 1)
                        pe.sem_inc(out_free, -1)
                        nc.tensor.matmul(psO[r][:, 0:D], K.ones[0:1, :], bout[:, :], start=True, stop=False)
                        for c in range(C):
                            last = nc.tensor.matmul(psO[r][:, 0:D], oT[:, k, c, r * P:(r + 1) * P], wout[:, c, :],
                                                    start=False, stop=(c == C - 1))
                        last.then_inc(out_full, 1)
                numden(0, 0)
                with pe.Fori(0, T // 4) as i:
                    numden(2 * i + 1, 1)
                    out(0)
                    numden(2 * i + 2, 0)
                    out(1)
                out(0)

            @block.vector
            def _(dve):
                nc.vector.tensor_scalar(nmr[:, :], K.mean[:, :], -1.0, None, ALU.mult).then_inc(chain, 1)
                dve.wait_ge(chain, 1)
                dve.sem_inc(chain, -1)
                nc.vector.tensor_tensor(nmr[:, :], nmr[:, :], K.rstd[:, :], ALU.mult).then_inc(nmr_ready, 1)

                def pair(i, k):
                    dve.wait_ge(n_full, 1)
                    dve.sem_inc(n_full, -1)
                    dve.wait_ge(d_full, 1)
                    dve.sem_inc(d_full, -1)
                    nc.vector.tensor_scalar(den[:, k, :], psD[k][:, :], 1e-6, None, ALU.add).then_inc(chain, 1)
                    dve.wait_ge(chain, 1)
                    dve.sem_inc(chain, -1)
                    nc.vector.reciprocal(den[:, k, :], den[:, k, :]).then_inc(chain, 1)
                    dve.wait_ge(chain, 1)
                    dve.sem_inc(chain, -1)
                    nc.vector.tensor_tensor(oT[:, k, :, :].rearrange("p c n -> p (c n)"), psN[k][:, :],
                                            den[:, k, :], ALU.mult).then_inc(chain, 1)
                    dve.wait_ge(chain, 1)
                    dve.sem_inc(chain, -1)
                    dve.sem_inc(nd_free, 1)
                    dve.sem_inc(o_ready, 1)
                    for r in range(2):
                        t = 2 * i + r
                        dve.wait_ge(out_full, 1)
                        dve.sem_inc(out_full, -1)
                        dve.wait_ge(xn_ready, 1)
                        dve.sem_inc(xn_ready, -1)
                        nc.vector.tensor_tensor(h0[:, bass.ds(t, 1), :], psO[r][:, 0:D].unsqueeze(1),
                                                xn[:, r, :].unsqueeze(1), ALU.add).then_inc(h0_ready, 1)
                with dve.Fori(0, T // 4) as i:
                    pair(2 * i, 0)
                    pair(2 * i + 1, 1)
                pair(T // 2 - 1, 0)
                dve.wait_ge(sq_done, 1)
                dve.sem_inc(sq_done, -1)
                nc.vector.tensor_scalar(tmp[:, :], ssq[:, :], 1.0 / D, 1e-6, ALU.mult, ALU.add).then_inc(chain, 1)
                dve.wait_ge(chain, 1)
                dve.sem_inc(chain, -1)
                nc.vector.tensor_copy(ssq[:, :], tmp[:, :]).then_inc(ms_ready, 1)
                dve.wait_ge(root_ready, 1)
                dve.sem_inc(root_ready, -1)
                nc.vector.reciprocal(tmp[:, :], ssq[:, :]).then_inc(chain, 1)
                dve.wait_ge(chain, 1)
                dve.sem_inc(chain, -1)
                dve.sem_inc(gain_free, 2)
                dve.wait_ge(wn2_loaded, 16)
                with dve.Fori(0, T // 2) as i:
                    for r in range(2):
                        t = 2 * i + r
                        nc.vector.tensor_scalar(gain[:, r, :], wn2[:, :], tmp[:, bass.ds(t, 1)], 1.0,
                                                ALU.mult, ALU.add).then_inc(chain, 1)
                        dve.wait_ge(chain, 1)
                        dve.sem_inc(chain, -1)
                        nc.vector.tensor_tensor(gain[:, r, :].unsqueeze(1), gain[:, r, :].unsqueeze(1),
                                                h0[:, bass.ds(t, 1), :], ALU.mult).then_inc(chain, 1)
                        dve.wait_ge(chain, 1)
                        dve.sem_inc(chain, -1)
                        nc.vector.tensor_tensor(K.X[:, bass.ds(t, 1), :], K.X[:, bass.ds(t, 1), :],
                                                gain[:, r, :].unsqueeze(1), ALU.add)

            @block.scalar
            def _(act):
                act.wait_ge(nmr_ready, 1)
                act.sem_inc(nmr_ready, -1)
                act.sem_inc(xn_free, 2)

                def normal(t, r):
                    nc.scalar.activation(xn[:, r, :].unsqueeze(1), K.X[:, bass.ds(t, 1), :], ACT.Identity,
                                         bias=nmr[:, bass.ds(t, 1)], scale=K.rstd[:, bass.ds(t, 1)]).then_inc(xn_ready, 1)

                def square(t, r):
                    act.wait_ge(h0_ready, 1)
                    act.sem_inc(h0_ready, -1)
                    nc.scalar.activation(junk[:, r, :].unsqueeze(1), h0[:, bass.ds(t, 1), :], ACT.Square,
                                         accum_out=ssq[:, bass.ds(t, 1)]).then_inc(out_free, 1)
                normal(0, 0)
                normal(1, 1)
                with act.Fori(0, T // 2 - 1) as i:
                    for r in range(2):
                        square(2 * i + r, r)
                        normal(2 * i + 2 + r, r)
                square(T - 2, 0)
                square(T - 1, 1)
                act.drain().then_inc(sq_done, 1)
                act.wait_ge(ms_ready, 1)
                act.sem_inc(ms_ready, -1)
                nc.scalar.activation(ssq[:, :], ssq[:, :], ACT.Sqrt).then_inc(root_ready, 1)


def edge_tables(nc, I, K, atab):
    fp32, i32, bf16, ALU = mybir.dt.float32, mybir.dt.int32, mybir.dt.bfloat16, mybir.AluOpType
    with ExitStack() as ctx:
        def sb(n, shape, dt=fp32):
            return ctx.enter_context(nc.sbuf_tensor(f"et_{n}", shape, dt))

        def ps(n):
            return ctx.enter_context(nc.psum_tensor(f"et_{n}", [P, 512], fp32))

        def sem(n):
            return K.sem(f"et_{n}")
        dst_i, lo_i, hi_i = sb("dst_i", [P, ET], i32), sb("lo_i", [P, ET], i32), sb("hi_i", [P, ET], i32)
        prev_i, prev = sb("prev_i", [P, 1], i32), sb("prev", [P, 1])
        dstf, lo, hi, hits = sb("dstf", [P, ET]), sb("lo", [P, ET]), sb("hi", [P, ET]), sb("hits", [P, ET])
        bound, cnt, ends, ends_i, rank = sb("bound", [P, T]), sb("cnt", [P, T]), sb("ends", [P, T]), sb("ends_i", [P, T], i32), sb("rank", [P, T])
        ns, cs_i, cs, es = sb("ns", [P, S]), sb("cs_i", [SQ, SG], i32), sb("cs", [SQ, SG]), sb("es", [SQ, SG])
        es_i = sb("es_i", [SQ, SG], i32)
        rows_i, rows = sb("rows_i", [SQ, 2, SG, P], i32), sb("rows", [SQ, 2, SG, P])
        onelo, onehi = sb("onelo", [P, HJ, P], bf16), sb("onehi", [P, HJ, T], bf16)
        zero = sb("zero", [P, P], bf16)
        last_e = sb("last_e", [P, T])
        psC, psH, psU, psR = ps("psC"), ps("psH"), ps("psU"), [ps("psR0"), ps("psR1")]
        prev_set, loaded, chain, cs_ready = sem("prev_set"), sem("loaded"), sem("chain"), sem("cs_ready")
        cnt_ready, ends_full, es_ready, rows_in, rows_ready, rows_full = (
            sem("cnt_ready"), sem("ends_full"), sem("es_ready"), sem("rows_in"), sem("rows_ready"), sem("rows_full"))
        hot_ready, hot_free = [sem("hot_ready0"), sem("hot_ready1")], [sem("hot_free0"), sem("hot_free1")]
        hist_full, deg_ready, cum_full = sem("hist_full"), sem("deg_ready"), sem("cum_full")
        zero_set = sem("zero_set")
        with nc.Block() as block:
            @block.sync
            def _(sp):
                sp.dma_start(dst_i[:, :], I["dst"].rearrange("(p f) -> p f", p=P)).then_inc(loaded, 16)
                sp.wait_ge(prev_set, 1)
                sp.sem_inc(prev_set, -1)
                sp.dma_start(prev_i[1:P, :], I["dst"].rearrange("(p f) -> p f", p=P)[0:P - 1, ET - 1:ET],
                             allow_slow_non_contiguous=True).then_inc(loaded, 16)

            @block.gpsimd
            def _(pool):
                pool.iota(cs_i[:, :], pattern=[[SQ, SG]], base=0, channel_multiplier=1).then_inc(cs_ready, 1)
                pool.wait_ge(es_ready, 1)
                pool.sem_inc(es_ready, -1)
                for g in range(SG):
                    for j, table in enumerate(("src", "dst")):
                        nc.gpsimd.indirect_dma_start(
                            out=rows_i[:, j, g, :], out_offset=None, in_=I[table].rearrange("(t e) -> t e", e=P),
                            in_offset=bass.IndirectOffsetOnAxis(ap=es_i[:, g:g + 1].bitcast(mybir.dt.uint32), axis=0)
                        ).then_inc(rows_in, 16)
                gather_terms(nc, K, pool, atab, 21, ET // HJ)

            @block.vector
            def _(dve):
                nc.vector.memset(prev_i[:, :], -1).then_inc(prev_set, 1)
                nc.vector.memset(zero[:, :], 0.0).then_inc(zero_set, 1)
                nc.vector.memset(ns[:, :], 0.0)
                nc.vector.memset(es[:, :], 0.0)
                nc.vector.memset(K.base[:, S:S + 8], 0.0)
                nc.vector.memset(K.ns[:, 0:4], T - 1)
                nc.vector.memset(K.ns[:, 4 + S:], 0)
                dve.wait_ge(loaded, 32)
                nc.vector.tensor_copy(dstf[:, :], dst_i[:, :])
                nc.vector.tensor_copy(prev[:, :], prev_i[:, :])
                nc.vector.tensor_scalar(lo_i[:, :], dst_i[:, :], P - 1, None, ALU.bitwise_and)
                nc.vector.tensor_scalar(hi_i[:, :], dst_i[:, :], 7, None, ALU.arith_shift_right)
                nc.vector.tensor_scalar(bound[:, :], K.iota[:, 0:T], float(P), float(P), ALU.mult, ALU.add).then_inc(chain, 1)
                dve.wait_ge(chain, 1)
                dve.sem_inc(chain, -1)
                nc.vector.tensor_copy(lo[:, :], lo_i[:, :])
                nc.vector.tensor_copy(hi[:, :], hi_i[:, :])
                nc.vector.tensor_tensor(K.cap[:, 1:ET], dstf[:, 1:ET], dstf[:, 0:ET - 1], ALU.is_equal)
                nc.vector.tensor_tensor(K.cap[:, 0:1], dstf[:, 0:1], prev[:, :], ALU.is_equal).then_inc(chain, 1)
                dve.wait_ge(chain, 1)
                dve.sem_inc(chain, -1)
                nc.vector.tensor_reduce(K.capall[:, :], K.cap[:, :], mybir.AxisListType.X, ALU.min).then_inc(chain, 1)
                dve.wait_ge(chain, 1)
                dve.sem_inc(chain, -1)
                nc.vector.tensor_scalar(K.cap[:, :], K.cap[:, :], 2 * BIG, -BIG, ALU.mult, ALU.add)
                nc.vector.tensor_scalar(K.capall[:, :], K.capall[:, :], 2 * BIG, -BIG, ALU.mult, ALU.add).then_inc(chain, 1)
                dve.wait_ge(chain, 1)
                dve.sem_inc(chain, -1)
                with dve.Fori(0, T) as n:
                    nc.vector.tensor_scalar(hits[:, :], dstf[:, :], bound[:, bass.ds(n, 1)], None,
                                            ALU.is_lt, ALU.add, accum_out=cnt[:, bass.ds(n, 1)]).then_inc(chain, 1)
                    dve.wait_ge(chain, 1)
                    dve.sem_inc(chain, -1)
                nc.vector.tensor_copy(bound[:, 0:1], cnt[:, 0:1]).then_inc(cnt_ready, 1)
                dve.wait_ge(ends_full, 1)
                dve.sem_inc(ends_full, -1)
                nc.vector.tensor_copy(ends[:, :], psC[:, 0:T])
                nc.vector.tensor_copy(ends_i[:, :], psC[:, 0:T]).then_inc(chain, 1)
                dve.wait_ge(chain, 1)
                dve.sem_inc(chain, -1)
                nc.vector.tensor_scalar(ends_i[:, :], ends_i[:, :], 7, None, ALU.arith_shift_right).then_inc(chain, 1)
                dve.wait_ge(chain, 1)
                dve.sem_inc(chain, -1)
                nc.vector.tensor_tensor(rank[:, :], ends_i[:, :], K.iota[:, 0:T], ALU.add).then_inc(chain, 1)
                dve.wait_ge(chain, 1)
                dve.sem_inc(chain, -1)
                dve.wait_ge(cs_ready, 1)
                dve.sem_inc(cs_ready, -1)
                nc.vector.tensor_copy(cs[:, :], cs_i[:, :]).then_inc(chain, 1)
                dve.wait_ge(chain, 1)
                dve.sem_inc(chain, -1)
                with dve.Fori(0, T - 1) as n:
                    nc.vector.scalar_tensor_tensor(ns[:, :], K.iota[:, 0:S], rank[:, bass.ds(n, 1)], ns[:, :],
                                                   ALU.is_gt, ALU.add)
                    nc.vector.scalar_tensor_tensor(es[:, :], cs[:, :], rank[0:SQ, bass.ds(n, 1)], es[:, :],
                                                   ALU.is_gt, ALU.add).then_inc(chain, 1)
                    dve.wait_ge(chain, 1)
                    dve.sem_inc(chain, -1)
                nc.vector.tensor_tensor(es[:, :], cs[:, :], es[:, :], ALU.subtract).then_inc(chain, 1)
                dve.wait_ge(chain, 1)
                dve.sem_inc(chain, -1)
                nc.vector.tensor_copy(K.ns[:, 4:4 + S], ns[:, :])
                nc.vector.tensor_copy(es_i[:, :], es[:, :]).then_inc(es_ready, 1)

                with dve.Fori(0, ET // HJ) as i:
                    for h, (a, b) in enumerate(PART):
                        n = b - a
                        dve.wait_ge(hot_free[h], 1)
                        dve.sem_inc(hot_free[h], -1)
                        nc.vector.tensor_tensor(onehi[:, a:b, :], hi[:, bass.ds(i * HJ + a, n)].unsqueeze(2).broadcast_to([P, n, T]),
                                                K.iota[:, 0:T].unsqueeze(1).broadcast_to([P, n, T]), ALU.is_equal)
                        nc.vector.tensor_tensor(onelo[:, a:b, :], lo[:, bass.ds(i * HJ + a, n)].unsqueeze(2).broadcast_to([P, n, P]),
                                                K.iota[:, 0:P].unsqueeze(1).broadcast_to([P, n, P]), ALU.is_equal).then_inc(hot_ready[h], 1)
                dve.wait_ge(rows_in, 16 * 2 * SG)
                nc.vector.tensor_copy(rows[:, :, :, :], rows_i[:, :, :, :]).then_inc(rows_ready, 1)
                dve.wait_ge(hist_full, 1)
                dve.sem_inc(hist_full, -1)
                nc.vector.tensor_copy(K.deg[:, :], psH[:, 0:T]).then_inc(deg_ready, 1)
                dve.wait_ge(rows_full, 1)
                dve.sem_inc(rows_full, -1)
                nc.vector.tensor_copy(K.src_s[:, :], psR[0][:, 0:S])
                nc.vector.scalar_tensor_tensor(K.base[:, 0:S], ns[:, :], float(P), psR[1][:, 0:S], ALU.mult, ALU.subtract)
                dve.wait_ge(cum_full, 1)
                dve.sem_inc(cum_full, -1)
                nc.vector.tensor_scalar(last_e[:, 0:1], psU[:, 0:1], -1.0, None, ALU.add)
                nc.vector.scalar_tensor_tensor(last_e[:, 1:T], psU[:, 1:T], -1.0, ends[:, 0:T - 1],
                                               ALU.add, ALU.add).then_inc(chain, 1)
                dve.wait_ge(chain, 1)
                dve.sem_inc(chain, -1)
                nc.vector.tensor_scalar(last_e[:, :], last_e[:, :], 0.0, None, ALU.max).then_inc(chain, 1)
                dve.wait_ge(chain, 1)
                dve.sem_inc(chain, -1)
                nc.vector.tensor_copy(K.last_edge[:, :], last_e[:, :])

            @block.tensor
            def _(pe):
                pe.wait_ge(zero_set, 1)
                pe.sem_inc(zero_set, -1)
                nc.tensor.matmul(psH[:, 0:T], zero[:, :], zero[:, 0:T], start=True, stop=False)
                pe.sem_inc(hot_free[0], 1)
                pe.sem_inc(hot_free[1], 1)
                pe.wait_ge(cnt_ready, 1)
                pe.sem_inc(cnt_ready, -1)
                nc.tensor.matmul(psC[:, 0:T], K.ones[:, :], cnt[:, :], start=True, stop=True).then_inc(ends_full, 1)
                with pe.Fori(0, ET // HJ) as i:
                    for h, (a, b) in enumerate(PART):
                        pe.wait_ge(hot_ready[h], 1)
                        pe.sem_inc(hot_ready[h], -1)
                        for k in range(a, b):
                            last = nc.tensor.matmul(psH[:, 0:T], onelo[:, k, :], onehi[:, k, :], start=False, stop=False)
                        last.then_inc(hot_free[h], 1)
                nc.tensor.matmul(psH[:, 0:T], zero[:, :], zero[:, 0:T], start=False, stop=True).then_inc(hist_full, 1)
                pe.wait_ge(rows_ready, 1)
                pe.sem_inc(rows_ready, -1)
                for j in range(2):
                    for g in range(SG):
                        last = nc.tensor.transpose(psR[j][:, g * SQ:(g + 1) * SQ], rows[:, j, g, :], K.ident[0:SQ, 0:SQ])
                last.then_inc(rows_full, 1)
                pe.wait_ge(deg_ready, 1)
                pe.sem_inc(deg_ready, -1)
                nc.tensor.matmul(psU[:, 0:T], K.upper[:, :], K.deg[:, :], start=True, stop=True).then_inc(cum_full, 1)


def softmax_maxima(nc, K, ftab):
    fp32, i32, ALU, ACT = mybir.dt.float32, mybir.dt.int32, mybir.AluOpType, mybir.ActivationFunctionType
    with ExitStack() as ctx:
        def sb(n, shape, dt=fp32):
            return ctx.enter_context(nc.sbuf_tensor(f"sm_{n}", shape, dt))

        def sem(n):
            return K.sem(f"sm_{n}")
        run = sb("run", [P, ET, HEADS])
        part, partT, capT = sb("part", [P, 2, HEADS]), sb("partT", [HEADS, P]), sb("capT", [HEADS, P])
        carryT, carry = sb("carryT", [HEADS, P + 1]), sb("carry", [P, HEADS])
        top, has = sb("top", [P, T, HEADS]), sb("has", [P, T, 2])
        tmp = sb("tmp", [P, T, HEADS])
        psT = ctx.enter_context(nc.psum_tensor("sm_psT", [P, 512], fp32))
        psB = ctx.enter_context(nc.psum_tensor("sm_psB", [P, 512], fp32))
        chain = sem("chain")
        part_ready, partT_full, carry_ready, carry_full = sem("part_ready"), sem("partT_full"), sem("carry_ready"), sem("carry_full")
        run_ready, stored, top_in, self_ready = sem("run_ready"), sem("stored"), sem("top_in"), sem("self_ready")
        with nc.Block() as block:
            @block.gpsimd
            def _(pool):
                pool.wait_ge(stored, 16)
                for t in range(T):
                    nc.gpsimd.indirect_dma_start(
                        out=top[:, t, :], out_offset=None, in_=ftab,
                        in_offset=bass.IndirectOffsetOnAxis(ap=K.last_edge[:, t:t + 1].bitcast(mybir.dt.uint32), axis=0)
                    ).then_inc(top_in, 16)

            @block.sync
            def _(sp):
                sp.wait_ge(run_ready, 1)
                sp.sem_inc(run_ready, -1)
                sp.dma_start(ftab.rearrange("(p f) h -> p (f h)", p=P), run[:, :, :].rearrange("p f h -> p (f h)")).then_inc(stored, 16)

            @block.vector
            def _(dve):
                nc.vector.memset(carryT[:, 0:1], -BIG).then_inc(chain, 1)
                dve.wait_ge(chain, 1)
                dve.sem_inc(chain, -1)
                for h in range(HEADS):
                    last = nc.vector.tensor_tensor_scan(run[:, :, h], K.cap[:, :], K.term[:, :, h], -BIG, ALU.min, ALU.max)
                last.then_inc(chain, 1)
                dve.wait_ge(chain, 1)
                dve.sem_inc(chain, -1)
                nc.vector.tensor_copy(part[:, 0, :], run[:, ET - 1, :])
                nc.vector.tensor_copy(part[:, 1, :], K.capall[:, 0:1].broadcast_to([P, HEADS])).then_inc(part_ready, 1)
                dve.wait_ge(partT_full, 1)
                dve.sem_inc(partT_full, -1)
                nc.vector.tensor_copy(partT[:, :], psT[0:HEADS, 0:P])
                nc.vector.tensor_copy(capT[:, :], psT[0:HEADS, P:2 * P]).then_inc(chain, 1)
                dve.wait_ge(chain, 1)
                dve.sem_inc(chain, -1)
                nc.vector.tensor_tensor_scan(carryT[:, 1:P + 1], capT[:, :], partT[:, :], -BIG, ALU.min, ALU.max).then_inc(carry_ready, 1)
                dve.wait_ge(carry_full, 1)
                dve.sem_inc(carry_full, -1)
                nc.vector.tensor_copy(carry[:, :], psB[:, 0:HEADS]).then_inc(chain, 1)
                dve.wait_ge(chain, 1)
                dve.sem_inc(chain, -1)
                for h in range(HEADS):
                    last = nc.vector.tensor_tensor_scan(run[:, :, h], K.cap[:, :], K.term[:, :, h], carry[:, h:h + 1], ALU.min, ALU.max)
                last.then_inc(run_ready, 1)
                nc.vector.tensor_scalar(has[:, :, 0], K.deg[:, :], 1.0, None, ALU.min).then_inc(chain, 1)
                dve.wait_ge(chain, 1)
                dve.sem_inc(chain, -1)
                nc.vector.tensor_scalar(has[:, :, 1], has[:, :, 0], BIG, -BIG, ALU.mult, ALU.add).then_inc(chain, 1)
                dve.wait_ge(chain, 1)
                dve.sem_inc(chain, -1)
                dve.wait_ge(top_in, 16 * T)
                a_s, a_d = K.H[:, :, D:TW], K.H[:, :, TW:HW]
                nc.vector.tensor_tensor(top[:, :, :], top[:, :, :], has[:, :, 0:1].broadcast_to([P, T, HEADS]), ALU.mult).then_inc(chain, 1)
                dve.wait_ge(chain, 1)
                dve.sem_inc(chain, -1)
                nc.vector.tensor_tensor(top[:, :, :], top[:, :, :], has[:, :, 1:2].broadcast_to([P, T, HEADS]), ALU.add).then_inc(chain, 1)
                dve.wait_ge(chain, 1)
                dve.sem_inc(chain, -1)
                nc.vector.tensor_tensor(top[:, :, :], top[:, :, :], a_s, ALU.max).then_inc(chain, 1)
                dve.wait_ge(chain, 1)
                dve.sem_inc(chain, -1)
                nc.vector.tensor_tensor(top[:, :, :], top[:, :, :], a_d, ALU.add).then_inc(chain, 1)
                dve.wait_ge(chain, 1)
                dve.sem_inc(chain, -1)
                nc.vector.scalar_tensor_tensor(K.node[:, :, HEADS:], top[:, :, :], 0.2, top[:, :, :], ALU.mult, ALU.max)
                nc.vector.tensor_copy(K.node[:, :, 0:HEADS], a_d)
                nc.vector.tensor_tensor(tmp[:, :, :], a_s, a_d, ALU.add).then_inc(chain, 1)
                dve.wait_ge(chain, 1)
                dve.sem_inc(chain, -1)
                nc.vector.scalar_tensor_tensor(tmp[:, :, :], tmp[:, :, :], 0.2, tmp[:, :, :], ALU.mult, ALU.max).then_inc(chain, 1)
                dve.wait_ge(chain, 1)
                dve.sem_inc(chain, -1)
                nc.vector.tensor_tensor(tmp[:, :, :], tmp[:, :, :], K.node[:, :, HEADS:], ALU.subtract).then_inc(self_ready, 1)

            @block.scalar
            def _(act):
                act.wait_ge(self_ready, 1)
                act.sem_inc(self_ready, -1)
                nc.scalar.activation(K.selfw[:, :, :], tmp[:, :, :], ACT.Exp)

            @block.tensor
            def _(pe):
                pe.wait_ge(part_ready, 1)
                pe.sem_inc(part_ready, -1)
                nc.tensor.transpose(psT[0:HEADS, 0:P], part[:, 0, :], K.ident[:, :])
                nc.tensor.transpose(psT[0:HEADS, P:2 * P], part[:, 1, :], K.ident[:, :]).then_inc(partT_full, 1)
                pe.wait_ge(carry_ready, 1)
                pe.sem_inc(carry_ready, -1)
                nc.tensor.transpose(psB[:, 0:HEADS], carryT[:, 0:P], K.ident[0:HEADS, 0:HEADS]).then_inc(carry_full, 1)


def gat(nc, I, K, htab):
    fp32, i32, ALU, ACT = mybir.dt.float32, mybir.dt.int32, mybir.AluOpType, mybir.ActivationFunctionType
    G = 4
    R = 4
    with ExitStack() as ctx:
        def sb(n, shape, dt=fp32):
            return ctx.enter_context(nc.sbuf_tensor(f"ga_{n}", shape, dt))

        def ps(n):
            return ctx.enter_context(nc.psum_tensor(f"ga_{n}", [P, 512], fp32))

        def sem(n):
            return K.sem(f"ga_{n}")
        cur, rows, wrows = sb("cur", [P, R, G], i32), sb("rows", [P, R, G, TW]), sb("wrows", [P, 2, G, TW])
        hot, hotT, z = sb("hot", [P, R, G, P]), sb("hotT", [P, 2, G, P]), sb("z", [P, 2, G, HEADS])
        acc, zero, b0 = sb("acc", [P, 2, T, TW]), sb("zero", [P, P]), sb("b0", [P, D])
        off = sb("off", [P, 2, G, P])
        psT, psN, psA = ps("psT"), [ps("psN0"), ps("psN1")], [ps(f"psA{k}") for k in range(G)]
        chain, pchain, achain, passed = sem("chain"), sem("pchain"), sem("achain"), sem("passed")
        rows_in, rows_free = [sem(f"rows_in{h}") for h in range(R)], sem("rows_free")
        hot_ready, hotT_full, hotT_ready, node_full = sem("hot_ready"), sem("hotT_full"), sem("hotT_ready"), sem("node_full")
        z_ready, w_ready, wrows_ready, acc_full, acc_free = sem("z_ready"), sem("w_ready"), sem("wrows_ready"), sem("acc_full"), sem("acc_free")
        zero_set, b0_in, low_ready, exp_ready = sem("zero_set"), sem("b0_in"), sem("low_ready"), sem("exp_ready")
        added, sums_ready, pool_low, pool_exp, self_ready = [sem("added0"), sem("added1")], sem("sums_ready"), sem("pool_low"), sem("pool_exp"), sem("self_ready")
        by_head = lambda x: x.rearrange("p (a d) -> p a d", d=HD)

        def finish(eng, ops, chain, t0, t1, low, exp):
            hs, a = K.H[:, t0:t1, 0:D], acc[:, 0, t0:t1, 0:D]
            ops.tensor_tensor(a, a, hs, ALU.add).then_inc(chain, 1)
            eng.wait_ge(chain, 1)
            eng.sem_inc(chain, -1)
            for t in range(t0, t1):
                last = ops.tensor_tensor(by_head(acc[:, 0, t, 0:D]), by_head(acc[:, 0, t, 0:D]),
                                         acc[:, 0, t, D:TW].unsqueeze(2).broadcast_to([P, HEADS, HD]), ALU.mult)
            last.then_inc(chain, 1)
            eng.wait_ge(chain, 1)
            eng.sem_inc(chain, -1)
            ops.tensor_tensor(a, a, b0[:, :].unsqueeze(1).broadcast_to([P, t1 - t0, D]), ALU.add).then_inc(chain, 1)
            eng.wait_ge(chain, 1)
            eng.sem_inc(chain, -1)
            ops.tensor_scalar(hs, a, 0.0, None, ALU.min).then_inc(low, 1)
            ops.tensor_scalar(a, a, 0.0, -1.0, ALU.max, ALU.add).then_inc(chain, 1)
            eng.wait_ge(chain, 1)
            eng.sem_inc(chain, -1)
            ops.tensor_tensor(K.X[:, t0:t1, :], K.X[:, t0:t1, :], a, ALU.add).then_inc(chain, 1)
            eng.wait_ge(chain, 1)
            eng.sem_inc(chain, -1)
            eng.wait_ge(exp, 1)
            eng.sem_inc(exp, -1)
            ops.tensor_tensor(K.X[:, t0:t1, :], K.X[:, t0:t1, :], hs, ALU.add)
        CUTS = (0, 9, 18, T)
        STAGES = S // G
        with nc.Block() as block:
            @block.gpsimd
            def _(pool):
                pool.sem_inc(rows_free, R)
                with pool.Fori(0, STAGES // R) as i:
                    for h in range(R):
                        pool.wait_ge(rows_free, 1)
                        pool.sem_inc(rows_free, -1)
                        nc.gpsimd.tensor_copy(cur[:, h, :], K.src_s[:, bass.ds((R * i + h) * G, G)]).then_inc(pchain, 1)
                        pool.wait_ge(pchain, 1)
                        pool.sem_inc(pchain, -1)
                        for k in range(G):
                            nc.gpsimd.indirect_dma_start(
                                out=rows[:, h, k, :], out_offset=None, in_=htab,
                                in_offset=bass.IndirectOffsetOnAxis(ap=cur[:, h, k:k + 1].bitcast(mybir.dt.uint32), axis=0)
                            ).then_inc(rows_in[h], 16)
                        if h == R - 1:
                            own = K.H[:, bass.ds(i, 1), 0:D].rearrange("p t (a d) -> p (t a) d", d=HD)
                            weight = K.selfw[:, bass.ds(i, 1), :].rearrange("p t a -> p (t a)").unsqueeze(2).broadcast_to([P, HEADS, HD])
                            nc.gpsimd.tensor_tensor(own, own, weight, ALU.mult).then_inc(pchain, 1)
                            pool.wait_ge(pchain, 1)
                            pool.sem_inc(pchain, -1)
                pool.sem_inc(self_ready, 1)
                pool.wait_ge(b0_in, 16)
                pool.wait_ge(sums_ready, 1)
                pool.sem_inc(sums_ready, -1)
                finish(pool, nc.gpsimd, pchain, CUTS[2], CUTS[3], pool_low, pool_exp)

            @block.sync
            def _(sp):
                sp.dma_start(b0[:, :], I["b0"].partition_broadcast(P)).then_inc(b0_in, 16)

            @block.vector
            def _(dve):
                nc.vector.memset(zero[:, :], 0.0).then_inc(zero_set, 1)
                nc.vector.memset(acc[:, :, :, :], 0.0).then_inc(chain, 1)
                dve.wait_ge(chain, 1)
                dve.sem_inc(chain, -1)

                def add(ns, steps):
                    for k in steps:
                        dve.wait_ge(acc_full, 1)
                        dve.sem_inc(acc_full, -1)
                        nc.vector.tensor_tensor(acc[:, k % 2, bass.ds(ns[k], 1), :], acc[:, k % 2, bass.ds(ns[k], 1), :],
                                                psA[k][:, 0:TW].unsqueeze(1), ALU.add).then_inc(added[k % 2], 1)

                def added_both():
                    for k in range(2):
                        dve.wait_ge(added[k], 1)
                        dve.sem_inc(added[k], -1)
                        dve.sem_inc(acc_free, 1)

                dve.sem_inc(added[0], 1)
                dve.sem_inc(added[1], 1)
                with dve.Fori(0, STAGES // R) as i:
                    for h in range(R):
                        q, w2 = R * i + h, h % 2
                        ns = node_tiles(nc, K, dve, q * G, G)
                        dve.wait_ge(node_full, 1)
                        dve.sem_inc(node_full, -1)
                        dve.wait_ge(rows_in[h], (i + 1) * (16 * G))
                        dve.sem_inc(passed, 1)
                        nd = psN[w2][:, 0:G * 16].rearrange("p (k n) -> p k n", k=G)
                        nc.vector.tensor_tensor(z[:, w2, :, :], rows[:, h, :, D:TW], nd[:, :, 0:HEADS], ALU.add).then_inc(chain, 1)
                        added_both()
                        dve.wait_ge(chain, 1)
                        dve.sem_inc(chain, -1)
                        nc.vector.scalar_tensor_tensor(z[:, w2, :, :], z[:, w2, :, :], 0.2, z[:, w2, :, :], ALU.mult, ALU.max).then_inc(chain, 1)
                        dve.wait_ge(chain, 1)
                        dve.sem_inc(chain, -1)
                        nc.vector.tensor_tensor(z[:, w2, :, :], z[:, w2, :, :], nd[:, :, HEADS:], ALU.subtract).then_inc(chain, 1)
                        dve.wait_ge(chain, 1)
                        dve.sem_inc(chain, -1)
                        nc.vector.tensor_scalar(z[:, w2, :, :], z[:, w2, :, :], 1.0, None, ALU.min).then_inc(z_ready, 1)
                        add(ns, (0, 1))
                        dve.wait_ge(w_ready, 1)
                        dve.sem_inc(w_ready, -1)
                        nc.vector.tensor_tensor(
                            wrows[:, w2, :, 0:D].rearrange("p k (a d) -> p k a d", d=HD),
                            rows[:, h, :, 0:D].rearrange("p k (a d) -> p k a d", d=HD),
                            wrows[:, w2, :, D:TW].unsqueeze(3).broadcast_to([P, G, HEADS, HD]), ALU.mult).then_inc(chain, 1)
                        added_both()
                        dve.wait_ge(chain, 1)
                        dve.sem_inc(chain, -1)
                        dve.sem_inc(wrows_ready, 1)
                        dve.sem_inc(rows_free, 1)
                        add(ns, (2, 3))
                ns = node_tiles(nc, K, dve, STAGES * G, G)
                added_both()
                add(ns, (0, 1))
                added_both()
                add(ns, (2, 3))
                added_both()
                nc.vector.tensor_tensor(acc[:, 0, :, :], acc[:, 0, :, :], acc[:, 1, :, :], ALU.add).then_inc(chain, 1)
                dve.wait_ge(chain, 1)
                dve.sem_inc(chain, -1)
                a_den = acc[:, 0, :, D:TW]
                nc.vector.tensor_tensor(a_den, a_den, K.selfw[:, :, :], ALU.add).then_inc(chain, 1)
                dve.wait_ge(chain, 1)
                dve.sem_inc(chain, -1)
                nc.vector.tensor_scalar(a_den, a_den, 1e-16, None, ALU.add).then_inc(chain, 1)
                dve.wait_ge(chain, 1)
                dve.sem_inc(chain, -1)
                nc.vector.reciprocal(a_den, a_den).then_inc(chain, 1)
                dve.wait_ge(chain, 1)
                dve.sem_inc(chain, -1)
                dve.sem_inc(sums_ready, 1)
                dve.wait_ge(b0_in, 16)
                dve.wait_ge(self_ready, 1)
                dve.sem_inc(self_ready, -1)
                finish(dve, nc.vector, chain, CUTS[0], CUTS[1], low_ready, exp_ready)
                finish(dve, nc.vector, chain, CUTS[1], CUTS[2], low_ready, exp_ready)

            @block.scalar
            def _(act):
                def onehot(q, h):
                    for k in range(G):
                        last = nc.scalar.activation(off[:, h % 2, k, :], K.iota[:, 0:P], ACT.Abs, bias=K.base[:, bass.ds(q * G + k, 1)])
                    last.then_inc(achain, 1)
                    act.wait_ge(achain, 1)
                    act.sem_inc(achain, -1)
                    nc.scalar.activation(hot[:, h, :, :], off[:, h % 2, :, :], ACT.Relu, bias=K.ones[:, 0:1], scale=-1.0).then_inc(hot_ready, 1)

                def copy(h):
                    act.wait_ge(hotT_full, 1)
                    act.sem_inc(hotT_full, -1)
                    nc.scalar.activation(hotT[:, h, :, :].rearrange("p k n -> p (k n)"), psT[:, :], ACT.Copy).then_inc(hotT_ready, 1)
                onehot(0, 0)
                onehot(1, 1)
                copy(0)
                with act.Fori(0, STAGES // R) as i:
                    for h in range(R):
                        copy((h + 1) % 2)
                        onehot(R * i + h + 2, (h + 2) % R)
                        act.wait_ge(z_ready, 1)
                        act.sem_inc(z_ready, -1)
                        nc.scalar.activation(wrows[:, h % 2, :, D:TW], z[:, h % 2, :, :], ACT.Exp).then_inc(w_ready, 1)
                for t0, t1, low, exp in zip(CUTS[0:3], CUTS[1:4], (low_ready, low_ready, pool_low), (exp_ready, exp_ready, pool_exp)):
                    act.wait_ge(low, 1)
                    act.sem_inc(low, -1)
                    nc.scalar.activation(K.H[:, t0:t1, 0:D], K.H[:, t0:t1, 0:D], ACT.Exp).then_inc(exp, 1)

            @block.tensor
            def _(pe):
                def transposes(h):
                    pe.wait_ge(hot_ready, 1)
                    pe.sem_inc(hot_ready, -1)
                    for k in range(G):
                        last = nc.tensor.transpose(psT[:, k * P:(k + 1) * P], hot[:, h, k, :], K.ident[:, :])
                    last.then_inc(hotT_full, 1)

                def node_terms(q, h):
                    pe.wait_ge(hotT_ready, 1)
                    pe.sem_inc(hotT_ready, -1)
                    ns = node_tiles(nc, K, pe, (q + 1) * G, G)
                    for k in range(G):
                        last = nc.tensor.matmul(psN[h][:, k * 16:(k + 1) * 16], hotT[:, h, k, :],
                                                K.node[:, bass.ds(ns[k], 1), :].rearrange("p a b -> p (a b)"), start=True, stop=True)
                    last.then_inc(node_full, 1)
                pe.wait_ge(zero_set, 1)
                pe.sem_inc(zero_set, -1)
                for k in range(G):
                    nc.tensor.matmul(psA[k][:, 0:TW], zero[:, :], K.iota[:, 0:TW], start=True, stop=True).then_inc(acc_full, 1)
                transposes(0)
                node_terms(0, 0)
                transposes(1)
                pe.wait_ge(acc_free, 2)
                pe.sem_inc(acc_free, -2)
                with pe.Fori(0, STAGES // R) as i:
                    for h in range(R):
                        node_terms(R * i + h + 1, (h + 1) % 2)
                        transposes((h + 2) % R)
                        pe.wait_ge(wrows_ready, 1)
                        pe.sem_inc(wrows_ready, -1)
                        for k in range(G):
                            pe.wait_ge(acc_free, 1)
                            pe.sem_inc(acc_free, -1)
                            nc.tensor.matmul(psA[k][:, 0:TW], hot[:, h, k, :], wrows[:, h % 2, k, :],
                                             start=True, stop=True).then_inc(acc_full, 1)


def choose(nc, I, K, wtab):
    fp32, ALU = mybir.dt.float32, mybir.AluOpType
    AX = mybir.AxisListType.X
    with ExitStack() as ctx:
        def sb(n, shape):
            return ctx.enter_context(nc.sbuf_tensor(f"ch_{n}", shape, fp32))

        def sem(n):
            return K.sem(f"ch_{n}")
        wr, br, w, tmp = sb("wr", [P, D]), sb("br", [P, 1]), sb("w", [P, T]), sb("tmp", [P, T])
        prod, wT, every, above = sb("prod", [P, 2, D]), sb("wT", [T, P]), sb("every", [P, T * P]), sb("above", [P, 2, T * P])
        rank, least, leastT, edge = sb("rank", [P, T]), sb("least", [P, 1]), sb("leastT", [1, P]), sb("edge", [1, 1])
        gt, eq, cum, tot, both, need = sb("gt", [P, T]), sb("eq", [P, T]), sb("cum", [P, T]), sb("tot", [P, T + 1]), sb("both", [P, 2]), sb("need", [P, 1])
        zeros, tau = sb("zeros", [P, T]), sb("tau", [P, 1])
        ps = [ctx.enter_context(nc.psum_tensor(f"ch_ps{j}", [P, 512], fp32)) for j in range(4)]
        loaded, chain, w_ready, wT_full, wT_ready, stored, every_in = (
            sem("loaded"), sem("chain"), sem("w_ready"), sem("wT_full"), sem("wT_ready"), sem("stored"), sem("every_in"))
        least_ready, leastT_full, edge_ready, tau_full, marks_ready, marks_full = (
            sem("least_ready"), sem("leastT_full"), sem("edge_ready"), sem("tau_full"), sem("marks_ready"), sem("marks_full"))
        with nc.Block() as block:
            @block.sync
            def _(sp):
                sp.dma_start(wr[:, :], I["f0_wr"].partition_broadcast(P)).then_inc(loaded, 16)
                sp.dma_start(br[:, :], I["f0_br"].partition_broadcast(P)).then_inc(loaded, 16)
                sp.wait_ge(wT_ready, 1)
                sp.sem_inc(wT_ready, -1)
                sp.dma_start(wtab.rearrange("(t p) -> t p", p=P), wT[:, :]).then_inc(stored, 16)
                sp.wait_ge(stored, 16)
                sp.dma_start(every[:, :], wtab.partition_broadcast(P)).then_inc(every_in, 16)

            @block.vector
            def _(dve):
                nc.vector.memset(zeros[:, :], 0.0)
                nc.vector.memset(tot[:, 0:1], 0.0)
                dve.wait_ge(loaded, 32)
                with dve.Fori(0, T // 2) as i:
                    for k in range(2):
                        nc.vector.scalar_tensor_tensor(
                            prod[:, k, :].unsqueeze(1), K.X[:, bass.ds(2 * i + k, 1), :], K.mean[:, bass.ds(2 * i + k, 1)],
                            wr[:, :].unsqueeze(1), ALU.subtract, ALU.mult, accum_out=w[:, bass.ds(2 * i + k, 1)]).then_inc(chain, 1)
                        dve.wait_ge(chain, 1)
                        dve.sem_inc(chain, -1)
                nc.vector.tensor_tensor(w[:, :], w[:, :], K.rstd[:, :], ALU.mult).then_inc(chain, 1)
                dve.wait_ge(chain, 1)
                dve.sem_inc(chain, -1)
                nc.vector.tensor_scalar(w[:, :], w[:, :], br[:, 0:1], None, ALU.add).then_inc(chain, 1)
                dve.wait_ge(chain, 1)
                dve.sem_inc(chain, -1)
                nc.vector.tensor_tensor(w[:, :], w[:, :], K.real[:, :], ALU.mult).then_inc(chain, 1)
                dve.wait_ge(chain, 1)
                dve.sem_inc(chain, -1)
                nc.vector.tensor_scalar(tmp[:, :], K.real[:, :], BIG, -BIG, ALU.mult, ALU.add).then_inc(chain, 1)
                dve.wait_ge(chain, 1)
                dve.sem_inc(chain, -1)
                nc.vector.tensor_tensor(w[:, :], w[:, :], tmp[:, :], ALU.add).then_inc(w_ready, 1)
                dve.wait_ge(wT_full, 1)
                dve.sem_inc(wT_full, -1)
                nc.vector.tensor_copy(wT[:, :], ps[0][0:T, 0:P]).then_inc(wT_ready, 1)
                dve.wait_ge(every_in, 16)
                with dve.Fori(0, T // 2) as i:
                    for k in range(2):
                        nc.vector.tensor_scalar(above[:, k, :], every[:, :], w[:, bass.ds(2 * i + k, 1)], None,
                                                ALU.is_gt, ALU.add, accum_out=rank[:, bass.ds(2 * i + k, 1)]).then_inc(chain, 1)
                        dve.wait_ge(chain, 1)
                        dve.sem_inc(chain, -1)
                nc.vector.tensor_scalar(gt[:, :], rank[:, :], float(KEEP), None, ALU.is_lt).then_inc(chain, 1)
                dve.wait_ge(chain, 1)
                dve.sem_inc(chain, -1)
                nc.vector.tensor_tensor(cum[:, :], w[:, :], gt[:, :], ALU.mult).then_inc(chain, 1)
                dve.wait_ge(chain, 1)
                dve.sem_inc(chain, -1)
                nc.vector.tensor_scalar(gt[:, :], gt[:, :], -BIG, BIG, ALU.mult, ALU.add).then_inc(chain, 1)
                dve.wait_ge(chain, 1)
                dve.sem_inc(chain, -1)
                nc.vector.tensor_tensor(cum[:, :], cum[:, :], gt[:, :], ALU.add).then_inc(chain, 1)
                dve.wait_ge(chain, 1)
                dve.sem_inc(chain, -1)
                nc.vector.tensor_reduce(least[:, :], cum[:, :], AX, ALU.min).then_inc(least_ready, 1)
                dve.wait_ge(leastT_full, 1)
                dve.sem_inc(leastT_full, -1)
                nc.vector.tensor_reduce(edge[:, :], ps[1][0:1, 0:P], AX, ALU.min).then_inc(edge_ready, 1)
                dve.wait_ge(tau_full, 1)
                dve.sem_inc(tau_full, -1)
                nc.vector.tensor_copy(tau[:, :], ps[2][:, 0:1]).then_inc(chain, 1)
                dve.wait_ge(chain, 1)
                dve.sem_inc(chain, -1)
                nc.vector.tensor_scalar(gt[:, :], w[:, :], tau[:, 0:1], None, ALU.is_gt)
                nc.vector.tensor_scalar(eq[:, :], w[:, :], tau[:, 0:1], None, ALU.is_equal).then_inc(chain, 1)
                dve.wait_ge(chain, 1)
                dve.sem_inc(chain, -1)
                nc.vector.tensor_reduce(both[:, 0:1], gt[:, :], AX, ALU.add).then_inc(marks_ready, 1)
                dve.wait_ge(marks_full, 1)
                dve.sem_inc(marks_full, -1)
                nc.vector.tensor_scalar(need[:, :], ps[3][:, 0:1], -1.0, float(KEEP), ALU.mult, ALU.add)
                nc.vector.tensor_copy(cum[:, :], ps[3][:, 64:64 + T])
                nc.vector.tensor_tensor_scan(tot[:, 1:T + 1], zeros[:, :], ps[3][:, 128:128 + T], 0.0, ALU.add, ALU.add).then_inc(chain, 1)
                dve.wait_ge(chain, 1)
                dve.sem_inc(chain, -1)
                nc.vector.tensor_tensor(cum[:, :], cum[:, :], tot[:, 0:T], ALU.add).then_inc(chain, 1)
                dve.wait_ge(chain, 1)
                dve.sem_inc(chain, -1)
                nc.vector.tensor_scalar(cum[:, :], cum[:, :], need[:, 0:1], None, ALU.is_le).then_inc(chain, 1)
                dve.wait_ge(chain, 1)
                dve.sem_inc(chain, -1)
                nc.vector.tensor_tensor(eq[:, :], eq[:, :], cum[:, :], ALU.mult).then_inc(chain, 1)
                dve.wait_ge(chain, 1)
                dve.sem_inc(chain, -1)
                nc.vector.tensor_tensor(gt[:, :], gt[:, :], eq[:, :], ALU.add).then_inc(chain, 1)
                dve.wait_ge(chain, 1)
                dve.sem_inc(chain, -1)
                nc.vector.tensor_tensor(K.coef[:, :], gt[:, :], w[:, :], ALU.mult)

            @block.tensor
            def _(pe):
                pe.wait_ge(w_ready, 1)
                pe.sem_inc(w_ready, -1)
                nc.tensor.transpose(ps[0][0:T, 0:P], w[:, :], K.ident[:, :]).then_inc(wT_full, 1)
                pe.wait_ge(least_ready, 1)
                pe.sem_inc(least_ready, -1)
                nc.tensor.transpose(ps[1][0:1, 0:P], least[:, :], K.ident[:, :]).then_inc(leastT_full, 1)
                pe.wait_ge(edge_ready, 1)
                pe.sem_inc(edge_ready, -1)
                nc.tensor.matmul(ps[2][:, 0:1], K.ones[0:1, :], edge[:, :], start=True, stop=True).then_inc(tau_full, 1)
                pe.wait_ge(marks_ready, 1)
                pe.sem_inc(marks_ready, -1)
                nc.tensor.matmul(ps[3][:, 0:1], K.ones[:, :], both[:, 0:1], start=True, stop=True)
                nc.tensor.matmul(ps[3][:, 64:64 + T], K.upper[:, :], eq[:, :], start=True, stop=True)
                nc.tensor.matmul(ps[3][:, 128:128 + T], K.ones[:, :], eq[:, :], start=True, stop=True).then_inc(marks_full, 1)


def ffn0(nc, I, K):
    fp32, ALU, ACT = mybir.dt.float32, mybir.AluOpType, mybir.ActivationFunctionType
    M = FF0 // P
    with ExitStack() as ctx:
        def sb(n, shape):
            return ctx.enter_context(nc.sbuf_tensor(f"f0_{n}", shape, fp32))

        def ps(n):
            return ctx.enter_context(nc.psum_tensor(f"f0_{n}", [P, 512], fp32))

        def sem(n):
            return K.sem(f"f0_{n}")
        w1, b1, w2, b2 = sb("w1", [P, C, FF0]), sb("b1", [P, M]), sb("w2", [P, M, D]), sb("b2", [1, D])
        xs, xT, hT = sb("xs", [P, 2, D]), sb("xT", [P, C, 2 * P]), sb("hT", [P, M, 2 * P])
        gain, shift = sb("gain", [P, T]), sb("shift", [P, T])
        psT, psU, psO = ps("psT"), [ps("psU0"), ps("psU1")], [ps("psO0"), ps("psO1")]
        loaded, chain = sem("loaded"), sem("chain")
        xs_ready, xT_full, xT_ready, up_full, up_free, hT_ready, out_full, out_free = (
            sem(n) for n in ("xs_ready", "xT_full", "xT_ready", "up_full", "up_free", "hT_ready", "out_full", "out_free"))
        xs_free = sem("xs_free")
        with nc.Block() as block:
            @block.sync
            def _(sp):
                sp.dma_start(w1[:, :, :], I["f0_w1"].rearrange("(c p) n -> p c n", p=P)).then_inc(loaded, 16)
                sp.dma_start(w2[:, :, :], I["f0_w2"].rearrange("(m p) n -> p m n", p=P)).then_inc(loaded, 16)
                sp.dma_start(b1[:, :], I["f0_b1"]).then_inc(loaded, 16)
                sp.dma_start(b2[:, :], I["f0_b2"].rearrange("(a n) -> a n", a=1)).then_inc(loaded, 16)

            @block.vector
            def _(dve):
                nc.vector.tensor_scalar(gain[:, :], K.rstd[:, :], 1.0, None, ALU.add)
                nc.vector.tensor_tensor(shift[:, :], K.mean[:, :], K.rstd[:, :], ALU.mult).then_inc(chain, 1)
                dve.wait_ge(chain, 1)
                dve.sem_inc(chain, -1)
                nc.vector.tensor_scalar(shift[:, :], shift[:, :], -1.0, None, ALU.mult).then_inc(chain, 1)
                dve.wait_ge(chain, 1)
                dve.sem_inc(chain, -1)

                def norm(i):
                    for r in range(2):
                        t = 2 * i + r
                        last = nc.vector.tensor_scalar(xs[:, r, :].unsqueeze(1), K.X[:, bass.ds(t, 1), :],
                                                       K.mean[:, bass.ds(t, 1)], K.rstd[:, bass.ds(t, 1)],
                                                       ALU.subtract, ALU.mult)
                    last.then_inc(xs_ready, 1)

                def finish(i):
                    for r in range(2):
                        t = 2 * i + r
                        x = K.X[:, bass.ds(t, 1), :]
                        nc.vector.tensor_scalar(x, x, gain[:, bass.ds(t, 1)], shift[:, bass.ds(t, 1)],
                                                ALU.mult, ALU.add).then_inc(chain, 1)
                        dve.wait_ge(chain, 1)
                        dve.sem_inc(chain, -1)
                        dve.wait_ge(out_full, 1)
                        dve.sem_inc(out_full, -1)
                        nc.vector.scalar_tensor_tensor(x, psO[r][:, 0:D].unsqueeze(1), K.coef[:, bass.ds(t, 1)], x,
                                                       ALU.mult, ALU.add).then_inc(out_free, 1)
                norm(0)
                with dve.Fori(0, T // 2 - 1) as i:
                    dve.wait_ge(xs_free, 1)
                    dve.sem_inc(xs_free, -1)
                    norm(i + 1)
                    finish(i)
                finish(T // 2 - 1)

            @block.scalar
            def _(act):
                with act.Fori(0, T // 2) as i:
                    act.wait_ge(xT_full, 1)
                    act.sem_inc(xT_full, -1)
                    nc.scalar.activation(xT[:, :, :].rearrange("p c n -> p (c n)"), psT[:, :], ACT.Copy).then_inc(xT_ready, 1)
                    for m in range(M):
                        act.wait_ge(up_full, 1)
                        act.sem_inc(up_full, -1)
                        nc.scalar.activation(hT[:, m, :], psU[m % 2][:, 0:2 * P], ACT.Gelu_apprx_tanh,
                                             bias=b1[:, m:m + 1]).then_inc(up_free, 1)

            @block.tensor
            def _(pe):
                pe.sem_inc(out_free, 2)
                pe.sem_inc(up_free, 2)
                pe.wait_ge(loaded, 64)

                def transposes():
                    pe.wait_ge(xs_ready, 1)
                    pe.sem_inc(xs_ready, -1)
                    for c in range(C):
                        for r in range(2):
                            last = nc.tensor.transpose(psT[:, (2 * c + r) * P:(2 * c + r + 1) * P],
                                                       xs[:, r, c * P:(c + 1) * P], K.ident[:, :])
                    last.then_inc(xT_full, 1)

                def body(final):
                    pe.wait_ge(xT_ready, 1)
                    pe.sem_inc(xT_ready, -1)
                    pe.sem_inc(xs_free, 1)
                    for m in range(M):
                        pe.wait_ge(up_free, 1)
                        pe.sem_inc(up_free, -1)
                        for c in range(C):
                            last = nc.tensor.matmul(psU[m % 2][:, 0:2 * P], w1[:, c, m * P:(m + 1) * P], xT[:, c, :],
                                                    start=(c == 0), stop=(c == C - 1))
                        last.then_inc(up_full, 1)
                    if not final:
                        transposes()
                    pe.wait_ge(up_free, 2)
                    pe.sem_inc(up_free, -2)
                    pe.sem_inc(up_free, 2)
                    for r in range(2):
                        pe.wait_ge(out_free, 1)
                        pe.sem_inc(out_free, -1)
                        nc.tensor.matmul(psO[r][:, 0:D], K.ones[0:1, :], b2[:, :], start=True, stop=False)
                        for m in range(M):
                            last = nc.tensor.matmul(psO[r][:, 0:D], hT[:, m, r * P:(r + 1) * P], w2[:, m, :],
                                                    start=False, stop=(m == M - 1))
                        last.then_inc(out_full, 1)
                transposes()
                with pe.Fori(0, T // 2 - 1) as i:
                    body(False)
                body(True)


def normalise(nc, K, ztab):
    fp32, ALU = mybir.dt.float32, mybir.AluOpType
    with ExitStack() as ctx:
        done, stored = K.sem("no_done"), K.sem("no_stored")
        with nc.Block() as block:
            @block.vector
            def _(dve):
                with dve.Fori(0, T // 2) as i:
                    for k in range(2):
                        t = 2 * i + k
                        nc.vector.tensor_scalar(K.Z[:, bass.ds(t, 1), :], K.X[:, bass.ds(t, 1), :], K.mean[:, bass.ds(t, 1)],
                                                K.rstd[:, bass.ds(t, 1)], ALU.subtract, ALU.mult).then_inc(done, 1)

            @block.sync
            def _(sp):
                sp.wait_ge(done, T)
                sp.sem_inc(done, -T)
                sp.dma_start(ztab.rearrange("(t p) n -> p t n", p=P), K.Z[:, :, :]).then_inc(stored, 16)
                sp.wait_ge(stored, 16)


def aggregate(nc, I, K, ztab, stab):
    fp32, i32, ALU, ACT = mybir.dt.float32, mybir.dt.int32, mybir.AluOpType, mybir.ActivationFunctionType
    G = 4
    R = 4
    with ExitStack() as ctx:
        def sb(n, shape, dt=fp32):
            return ctx.enter_context(nc.sbuf_tensor(f"ag_{n}", shape, dt))

        def sem(n):
            return K.sem(f"ag_{n}")
        cur, rows, hot, zero = sb("cur", [P, R, G], i32), sb("rows", [P, R, G, D]), sb("hot", [P, 2, G, P]), sb("zero", [P, P])
        off = sb("off", [P, 2, G, P])
        psA = [ctx.enter_context(nc.psum_tensor(f"ag_psA{k}", [P, 512], fp32)) for k in range(G)]
        chain, pchain, achain, hot_free = sem("chain"), sem("pchain"), sem("achain"), sem("hot_free")
        rows_in, rows_free, passed = [sem(f"rows_in{h}") for h in range(R)], sem("rows_free"), sem("passed")
        hot_ready, acc_full, acc_free, zero_set = sem("hot_ready"), sem("acc_full"), sem("acc_free"), sem("zero_set")
        STAGES = S // G
        wself, bg, xs, ps = sb("wself", [P, C, D]), sb("bg", [P, D]), sb("xs", [P, 2, D + 1]), [
            ctx.enter_context(nc.psum_tensor(f"ag_{n}", [P, 512], fp32)) for n in ("psG0", "psG1", "psT", "psS")]
        xT = sb("xT", [P, D])
        loaded, z_ready, zT_full, zT_ready, s_full, gram_full = (sem(n) for n in ("loaded", "z_ready", "zT_full", "zT_ready", "s_full", "gram_full"))
        wide_zero, stab_zero = sb("wide_zero", [P, 8, D]), sem("stab_zero")
        wide_zero_set = sem("wide_zero_set")
        with nc.Block() as block:
            @block.sync
            def _(sp):
                sp.dma_start(wself[:, :, :], I["Wself"].rearrange("(c p) n -> p c n", p=P)).then_inc(loaded, 16)
                sp.dma_start(bg[:, :], I["bgnn"].partition_broadcast(P)).then_inc(loaded, 16)
                sp.wait_ge(wide_zero_set, 1)
                sp.sem_inc(wide_zero_set, -1)
                slots = stab[0:ST * P, :].rearrange("(j p r) d -> j p r d", p=P, r=8)
                for j in range(ST // 8):
                    sp.dma_start(slots[j], wide_zero[:, :, :]).then_inc(stab_zero, 16)
                sp.wait_ge(stab_zero, ST // 8 * 16)

            @block.gpsimd
            def _(pool):
                pool.sem_inc(rows_free, R - 1)
                with pool.Fori(0, STAGES // R) as i:
                    for h in range(R):
                        pool.wait_ge(rows_free, 1)
                        pool.sem_inc(rows_free, -1)
                        nc.gpsimd.tensor_copy(cur[:, h, :], K.src_s[:, bass.ds((R * i + h) * G, G)]).then_inc(pchain, 1)
                        pool.wait_ge(pchain, 1)
                        pool.sem_inc(pchain, -1)
                        for k in range(G):
                            nc.gpsimd.indirect_dma_start(
                                out=rows[:, h, k, :], out_offset=None, in_=ztab,
                                in_offset=bass.IndirectOffsetOnAxis(ap=cur[:, h, k:k + 1].bitcast(mybir.dt.uint32), axis=0)
                            ).then_inc(rows_in[h], 16)

            @block.vector
            def _(dve):
                nc.vector.memset(wide_zero[:, :, :], 0.0).then_inc(wide_zero_set, 1)
                nc.vector.memset(zero[:, :], 0.0).then_inc(zero_set, 1)
                nc.vector.memset(K.agg[:, :, :], 0.0).then_inc(chain, 1)
                dve.wait_ge(chain, 1)
                dve.sem_inc(chain, -1)

                def add(q):
                    ns = node_tiles(nc, K, dve, q * G, G)
                    for k in range(G):
                        dve.wait_ge(acc_full, 1)
                        dve.sem_inc(acc_full, -1)
                        n = ns[k]
                        nc.vector.tensor_tensor(K.agg[:, bass.ds(n, 1), :], K.agg[:, bass.ds(n, 1), :],
                                                psA[k][:, 0:D].unsqueeze(1), ALU.add).then_inc(chain, 1)
                        dve.wait_ge(chain, 1)
                        dve.sem_inc(chain, -1)
                        dve.sem_inc(acc_free, 1)
                    dve.sem_inc(rows_free, 1)
                    dve.sem_inc(hot_free, 1)

                def rows_of(t, k):
                    nc.vector.tensor_copy(xs[:, k, D:D + 1], K.real[:, bass.ds(t, 1)])
                    nc.vector.tensor_scalar(xs[:, k, 0:D].unsqueeze(1), K.Z[:, bass.ds(t, 1), :],
                                            K.real[:, bass.ds(t, 1)], None, ALU.mult).then_inc(z_ready, 1)

                def self_part(t):
                    dve.wait_ge(s_full, 1)
                    dve.sem_inc(s_full, -1)
                    nc.vector.tensor_tensor(K.G[:, bass.ds(t, 1), :], ps[3][:, 0:D].unsqueeze(1), bg[:, :].unsqueeze(1), ALU.add)
                dve.wait_ge(loaded, 32)
                with dve.Fori(0, STAGES // R // 2) as i:
                    for k in range(2):
                        for h in range(R):
                            if h == 0:
                                rows_of(2 * i + k, k)
                            add(R * (2 * i + k) + h)
                        self_part(2 * i + k)
                add(STAGES)
                dve.wait_ge(gram_full, 1)
                dve.sem_inc(gram_full, -1)
                for c in range(C):
                    nc.vector.tensor_copy(K.gram[:, c, :], ps[c][:, 0:D + 1])

            @block.scalar
            def _(act):
                act.sem_inc(hot_free, 1)
                with act.Fori(0, STAGES // R) as i:
                    for h in range(R):
                        if h == 2:
                            act.wait_ge(zT_full, 1)
                            act.sem_inc(zT_full, -1)
                            nc.scalar.activation(K.ZT[:, bass.ds(i, 1), :], ps[2][:, 0:D].unsqueeze(1), ACT.Copy)
                            nc.scalar.activation(xT[:, :], ps[2][:, 0:D], ACT.Copy).then_inc(zT_ready, 1)
                        act.wait_ge(hot_free, 1)
                        act.sem_inc(hot_free, -1)
                        for k in range(G):
                            last = nc.scalar.activation(off[:, h % 2, k, :], K.iota[:, 0:P], ACT.Abs, bias=K.base[:, bass.ds((R * i + h) * G + k, 1)])
                        last.then_inc(achain, 1)
                        act.wait_ge(achain, 1)
                        act.sem_inc(achain, -1)
                        nc.scalar.activation(hot[:, h % 2, :, :], off[:, h % 2, :, :], ACT.Relu, bias=K.ones[:, 0:1], scale=-1.0).then_inc(hot_ready, 1)

            @block.tensor
            def _(pe):
                pe.wait_ge(zero_set, 1)
                pe.sem_inc(zero_set, -1)
                for k in range(G):
                    nc.tensor.matmul(psA[k][:, 0:D], zero[:, :], K.iota[:, 0:D], start=True, stop=True).then_inc(acc_full, 1)
                for c in range(C):
                    nc.tensor.matmul(ps[c][:, 0:D + 1], zero[:, :], K.iota[:, 0:D + 1], start=True, stop=False)
                pe.wait_ge(loaded, 32)

                def beside(k, h):
                    if h == 0:
                        pe.wait_ge(z_ready, 1)
                        pe.sem_inc(z_ready, -1)
                        for c in range(C):
                            last = nc.tensor.transpose(ps[2][:, c * P:(c + 1) * P], xs[:, k, c * P:(c + 1) * P], K.ident[:, :])
                        last.then_inc(zT_full, 1)
                    if h == 1:
                        for c in range(C):
                            nc.tensor.matmul(ps[c][:, 0:D + 1], xs[:, k, c * P:(c + 1) * P], xs[:, k, :], start=False, stop=False)
                    if h == 2:
                        pe.wait_ge(zT_ready, 1)
                        pe.sem_inc(zT_ready, -1)
                        for c in range(C):
                            last = nc.tensor.matmul(ps[3][:, 0:D], xT[:, c * P:(c + 1) * P], wself[:, c, :], start=(c == 0), stop=(c == C - 1))
                        last.then_inc(s_full, 1)
                with pe.Fori(0, STAGES // R // 2) as i:
                    for k in range(2):
                        for h in range(R):
                            pe.wait_ge(hot_ready, 1)
                            pe.sem_inc(hot_ready, -1)
                            pe.wait_ge(rows_in[h], (2 * i + (k + 1)) * (16 * G))
                            pe.sem_inc(passed, 1)
                            for j in range(G):
                                pe.wait_ge(acc_free, 1)
                                pe.sem_inc(acc_free, -1)
                                nc.tensor.matmul(psA[j][:, 0:D], hot[:, h % 2, j, :], rows[:, h, j, :],
                                                 start=True, stop=True).then_inc(acc_full, 1)
                            beside(k, h)
                for c in range(C):
                    last = nc.tensor.matmul(ps[c][:, 0:D + 1], zero[:, :], K.iota[:, 0:D + 1], start=False, stop=True)
                last.then_inc(gram_full, 1)


def combine1(nc, I, K):
    fp32, ALU, ACT = mybir.dt.float32, mybir.AluOpType, mybir.ActivationFunctionType
    with ExitStack() as ctx:
        def sb(n, shape):
            return ctx.enter_context(nc.sbuf_tensor(f"c1_{n}", shape, fp32))

        def sem(n):
            return K.sem(f"c1_{n}")
        wk, wv, wfc, wq = (sb(n, [P, C, D]) for n in ("wk", "wv", "wfc", "wq"))
        wneigh, gram = sb("wneigh", [P, C, D]), K.gram
        bk, bv, bfc, bq = sb("bk", [1, D]), sb("bv", [1, D]), sb("bfc", [1, D]), sb("bq", [P, C])
        col, b3_row = sb("col", [1, D + 1]), sb("b3_row", [P, D])
        t1, t1a, kvT, m2, m3, b3 = sb("t1", [P, C, D]), sb("t1a", [1, D]), sb("kvT", [P, C, P]), sb("m2", [P, C, D]), sb("m3", [P, C, D]), sb("b3", [1, D])
        rdeg, ys, zT, yT, g = sb("rdeg", [P, T]), sb("ys", [P, 2, D]), sb("zT", [P, 2, D]), sb("yT", [P, 2, D]), sb("g", [P, 2, D])
        ps = [ctx.enter_context(nc.psum_tensor(f"c1_ps{j}", [P, 512], fp32)) for j in range(8)]
        loaded, chain, step = sem("loaded"), sem("chain"), sem("step")
        ready, full, b3_ready, b3_added, pchain = sem("ready"), sem("full"), sem("b3_ready"), sem("b3_added"), sem("pchain")
        ys_ready, yT_full, yT_ready, m_full, g_full, g_ready, relu_ready, m_free = (
            sem(n) for n in ("ys_ready", "yT_full", "yT_ready", "m_full", "g_full", "g_ready", "relu_ready", "m_free"))
        with nc.Block() as block:
            @block.sync
            def _(sp):
                for a, n in ((wk, "WkT"), (wv, "WvT"), (wfc, "WfcT"), (wq, "Wq"), (wneigh, "Wneigh")):
                    sp.dma_start(a[:, :, :], I[n].rearrange("(c p) n -> p c n", p=P)).then_inc(loaded, 16)
                for a, n in ((bk, "bk"), (bv, "bv"), (bfc, "bfc")):
                    sp.dma_start(a[:, :], I[n].rearrange("(a n) -> a n", a=1)).then_inc(loaded, 16)
                sp.dma_start(bq[:, :], I["bq"]).then_inc(loaded, 16)

            @block.vector
            def _(dve):
                nc.vector.memset(col[:, D:D + 1], float(N))
                dve.wait_ge(full, 1)
                dve.sem_inc(full, -1)
                nc.vector.tensor_copy(col[:, 0:D], ps[2][0:1, 0:D]).then_inc(ready, 1)
                dve.wait_ge(full, 1)
                dve.sem_inc(full, -1)
                for c in range(C):
                    nc.vector.tensor_copy(t1[:, c, :], ps[3 + c][:, 0:D])
                nc.vector.tensor_copy(t1a[:, :], ps[5][0:1, 0:D]).then_inc(ready, 1)
                dve.wait_ge(full, 1)
                dve.sem_inc(full, -1)
                for c in range(C):
                    mask = K.blockmask[:, c, 4 * c:4 * c + 4].unsqueeze(2).broadcast_to([P, 4, HD])
                    last = nc.vector.scalar_tensor_tensor(
                        kvT[:, c, :].rearrange("p (h m) -> p h m", m=HD),
                        ps[6 + c][:, c * P:(c + 1) * P].rearrange("p (h m) -> p h m", m=HD), 1.0 / N, mask, ALU.mult, ALU.mult)
                last.then_inc(ready, 1)
                dve.wait_ge(full, 1)
                dve.sem_inc(full, -1)
                for c in range(C):
                    last = nc.vector.tensor_copy(m2[:, c, :], ps[c][:, 0:D])
                last.then_inc(ready, 1)
                dve.wait_ge(full, 1)
                dve.sem_inc(full, -1)
                for c in range(C):
                    nc.vector.tensor_copy(m3[:, c, :], ps[2 + c][:, 0:D])
                nc.vector.tensor_copy(b3[:, :], ps[4][0:1, 0:D]).then_inc(ready, 1)
                dve.wait_ge(full, 1)
                dve.sem_inc(full, -1)
                nc.vector.tensor_copy(b3_row[:, :], ps[5][:, 0:D]).then_inc(b3_ready, 1)

                nc.vector.tensor_scalar(rdeg[:, :], K.deg[:, :], 1.0, None, ALU.max).then_inc(chain, 1)
                dve.wait_ge(chain, 1)
                dve.sem_inc(chain, -1)
                nc.vector.reciprocal(rdeg[:, :], rdeg[:, :]).then_inc(chain, 1)
                dve.wait_ge(chain, 1)
                dve.sem_inc(chain, -1)

                def stage(t, k):
                    nc.vector.tensor_scalar(ys[:, k, :].unsqueeze(1), K.agg[:, bass.ds(t, 1), :], rdeg[:, bass.ds(t, 1)],
                                            None, ALU.mult).then_inc(ys_ready, 1)

                def finish(t, k, final):
                    x = K.X[:, bass.ds(t, 1), :]
                    dve.wait_ge(g_full, 1)
                    dve.sem_inc(g_full, -1)
                    nc.vector.tensor_tensor(g[:, k, :].unsqueeze(1), K.G[:, bass.ds(t, 1), :], ps[k][:, 0:D].unsqueeze(1), ALU.add).then_inc(g_ready, 1)
                    dve.wait_ge(m_full, 1)
                    dve.sem_inc(m_full, -1)
                    dve.wait_ge(b3_added, 1)
                    dve.sem_inc(b3_added, -1)
                    nc.vector.tensor_tensor(x, x, ps[4 + k][:, 0:D].unsqueeze(1), ALU.add).then_inc(chain, 1)
                    if not final:
                        stage(t + 2, k)
                    dve.wait_ge(chain, 1)
                    dve.sem_inc(chain, -1)
                    dve.wait_ge(relu_ready, 1)
                    dve.sem_inc(relu_ready, -1)
                    nc.vector.tensor_tensor(x, x, g[:, k, :].unsqueeze(1), ALU.add).then_inc(chain, 1)
                    dve.wait_ge(chain, 1)
                    dve.sem_inc(chain, -1)
                stage(0, 0)
                stage(1, 1)
                with dve.Fori(0, T // 2 - 1) as i:
                    for k in range(2):
                        finish(2 * i + k, k, False)
                finish(T - 2, 0, True)
                finish(T - 1, 1, True)

            @block.gpsimd
            def _(pool):
                pool.wait_ge(b3_ready, 1)
                pool.sem_inc(b3_ready, -1)
                with pool.Fori(0, T) as t:
                    x = K.X[:, bass.ds(t, 1), :]
                    nc.gpsimd.tensor_tensor(x, x, b3_row[:, :].unsqueeze(1), ALU.add).then_inc(b3_added, 1)

            @block.scalar
            def _(act):
                with act.Fori(0, T // 2) as i:
                    for k in range(2):
                        nc.scalar.activation(zT[:, k, :].unsqueeze(1), K.ZT[:, bass.ds(2 * i + k, 1), :], ACT.Copy)
                        act.wait_ge(yT_full, 1)
                        act.sem_inc(yT_full, -1)
                        nc.scalar.activation(yT[:, k, :], ps[6 + k][:, 0:D], ACT.Copy).then_inc(yT_ready, 1)
                        act.wait_ge(g_ready, 1)
                        act.sem_inc(g_ready, -1)
                        nc.scalar.activation(g[:, k, :], g[:, k, :], ACT.Relu).then_inc(relu_ready, 1)

            @block.tensor
            def _(pe):
                pe.wait_ge(loaded, 16 * 9)
                for c in range(C):
                    last = nc.tensor.transpose(ps[2][0:1, c * P:(c + 1) * P], gram[:, c, D:D + 1], K.ident[:, :])
                last.then_inc(full, 1)
                pe.wait_ge(ready, 1)
                pe.sem_inc(ready, -1)
                for m in range(C):
                    for c in range(C):
                        nc.tensor.matmul(ps[3 + m][:, 0:D], gram[:, c, m * P:(m + 1) * P], wk[:, c, :], start=(c == 0), stop=False)
                    nc.tensor.matmul(ps[3 + m][:, 0:D], col[:, m * P:(m + 1) * P], bk[:, :], start=False, stop=True)
                for c in range(C):
                    nc.tensor.matmul(ps[5][0:1, 0:D], gram[:, c, D:D + 1], wk[:, c, :], start=(c == 0), stop=False)
                nc.tensor.matmul(ps[5][0:1, 0:D], col[:, D:D + 1], bk[:, :], start=False, stop=True).then_inc(full, 1)
                pe.wait_ge(ready, 1)
                pe.sem_inc(ready, -1)
                for m in range(C):
                    for c in range(C):
                        nc.tensor.matmul(ps[6 + m][:, 0:D], wv[:, c, m * P:(m + 1) * P], t1[:, c, :], start=(c == 0), stop=False)
                    last = nc.tensor.matmul(ps[6 + m][:, 0:D], bv[:, m * P:(m + 1) * P], t1a[:, :], start=False, stop=True)
                last.then_inc(full, 1)
                pe.wait_ge(ready, 1)
                pe.sem_inc(ready, -1)
                for c in range(C):
                    last = nc.tensor.matmul(ps[c][:, 0:D], kvT[:, c, :], wfc[:, c, :], start=True, stop=True)
                last.then_inc(full, 1)
                pe.wait_ge(ready, 1)
                pe.sem_inc(ready, -1)
                for m in range(C):
                    for c in range(C):
                        nc.tensor.matmul(ps[2 + m][:, 0:D], wq[:, c, m * P:(m + 1) * P], m2[:, c, :], start=(c == 0), stop=(c == C - 1))
                nc.tensor.matmul(ps[4][0:1, 0:D], K.ones[0:1, 0:1], bfc[:, :], start=True, stop=False)
                for c in range(C):
                    last = nc.tensor.matmul(ps[4][0:1, 0:D], bq[:, c:c + 1], m2[:, c, :], start=False, stop=(c == C - 1))
                last.then_inc(full, 1)
                pe.wait_ge(ready, 1)
                pe.sem_inc(ready, -1)

                nc.tensor.matmul(ps[5][:, 0:D], K.ones[0:1, :], b3[:, :], start=True, stop=True).then_inc(full, 1)

                def transposes(k):
                    pe.wait_ge(ys_ready, 1)
                    pe.sem_inc(ys_ready, -1)
                    for c in range(C):
                        last = nc.tensor.transpose(ps[6 + k][:, c * P:(c + 1) * P], ys[:, k, c * P:(c + 1) * P], K.ident[:, :])
                    last.then_inc(yT_full, 1)

                def body(final):
                    for k in range(2):
                        pe.wait_ge(yT_ready, 1)
                        pe.sem_inc(yT_ready, -1)
                        if not (final and k == 1):
                            transposes(1 - k)
                        for c in range(C):
                            last = nc.tensor.matmul(ps[k][:, 0:D], yT[:, k, c * P:(c + 1) * P], wneigh[:, c, :], start=(c == 0), stop=(c == C - 1))
                        last.then_inc(g_full, 1)
                        for c in range(C):
                            last = nc.tensor.matmul(ps[4 + k][:, 0:D], zT[:, k, c * P:(c + 1) * P], m3[:, c, :], start=(c == 0), stop=(c == C - 1))
                        last.then_inc(m_full, 1)
                transposes(0)
                with pe.Fori(0, T // 2 - 1) as i:
                    body(False)
                body(True)


def route(nc, I, K):
    fp32, i32, ALU, ACT = mybir.dt.float32, mybir.dt.int32, mybir.AluOpType, mybir.ActivationFunctionType
    AX = mybir.AxisListType.X
    with ExitStack() as ctx:
        def sb(n, shape, dt=fp32):
            return ctx.enter_context(nc.sbuf_tensor(f"ro_{n}", shape, dt))

        def sem(n):
            return K.sem(f"ro_{n}")
        wr, br, gamma, beta = sb("wr", [P, C, NE]), sb("br", [1, NE]), sb("gamma", [P, C]), sb("beta", [P, C])
        xs, xT, logit = sb("xs", [P, 2, D]), sb("xT", [P, 2, C, P]), sb("logit", [P, T, NE])
        eq, which, left, order = sb("eq", [P, T, NE]), sb("which", [P, T]), sb("left", [P, T, NE]), sb("order", [P, NE])
        one, two = sb("one", [P, T, NE]), sb("two", [P, T, NE])
        top, top2, e = (sb(n, [P, T]) for n in ("top", "top2", "e"))
        marks, before, place, zeros = sb("marks", [P, T, NE]), sb("before", [P, T + 1, NE]), sb("place", [P, T, NE]), sb("zeros", [P, T])
        tiles_i, tiles, ends, start = sb("tiles_i", [P, NE], i32), sb("tiles", [P, NE]), sb("ends", [P, NE + 1]), sb("start", [P, NE])
        slot, spare_i, spare = sb("slot", [P, T, 2]), sb("spare_i", [P, T, 2], i32), sb("spare", [P, T, 2])
        past, expert = sb("past", [P, ST + 4, NE]), sb("expert", [P, ST + 4])
        psT = [ctx.enter_context(nc.psum_tensor(f"ro_psT{j}", [P, 512], fp32)) for j in range(2)]
        psL = [ctx.enter_context(nc.psum_tensor(f"ro_psL{j}", [P, 512], fp32)) for j in range(2)]
        loaded, chain, xs_ready, xT_full, xT_ready, l_full, gap_ready, e_ready = (
            sem(n) for n in ("loaded", "chain", "xs_ready", "xT_full", "xT_ready", "l_full", "gap_ready", "e_ready"))
        marks_ready, ranks_full, spare_ready = sem("marks_ready"), sem("ranks_full"), sem("spare_ready")
        with nc.Block() as block:
            @block.gpsimd
            def _(pool):
                pool.iota(spare_i[:, :, :], pattern=[[P, T], [T * P - N, 2]], base=ST * P - N, channel_multiplier=1).then_inc(spare_ready, 1)

            @block.sync
            def _(sp):
                sp.dma_start(wr[:, :, :], I["f1_Wr"].rearrange("(c p) n -> p c n", p=P)).then_inc(loaded, 16)
                sp.dma_start(br[:, :], I["f1_br"].rearrange("(a n) -> a n", a=1)).then_inc(loaded, 16)
                sp.dma_start(gamma[:, :], I["f1_gamma"]).then_inc(loaded, 16)
                sp.dma_start(beta[:, :], I["f1_beta"]).then_inc(loaded, 16)
                sp.dma_start(K.w1[:, :, :, :], I["f1_W1"].rearrange("e (c p) n -> p e c n", p=P)).then_inc(K.experts_loaded, 16)
                sp.dma_start(K.b1[:, :, :], I["f1_b1"].partition_broadcast(P)).then_inc(K.experts_loaded, 16)
                sp.dma_start(K.w2[:, :, :, :], I["f1_W2"].rearrange("e (m p) n -> p e m n", p=P)).then_inc(K.experts_loaded, 16)
                sp.dma_start(K.b2[:, :, :], I["f1_b2"].partition_broadcast(P)).then_inc(K.experts_loaded, 16)

            @block.vector
            def _(dve):
                def norm(t, k):
                    nc.vector.tensor_scalar(xs[:, k, :].unsqueeze(1), K.X[:, bass.ds(t, 1), :], K.mean[:, bass.ds(t, 1)],
                                            K.rstd[:, bass.ds(t, 1)], ALU.subtract, ALU.mult).then_inc(xs_ready, 1)

                def keep(t, k):
                    dve.wait_ge(l_full, 1)
                    dve.sem_inc(l_full, -1)
                    nc.vector.tensor_copy(logit[:, bass.ds(t, 1), :], psL[k][:, 0:NE].unsqueeze(1))
                norm(0, 0)
                norm(1, 1)
                with dve.Fori(0, T // 2 - 1) as i:
                    for k in range(2):
                        keep(2 * i + k, k)
                        norm(2 * i + k + 2, k)
                keep(T - 2, 0)
                dve.wait_ge(l_full, 1)
                dve.sem_inc(l_full, -1)
                nc.vector.tensor_copy(logit[:, T - 1, :], psL[1][:, 0:NE]).then_inc(chain, 1)
                dve.wait_ge(chain, 1)
                dve.sem_inc(chain, -1)
                wide = lambda a: a.unsqueeze(2).broadcast_to([P, T, NE])
                nc.vector.tensor_scalar(order[:, :], K.iota[:, 0:NE], -1.0, float(NE), ALU.mult, ALU.add).then_inc(chain, 1)
                dve.wait_ge(chain, 1)
                dve.sem_inc(chain, -1)

                def first(values, largest, hot):
                    nc.vector.tensor_reduce(largest, values, AX, ALU.max).then_inc(chain, 1)
                    dve.wait_ge(chain, 1)
                    dve.sem_inc(chain, -1)
                    nc.vector.tensor_tensor(eq[:, :, :], values, wide(largest), ALU.is_equal).then_inc(chain, 1)
                    dve.wait_ge(chain, 1)
                    dve.sem_inc(chain, -1)
                    nc.vector.tensor_tensor(eq[:, :, :], eq[:, :, :], order[:, :].unsqueeze(1).broadcast_to([P, T, NE]), ALU.mult).then_inc(chain, 1)
                    dve.wait_ge(chain, 1)
                    dve.sem_inc(chain, -1)
                    nc.vector.tensor_reduce(which[:, :], eq[:, :, :], AX, ALU.max).then_inc(chain, 1)
                    dve.wait_ge(chain, 1)
                    dve.sem_inc(chain, -1)
                    nc.vector.tensor_tensor(hot, eq[:, :, :], wide(which[:, :]), ALU.is_equal).then_inc(chain, 1)
                    dve.wait_ge(chain, 1)
                    dve.sem_inc(chain, -1)
                first(logit[:, :, :], top[:, :], one[:, :, :])
                nc.vector.scalar_tensor_tensor(left[:, :, :], one[:, :, :], -2 * BIG, logit[:, :, :], ALU.mult, ALU.add).then_inc(chain, 1)
                dve.wait_ge(chain, 1)
                dve.sem_inc(chain, -1)
                first(left[:, :, :], top2[:, :], two[:, :, :])
                nc.vector.tensor_tensor(e[:, :], top2[:, :], top[:, :], ALU.subtract).then_inc(gap_ready, 1)
                nc.vector.tensor_tensor(marks[:, :, :], one[:, :, :], two[:, :, :], ALU.add).then_inc(chain, 1)
                dve.wait_ge(chain, 1)
                dve.sem_inc(chain, -1)
                nc.vector.tensor_tensor(marks[:, :, :], marks[:, :, :], wide(K.real[:, :]), ALU.mult).then_inc(marks_ready, 1)
                nc.vector.memset(zeros[:, :], 0.0)
                nc.vector.memset(before[:, 0, :], 0.0)
                nc.vector.memset(ends[:, 0:1], 0.0)
                dve.wait_ge(e_ready, 1)
                dve.sem_inc(e_ready, -1)
                nc.vector.tensor_scalar(top[:, :], e[:, :], 1.0, None, ALU.add).then_inc(chain, 1)
                dve.wait_ge(chain, 1)
                dve.sem_inc(chain, -1)
                nc.vector.reciprocal(K.share[:, :, 0], top[:, :]).then_inc(chain, 1)
                dve.wait_ge(chain, 1)
                dve.sem_inc(chain, -1)
                nc.vector.tensor_tensor(K.share[:, :, 1], K.share[:, :, 0], e[:, :], ALU.mult)
                dve.wait_ge(ranks_full, 1)
                dve.sem_inc(ranks_full, -1)
                for x in range(NE):
                    last = nc.vector.tensor_tensor_scan(before[:, 1:T + 1, x], zeros[:, :],
                                                        psL[1][:, 0:T * NE].rearrange("p (t e) -> p t e", e=NE)[:, :, x], 0.0, ALU.add, ALU.add)
                last.then_inc(chain, 1)
                dve.wait_ge(chain, 1)
                dve.sem_inc(chain, -1)
                nc.vector.tensor_scalar(tiles_i[:, :], before[:, T, :], float(P - 1), None, ALU.add).then_inc(chain, 1)
                dve.wait_ge(chain, 1)
                dve.sem_inc(chain, -1)
                nc.vector.tensor_scalar(tiles_i[:, :], tiles_i[:, :], 7, None, ALU.arith_shift_right).then_inc(chain, 1)
                dve.wait_ge(chain, 1)
                dve.sem_inc(chain, -1)
                nc.vector.tensor_copy(tiles[:, :], tiles_i[:, :]).then_inc(chain, 1)
                dve.wait_ge(chain, 1)
                dve.sem_inc(chain, -1)
                nc.vector.tensor_tensor_scan(ends[:, 1:NE + 1], zeros[:, 0:NE], tiles[:, :], 0.0, ALU.add, ALU.add).then_inc(chain, 1)
                dve.wait_ge(chain, 1)
                dve.sem_inc(chain, -1)
                nc.vector.tensor_tensor(past[:, :, :], K.iota[:, 0:ST + 4].unsqueeze(2).broadcast_to([P, ST + 4, NE]),
                                        ends[:, 1:NE + 1].unsqueeze(1).broadcast_to([P, ST + 4, NE]), ALU.is_ge)
                nc.vector.tensor_scalar(start[:, :], ends[:, 0:NE], float(P), -1.0, ALU.mult, ALU.add).then_inc(chain, 1)
                dve.wait_ge(chain, 1)
                dve.sem_inc(chain, -1)
                nc.vector.tensor_reduce(expert[:, :], past[:, :, :], AX, ALU.add).then_inc(chain, 1)
                dve.wait_ge(chain, 1)
                dve.sem_inc(chain, -1)
                nc.vector.tensor_scalar(K.expert[:, :], expert[:, :], float(NE - 1), None, ALU.min)
                nc.vector.tensor_tensor(place[:, :, :], psL[0][:, 0:T * NE].rearrange("p (t e) -> p t e", e=NE),
                                        before[:, 0:T, :], ALU.add).then_inc(chain, 1)
                dve.wait_ge(chain, 1)
                dve.sem_inc(chain, -1)
                nc.vector.tensor_tensor(place[:, :, :], place[:, :, :], start[:, :].unsqueeze(1).broadcast_to([P, T, NE]), ALU.add).then_inc(chain, 1)
                dve.wait_ge(chain, 1)
                dve.sem_inc(chain, -1)
                nc.vector.tensor_tensor(one[:, :, :], one[:, :, :], place[:, :, :], ALU.mult)
                nc.vector.tensor_tensor(two[:, :, :], two[:, :, :], place[:, :, :], ALU.mult).then_inc(chain, 1)
                dve.wait_ge(chain, 1)
                dve.sem_inc(chain, -1)
                nc.vector.tensor_reduce(slot[:, :, 0], one[:, :, :], AX, ALU.add)
                nc.vector.tensor_reduce(slot[:, :, 1], two[:, :, :], AX, ALU.add).then_inc(chain, 1)
                dve.wait_ge(chain, 1)
                dve.sem_inc(chain, -1)
                dve.wait_ge(spare_ready, 1)
                dve.sem_inc(spare_ready, -1)
                nc.vector.tensor_copy(spare[:, :, :], spare_i[:, :, :]).then_inc(chain, 1)
                dve.wait_ge(chain, 1)
                dve.sem_inc(chain, -1)
                nc.vector.tensor_tensor(slot[:, :, :], slot[:, :, :], spare[:, :, :], ALU.subtract).then_inc(chain, 1)
                dve.wait_ge(chain, 1)
                dve.sem_inc(chain, -1)
                nc.vector.tensor_tensor(slot[:, :, :], slot[:, :, :], K.real[:, :].unsqueeze(2).broadcast_to([P, T, 2]), ALU.mult).then_inc(chain, 1)
                dve.wait_ge(chain, 1)
                dve.sem_inc(chain, -1)
                nc.vector.tensor_tensor(slot[:, :, :], slot[:, :, :], spare[:, :, :], ALU.add).then_inc(chain, 1)
                dve.wait_ge(chain, 1)
                dve.sem_inc(chain, -1)
                nc.vector.tensor_copy(K.slot[:, :, :], slot[:, :, :])
                nc.vector.tensor_scalar(K.back[:, :, :], slot[:, :, :], float(ST * P - 1), None, ALU.min)

            @block.scalar
            def _(act):
                act.wait_ge(loaded, 64)
                with act.Fori(0, T // 2) as i:
                    for k in range(2):
                        act.wait_ge(xT_full, 1)
                        act.sem_inc(xT_full, -1)
                        for c in range(C):
                            last = nc.scalar.activation(xT[:, k, c, :], psT[k][:, c * P:(c + 1) * P], ACT.Identity,
                                                        bias=beta[:, c:c + 1], scale=gamma[:, c:c + 1])
                        last.then_inc(xT_ready, 1)
                act.wait_ge(gap_ready, 1)
                act.sem_inc(gap_ready, -1)
                nc.scalar.activation(e[:, :], e[:, :], ACT.Exp).then_inc(e_ready, 1)

            @block.tensor
            def _(pe):
                pe.wait_ge(loaded, 64)

                def transposes(k):
                    pe.wait_ge(xs_ready, 1)
                    pe.sem_inc(xs_ready, -1)
                    for c in range(C):
                        last = nc.tensor.transpose(psT[k][:, c * P:(c + 1) * P], xs[:, k, c * P:(c + 1) * P], K.ident[:, :])
                    last.then_inc(xT_full, 1)

                def body(final):
                    for k in range(2):
                        pe.wait_ge(xT_ready, 1)
                        pe.sem_inc(xT_ready, -1)
                        if not (final and k == 1):
                            transposes(1 - k)
                        nc.tensor.matmul(psL[k][:, 0:NE], K.ones[0:1, :], br[:, :], start=True, stop=False)
                        for c in range(C):
                            last = nc.tensor.matmul(psL[k][:, 0:NE], xT[:, k, c, :], wr[:, c, :], start=False, stop=(c == C - 1))
                        last.then_inc(l_full, 1)
                transposes(0)
                with pe.Fori(0, T // 2 - 1) as i:
                    body(False)
                body(True)
                pe.wait_ge(marks_ready, 1)
                pe.sem_inc(marks_ready, -1)
                nc.tensor.matmul(psL[0][:, 0:T * NE], K.upper[:, :], marks[:, :, :].rearrange("p t e -> p (t e)"), start=True, stop=True)
                nc.tensor.matmul(psL[1][:, 0:T * NE], K.ones[:, :], marks[:, :, :].rearrange("p t e -> p (t e)"),
                                 start=True, stop=True).then_inc(ranks_full, 1)


def dispatch(nc, K, stab):
    fp32, i32, ALU = mybir.dt.float32, mybir.dt.int32, mybir.AluOpType
    R = 5
    with ExitStack() as ctx:
        def sem(n):
            return K.sem(f"di_{n}")
        xs = ctx.enter_context(nc.sbuf_tensor("di_xs", [P, R, D], fp32))
        cur = ctx.enter_context(nc.sbuf_tensor("di_cur", [P, R, 2], i32))
        xs_ready, pchain, passed, sent = sem("xs_ready"), sem("pchain"), sem("passed"), [sem(f"sent{h}") for h in range(R)]
        with nc.Block() as block:
            @block.vector
            def _(dve):
                def norm(t, h):
                    nc.vector.tensor_scalar(xs[:, h, :].unsqueeze(1), K.X[:, bass.ds(t, 1), :], K.mean[:, bass.ds(t, 1)],
                                            K.rstd[:, bass.ds(t, 1)], ALU.subtract, ALU.mult).then_inc(xs_ready, 1)
                for h in range(R):
                    norm(h, h)
                with dve.Fori(1, TN // R) as i:
                    for h in range(R):
                        dve.wait_ge(sent[h], i * (16 * 2))
                        dve.sem_inc(passed, 1)
                        norm(R * i + h, h)

            @block.gpsimd
            def _(pool):
                with pool.Fori(0, TN // R) as i:
                    for h in range(R):
                        pool.wait_ge(xs_ready, 1)
                        pool.sem_inc(xs_ready, -1)
                        nc.gpsimd.tensor_copy(cur[:, h, :].unsqueeze(1), K.slot[:, bass.ds(R * i + h, 1), :]).then_inc(pchain, 1)
                        pool.wait_ge(pchain, 1)
                        pool.sem_inc(pchain, -1)
                        for k in range(2):
                            nc.gpsimd.indirect_dma_start(
                                out=stab, out_offset=bass.IndirectOffsetOnAxis(ap=cur[:, h, k:k + 1].bitcast(mybir.dt.uint32), axis=0),
                                in_=xs[:, h, :], in_offset=None).then_inc(sent[h], 16)
                for h in range(R):
                    pool.wait_ge(sent[h], TN // R * (16 * 2))


def experts(nc, I, K, stab, ytab):
    fp32, ALU, ACT = mybir.dt.float32, mybir.AluOpType, mybir.ActivationFunctionType
    M = FF1 // P
    R = 4
    with ExitStack() as ctx:
        def sb(n, shape):
            return ctx.enter_context(nc.sbuf_tensor(f"ex_{n}", shape, fp32))

        def ps(n):
            return ctx.enter_context(nc.psum_tensor(f"ex_{n}", [P, 512], fp32))

        def sem(n):
            return K.sem(f"ex_{n}")
        w1, b1, w2, b2, loaded = K.w1, K.b1, K.w2, K.b2, K.experts_loaded
        gamma, beta = sb("gamma", [P, C]), sb("beta", [P, C])
        rows, xT, pre, act_h = sb("rows", [P, R, D]), sb("xT", [P, 2, C, P]), sb("pre", [P, 2, FF1]), sb("h", [P, 2, FF1])
        hT, y = sb("hT", [P, 2, FF1]), sb("y", [P, R, D])
        psX, psH, psU, psO = ps("psX"), ps("psH"), [ps("psU0"), ps("psU1")], [ps("psO0"), ps("psO1")]
        rows_in, y_out = [sem(f"rows_in{h}") for h in range(R)], [sem(f"y_out{h}") for h in range(R)]
        rows_free, x_full, xT_ready, u_full, pre_ready, h_ready, hT_full, hT_ready, o_full, y_ready = (
            sem(n) for n in ("rows_free", "x_full", "xT_ready", "u_full", "pre_ready", "h_ready", "hT_full", "hT_ready", "o_full", "y_ready"))
        flat = lambda a: a.rearrange("p a n -> p (a n)")

        def tile_experts(eng, i):
            return nc.values_load_multi_w_load_instructions(
                K.expert[0:1, bass.ds(R * i, R + 1)], [eng.engine], min_val=0, max_val=NE - 1,
                skip_runtime_bounds_check_because="route keeps them below NE")[1]
        with nc.Block() as block:
            @block.sync
            def _(sp):
                sp.dma_start(gamma[:, :], I["f1_gamma"]).then_inc(loaded, 16)
                sp.dma_start(beta[:, :], I["f1_beta"]).then_inc(loaded, 16)

                def load(j, h):
                    sp.dma_start(rows[:, h, :], stab[bass.ds(j * P, P), :]).then_inc(rows_in[h], 16)

                def save(j, h):
                    sp.wait_ge(y_ready, 1)
                    sp.sem_inc(y_ready, -1)
                    sp.dma_start(ytab[bass.ds(j * P, P), :], y[:, h, :]).then_inc(y_out[h], 16)
                for h in range(R):
                    load(h, h)
                with sp.Fori(0, ST // R - 1) as i:
                    for h in range(R):
                        save(R * i + h, h)
                        sp.wait_ge(rows_free, 1)
                        sp.sem_inc(rows_free, -1)
                        load(R * (i + 1) + h, h)
                for h in range(R):
                    save(ST - R + h, h)

            @block.vector
            def _(dve):
                for h in range(R):
                    dve.sem_inc(y_out[h], 16)
                dve.wait_ge(loaded, 96)

                def add_b1(e, h):
                    dve.wait_ge(u_full, 1)
                    dve.sem_inc(u_full, -1)
                    nc.vector.tensor_tensor(pre[:, h, :].unsqueeze(1), psU[h][:, :].unsqueeze(1), b1[:, bass.ds(e, 1), :], ALU.add).then_inc(pre_ready, 1)

                def body(i, final):
                    e = tile_experts(dve, i)
                    for h in range(R):
                        dve.wait_ge(hT_full, 1)
                        dve.sem_inc(hT_full, -1)
                        nc.vector.tensor_copy(hT[:, h % 2, :], psH[:, :]).then_inc(hT_ready, 1)
                        if not (final and h == R - 1):
                            add_b1(e[h + 1], (h + 1) % 2)
                        dve.wait_ge(o_full, 1)
                        dve.sem_inc(o_full, -1)
                        dve.wait_ge(y_out[h], 16)
                        dve.sem_inc(y_out[h], -16)
                        nc.vector.tensor_tensor(y[:, h, :].unsqueeze(1), psO[h % 2][:, 0:D].unsqueeze(1), b2[:, bass.ds(e[h], 1), :], ALU.add).then_inc(y_ready, 1)
                add_b1(tile_experts(dve, 0)[0], 0)
                with dve.Fori(0, ST // R - 1) as i:
                    body(i, False)
                body(ST // R - 1, True)
                for h in range(R):
                    dve.wait_ge(y_out[h], 16)
                    dve.sem_inc(y_out[h], -16)

            @block.scalar
            def _(act):
                act.wait_ge(loaded, 96)

                def turn(h):
                    act.wait_ge(x_full, 1)
                    act.sem_inc(x_full, -1)
                    act.sem_inc(rows_free, 1)
                    for c in range(C):
                        last = nc.scalar.activation(xT[:, h, c, :], psX[:, c * P:(c + 1) * P], ACT.Identity,
                                                    bias=beta[:, c:c + 1], scale=gamma[:, c:c + 1])
                    last.then_inc(xT_ready, 1)

                def gelu(h):
                    act.wait_ge(pre_ready, 1)
                    act.sem_inc(pre_ready, -1)
                    nc.scalar.activation(act_h[:, h, :], pre[:, h, :], ACT.Gelu).then_inc(h_ready, 1)
                turn(0)
                turn(1)
                gelu(0)
                with act.Fori(0, ST // 2 - 1) as i:
                    for h in range(2):
                        turn(h)
                        gelu(1 - h)
                gelu(1)

            @block.tensor
            def _(pe):
                pe.wait_ge(loaded, 96)

                def turn(h):
                    pe.wait_ge(rows_in[h], 16)
                    pe.sem_inc(rows_in[h], -16)
                    for c in range(C):
                        last = nc.tensor.transpose(psX[:, c * P:(c + 1) * P], rows[:, h, c * P:(c + 1) * P], K.ident[:, :])
                    last.then_inc(x_full, 1)

                def up(e, h):
                    pe.wait_ge(xT_ready, 1)
                    pe.sem_inc(xT_ready, -1)
                    for c in range(C):
                        last = nc.tensor.matmul(psU[h][:, :], xT[:, h, c, :], flat(w1[:, bass.ds(e, 1), c, :]), start=(c == 0), stop=(c == C - 1))
                    last.then_inc(u_full, 1)

                def body(i, final):
                    e = tile_experts(pe, i)
                    for h in range(R):
                        pe.wait_ge(h_ready, 1)
                        pe.sem_inc(h_ready, -1)
                        for m in range(M):
                            last = nc.tensor.transpose(psH[:, m * P:(m + 1) * P], act_h[:, h % 2, m * P:(m + 1) * P], K.ident[:, :])
                        last.then_inc(hT_full, 1)
                        if not (final and h == R - 1):
                            up(e[h + 1], (h + 1) % 2)
                        if not (final and h >= R - 2):
                            turn((h + 2) % R)
                        pe.wait_ge(hT_ready, 1)
                        pe.sem_inc(hT_ready, -1)
                        for m in range(M):
                            last = nc.tensor.matmul(psO[h % 2][:, 0:D], hT[:, h % 2, m * P:(m + 1) * P], flat(w2[:, bass.ds(e[h], 1), m, :]),
                                                    start=(m == 0), stop=(m == M - 1))
                        last.then_inc(o_full, 1)
                turn(0)
                up(tile_experts(pe, 0)[0], 0)
                turn(1)
                with pe.Fori(0, ST // R - 1) as i:
                    body(i, False)
                body(ST // R - 1, True)


def collect(nc, K, ytab):
    fp32, i32, ALU = mybir.dt.float32, mybir.dt.int32, mybir.AluOpType
    R = 5
    with ExitStack() as ctx:
        def sem(n):
            return K.sem(f"co_{n}")
        y = ctx.enter_context(nc.sbuf_tensor("co_y", [P, R, 2, D], fp32))
        cur = ctx.enter_context(nc.sbuf_tensor("co_cur", [P, R, 2], i32))
        y_in, y_free, passed, pchain, chain = [sem(f"y_in{h}") for h in range(R)], sem("y_free"), sem("passed"), sem("pchain"), sem("chain")
        with nc.Block() as block:
            @block.gpsimd
            def _(pool):
                pool.sem_inc(y_free, R)
                with pool.Fori(0, TN // R) as i:
                    for h in range(R):
                        pool.wait_ge(y_free, 1)
                        pool.sem_inc(y_free, -1)
                        nc.gpsimd.tensor_copy(cur[:, h, :].unsqueeze(1), K.back[:, bass.ds(R * i + h, 1), :]).then_inc(pchain, 1)
                        pool.wait_ge(pchain, 1)
                        pool.sem_inc(pchain, -1)
                        for k in range(2):
                            nc.gpsimd.indirect_dma_start(
                                out=y[:, h, k, :], out_offset=None, in_=ytab,
                                in_offset=bass.IndirectOffsetOnAxis(ap=cur[:, h, k:k + 1].bitcast(mybir.dt.uint32), axis=0)
                            ).then_inc(y_in[h], 16)

            @block.vector
            def _(dve):
                with dve.Fori(0, TN // R) as i:
                    for h in range(R):
                        t = R * i + h
                        x = K.X[:, bass.ds(t, 1), :]
                        dve.wait_ge(y_in[h], (i + 1) * (16 * 2))
                        dve.sem_inc(passed, 1)
                        for k in range(2):
                            nc.vector.scalar_tensor_tensor(
                                x, y[:, h, k, :].unsqueeze(1), K.share[:, bass.ds(t, 1), k:k + 1].rearrange("p a b -> p (a b)"), x,
                                ALU.mult, ALU.add).then_inc(chain, 1)
                            dve.wait_ge(chain, 1)
                            dve.sem_inc(chain, -1)
                        dve.sem_inc(y_free, 1)


def store(nc, K, out):
    with ExitStack() as ctx:
        stored = K.sem("x_stored")
        full = N // P * P
        with nc.Block() as block:
            @block.sync
            def _(sp):
                sp.dma_start(out[0:full, :].rearrange("(t p) d -> p t d", p=P), K.X[:, 0:N // P, :]).then_inc(stored, 16)
                sp.dma_start(out[full:N, :], K.X[0:N - full, N // P, :]).then_inc(stored, 16)
                sp.wait_ge(stored, 32)


class Kept:

    def __init__(self, nc):
        self.nc, self.sems = nc, []

    def sem(self, name):
        self.sems.append(self.nc.alloc_semaphore(name))
        return self.sems[-1]

    def clear(self):
        self.nc.clear_and_free_semaphores(self.sems)
        self.nc.all_engine_barrier()
        self.sems = []


def program(nc, I, out):
    fp32, i32 = mybir.dt.float32, mybir.dt.int32
    htab = nc.dram_tensor("htab", (T * P, TW), fp32, kind="Internal").ap()
    atab = nc.dram_tensor("atab", (T * P, HEADS), fp32, kind="Internal").ap()
    ztab = nc.dram_tensor("ztab", (T * P, D), fp32, kind="Internal").ap()
    wtab = nc.dram_tensor("wtab", (T * P,), fp32, kind="Internal").ap()
    stab = nc.dram_tensor("stab", (ST * P + 2 * (T * P - N), D), fp32, kind="Internal").ap()
    ytab = nc.dram_tensor("ytab", (ST * P, D), fp32, kind="Internal").ap()
    ftab = nc.dram_tensor("ftab", (EP, HEADS), fp32, kind="Internal").ap()
    with ExitStack() as ctx:
        def sb(n, shape, dt=fp32):
            return ctx.enter_context(nc.sbuf_tensor(n, shape, dt))
        K = Kept(nc)
        K.X = sb("X", [P, T, D])
        K.ident, K.upper, K.ones = sb("ident", [P, P]), sb("upper", [P, P]), sb("ones", [P, P])
        K.iota, K.iotai = sb("iota", [P, 512]), sb("iotai", [P, 512], i32)
        K.real, K.blockmask = sb("real", [P, T]), sb("blockmask", [P, C, HEADS])
        K.mean, K.rstd, K.meansq = sb("mean", [P, T]), sb("rstd", [P, T]), sb("meansq", [P, T])
        K.coef, K.share, K.expert = sb("coef", [P, T]), sb("share", [P, T, 2]), sb("expert", [P, ST + 4], i32)
        K.slot, K.back = sb("slot", [P, T, 2], i32), sb("back", [P, T, 2], i32)
        K.src_s, K.base, K.ns = sb("src_s", [P, S], i32), sb("base", [P, S + 8]), sb("node_tile", [P, S + 8], i32)
        K.src_p, K.cap, K.capall = sb("src_p", [P, ET], i32), sb("cap", [P, ET]), sb("capall", [P, 1])
        K.deg, K.last_edge = sb("deg", [P, T]), sb("last_edge", [P, T], i32)
        setup(nc, I, K)
        row_stats(nc, K, "ln0")
        K.got_in, K.cur_set, K.passed = [K.sem("got_in0"), K.sem("got_in1")], K.sem("cur_set"), K.sem("passed")
        with ExitStack() as layer:
            K.cur = layer.enter_context(nc.sbuf_tensor("cur", [P, HJ], i32))
            K.got = layer.enter_context(nc.sbuf_tensor("got", [P, HJ, HEADS], fp32))
            K.term = layer.enter_context(nc.sbuf_tensor("term", [P, ET, HEADS], fp32))
            K.wa = layer.enter_context(nc.sbuf_tensor("wa", [P, C, 2 * HEADS], fp32))
            source_terms(nc, I, K, atab)
            K.H = layer.enter_context(nc.sbuf_tensor("H", [P, T, HW], fp32))
            with ExitStack() as mixing:
                K.Q = mixing.enter_context(nc.sbuf_tensor("Q", [P, T, D], fp32))
                K.kvbd = mixing.enter_context(nc.sbuf_tensor("kvbd", [P, C, 2, P], fp32))
                project(nc, I, K, htab, atab)
                mix0(nc, I, K, atab)
            K.node = layer.enter_context(nc.sbuf_tensor("node", [P, T, 2 * HEADS], fp32))
            K.selfw = layer.enter_context(nc.sbuf_tensor("selfw", [P, T, HEADS], fp32))
            edge_tables(nc, I, K, atab)
            softmax_maxima(nc, K, ftab)
            gat(nc, I, K, htab)
        row_stats(nc, K, "ln1")
        choose(nc, I, K, wtab)
        ffn0(nc, I, K)
        K.clear()
        row_stats(nc, K, "ln2")
        with ExitStack() as layer:
            K.Z = layer.enter_context(nc.sbuf_tensor("Z", [P, T, D], fp32))
            K.ZT = layer.enter_context(nc.sbuf_tensor("ZT", [P, T, D], fp32))
            K.G = layer.enter_context(nc.sbuf_tensor("G", [P, T, D], fp32))
            K.gram = layer.enter_context(nc.sbuf_tensor("gram", [P, C, D + 1], fp32))
            K.agg = layer.enter_context(nc.sbuf_tensor("agg", [P, T, D], fp32))
            normalise(nc, K, ztab)
            aggregate(nc, I, K, ztab, stab)
            combine1(nc, I, K)
        row_stats(nc, K, "ln3")
        K.experts_loaded = K.sem("experts_loaded")
        with ExitStack() as layer:
            K.w1 = layer.enter_context(nc.sbuf_tensor("w1", [P, NE, C, FF1], fp32))
            K.b1 = layer.enter_context(nc.sbuf_tensor("b1", [P, NE, FF1], fp32))
            K.w2 = layer.enter_context(nc.sbuf_tensor("w2", [P, NE, FF1 // P, D], fp32))
            K.b2 = layer.enter_context(nc.sbuf_tensor("b2", [P, NE, D], fp32))
            route(nc, I, K)
            dispatch(nc, K, stab)
            experts(nc, I, K, stab, ytab)
        collect(nc, K, ytab)
        store(nc, K, out)


def laid_out(x, src, dst, **w):
    import numpy as np
    f = {k: np.asarray(v) for k, v in w.items()}
    x, src, dst = np.asarray(x), np.asarray(src), np.asarray(dst)
    o = {}
    o["x"] = np.concatenate([x, np.zeros((T * P - N, D), x.dtype)])
    o["src"] = np.concatenate([src, np.zeros(EP - E, src.dtype)])
    o["dst"] = np.concatenate([dst, np.full(EP - E, 4000, dst.dtype)])
    o["W0"], o["W0T"] = f["L0_gnn_W0"], f["L0_gnn_W0"].T
    o["att"] = np.stack([f["L0_gnn_att_src0"].reshape(D), f["L0_gnn_att_dst0"].reshape(D)], axis=1)
    o["b0"] = f["L0_gnn_b0"]
    for n in ("w_qkv", "w_out", "b_out", "w_norm2"):
        o[n] = f["L0_mix_" + n]
    o["w_norm1"] = f["L0_mix_w_norm1"].reshape(C, P).T
    for n in ("wr", "br", "w1", "b1", "w2", "b2"):
        o["f0_" + n] = f["L0_ffn_" + n]
    o["f0_wr"] = o["f0_wr"].reshape(D)
    o["f0_b1"] = o["f0_b1"].reshape(FF0 // P, P).T
    o["Wself"], o["Wneigh"], o["bgnn"] = f["L1_gnn_W_self"], f["L1_gnn_W_neigh"], f["L1_gnn_b"]
    o["Wq"], o["WkT"], o["WvT"], o["WfcT"] = f["L1_mix_Wq"], f["L1_mix_Wk"].T, f["L1_mix_Wv"].T, f["L1_mix_Wfc"].T
    for n in ("bk", "bv", "bfc"):
        o[n] = f["L1_mix_" + n]
    o["bq"] = f["L1_mix_bq"].reshape(C, P).T
    for n in ("gamma", "beta", "Wr", "br", "W1", "b1", "W2", "b2"):
        o["f1_" + n] = f["L1_ffn_" + n]
    o["f1_gamma"], o["f1_beta"] = (o["f1_" + n].reshape(C, P).T for n in ("gamma", "beta"))
    return o


def kernel(**inputs):
    import numpy as _np
    import concourse.bacc as _bacc
    from concourse import mybir as _mybir
    from concourse.bass_utils import run_bass_kernel_spmd as _run

    nc = _bacc.Bacc("TRN2", target_bir_lowering=False, num_devices=1)
    arrays, args = {}, {}
    for name, a in laid_out(**inputs).items():
        a = _np.ascontiguousarray(a)
        arrays[f"in_{name}"] = a
        args[name] = nc.dram_tensor(f"in_{name}", a.shape, _mybir.dt.from_np(a.dtype), kind="ExternalInput").ap()
    out = nc.dram_tensor("out_x", (N, D), _mybir.dt.float32, kind="ExternalOutput").ap()
    program(nc, args, out)
    r = _run(nc, [arrays], core_ids=[0])
    return r.results[0]["out_x"]
```

```python
import concourse.bass as bass
from concourse import mybir
from contextlib import ExitStack

P = 128
N = 3125
D = 256
C = D // P
T = 26
HEADS = 8
HD = D // HEADS
E = 50000
ET = 391
EP = ET * P
SQ = 104
SG = 4
SHIFT = 6
S = SQ * SG
HW = 272
TW = 264
BIG = 1.5e38
FF0 = 1024
KEEP = int(0.5 * N) - 1
NE = 8
TN = (N + P - 1) // P
ST = (2 * N + NE * (P - 1)) // P
FF1 = 512
HJ = 17
PART = [(0, 8), (8, HJ)]
GJ = 23
GPART = [(0, 11), (11, GJ)]


def node_tiles(nc, K, eng, s, n):
    return nc.values_load_multi_w_load_instructions(
        K.ns[0:1, bass.ds(s, n)], [eng.engine], min_val=0, max_val=T - 1,
        skip_runtime_bounds_check_because="edge_tables counts at most T - 1 ends of node tiles")[1]


def setup(nc, I, K):
    fp32, ALU = mybir.dt.float32, mybir.AluOpType
    with ExitStack() as ctx:
        loaded = K.sem("x_loaded")
        made = K.sem("constants_made")
        with nc.Block() as block:
            @block.sync
            def _(sp):
                sp.dma_start(K.X[:, :, :], I["x"].rearrange("(t p) d -> p t d", p=P)).then_inc(loaded, 16)
                sp.dma_start(K.src_p[:, :], I["src"].rearrange("(p f) -> p f", p=P)).then_inc(loaded, 16)
                sp.wait_ge(loaded, 32)

            @block.gpsimd
            def _(pool):
                pool.memset(K.ident[:, :], 0.0)
                pool.memset(K.real[:, :], 1.0)
                pool.memset(K.upper[:, :], 1.0)
                pool.memset(K.ones[:, :], 1.0)
                pool.memset(K.blockmask[:, :, :], 1.0).then_inc(made, 1)
                pool.wait_ge(made, 1)
                pool.sem_inc(made, -1)
                pool.affine_select(out=K.ident[:, :], in_=K.ident[:, :], compare_op=ALU.not_equal, fill=1.0,
                                   base=0, pattern=[[-1, P]], channel_multiplier=1)
                pool.affine_select(out=K.real[:, :], in_=K.real[:, :], compare_op=ALU.is_ge, fill=0.0,
                                   base=N - 1, pattern=[[-P, T]], channel_multiplier=-1)
                pool.affine_select(out=K.upper[:, :], in_=K.upper[:, :], compare_op=ALU.is_ge, fill=0.0,
                                   base=0, pattern=[[1, P]], channel_multiplier=-1)
                pool.affine_select(out=K.blockmask[:, :, :], in_=K.blockmask[:, :, :], compare_op=ALU.is_ge,
                                   fill=0.0, base=0, pattern=[[P, C], [-HD, HEADS]],
                                   channel_multiplier=1).then_inc(made, 1)
                pool.wait_ge(made, 1)
                pool.sem_inc(made, -1)
                pool.affine_select(out=K.blockmask[:, :, :], in_=K.blockmask[:, :, :], compare_op=ALU.is_ge,
                                   fill=0.0, base=HD - 1, pattern=[[-P, C], [HD, HEADS]], channel_multiplier=-1)
                pool.iota(K.iotai[:, :], pattern=[[1, 512]], base=0, channel_multiplier=0).then_inc(made, 1)
                pool.wait_ge(made, 1)
                pool.sem_inc(made, -1)
                pool.tensor_copy(K.iota[:, :], K.iotai[:, :])


def row_stats(nc, K, name, prefetch=None):
    fp32, ALU, ACT = mybir.dt.float32, mybir.AluOpType, mybir.ActivationFunctionType
    with ExitStack() as ctx:
        def sb(n, shape):
            return ctx.enter_context(nc.sbuf_tensor(f"{name}_{n}", shape, fp32))
        halves, mv = sb("halves", [P, T, 6]), sb("mv", [P, T])
        var, root, tmp = sb("var", [P, T]), sb("root", [P, T]), sb("tmp", [P, T])
        chain = K.sem(f"{name}_chain")
        var_ready = K.sem(f"{name}_var_ready")
        root_ready = K.sem(f"{name}_root_ready")
        with nc.Block() as block:
            @block.sync
            def _(sp):
                if prefetch:
                    prefetch(sp)

            @block.vector
            def _(dve):
                with dve.Fori(0, T // 2 - 1) as i:
                    for k in range(2):
                        nc.vector.bn_stats(halves[:, bass.ds(2 * i + k, 1), :], K.X[:, bass.ds(2 * i + k, 1), :])
                nc.vector.bn_stats(halves[:, T - 2, :], K.X[:, T - 2, :])
                nc.vector.bn_stats(halves[:, T - 1, :], K.X[:, T - 1, :]).then_inc(chain, 1)
                dve.wait_ge(chain, 1)
                dve.sem_inc(chain, -1)
                nc.vector.tensor_tensor(K.mean[:, :], halves[:, :, 1], halves[:, :, 4], ALU.add)
                nc.vector.tensor_tensor(tmp[:, :], halves[:, :, 1], halves[:, :, 4], ALU.subtract)
                nc.vector.tensor_tensor(mv[:, :], halves[:, :, 2], halves[:, :, 5], ALU.add).then_inc(chain, 1)
                dve.wait_ge(chain, 1)
                dve.sem_inc(chain, -1)
                nc.vector.tensor_scalar(K.mean[:, :], K.mean[:, :], 0.5, None, ALU.mult)
                nc.vector.tensor_tensor(tmp[:, :], tmp[:, :], tmp[:, :], ALU.mult).then_inc(chain, 1)
                dve.wait_ge(chain, 1)
                dve.sem_inc(chain, -1)
                nc.vector.tensor_scalar(tmp[:, :], tmp[:, :], 0.25 * D, None, ALU.mult).then_inc(chain, 1)
                dve.wait_ge(chain, 1)
                dve.sem_inc(chain, -1)
                nc.vector.tensor_tensor(mv[:, :], mv[:, :], tmp[:, :], ALU.add).then_inc(chain, 1)
                dve.wait_ge(chain, 1)
                dve.sem_inc(chain, -1)
                nc.vector.tensor_scalar(mv[:, :], mv[:, :], 1.0 / D, None, ALU.mult).then_inc(chain, 1)
                dve.wait_ge(chain, 1)
                dve.sem_inc(chain, -1)
                nc.vector.tensor_scalar(var[:, :], mv[:, :], 1e-5, None, ALU.add).then_inc(var_ready, 1)
                dve.wait_ge(root_ready, 1)
                dve.sem_inc(root_ready, -1)
                nc.vector.reciprocal(root[:, :], root[:, :]).then_inc(chain, 1)
                dve.wait_ge(chain, 1)
                dve.sem_inc(chain, -1)
                nc.vector.tensor_tensor(tmp[:, :], root[:, :], root[:, :], ALU.mult).then_inc(chain, 1)
                dve.wait_ge(chain, 1)
                dve.sem_inc(chain, -1)
                nc.vector.tensor_tensor(tmp[:, :], tmp[:, :], var[:, :], ALU.mult).then_inc(chain, 1)
                dve.wait_ge(chain, 1)
                dve.sem_inc(chain, -1)
                nc.vector.tensor_scalar(tmp[:, :], tmp[:, :], -0.5, 1.5, ALU.mult, ALU.add).then_inc(chain, 1)
                dve.wait_ge(chain, 1)
                dve.sem_inc(chain, -1)
                nc.vector.tensor_tensor(K.rstd[:, :], root[:, :], tmp[:, :], ALU.mult).then_inc(chain, 1)
                dve.wait_ge(chain, 1)
                dve.sem_inc(chain, -1)
                nc.vector.tensor_tensor(tmp[:, :], K.rstd[:, :], K.rstd[:, :], ALU.mult).then_inc(chain, 1)
                dve.wait_ge(chain, 1)
                dve.sem_inc(chain, -1)
                nc.vector.tensor_tensor(K.meansq[:, :], tmp[:, :], mv[:, :], ALU.mult)

            @block.scalar
            def _(act):
                act.wait_ge(var_ready, 1)
                act.sem_inc(var_ready, -1)
                nc.scalar.activation(root[:, :], var[:, :], ACT.Sqrt).then_inc(root_ready, 1)


def load_source_terms(I, K, sp):
    sp.dma_start(K.w0[:, :, :], I["W0"].rearrange("(c p) n -> p c n", p=P)).then_inc(K.w0_loaded, 16)
    sp.dma_start(K.att[:, :, :], I["att"].rearrange("(c p) n -> p c n", p=P)).then_inc(K.w0_loaded, 16)


def source_terms(nc, I, K, atab):
    fp32, ALU, ACT = mybir.dt.float32, mybir.AluOpType, mybir.ActivationFunctionType
    with ExitStack() as ctx:
        def sb(n, shape):
            return ctx.enter_context(nc.sbuf_tensor(f"st_{n}", shape, fp32))

        def ps(n):
            return ctx.enter_context(nc.psum_tensor(f"st_{n}", [P, 512], fp32))

        def sem(n):
            return K.sem(f"st_{n}")
        w0, att, attbd, terms = K.w0, K.att, sb("attbd", [P, C, 2 * HEADS]), sb("terms", [P, T, HEADS])
        xs, xT = sb("xs", [P, 2, 2, D]), sb("xT", [P, 2, 2 * D])
        psW, psT, psL = ps("psW"), [ps("psT0"), ps("psT1")], [ps("psL0"), ps("psL1")]
        loaded = K.w0_loaded
        stored, att_ready, wa_full, wa_ready = (sem(n) for n in ("stored", "att_ready", "wa_full", "wa_ready"))
        xs_ready, xt_full, xt_ready, l_full, l_free, chain = (sem(n) for n in ("xs_ready", "xt_full", "xt_ready", "l_full", "l_free", "chain"))
        terms_ready, xs_free = sem("terms_ready"), sem("xs_free")
        with nc.Block() as block:
            @block.sync
            def _(sp):
                sp.wait_ge(terms_ready, 1)
                sp.sem_inc(terms_ready, -1)
                sp.dma_start(atab.rearrange("(t p) n -> p t n", p=P), terms[:, :, :]).then_inc(stored, 16)
                sp.wait_ge(stored, 16)

            @block.vector
            def _(dve):
                def norm(i, k):
                    for r in range(2):
                        t = 2 * i + r
                        last = nc.vector.tensor_scalar(xs[:, k, r, :].unsqueeze(1), K.X[:, bass.ds(t, 1), :],
                                                       K.mean[:, bass.ds(t, 1)], K.rstd[:, bass.ds(t, 1)], ALU.subtract, ALU.mult)
                    last.then_inc(xs_ready, 1)

                def keep(i, k):
                    dve.wait_ge(l_full, 1)
                    dve.sem_inc(l_full, -1)
                    return nc.vector.tensor_copy(terms[:, bass.ds(2 * i, 2), :], psL[k][:, 0:2 * HEADS].rearrange("p (r n) -> p r n", r=2))
                norm(0, 0)
                norm(1, 1)
                dve.wait_ge(loaded, 32)
                for c in range(C):
                    for s in range(2):
                        last = nc.vector.tensor_scalar(attbd[:, c, s * HEADS:(s + 1) * HEADS], K.blockmask[:, c, :],
                                                       att[:, c, s:s + 1], None, ALU.mult)
                last.then_inc(att_ready, 1)
                dve.wait_ge(wa_full, 1)
                dve.sem_inc(wa_full, -1)
                nc.vector.tensor_copy(K.wa[:, :, :], psW[:, 0:C * 16].rearrange("p (c n) -> p c n", c=C)).then_inc(wa_ready, 1)
                with dve.Fori(0, T // 4 - 1) as i:
                    for k in range(2):
                        dve.wait_ge(xs_free, 1)
                        dve.sem_inc(xs_free, -1)
                        norm(2 * i + k + 2, k)
                        keep(2 * i + k, k).then_inc(l_free, 1)
                dve.wait_ge(xs_free, 1)
                dve.sem_inc(xs_free, -1)
                norm(T // 2 - 1, 0)
                keep(T // 2 - 3, 0).then_inc(l_free, 1)
                keep(T // 2 - 2, 1)
                keep(T // 2 - 1, 0).then_inc(chain, 1)
                dve.wait_ge(chain, 1)
                dve.sem_inc(chain, -1)
                dve.sem_inc(terms_ready, 1)

            @block.scalar
            def _(act):
                def copy(k):
                    act.wait_ge(xt_full, 1)
                    act.sem_inc(xt_full, -1)
                    act.sem_inc(xs_free, 1)
                    nc.scalar.activation(xT[:, k, :], psT[k][:, :], ACT.Identity).then_inc(xt_ready, 1)
                with act.Fori(0, T // 4) as i:
                    for k in range(2):
                        copy(k)
                copy(0)

            @block.tensor
            def _(pe):
                def transposes(k):
                    pe.wait_ge(xs_ready, 1)
                    pe.sem_inc(xs_ready, -1)
                    for r in range(2):
                        for c in range(C):
                            last = nc.tensor.transpose(psT[k][:, (2 * r + c) * P:(2 * r + c + 1) * P], xs[:, k, r, c * P:(c + 1) * P], K.ident[:, :])
                    last.then_inc(xt_full, 1)

                def terms_of(k, final=False):
                    pe.wait_ge(xt_ready, 1)
                    pe.sem_inc(xt_ready, -1)
                    if not final:
                        transposes(1 - k)
                    pe.wait_ge(l_free, 1)
                    pe.sem_inc(l_free, -1)
                    for r in range(2):
                        for c in range(C):
                            last = nc.tensor.matmul(psL[k][:, r * HEADS:(r + 1) * HEADS], xT[:, k, (2 * r + c) * P:(2 * r + c + 1) * P],
                                                    K.wa[:, c, 0:HEADS], start=(c == 0), stop=(c == C - 1))
                    last.then_inc(l_full, 1)
                pe.sem_inc(l_free, 2)
                transposes(0)
                pe.wait_ge(att_ready, 1)
                pe.sem_inc(att_ready, -1)
                for m in range(C):
                    for c in range(C):
                        last = nc.tensor.matmul(psW[:, m * 16:(m + 1) * 16], w0[:, c, m * P:(m + 1) * P],
                                                attbd[:, c, :], start=(c == 0), stop=(c == C - 1))
                last.then_inc(wa_full, 1)
                pe.wait_ge(wa_ready, 1)
                pe.sem_inc(wa_ready, -1)
                with pe.Fori(0, T // 4) as i:
                    for k in range(2):
                        terms_of(k)
                terms_of(0, True)


def gather_terms(nc, K, pool, atab, first, last):
    def issue(i, h):
        a, b = GPART[h]
        nc.gpsimd.tensor_copy(K.cur[:, a:b], K.src_p[:, bass.ds(i * GJ + a, b - a)]).then_inc(K.cur_set, 1)
        pool.wait_ge(K.cur_set, 1)
        pool.sem_inc(K.cur_set, -1)
        for k in range(a, b):
            nc.gpsimd.indirect_dma_start(
                out=K.got[:, k, :], out_offset=None, in_=atab,
                in_offset=bass.IndirectOffsetOnAxis(ap=K.cur[:, k:k + 1].bitcast(mybir.dt.uint32), axis=0)
            ).then_inc(K.got_in[h], 16)

    def collect(i, h):
        a, b = GPART[h]
        pool.wait_ge(K.got_in[h], (i + 1) * (16 * (b - a)))
        pool.sem_inc(K.passed, 1)
        nc.gpsimd.tensor_copy(K.term[:, bass.ds(i * GJ + a, b - a), :], K.got[:, a:b, :]).then_inc(K.cur_set, 1)
        pool.wait_ge(K.cur_set, 1)
        pool.sem_inc(K.cur_set, -1)
    issue(first, 0)
    if last - first > 1:
        with pool.Fori(first, last - 1) as i:
            issue(i, 1)
            collect(i, 0)
            issue(i + 1, 0)
            collect(i, 1)
    issue(last - 1, 1)
    collect(last - 1, 0)
    collect(last - 1, 1)


def project(nc, I, K, htab, atab):
    fp32, ALU, ACT = mybir.dt.float32, mybir.AluOpType, mybir.ActivationFunctionType
    with ExitStack() as ctx:
        def sb(n, shape):
            return ctx.enter_context(nc.sbuf_tensor(f"pj_{n}", shape, fp32))

        def ps(n):
            return ctx.enter_context(nc.psum_tensor(f"pj_{n}", [P, 512], fp32))

        def sem(n):
            return K.sem(f"pj_{n}")
        w0t, wqkv, wn1 = sb("w0t", [P, C, HW]), sb("wqkv", [P, C, 3 * D]), sb("wn1", [P, C])
        root, scale, tmp = sb("root", [P, T]), sb("scale", [P, T]), sb("tmp", [P, T])
        xs, xT = sb("xs", [P, 2, D]), sb("xT", [P, 2, C, P])
        low, pos = sb("low", [P, 2, 2 * D]), sb("pos", [P, 2, 2 * D])
        kb, vb = sb("kb", [P, 2, D]), sb("vb", [P, 2, C, P + 1])
        warm = sb("warm", [P, 1])
        psT, psKV = ps("psT"), ps("psKV")
        psH, psQ, psV = ([ps(f"ps{x}{j}") for j in range(2)] for x in "HQV")
        loaded, stored, chain = sem("weights_loaded"), sem("tables_stored"), sem("chain")
        ms_ready, root_ready = sem("ms_ready"), sem("root_ready")
        w_ready = sem("w_ready")
        xs_ready, xt_full, xt_ready = sem("xs_ready"), sem("xt_full"), sem("xt_ready")
        h_full, q_full, v_full = sem("h_full"), sem("q_full"), sem("v_full")
        h_free, q_free, v_free = sem("h_free"), sem("q_free"), sem("v_free")
        low_ready, exp_ready, k_ready, v_ready = sem("low_ready"), sem("exp_ready"), sem("k_ready"), sem("v_ready")
        kv_used, kv_done, h_done = sem("kv_used"), sem("kv_done"), sem("h_done")
        with nc.Block() as block:
            @block.sync
            def _(sp):
                sp.dma_start(w0t[:, :, 0:D], I["W0T"].rearrange("(c p) n -> p c n", p=P)).then_inc(loaded, 16)
                sp.dma_start(wqkv[:, :, :], I["w_qkv"].rearrange("(c p) n -> p c n", p=P)).then_inc(loaded, 16)
                sp.dma_start(wn1[:, :], I["w_norm1"]).then_inc(loaded, 16)
                sp.wait_ge(h_done, 1)
                sp.sem_inc(h_done, -1)
                sp.dma_start(htab.rearrange("(t p) n -> p t n", p=P), K.H[:, :, 0:TW]).then_inc(stored, 16)
                sp.wait_ge(stored, 16)

            @block.vector
            def _(dve):
                nc.vector.memset(kb[:, :, :], 0.0)
                nc.vector.memset(vb[:, :, :, :], 0.0)
                nc.vector.tensor_scalar(tmp[:, :], K.meansq[:, :], 1e-6, None, ALU.add).then_inc(chain, 1)
                dve.wait_ge(chain, 1)
                dve.sem_inc(chain, -1)
                nc.vector.tensor_copy(root[:, :], tmp[:, :]).then_inc(ms_ready, 1)
                dve.wait_ge(root_ready, 1)
                dve.sem_inc(root_ready, -1)
                nc.vector.reciprocal(scale[:, :], root[:, :]).then_inc(chain, 1)
                dve.wait_ge(chain, 1)
                dve.sem_inc(chain, -1)
                nc.vector.tensor_tensor(scale[:, :], scale[:, :], K.rstd[:, :], ALU.mult).then_inc(chain, 1)
                dve.wait_ge(chain, 1)
                dve.sem_inc(chain, -1)
                dve.wait_ge(loaded, 48)
                nc.vector.tensor_copy(w0t[:, :, D:HW], K.wa[:, :, :])
                for c in range(C):
                    last = nc.vector.tensor_scalar(wqkv[:, c, :], wqkv[:, c, :], wn1[:, c:c + 1], None, ALU.mult)
                last.then_inc(w_ready, 1)

                def norm(t, k):
                    nc.vector.tensor_scalar(xs[:, k, :].unsqueeze(1), K.X[:, bass.ds(t, 1), :],
                                            K.mean[:, bass.ds(t, 1)], scale[:, bass.ds(t, 1)],
                                            ALU.subtract, ALU.mult).then_inc(xs_ready, 1)

                def body(i, final):
                    for k in range(2):
                        t = 2 * i + k
                        dve.wait_ge(h_full, 1)
                        dve.sem_inc(h_full, -1)
                        nc.vector.tensor_scalar(K.H[:, bass.ds(t, 1), :], psH[k][:, 0:HW].unsqueeze(1),
                                                root[:, bass.ds(t, 1)], None, ALU.mult).then_inc(h_free, 1)
                        dve.wait_ge(kv_used, 1)
                        dve.sem_inc(kv_used, -1)
                        dve.wait_ge(q_full, 1)
                        dve.sem_inc(q_full, -1)
                        nc.vector.tensor_scalar(low[:, k, :], psQ[k][:, :], 0.0, None, ALU.min).then_inc(low_ready, 1)
                        nc.vector.tensor_copy(vb[:, k, :, P:P + 1],
                                              K.real[:, bass.ds(t, 1)].unsqueeze(1).broadcast_to([P, C, 1]))
                        dve.wait_ge(v_full, 1)
                        dve.sem_inc(v_full, -1)
                        nc.vector.tensor_copy(vb[:, k, :, 0:P],
                                              psV[k][:, 0:D].rearrange("p (c n) -> p c n", c=C)).then_inc(v_ready, 1)
                        if not final:
                            norm(t + 2, k)
                        dve.wait_ge(exp_ready, 1)
                        dve.sem_inc(exp_ready, -1)
                        nc.vector.tensor_tensor(kb[:, k, :], pos[:, k, D:2 * D], low[:, k, D:2 * D],
                                                ALU.add).then_inc(k_ready, 1)
                        nc.vector.tensor_tensor(K.Q[:, bass.ds(t, 1), :], pos[:, k, 0:D].unsqueeze(1),
                                                low[:, k, 0:D].unsqueeze(1), ALU.add)
                norm(0, 0)
                norm(1, 1)
                with dve.Fori(0, T // 2 - 1) as i:
                    body(i, False)
                body(T // 2 - 1, True)
                nc.vector.memset(K.kvbd[:, :, :, :], 0.0).then_inc(chain, 1)
                dve.wait_ge(chain, 1)
                dve.sem_inc(chain, -1)
                dve.wait_ge(kv_done, 1)
                dve.sem_inc(kv_done, -1)
                for c in range(C):
                    psk = psKV[:, c * (P + 1):(c + 1) * (P + 1)]
                    mask = K.blockmask[:, c, 4 * c:4 * c + 4].unsqueeze(2).broadcast_to([P, 4, HD])
                    nc.vector.tensor_tensor(K.kvbd[:, c, 0, :].rearrange("p (h m) -> p h m", m=HD),
                                            psk[:, 0:P].rearrange("p (h m) -> p h m", m=HD), mask, ALU.mult)
                    last = nc.vector.tensor_tensor(K.kvbd[:, c, 1, :].rearrange("p (h m) -> p h m", m=HD),
                                                   psk[:, P:P + 1].unsqueeze(2).broadcast_to([P, 4, HD]), mask, ALU.mult)
                last.then_inc(h_done, 1)

            @block.scalar
            def _(act):
                act.wait_ge(ms_ready, 1)
                act.sem_inc(ms_ready, -1)
                nc.scalar.activation(root[:, :], root[:, :], ACT.Sqrt).then_inc(root_ready, 1)
                nc.scalar.activation(warm[:, :], K.ones[:, 0:1], ACT.Exp)
                def copy(k):
                    act.wait_ge(xt_full, 1)
                    act.sem_inc(xt_full, -1)
                    nc.scalar.activation(xT[:, k, :, :], psT[:, 0:D].rearrange("p (c n) -> p c n", c=C),
                                         ACT.Identity).then_inc(xt_ready, 1)

                def parts(k):
                    act.wait_ge(low_ready, 1)
                    act.sem_inc(low_ready, -1)
                    nc.scalar.activation(pos[:, k, :], psQ[k][:, :], ACT.Relu).then_inc(q_free, 1)
                    nc.scalar.activation(low[:, k, :], low[:, k, :], ACT.Exp).then_inc(exp_ready, 1)
                copy(0)
                with act.Fori(0, T // 2 - 1) as i:
                    for k in range(2):
                        copy(1 - k)
                        parts(k)
                copy(1)
                parts(0)
                parts(1)

            @block.gpsimd
            def _(pool):
                gather_terms(nc, K, pool, atab, 0, 5)

            @block.tensor
            def _(pe):
                pe.wait_ge(w_ready, 1)
                pe.sem_inc(w_ready, -1)
                nc.tensor.matmul(psKV[:, 0:C * (P + 1)], kb[:, 0, 0:P], vb[:, 0, :, :].rearrange("p c n -> p (c n)"),
                                 start=True, stop=False, skip_group_check=True)
                pe.sem_inc(k_ready, 1)
                pe.sem_inc(v_ready, 1)
                pe.sem_inc(kv_used, 1)
                pe.sem_inc(h_free, 2)
                pe.sem_inc(q_free, 2)

                def transposes(k):
                    pe.wait_ge(xs_ready, 1)
                    pe.sem_inc(xs_ready, -1)
                    for c in range(C):
                        last = nc.tensor.transpose(psT[:, c * P:(c + 1) * P], xs[:, k, c * P:(c + 1) * P], K.ident[:, :])
                    last.then_inc(xt_full, 1)

                def kv(k, stop=False):
                    pe.wait_ge(k_ready, 1)
                    pe.sem_inc(k_ready, -1)
                    pe.wait_ge(v_ready, 1)
                    pe.sem_inc(v_ready, -1)
                    for c in range(C):
                        last = nc.tensor.matmul(psKV[:, c * (P + 1):(c + 1) * (P + 1)], kb[:, k, c * P:(c + 1) * P],
                                                vb[:, k, c, :], start=False, stop=stop, skip_group_check=True)
                    return last

                def body(i, final):
                    for k in range(2):
                        pe.wait_ge(xt_ready, 1)
                        pe.sem_inc(xt_ready, -1)
                        if not (final and k == 1):
                            transposes(1 - k)
                        pe.wait_ge(h_free, 1)
                        pe.sem_inc(h_free, -1)
                        for c in range(C):
                            last = nc.tensor.matmul(psH[k][:, 0:HW], xT[:, k, c, :], w0t[:, c, :],
                                                    start=(c == 0), stop=(c == C - 1))
                        last.then_inc(h_full, 1)
                        pe.wait_ge(q_free, 1)
                        pe.sem_inc(q_free, -1)
                        for m in range(C):
                            for c in range(C):
                                nc.tensor.matmul(psQ[k][:, m * P:(m + 1) * P], wqkv[:, c, m * P:(m + 1) * P],
                                                 xT[:, k, c, :], start=(c == 0), stop=(c == C - 1))
                        for c in range(C):
                            last = nc.tensor.matmul(psQ[k][:, D:2 * D], xT[:, k, c, :], wqkv[:, c, D:2 * D],
                                                    start=(c == 0), stop=(c == C - 1))
                        last.then_inc(q_full, 1)
                        for c in range(C):
                            last = nc.tensor.matmul(psV[k][:, 0:D], xT[:, k, c, :], wqkv[:, c, 2 * D:3 * D],
                                                    start=(c == 0), stop=(c == C - 1))
                        last.then_inc(v_full, 1)
                        kv(1 - k).then_inc(kv_used, 1)
                transposes(0)
                with pe.Fori(0, T // 2 - 1) as i:
                    body(i, False)
                body(T // 2 - 1, True)
                kv(1, stop=True).then_inc(kv_done, 1)


def mix0(nc, I, K, atab):
    fp32, ALU, ACT = mybir.dt.float32, mybir.AluOpType, mybir.ActivationFunctionType
    with ExitStack() as ctx:
        def sb(n, shape):
            return ctx.enter_context(nc.sbuf_tensor(f"mx_{n}", shape, fp32))

        def ps(n):
            return ctx.enter_context(nc.psum_tensor(f"mx_{n}", [P, 512], fp32))

        def sem(n):
            return K.sem(f"mx_{n}")
        wout, bout, wn2, h0 = sb("wout", [P, C, D]), sb("bout", [1, D]), sb("wn2", [P, D]), sb("h0", [P, T, D])
        den, oT, junk = sb("den", [P, 2, 2 * D]), sb("oT", [P, 2, C, D]), sb("sq", [P, 2, D])
        nmr, xn, ssq, tmp, gain = sb("nmr", [P, T]), sb("xn", [P, 2, D]), sb("ssq", [P, T]), sb("tmp", [P, T]), sb("gain", [P, 2, 2, D])
        psN, psD = [ps("psN0"), ps("psN1")], [ps("psD0"), ps("psD1")]
        psO = [ps("psO0"), ps("psO1")]
        loaded, chain = sem("weights_loaded"), sem("chain")
        n_full, d_full, nd_free, o_ready = sem("num_full"), sem("den_full"), sem("numden_free"), sem("o_ready")
        out_full, out_free, xn_ready, xn_free = sem("out_full"), sem("out_free"), sem("xn_ready"), sem("xn_free")
        nmr_ready, h0_ready, root_ready, ms_ready = sem("nmr_ready"), sem("h0_ready"), sem("root_ready"), sem("ms_ready")
        gain_ready, gain_free, wn2_loaded, sq_done, tmp_ready = sem("gain_ready"), sem("gain_free"), sem("wn2_loaded"), sem("sq_done"), sem("tmp_ready")
        with nc.Block() as block:
            @block.sync
            def _(sp):
                sp.dma_start(wout[:, :, :], I["w_out"].rearrange("(c p) n -> p c n", p=P)).then_inc(loaded, 16)
                sp.dma_start(bout[:, :], I["b_out"].rearrange("(a n) -> a n", a=1)).then_inc(loaded, 16)
                sp.dma_start(wn2[:, :], I["w_norm2"].partition_broadcast(P)).then_inc(wn2_loaded, 16)
                sp.wait_ge(wn2_loaded, 16)

            @block.gpsimd
            def _(pool):
                gather_terms(nc, K, pool, atab, 5, 10)

            @block.tensor
            def _(pe):
                pe.sem_inc(nd_free, 2)
                pe.sem_inc(out_free, 2)
                pe.wait_ge(loaded, 32)
                Qv = K.Q[:, :, :].rearrange("p t (c r) -> p c t r", c=C)

                def numden(i, k):
                    pe.wait_ge(nd_free, 1)
                    pe.sem_inc(nd_free, -1)
                    for ps, j, full in ((psN, 0, n_full), (psD, 1, d_full)):
                        for c in range(C):
                            last = nc.tensor.matmul(ps[k][:, c * D:(c + 1) * D].rearrange("p (t r) -> p t r", t=2),
                                                    K.kvbd[:, c, j, :], Qv[:, c, bass.ds(2 * i, 2), :], start=True, stop=True)
                        last.then_inc(full, 1)

                def out(k):
                    pe.wait_ge(o_ready, 1)
                    pe.sem_inc(o_ready, -1)
                    for r in range(2):
                        pe.wait_ge(out_free, 1)
                        pe.sem_inc(out_free, -1)
                        nc.tensor.matmul(psO[r][:, 0:D], K.ones[0:1, :], bout[:, :], start=True, stop=False)
                        for c in range(C):
                            last = nc.tensor.matmul(psO[r][:, 0:D], oT[:, k, c, r * P:(r + 1) * P], wout[:, c, :],
                                                    start=False, stop=(c == C - 1))
                        last.then_inc(out_full, 1)
                numden(0, 0)
                numden(1, 1)
                with pe.Fori(0, T // 4 - 1) as i:
                    out(0)
                    numden(2 * i + 2, 0)
                    out(1)
                    numden(2 * i + 3, 1)
                out(0)
                numden(T // 2 - 1, 0)
                out(1)
                out(0)

            @block.vector
            def _(dve):
                nc.vector.tensor_scalar(nmr[:, :], K.mean[:, :], -1.0, None, ALU.mult).then_inc(chain, 1)
                dve.wait_ge(chain, 1)
                dve.sem_inc(chain, -1)
                nc.vector.tensor_tensor(nmr[:, :], nmr[:, :], K.rstd[:, :], ALU.mult).then_inc(nmr_ready, 1)

                def head(k):
                    dve.wait_ge(n_full, 1)
                    dve.sem_inc(n_full, -1)
                    dve.wait_ge(d_full, 1)
                    dve.sem_inc(d_full, -1)
                    nc.vector.tensor_scalar(den[:, k, :], psD[k][:, :], 1e-6, None, ALU.add).then_inc(chain, 1)
                    dve.wait_ge(chain, 1)
                    dve.sem_inc(chain, -1)
                    nc.vector.reciprocal(den[:, k, :], den[:, k, :]).then_inc(chain, 1)
                    dve.wait_ge(chain, 1)
                    dve.sem_inc(chain, -1)
                    nc.vector.tensor_tensor(oT[:, k, :, :].rearrange("p c n -> p (c n)"), psN[k][:, :],
                                            den[:, k, :], ALU.mult).then_inc(chain, 1)
                    dve.wait_ge(chain, 1)
                    dve.sem_inc(chain, -1)
                    dve.sem_inc(nd_free, 1)
                    dve.sem_inc(o_ready, 1)

                def tail(i):
                    for r in range(2):
                        t = 2 * i + r
                        dve.wait_ge(out_full, 1)
                        dve.sem_inc(out_full, -1)
                        dve.wait_ge(xn_ready, 1)
                        dve.sem_inc(xn_ready, -1)
                        nc.vector.tensor_tensor(h0[:, bass.ds(t, 1), :], psO[r][:, 0:D].unsqueeze(1),
                                                xn[:, r, :].unsqueeze(1), ALU.add).then_inc(h0_ready, 1)
                head(0)
                with dve.Fori(0, T // 4) as i:
                    head(1)
                    tail(2 * i)
                    head(0)
                    tail(2 * i + 1)
                tail(T // 2 - 1)
                dve.wait_ge(sq_done, 1)
                dve.sem_inc(sq_done, -1)
                nc.vector.tensor_scalar(tmp[:, :], ssq[:, :], 1.0 / D, 1e-6, ALU.mult, ALU.add).then_inc(chain, 1)
                dve.wait_ge(chain, 1)
                dve.sem_inc(chain, -1)
                nc.vector.tensor_copy(ssq[:, :], tmp[:, :]).then_inc(ms_ready, 1)
                dve.wait_ge(root_ready, 1)
                dve.sem_inc(root_ready, -1)
                nc.vector.reciprocal(tmp[:, :], ssq[:, :]).then_inc(chain, 1)
                dve.wait_ge(chain, 1)
                dve.sem_inc(chain, -1)
                dve.sem_inc(gain_free, 2)
                dve.sem_inc(tmp_ready, 1)

                def add(i, k):
                    dve.wait_ge(gain_ready, 1)
                    dve.sem_inc(gain_ready, -1)
                    two, x = gain[:, k, :, :], K.X[:, bass.ds(2 * i, 2), :]
                    nc.vector.tensor_tensor(two, two, h0[:, bass.ds(2 * i, 2), :], ALU.mult).then_inc(chain, 1)
                    dve.wait_ge(chain, 1)
                    dve.sem_inc(chain, -1)
                    nc.vector.tensor_tensor(x, x, two, ALU.add).then_inc(gain_free, 1)
                with dve.Fori(0, T // 4) as i:
                    add(2 * i, 0)
                    add(2 * i + 1, 1)
                add(T // 2 - 1, 0)

            @block.scalar
            def _(act):
                act.wait_ge(nmr_ready, 1)
                act.sem_inc(nmr_ready, -1)
                act.sem_inc(xn_free, 2)

                def normal(t, r):
                    nc.scalar.activation(xn[:, r, :].unsqueeze(1), K.X[:, bass.ds(t, 1), :], ACT.Identity,
                                         bias=nmr[:, bass.ds(t, 1)], scale=K.rstd[:, bass.ds(t, 1)]).then_inc(xn_ready, 1)

                def square(t, r):
                    act.wait_ge(h0_ready, 1)
                    act.sem_inc(h0_ready, -1)
                    nc.scalar.activation(junk[:, r, :].unsqueeze(1), h0[:, bass.ds(t, 1), :], ACT.Square,
                                         accum_out=ssq[:, bass.ds(t, 1)]).then_inc(out_free, 1)
                normal(0, 0)
                normal(1, 1)
                with act.Fori(0, T // 2 - 1) as i:
                    for r in range(2):
                        square(2 * i + r, r)
                        normal(2 * i + 2 + r, r)
                square(T - 2, 0)
                square(T - 1, 1)
                act.drain().then_inc(sq_done, 1)
                act.wait_ge(ms_ready, 1)
                act.sem_inc(ms_ready, -1)
                nc.scalar.activation(ssq[:, :], ssq[:, :], ACT.Sqrt).then_inc(root_ready, 1)
                act.wait_ge(tmp_ready, 1)
                act.sem_inc(tmp_ready, -1)
                act.wait_ge(wn2_loaded, 16)

                def gains(i, k):
                    act.wait_ge(gain_free, 1)
                    act.sem_inc(gain_free, -1)
                    for r in range(2):
                        last = nc.scalar.activation(gain[:, k, r, :], wn2[:, :], ACT.Identity, bias=K.ones[:, 0:1],
                                                    scale=tmp[:, bass.ds(2 * i + r, 1)])
                    last.then_inc(gain_ready, 1)
                with act.Fori(0, T // 4) as i:
                    gains(2 * i, 0)
                    gains(2 * i + 1, 1)
                gains(T // 2 - 1, 0)


def edge_tables(nc, I, K, atab):
    fp32, i32, bf16, ALU = mybir.dt.float32, mybir.dt.int32, mybir.dt.bfloat16, mybir.AluOpType
    with ExitStack() as ctx:
        def sb(n, shape, dt=fp32):
            return ctx.enter_context(nc.sbuf_tensor(f"et_{n}", shape, dt))

        def ps(n):
            return ctx.enter_context(nc.psum_tensor(f"et_{n}", [P, 512], fp32))

        def sem(n):
            return K.sem(f"et_{n}")
        dst_i, lo_i, hi_i = sb("dst_i", [P, ET], i32), sb("lo_i", [P, ET], i32), sb("hi_i", [P, ET], i32)
        prev_i, prev = sb("prev_i", [P, 1], i32), sb("prev", [P, 1])
        dstf, lo, hi, hits = sb("dstf", [P, ET]), sb("lo", [P, ET]), sb("hi", [P, ET]), sb("hits", [P, 2, ET])
        bound, cnt, ends, ends_i, rank = sb("bound", [P, T]), sb("cnt", [P, T]), sb("ends", [P, T]), sb("ends_i", [P, T], i32), sb("rank", [P, T])
        ns, ns128, past = sb("ns", [SQ, SG]), sb("ns128", [SQ, SG]), sb("past", [SQ, SG, T - 1])
        cs_i, cs, es = sb("cs_i", [SQ, SG], i32), sb("cs", [SQ, SG]), sb("es", [SQ, SG])
        es_i = sb("es_i", [SQ, SG], i32)
        rows_i, rows = sb("rows_i", [SQ, 2, SG, P], i32), sb("rows", [SQ, 2, SG, P])
        onelo, onehi = sb("onelo", [P, HJ, P], bf16), sb("onehi", [P, HJ, T], bf16)
        zero = sb("zero", [P, P], bf16)
        last_e = sb("last_e", [P, T])
        psC, psH, psU, psR = ps("psC"), ps("psH"), ps("psU"), [ps("psR0"), ps("psR1")]
        prev_set, loaded, chain, cs_ready = sem("prev_set"), sem("loaded"), sem("chain"), sem("cs_ready")
        cnt_ready, ends_full, es_ready, rows_in, rows_ready, rows_full = (
            sem("cnt_ready"), sem("ends_full"), sem("es_ready"), sem("rows_in"), sem("rows_ready"), sem("rows_full"))
        hot_ready, hot_free = [sem("hot_ready0"), sem("hot_ready1")], [sem("hot_free0"), sem("hot_free1")]
        hist_full, deg_ready, cum_full = sem("hist_full"), sem("deg_ready"), sem("cum_full")
        zero_set = sem("zero_set")
        with nc.Block() as block:
            @block.sync
            def _(sp):
                sp.dma_start(dst_i[:, :], I["dst"].rearrange("(p f) -> p f", p=P)).then_inc(loaded, 16)
                sp.wait_ge(prev_set, 1)
                sp.sem_inc(prev_set, -1)
                sp.dma_start(prev_i[1:P, :], I["dst"].rearrange("(p f) -> p f", p=P)[0:P - 1, ET - 1:ET],
                             allow_slow_non_contiguous=True).then_inc(loaded, 16)

            @block.gpsimd
            def _(pool):
                pool.iota(cs_i[:, :], pattern=[[SQ, SG]], base=0, channel_multiplier=1).then_inc(cs_ready, 1)
                gather_terms(nc, K, pool, atab, 10, 12)
                pool.wait_ge(es_ready, 1)
                pool.sem_inc(es_ready, -1)
                for g in range(SG):
                    for j, table in enumerate(("src", "dst")):
                        nc.gpsimd.indirect_dma_start(
                            out=rows_i[:, j, g, :], out_offset=None, in_=I[table].rearrange("(t e) -> t e", e=P),
                            in_offset=bass.IndirectOffsetOnAxis(ap=es_i[:, g:g + 1].bitcast(mybir.dt.uint32), axis=0)
                        ).then_inc(rows_in, 16)
                gather_terms(nc, K, pool, atab, 12, ET // GJ)

            @block.vector
            def _(dve):
                nc.vector.memset(prev_i[:, :], -1).then_inc(prev_set, 1)
                nc.vector.memset(zero[:, :], 0.0).then_inc(zero_set, 1)
                nc.vector.memset(K.base[:, S:S + 8], 0.0)
                nc.vector.memset(K.ns[:, 0:SHIFT], T - 1)
                nc.vector.memset(K.ns[:, SHIFT + S:], 0)
                dve.wait_ge(loaded, 32)
                nc.vector.tensor_copy(dstf[:, :], dst_i[:, :])
                nc.vector.tensor_copy(prev[:, :], prev_i[:, :])
                nc.vector.tensor_scalar(lo_i[:, :], dst_i[:, :], P - 1, None, ALU.bitwise_and)
                nc.vector.tensor_scalar(hi_i[:, :], dst_i[:, :], 7, None, ALU.arith_shift_right)
                nc.vector.tensor_scalar(bound[:, :], K.iota[:, 0:T], float(P), float(P), ALU.mult, ALU.add).then_inc(chain, 1)
                dve.wait_ge(chain, 1)
                dve.sem_inc(chain, -1)
                nc.vector.tensor_copy(lo[:, :], lo_i[:, :])
                nc.vector.tensor_copy(hi[:, :], hi_i[:, :])
                nc.vector.tensor_tensor(K.cap[:, 1:ET], dstf[:, 1:ET], dstf[:, 0:ET - 1], ALU.is_equal)
                nc.vector.tensor_tensor(K.cap[:, 0:1], dstf[:, 0:1], prev[:, :], ALU.is_equal).then_inc(chain, 1)
                dve.wait_ge(chain, 1)
                dve.sem_inc(chain, -1)
                nc.vector.tensor_reduce(K.capall[:, :], K.cap[:, :], mybir.AxisListType.X, ALU.min).then_inc(chain, 1)
                dve.wait_ge(chain, 1)
                dve.sem_inc(chain, -1)
                nc.vector.tensor_scalar(K.cap[:, :], K.cap[:, :], 2 * BIG, -BIG, ALU.mult, ALU.add)
                nc.vector.tensor_scalar(K.capall[:, :], K.capall[:, :], 2 * BIG, -BIG, ALU.mult, ALU.add).then_inc(chain, 1)
                dve.wait_ge(chain, 1)
                dve.sem_inc(chain, -1)
                with dve.Fori(0, T // 2) as n:
                    for r in range(2):
                        last = nc.vector.tensor_scalar(hits[:, r, :], dstf[:, :], bound[:, bass.ds(2 * n + r, 1)], None,
                                                       ALU.is_lt, ALU.add, accum_out=cnt[:, bass.ds(2 * n + r, 1)])
                    last.then_inc(chain, 1)
                    dve.wait_ge(chain, 1)
                    dve.sem_inc(chain, -1)
                nc.vector.tensor_copy(bound[:, 0:1], cnt[:, 0:1]).then_inc(cnt_ready, 1)
                dve.wait_ge(ends_full, 1)
                dve.sem_inc(ends_full, -1)
                nc.vector.tensor_copy(ends[:, :], psC[:, 0:T])
                nc.vector.tensor_copy(ends_i[:, :], psC[:, 0:T]).then_inc(chain, 1)
                dve.wait_ge(chain, 1)
                dve.sem_inc(chain, -1)
                nc.vector.tensor_scalar(ends_i[:, :], ends_i[:, :], 7, None, ALU.arith_shift_right).then_inc(chain, 1)
                dve.wait_ge(chain, 1)
                dve.sem_inc(chain, -1)
                nc.vector.tensor_tensor(rank[:, :], ends_i[:, :], K.iota[:, 0:T], ALU.add).then_inc(chain, 1)
                dve.wait_ge(chain, 1)
                dve.sem_inc(chain, -1)
                dve.wait_ge(cs_ready, 1)
                dve.sem_inc(cs_ready, -1)
                nc.vector.tensor_copy(cs[:, :], cs_i[:, :]).then_inc(chain, 1)
                dve.wait_ge(chain, 1)
                dve.sem_inc(chain, -1)
                nc.vector.tensor_tensor(past[:, :, :], cs[:, :].unsqueeze(2).broadcast_to([SQ, SG, T - 1]),
                                        rank[0:SQ, 0:T - 1].unsqueeze(1).broadcast_to([SQ, SG, T - 1]), ALU.is_gt).then_inc(chain, 1)
                dve.wait_ge(chain, 1)
                dve.sem_inc(chain, -1)
                nc.vector.tensor_reduce(ns[:, :], past[:, :, :], mybir.AxisListType.X, ALU.add).then_inc(chain, 1)
                dve.wait_ge(chain, 1)
                dve.sem_inc(chain, -1)
                nc.vector.tensor_scalar(ns128[:, :], ns[:, :], float(P), None, ALU.mult)
                nc.vector.tensor_tensor(es[:, :], cs[:, :], ns[:, :], ALU.subtract).then_inc(chain, 1)
                dve.wait_ge(chain, 1)
                dve.sem_inc(chain, -1)
                nc.vector.tensor_copy(es_i[:, :], es[:, :]).then_inc(es_ready, 1)

                with dve.Fori(0, ET // HJ) as i:
                    for h, (a, b) in enumerate(PART):
                        n = b - a
                        dve.wait_ge(hot_free[h], 1)
                        dve.sem_inc(hot_free[h], -1)
                        nc.vector.tensor_tensor(onehi[:, a:b, :], hi[:, bass.ds(i * HJ + a, n)].unsqueeze(2).broadcast_to([P, n, T]),
                                                K.iota[:, 0:T].unsqueeze(1).broadcast_to([P, n, T]), ALU.is_equal)
                        nc.vector.tensor_tensor(onelo[:, a:b, :], lo[:, bass.ds(i * HJ + a, n)].unsqueeze(2).broadcast_to([P, n, P]),
                                                K.iota[:, 0:P].unsqueeze(1).broadcast_to([P, n, P]), ALU.is_equal).then_inc(hot_ready[h], 1)
                dve.wait_ge(rows_in, 16 * 2 * SG)
                nc.vector.tensor_copy(rows[:, 0, :, :], rows_i[:, 0, :, :])
                for k in range(SG):
                    last = nc.vector.tensor_scalar(rows[:, 1, k, :], rows_i[:, 1, k, :], -1.0, ns128[:, k:k + 1], ALU.mult, ALU.add)
                last.then_inc(rows_ready, 1)
                dve.wait_ge(hist_full, 1)
                dve.sem_inc(hist_full, -1)
                nc.vector.tensor_copy(K.deg[:, :], psH[:, 0:T]).then_inc(deg_ready, 1)
                dve.wait_ge(rows_full, 1)
                dve.sem_inc(rows_full, -1)
                nc.vector.tensor_copy(K.src_s[:, :], psR[0][:, 0:S])
                nc.vector.tensor_copy(K.base[:, 0:S], psR[1][:, 0:S])
                nc.vector.tensor_copy(K.ns[0:1, SHIFT:SHIFT + S], psC[0:1, 0:S])
                dve.wait_ge(cum_full, 1)
                dve.sem_inc(cum_full, -1)
                nc.vector.tensor_scalar(last_e[:, 0:1], psU[:, 0:1], -1.0, None, ALU.add)
                nc.vector.scalar_tensor_tensor(last_e[:, 1:T], psU[:, 1:T], -1.0, ends[:, 0:T - 1],
                                               ALU.add, ALU.add).then_inc(chain, 1)
                dve.wait_ge(chain, 1)
                dve.sem_inc(chain, -1)
                nc.vector.tensor_scalar(last_e[:, :], last_e[:, :], 0.0, None, ALU.max).then_inc(chain, 1)
                dve.wait_ge(chain, 1)
                dve.sem_inc(chain, -1)
                nc.vector.tensor_copy(K.last_edge[:, :], last_e[:, :])

            @block.tensor
            def _(pe):
                pe.wait_ge(zero_set, 1)
                pe.sem_inc(zero_set, -1)
                nc.tensor.matmul(psH[:, 0:T], zero[:, :], zero[:, 0:T], start=True, stop=False)
                pe.sem_inc(hot_free[0], 1)
                pe.sem_inc(hot_free[1], 1)
                pe.wait_ge(cnt_ready, 1)
                pe.sem_inc(cnt_ready, -1)
                nc.tensor.matmul(psC[:, 0:T], K.ones[:, :], cnt[:, :], start=True, stop=True).then_inc(ends_full, 1)
                with pe.Fori(0, ET // HJ) as i:
                    for h, (a, b) in enumerate(PART):
                        pe.wait_ge(hot_ready[h], 1)
                        pe.sem_inc(hot_ready[h], -1)
                        for k in range(a, b):
                            last = nc.tensor.matmul(psH[:, 0:T], onelo[:, k, :], onehi[:, k, :], start=False, stop=False)
                        last.then_inc(hot_free[h], 1)
                nc.tensor.matmul(psH[:, 0:T], zero[:, :], zero[:, 0:T], start=False, stop=True).then_inc(hist_full, 1)
                pe.wait_ge(rows_ready, 1)
                pe.sem_inc(rows_ready, -1)
                for j in range(2):
                    for g in range(SG):
                        nc.tensor.transpose(psR[j][:, g * SQ:(g + 1) * SQ], rows[:, j, g, :], K.ident[0:SQ, 0:SQ])
                for g in range(SG):
                    last = nc.tensor.transpose(psC[0:1, g * SQ:(g + 1) * SQ], ns[:, g:g + 1], K.ident[0:SQ, 0:SQ])
                last.then_inc(rows_full, 1)
                pe.wait_ge(deg_ready, 1)
                pe.sem_inc(deg_ready, -1)
                nc.tensor.matmul(psU[:, 0:T], K.upper[:, :], K.deg[:, :], start=True, stop=True).then_inc(cum_full, 1)


def softmax_maxima(nc, K, ftab):
    fp32, i32, ALU, ACT = mybir.dt.float32, mybir.dt.int32, mybir.AluOpType, mybir.ActivationFunctionType
    with ExitStack() as ctx:
        def sb(n, shape, dt=fp32):
            return ctx.enter_context(nc.sbuf_tensor(f"sm_{n}", shape, dt))

        def sem(n):
            return K.sem(f"sm_{n}")
        run = sb("run", [P, ET, HEADS])
        part, partT, capT = sb("part", [P, 2, HEADS]), sb("partT", [HEADS, P]), sb("capT", [HEADS, P])
        carryT, carry = sb("carryT", [HEADS, P + 1]), sb("carry", [P, HEADS])
        top, has = sb("top", [P, T, HEADS]), sb("has", [P, T, 2])
        tmp = sb("tmp", [P, T, HEADS])
        psT = ctx.enter_context(nc.psum_tensor("sm_psT", [P, 512], fp32))
        psB = ctx.enter_context(nc.psum_tensor("sm_psB", [P, 512], fp32))
        chain = sem("chain")
        part_ready, partT_full, carry_ready, carry_full = sem("part_ready"), sem("partT_full"), sem("carry_ready"), sem("carry_full")
        run_ready, stored, top_in, self_ready = sem("run_ready"), sem("stored"), sem("top_in"), sem("self_ready")
        with nc.Block() as block:
            @block.gpsimd
            def _(pool):
                pool.wait_ge(stored, 16)
                for t in range(T):
                    nc.gpsimd.indirect_dma_start(
                        out=top[:, t, :], out_offset=None, in_=ftab,
                        in_offset=bass.IndirectOffsetOnAxis(ap=K.last_edge[:, t:t + 1].bitcast(mybir.dt.uint32), axis=0)
                    ).then_inc(top_in, 16)

            @block.sync
            def _(sp):
                sp.wait_ge(run_ready, 1)
                sp.sem_inc(run_ready, -1)
                sp.dma_start(ftab.rearrange("(p f) h -> p (f h)", p=P), run[:, :, :].rearrange("p f h -> p (f h)")).then_inc(stored, 16)

            @block.vector
            def _(dve):
                nc.vector.memset(carryT[:, 0:1], -BIG).then_inc(chain, 1)
                dve.wait_ge(chain, 1)
                dve.sem_inc(chain, -1)
                for h in range(HEADS):
                    last = nc.vector.tensor_tensor_scan(run[:, :, h], K.cap[:, :], K.term[:, :, h], -BIG, ALU.min, ALU.max)
                last.then_inc(chain, 1)
                dve.wait_ge(chain, 1)
                dve.sem_inc(chain, -1)
                nc.vector.tensor_copy(part[:, 0, :], run[:, ET - 1, :])
                nc.vector.tensor_copy(part[:, 1, :], K.capall[:, 0:1].broadcast_to([P, HEADS])).then_inc(part_ready, 1)
                dve.wait_ge(partT_full, 1)
                dve.sem_inc(partT_full, -1)
                nc.vector.tensor_copy(partT[:, :], psT[0:HEADS, 0:P])
                nc.vector.tensor_copy(capT[:, :], psT[0:HEADS, P:2 * P]).then_inc(chain, 1)
                dve.wait_ge(chain, 1)
                dve.sem_inc(chain, -1)
                nc.vector.tensor_tensor_scan(carryT[:, 1:P + 1], capT[:, :], partT[:, :], -BIG, ALU.min, ALU.max).then_inc(carry_ready, 1)
                dve.wait_ge(carry_full, 1)
                dve.sem_inc(carry_full, -1)
                nc.vector.tensor_copy(carry[:, :], psB[:, 0:HEADS]).then_inc(chain, 1)
                dve.wait_ge(chain, 1)
                dve.sem_inc(chain, -1)
                for h in range(HEADS):
                    last = nc.vector.tensor_tensor_scan(run[:, :, h], K.cap[:, :], K.term[:, :, h], carry[:, h:h + 1], ALU.min, ALU.max)
                last.then_inc(run_ready, 1)
                nc.vector.tensor_scalar(has[:, :, 0], K.deg[:, :], 1.0, None, ALU.min).then_inc(chain, 1)
                dve.wait_ge(chain, 1)
                dve.sem_inc(chain, -1)
                nc.vector.tensor_scalar(has[:, :, 1], has[:, :, 0], BIG, -BIG, ALU.mult, ALU.add).then_inc(chain, 1)
                dve.wait_ge(chain, 1)
                dve.sem_inc(chain, -1)
                nc.vector.memset(K.acc[:, :, :, :], 0.0)
                dve.wait_ge(top_in, 16 * T)
                a_s, a_d = K.H[:, :, D:TW], K.H[:, :, TW:HW]
                nc.vector.tensor_tensor(top[:, :, :], top[:, :, :], has[:, :, 0:1].broadcast_to([P, T, HEADS]), ALU.mult).then_inc(chain, 1)
                dve.wait_ge(chain, 1)
                dve.sem_inc(chain, -1)
                nc.vector.tensor_tensor(top[:, :, :], top[:, :, :], has[:, :, 1:2].broadcast_to([P, T, HEADS]), ALU.add).then_inc(chain, 1)
                dve.wait_ge(chain, 1)
                dve.sem_inc(chain, -1)
                nc.vector.tensor_tensor(top[:, :, :], top[:, :, :], a_s, ALU.max).then_inc(chain, 1)
                dve.wait_ge(chain, 1)
                dve.sem_inc(chain, -1)
                nc.vector.tensor_tensor(top[:, :, :], top[:, :, :], a_d, ALU.add).then_inc(chain, 1)
                dve.wait_ge(chain, 1)
                dve.sem_inc(chain, -1)
                nc.vector.scalar_tensor_tensor(K.node[:, :, HEADS:], top[:, :, :], 0.2, top[:, :, :], ALU.mult, ALU.max)
                nc.vector.tensor_copy(K.node[:, :, 0:HEADS], a_d)
                nc.vector.tensor_tensor(tmp[:, :, :], a_s, a_d, ALU.add).then_inc(chain, 1)
                dve.wait_ge(chain, 1)
                dve.sem_inc(chain, -1)
                nc.vector.scalar_tensor_tensor(tmp[:, :, :], tmp[:, :, :], 0.2, tmp[:, :, :], ALU.mult, ALU.max).then_inc(chain, 1)
                dve.wait_ge(chain, 1)
                dve.sem_inc(chain, -1)
                nc.vector.tensor_tensor(tmp[:, :, :], tmp[:, :, :], K.node[:, :, HEADS:], ALU.subtract).then_inc(self_ready, 1)

            @block.scalar
            def _(act):
                act.wait_ge(self_ready, 1)
                act.sem_inc(self_ready, -1)
                nc.scalar.activation(K.selfw[:, :, :], tmp[:, :, :], ACT.Exp)

            @block.tensor
            def _(pe):
                pe.wait_ge(part_ready, 1)
                pe.sem_inc(part_ready, -1)
                nc.tensor.transpose(psT[0:HEADS, 0:P], part[:, 0, :], K.ident[:, :])
                nc.tensor.transpose(psT[0:HEADS, P:2 * P], part[:, 1, :], K.ident[:, :]).then_inc(partT_full, 1)
                pe.wait_ge(carry_ready, 1)
                pe.sem_inc(carry_ready, -1)
                nc.tensor.transpose(psB[:, 0:HEADS], carryT[:, 0:P], K.ident[0:HEADS, 0:HEADS]).then_inc(carry_full, 1)


def gat(nc, I, K, htab):
    fp32, i32, ALU, ACT = mybir.dt.float32, mybir.dt.int32, mybir.AluOpType, mybir.ActivationFunctionType
    G = 4
    R = 4
    with ExitStack() as ctx:
        def sb(n, shape, dt=fp32):
            return ctx.enter_context(nc.sbuf_tensor(f"ga_{n}", shape, dt))

        def ps(n):
            return ctx.enter_context(nc.psum_tensor(f"ga_{n}", [P, 512], fp32))

        def sem(n):
            return K.sem(f"ga_{n}")
        cur, rows, wrows = sb("cur", [P, 2, R * G], i32), sb("rows", [P, R, G, TW]), sb("wrows", [P, 2, G, TW])
        hot, hotT, z = sb("hot", [P, R, G, P]), sb("hotT", [P, 2, G, P]), sb("z", [P, 2, G, HEADS])
        acc, zero, b0 = K.acc, sb("zero", [P, P]), sb("b0", [P, D])
        off = sb("off", [P, 2, G, P])
        psT, psN, psA = ps("psT"), [ps("psN0"), ps("psN1")], [ps(f"psA{k}") for k in range(G)]
        chain, pchain, achain, passed = sem("chain"), sem("pchain"), sem("achain"), sem("passed")
        rows_in, rows_free = [sem(f"rows_in{h}") for h in range(R)], sem("rows_free")
        hot_ready, hotT_full, hotT_ready, node_full = sem("hot_ready"), sem("hotT_full"), sem("hotT_ready"), sem("node_full")
        z_ready, w_ready, wrows_ready, acc_full, acc_free = sem("z_ready"), sem("w_ready"), sem("wrows_ready"), sem("acc_full"), sem("acc_free")
        zero_set, b0_in, low_ready, exp_ready = sem("zero_set"), sem("b0_in"), sem("low_ready"), sem("exp_ready")
        added, sums_ready, pool_low, pool_exp = [sem("added0"), sem("added1")], sem("sums_ready"), sem("pool_low"), sem("pool_exp")
        by_head = lambda x: x.rearrange("p (a d) -> p a d", d=HD)

        def finish(eng, ops, chain, t0, t1, low, exp):
            hs, a = K.H[:, t0:t1, 0:D], acc[:, 0, t0:t1, 0:D]
            for t in range(t0, t1):
                last = ops.tensor_tensor(by_head(K.H[:, t, 0:D]), by_head(K.H[:, t, 0:D]),
                                         K.selfw[:, t, :].unsqueeze(2).broadcast_to([P, HEADS, HD]), ALU.mult)
            last.then_inc(chain, 1)
            eng.wait_ge(chain, 1)
            eng.sem_inc(chain, -1)
            ops.tensor_tensor(a, a, hs, ALU.add).then_inc(chain, 1)
            eng.wait_ge(chain, 1)
            eng.sem_inc(chain, -1)
            for t in range(t0, t1):
                last = ops.tensor_tensor(by_head(acc[:, 0, t, 0:D]), by_head(acc[:, 0, t, 0:D]),
                                         acc[:, 0, t, D:TW].unsqueeze(2).broadcast_to([P, HEADS, HD]), ALU.mult)
            last.then_inc(chain, 1)
            eng.wait_ge(chain, 1)
            eng.sem_inc(chain, -1)
            ops.tensor_tensor(a, a, b0[:, :].unsqueeze(1).broadcast_to([P, t1 - t0, D]), ALU.add).then_inc(chain, 1)
            eng.wait_ge(chain, 1)
            eng.sem_inc(chain, -1)
            ops.tensor_scalar(hs, a, 0.0, None, ALU.min).then_inc(low, 1)
            ops.tensor_scalar(a, a, 0.0, -1.0, ALU.max, ALU.add).then_inc(chain, 1)
            eng.wait_ge(chain, 1)
            eng.sem_inc(chain, -1)
            ops.tensor_tensor(K.X[:, t0:t1, :], K.X[:, t0:t1, :], a, ALU.add).then_inc(chain, 1)
            eng.wait_ge(chain, 1)
            eng.sem_inc(chain, -1)
            eng.wait_ge(exp, 1)
            eng.sem_inc(exp, -1)
            ops.tensor_tensor(K.X[:, t0:t1, :], K.X[:, t0:t1, :], hs, ALU.add)
        CUTS = (0, 9, 18, T)
        STAGES = S // G
        with nc.Block() as block:
            @block.gpsimd
            def _(pool):
                pool.sem_inc(rows_free, R)
                with pool.Fori(0, STAGES // R // 2) as i:
                    for turn in range(2):
                        for h in range(R):
                            pool.wait_ge(rows_free, 1)
                            pool.sem_inc(rows_free, -1)
                            if h == 0:
                                nc.gpsimd.tensor_copy(cur[:, turn, :], K.src_s[:, bass.ds((2 * i + turn) * (R * G), R * G)]).then_inc(pchain, 1)
                                pool.wait_ge(pchain, 1)
                                pool.sem_inc(pchain, -1)
                            for k in range(G):
                                nc.gpsimd.indirect_dma_start(
                                    out=rows[:, h, k, :], out_offset=None, in_=htab,
                                    in_offset=bass.IndirectOffsetOnAxis(ap=cur[:, turn, h * G + k:h * G + k + 1].bitcast(mybir.dt.uint32), axis=0)
                                ).then_inc(rows_in[h], 16)
                pool.wait_ge(b0_in, 16)
                pool.wait_ge(sums_ready, 1)
                pool.sem_inc(sums_ready, -1)
                finish(pool, nc.gpsimd, pchain, CUTS[2], CUTS[3], pool_low, pool_exp)

            @block.sync
            def _(sp):
                sp.dma_start(b0[:, :], I["b0"].partition_broadcast(P)).then_inc(b0_in, 16)

            @block.vector
            def _(dve):
                nc.vector.memset(zero[:, :], 0.0).then_inc(zero_set, 1)

                def add(n, k):
                    dve.wait_ge(acc_full, 1)
                    dve.sem_inc(acc_full, -1)
                    nc.vector.tensor_tensor(acc[:, k % 2, bass.ds(n, 1), :], acc[:, k % 2, bass.ds(n, 1), :],
                                            psA[k][:, 0:TW].unsqueeze(1), ALU.add).then_inc(added[k % 2], 1)

                def added_both():
                    for k in range(2):
                        dve.wait_ge(added[k], 1)
                        dve.sem_inc(added[k], -1)
                        dve.sem_inc(acc_free, 1)

                with dve.Fori(0, STAGES // R) as i:
                    turn_ns = node_tiles(nc, K, dve, i * (R * G), R * G)
                    for h in range(R):
                        w2 = h % 2
                        zs = z[:, w2, :, :]
                        ns = turn_ns[h * G:(h + 1) * G]
                        dve.wait_ge(node_full, 1)
                        dve.sem_inc(node_full, -1)
                        dve.wait_ge(rows_in[h], (i + 1) * (16 * G))
                        dve.sem_inc(passed, 1)
                        nd = psN[w2][:, 0:G * 16].rearrange("p (k n) -> p k n", k=G)
                        nc.vector.tensor_tensor(zs, rows[:, h, :, D:TW], nd[:, :, 0:HEADS], ALU.add).then_inc(chain, 1)
                        add(ns[0], 2)
                        dve.wait_ge(chain, 1)
                        dve.sem_inc(chain, -1)
                        nc.vector.scalar_tensor_tensor(zs, zs, 0.2, zs, ALU.mult, ALU.max).then_inc(chain, 1)
                        add(ns[1], 3)
                        dve.wait_ge(chain, 1)
                        dve.sem_inc(chain, -1)
                        nc.vector.tensor_tensor(zs, zs, nd[:, :, HEADS:], ALU.subtract).then_inc(chain, 1)
                        dve.wait_ge(chain, 1)
                        dve.sem_inc(chain, -1)
                        nc.vector.tensor_scalar(zs, zs, 1.0, None, ALU.min).then_inc(z_ready, 1)
                        added_both()
                        add(ns[2], 0)
                        add(ns[3], 1)
                        dve.wait_ge(w_ready, 1)
                        dve.sem_inc(w_ready, -1)
                        nc.vector.tensor_tensor(
                            wrows[:, w2, :, 0:D].rearrange("p k (a d) -> p k a d", d=HD),
                            rows[:, h, :, 0:D].rearrange("p k (a d) -> p k a d", d=HD),
                            wrows[:, w2, :, D:TW].unsqueeze(3).broadcast_to([P, G, HEADS, HD]), ALU.mult).then_inc(chain, 1)
                        added_both()
                        dve.wait_ge(chain, 1)
                        dve.sem_inc(chain, -1)
                        dve.sem_inc(wrows_ready, 1)
                        dve.sem_inc(rows_free, 1)
                for q, steps in ((STAGES, (2, 3, 0, 1)), (STAGES + 1, (2, 3))):
                    ns = node_tiles(nc, K, dve, q * G, len(steps))
                    for j, k in enumerate(steps):
                        add(ns[j], k)
                        if k % 2:
                            added_both()
                nc.vector.tensor_tensor(acc[:, 0, :, :], acc[:, 0, :, :], acc[:, 1, :, :], ALU.add).then_inc(chain, 1)
                dve.wait_ge(chain, 1)
                dve.sem_inc(chain, -1)
                a_den = acc[:, 0, :, D:TW]
                nc.vector.tensor_tensor(a_den, a_den, K.selfw[:, :, :], ALU.add).then_inc(chain, 1)
                dve.wait_ge(chain, 1)
                dve.sem_inc(chain, -1)
                nc.vector.tensor_scalar(a_den, a_den, 1e-16, None, ALU.add).then_inc(chain, 1)
                dve.wait_ge(chain, 1)
                dve.sem_inc(chain, -1)
                nc.vector.reciprocal(a_den, a_den).then_inc(chain, 1)
                dve.wait_ge(chain, 1)
                dve.sem_inc(chain, -1)
                dve.sem_inc(sums_ready, 1)
                dve.wait_ge(b0_in, 16)
                finish(dve, nc.vector, chain, CUTS[0], CUTS[1], low_ready, exp_ready)
                finish(dve, nc.vector, chain, CUTS[1], CUTS[2], low_ready, exp_ready)

            @block.scalar
            def _(act):
                def onehot(q, h):
                    for k in range(G):
                        last = nc.scalar.activation(off[:, h % 2, k, :], K.iota[:, 0:P], ACT.Abs, bias=K.base[:, bass.ds(q * G + k, 1)])
                    last.then_inc(achain, 1)
                    act.wait_ge(achain, 1)
                    act.sem_inc(achain, -1)
                    nc.scalar.activation(hot[:, h, :, :], off[:, h % 2, :, :], ACT.Relu, bias=K.ones[:, 0:1], scale=-1.0).then_inc(hot_ready, 1)

                def copy(h):
                    act.wait_ge(hotT_full, 1)
                    act.sem_inc(hotT_full, -1)
                    nc.scalar.activation(hotT[:, h, :, :].rearrange("p k n -> p (k n)"), psT[:, :], ACT.Identity).then_inc(hotT_ready, 1)
                onehot(0, 0)
                onehot(1, 1)
                copy(0)
                with act.Fori(0, STAGES // R) as i:
                    for h in range(R):
                        copy((h + 1) % 2)
                        onehot(R * i + h + 2, (h + 2) % R)
                        act.wait_ge(z_ready, 1)
                        act.sem_inc(z_ready, -1)
                        nc.scalar.activation(wrows[:, h % 2, :, D:TW], z[:, h % 2, :, :], ACT.Exp).then_inc(w_ready, 1)
                for t0, t1, low, exp in zip(CUTS[0:3], CUTS[1:4], (low_ready, low_ready, pool_low), (exp_ready, exp_ready, pool_exp)):
                    act.wait_ge(low, 1)
                    act.sem_inc(low, -1)
                    nc.scalar.activation(K.H[:, t0:t1, 0:D], K.H[:, t0:t1, 0:D], ACT.Exp).then_inc(exp, 1)

            @block.tensor
            def _(pe):
                def transposes(h):
                    pe.wait_ge(hot_ready, 1)
                    pe.sem_inc(hot_ready, -1)
                    for k in range(G):
                        last = nc.tensor.transpose(psT[:, k * P:(k + 1) * P], hot[:, h, k, :], K.ident[:, :])
                    last.then_inc(hotT_full, 1)

                def node_terms(q, h):
                    pe.wait_ge(hotT_ready, 1)
                    pe.sem_inc(hotT_ready, -1)
                    ns = node_tiles(nc, K, pe, q * G + SHIFT, G)
                    for k in range(G):
                        last = nc.tensor.matmul(psN[h][:, k * 16:(k + 1) * 16], hotT[:, h, k, :],
                                                K.node[:, bass.ds(ns[k], 1), :].rearrange("p a b -> p (a b)"), start=True, stop=True)
                    last.then_inc(node_full, 1)
                pe.wait_ge(zero_set, 1)
                pe.sem_inc(zero_set, -1)
                for k in (2, 3, 0, 1):
                    nc.tensor.matmul(psA[k][:, 0:TW], zero[:, :], K.iota[:, 0:TW], start=True, stop=True).then_inc(acc_full, 1)
                transposes(0)
                node_terms(0, 0)
                transposes(1)
                def sums(h, steps):
                    for k in steps:
                        pe.wait_ge(acc_free, 1)
                        pe.sem_inc(acc_free, -1)
                        nc.tensor.matmul(psA[k][:, 0:TW], hot[:, h, k, :], wrows[:, h % 2, k, :],
                                         start=True, stop=True).then_inc(acc_full, 1)

                def stage(i, h, first=False):
                    node_terms(R * i + h + 1, (h + 1) % 2)
                    if first:
                        for k in (2, 3):
                            pe.wait_ge(acc_free, 1)
                            pe.sem_inc(acc_free, -1)
                            nc.tensor.matmul(psA[k][:, 0:TW], zero[:, :], K.iota[:, 0:TW], start=True, stop=True).then_inc(acc_full, 1)
                    else:
                        sums((h - 1) % R, (2, 3))
                    transposes((h + 2) % R)
                    pe.wait_ge(wrows_ready, 1)
                    pe.sem_inc(wrows_ready, -1)
                    sums(h, (0, 1))
                for h in range(R):
                    stage(0, h, h == 0)
                with pe.Fori(1, STAGES // R) as i:
                    for h in range(R):
                        stage(i, h)
                sums(R - 1, (2, 3))


def load_ffn0(I, K, sp):
    sp.dma_start(K.f0_w1[:, :, :], I["f0_w1"].rearrange("(c p) n -> p c n", p=P)).then_inc(K.f0_loaded, 16)
    sp.dma_start(K.f0_b1[:, :], I["f0_b1"]).then_inc(K.f0_loaded, 16)
    sp.dma_start(K.f0_w2[:, :, :], I["f0_w2"].rearrange("(m p) n -> p m n", p=P)).then_inc(K.f0_loaded, 16)
    sp.dma_start(K.f0_b2[:, :], I["f0_b2"].partition_broadcast(P)).then_inc(K.f0_loaded, 16)


def ffn0(nc, I, K, wtab):
    fp32, ALU, ACT = mybir.dt.float32, mybir.AluOpType, mybir.ActivationFunctionType
    AX = mybir.AxisListType.X
    M = FF0 // P
    with ExitStack() as ctx:
        def sb(n, shape):
            return ctx.enter_context(nc.sbuf_tensor(f"f0_{n}", shape, fp32))

        def ps(n):
            return ctx.enter_context(nc.psum_tensor(f"f0_{n}", [P, 512], fp32))

        def sem(n):
            return K.sem(f"f0_{n}")
        w1, b1, w2, b2, loaded = K.f0_w1, K.f0_b1, K.f0_w2, K.f0_b2, K.f0_loaded
        xs, xT, hT = sb("xs", [P, 2, D]), sb("xT", [P, C, 2 * P]), sb("hT", [P, M, 2 * P])
        gain, shift = sb("gain", [P, T]), sb("shift", [P, T])
        psT, psU, psO = ps("psT"), [ps("psU0"), ps("psU1")], [ps("psO0"), ps("psO1")]
        y, wr, br, w, tmp = sb("y", [P, T, D]), sb("wr", [P, D]), sb("br", [P, 1]), sb("w", [P, T]), sb("tmp", [P, T])
        prod, every, above = sb("prod", [P, 2, D]), sb("every", [P, T * P]), sb("above", [P, 2, T * P])
        rank, least, edge, coef = sb("rank", [P, T]), sb("least", [P, 1]), sb("edge", [1, 1]), sb("coef", [P, T])
        gt, eq, cum, tot, both, need = sb("gt", [P, T]), sb("eq", [P, T]), sb("cum", [P, T]), sb("tot", [P, T + 1]), sb("both", [P, 1]), sb("need", [P, 1])
        zeros, tau = sb("zeros", [P, T]), sb("tau", [P, 1])
        warm = sb("warm", [P, 1])
        psL, psE, psM = ps("psL"), ps("psE"), ps("psM")
        chain, router_loaded = sem("chain"), sem("router_loaded")
        w_ready, stored, every_in = sem("w_ready"), sem("stored"), sem("every_in")
        least_ready, leastT_full, edge_ready, tau_full, marks_ready, marks_full = (
            sem("least_ready"), sem("leastT_full"), sem("edge_ready"), sem("tau_full"), sem("marks_ready"), sem("marks_full"))
        xs_ready, xT_full, xT_ready, up_full, up_free, hT_ready, out_full, out_free = (
            sem(n) for n in ("xs_ready", "xT_full", "xT_ready", "up_full", "up_free", "hT_ready", "out_full", "out_free"))
        xs_free = sem("xs_free")
        with nc.Block() as block:
            @block.sync
            def _(sp):
                sp.dma_start(wr[:, :], I["f0_wr"].partition_broadcast(P)).then_inc(router_loaded, 16)
                sp.dma_start(br[:, :], I["f0_br"].partition_broadcast(P)).then_inc(router_loaded, 16)
                sp.wait_ge(w_ready, 1)
                sp.sem_inc(w_ready, -1)
                sp.dma_start(wtab.rearrange("(p t) -> p t", p=P), w[:, :]).then_inc(stored, 16)
                sp.wait_ge(stored, 16)
                sp.dma_start(every[:, :], wtab.partition_broadcast(P)).then_inc(every_in, 16)

            @block.vector
            def _(dve):
                nc.vector.tensor_scalar(gain[:, :], K.rstd[:, :], 1.0, None, ALU.add)
                nc.vector.tensor_tensor(shift[:, :], K.mean[:, :], K.rstd[:, :], ALU.mult).then_inc(chain, 1)
                dve.wait_ge(chain, 1)
                dve.sem_inc(chain, -1)
                nc.vector.tensor_scalar(shift[:, :], shift[:, :], -1.0, None, ALU.mult).then_inc(chain, 1)
                dve.wait_ge(chain, 1)
                dve.sem_inc(chain, -1)

                def norm(i):
                    for r in range(2):
                        t = 2 * i + r
                        last = nc.vector.tensor_scalar(xs[:, r, :].unsqueeze(1), K.X[:, bass.ds(t, 1), :],
                                                       K.mean[:, bass.ds(t, 1)], K.rstd[:, bass.ds(t, 1)],
                                                       ALU.subtract, ALU.mult)
                    last.then_inc(xs_ready, 1)

                def finish(i):
                    for r in range(2):
                        t = 2 * i + r
                        x = K.X[:, bass.ds(t, 1), :]
                        dve.wait_ge(out_full, 1)
                        dve.sem_inc(out_full, -1)
                        nc.vector.tensor_tensor(y[:, bass.ds(t, 1), :], psO[r][:, 0:D].unsqueeze(1), b2[:, :].unsqueeze(1), ALU.add).then_inc(out_free, 1)
                        last = nc.vector.tensor_scalar(x, x, gain[:, bass.ds(t, 1)], shift[:, bass.ds(t, 1)], ALU.mult, ALU.add)
                    return last

                def ranks(i):
                    for k in range(2):
                        nc.vector.tensor_scalar(above[:, k, :], every[:, :], w[:, bass.ds(2 * i + k, 1)], None,
                                                ALU.is_gt, ALU.add, accum_out=rank[:, bass.ds(2 * i + k, 1)]).then_inc(chain, 1)
                        dve.wait_ge(chain, 1)
                        dve.sem_inc(chain, -1)
                norm(0)
                dve.wait_ge(xs_free, 1)
                dve.sem_inc(xs_free, -1)
                norm(1)
                nc.vector.memset(zeros[:, :], 0.0)
                nc.vector.memset(tot[:, 0:1], 0.0)
                dve.wait_ge(router_loaded, 32)
                with dve.Fori(0, T // 2) as i:
                    for k in range(2):
                        nc.vector.scalar_tensor_tensor(
                            prod[:, k, :].unsqueeze(1), K.X[:, bass.ds(2 * i + k, 1), :], K.mean[:, bass.ds(2 * i + k, 1)],
                            wr[:, :].unsqueeze(1), ALU.subtract, ALU.mult, accum_out=w[:, bass.ds(2 * i + k, 1)]).then_inc(chain, 1)
                        dve.wait_ge(chain, 1)
                        dve.sem_inc(chain, -1)
                nc.vector.tensor_tensor(w[:, :], w[:, :], K.rstd[:, :], ALU.mult).then_inc(chain, 1)
                dve.wait_ge(chain, 1)
                dve.sem_inc(chain, -1)
                nc.vector.tensor_scalar(w[:, :], w[:, :], br[:, 0:1], None, ALU.add).then_inc(chain, 1)
                dve.wait_ge(chain, 1)
                dve.sem_inc(chain, -1)
                nc.vector.tensor_tensor(w[:, :], w[:, :], K.real[:, :], ALU.mult).then_inc(chain, 1)
                dve.wait_ge(chain, 1)
                dve.sem_inc(chain, -1)
                nc.vector.tensor_scalar(tmp[:, :], K.real[:, :], BIG, -BIG, ALU.mult, ALU.add).then_inc(chain, 1)
                dve.wait_ge(chain, 1)
                dve.sem_inc(chain, -1)
                nc.vector.tensor_tensor(w[:, :], w[:, :], tmp[:, :], ALU.add).then_inc(w_ready, 1)
                dve.wait_ge(loaded, 64)
                with dve.Fori(0, T // 2 - 2) as i:
                    finish(i)
                    dve.wait_ge(xs_free, 1)
                    dve.sem_inc(xs_free, -1)
                    norm(i + 2)
                    dve.wait_ge(every_in, 16)
                    ranks(i)
                ranks(T // 2 - 2)
                ranks(T // 2 - 1)
                nc.vector.tensor_scalar(gt[:, :], rank[:, :], float(KEEP), None, ALU.is_lt).then_inc(chain, 1)
                dve.wait_ge(chain, 1)
                dve.sem_inc(chain, -1)
                nc.vector.tensor_tensor(cum[:, :], w[:, :], gt[:, :], ALU.mult).then_inc(chain, 1)
                dve.wait_ge(chain, 1)
                dve.sem_inc(chain, -1)
                nc.vector.tensor_scalar(gt[:, :], gt[:, :], -BIG, BIG, ALU.mult, ALU.add).then_inc(chain, 1)
                dve.wait_ge(chain, 1)
                dve.sem_inc(chain, -1)
                nc.vector.tensor_tensor(cum[:, :], cum[:, :], gt[:, :], ALU.add).then_inc(chain, 1)
                dve.wait_ge(chain, 1)
                dve.sem_inc(chain, -1)
                nc.vector.tensor_reduce(least[:, :], cum[:, :], AX, ALU.min).then_inc(least_ready, 1)
                finish(T // 2 - 2)
                dve.wait_ge(leastT_full, 1)
                dve.sem_inc(leastT_full, -1)
                nc.vector.tensor_reduce(edge[:, :], psL[0:1, 0:P], AX, ALU.min).then_inc(edge_ready, 1)
                dve.wait_ge(tau_full, 1)
                dve.sem_inc(tau_full, -1)
                nc.vector.tensor_copy(tau[:, :], psE[:, 0:1]).then_inc(chain, 1)
                dve.wait_ge(chain, 1)
                dve.sem_inc(chain, -1)
                nc.vector.tensor_scalar(gt[:, :], w[:, :], tau[:, 0:1], None, ALU.is_gt)
                nc.vector.tensor_scalar(eq[:, :], w[:, :], tau[:, 0:1], None, ALU.is_equal).then_inc(chain, 1)
                dve.wait_ge(chain, 1)
                dve.sem_inc(chain, -1)
                nc.vector.tensor_reduce(both[:, :], gt[:, :], AX, ALU.add).then_inc(marks_ready, 1)
                dve.wait_ge(marks_full, 1)
                dve.sem_inc(marks_full, -1)
                nc.vector.tensor_scalar(need[:, :], psM[:, 0:1], -1.0, float(KEEP), ALU.mult, ALU.add)
                nc.vector.tensor_copy(cum[:, :], psM[:, 64:64 + T])
                nc.vector.tensor_tensor_scan(tot[:, 1:T + 1], zeros[:, :], psM[:, 128:128 + T], 0.0, ALU.add, ALU.add).then_inc(chain, 1)
                dve.wait_ge(chain, 1)
                dve.sem_inc(chain, -1)
                nc.vector.tensor_tensor(cum[:, :], cum[:, :], tot[:, 0:T], ALU.add).then_inc(chain, 1)
                dve.wait_ge(chain, 1)
                dve.sem_inc(chain, -1)
                nc.vector.tensor_scalar(cum[:, :], cum[:, :], need[:, 0:1], None, ALU.is_le).then_inc(chain, 1)
                dve.wait_ge(chain, 1)
                dve.sem_inc(chain, -1)
                nc.vector.tensor_tensor(eq[:, :], eq[:, :], cum[:, :], ALU.mult).then_inc(chain, 1)
                dve.wait_ge(chain, 1)
                dve.sem_inc(chain, -1)
                nc.vector.tensor_tensor(gt[:, :], gt[:, :], eq[:, :], ALU.add).then_inc(chain, 1)
                dve.wait_ge(chain, 1)
                dve.sem_inc(chain, -1)
                nc.vector.tensor_tensor(coef[:, :], gt[:, :], w[:, :], ALU.mult).then_inc(chain, 1)
                dve.wait_ge(chain, 1)
                dve.sem_inc(chain, -1)

                def add_y(i):
                    for k in range(2):
                        x = K.X[:, bass.ds(2 * i + k, 1), :]
                        nc.vector.scalar_tensor_tensor(x, y[:, bass.ds(2 * i + k, 1), :], coef[:, bass.ds(2 * i + k, 1)], x,
                                                       ALU.mult, ALU.add)
                with dve.Fori(0, T // 2 - 1) as i:
                    add_y(i)
                finish(T // 2 - 1).then_inc(chain, 1)
                dve.wait_ge(chain, 1)
                dve.sem_inc(chain, -1)
                add_y(T // 2 - 1)

            @block.scalar
            def _(act):
                nc.scalar.activation(warm[:, :], K.ones[:, 0:1], ACT.Gelu_apprx_tanh)
                with act.Fori(0, T // 2) as i:
                    act.wait_ge(xT_full, 1)
                    act.sem_inc(xT_full, -1)
                    nc.scalar.activation(xT[:, :, :].rearrange("p c n -> p (c n)"), psT[:, :], ACT.Identity).then_inc(xT_ready, 1)
                    for m in range(M):
                        act.wait_ge(up_full, 1)
                        act.sem_inc(up_full, -1)
                        nc.scalar.activation(hT[:, m, :], psU[m % 2][:, 0:2 * P], ACT.Gelu_apprx_tanh,
                                             bias=b1[:, m:m + 1]).then_inc(up_free, 1)

            @block.tensor
            def _(pe):
                pe.sem_inc(out_free, 2)
                pe.sem_inc(up_free, 2)
                pe.wait_ge(loaded, 64)

                def transposes():
                    pe.wait_ge(xs_ready, 1)
                    pe.sem_inc(xs_ready, -1)
                    for c in range(C):
                        for r in range(2):
                            last = nc.tensor.transpose(psT[:, (2 * c + r) * P:(2 * c + r + 1) * P],
                                                       xs[:, r, c * P:(c + 1) * P], K.ident[:, :])
                    last.then_inc(xT_full, 1)

                def body(final):
                    pe.wait_ge(xT_ready, 1)
                    pe.sem_inc(xT_ready, -1)
                    pe.sem_inc(xs_free, 1)
                    for m in range(M):
                        pe.wait_ge(up_free, 1)
                        pe.sem_inc(up_free, -1)
                        for c in range(C):
                            last = nc.tensor.matmul(psU[m % 2][:, 0:2 * P], w1[:, c, m * P:(m + 1) * P], xT[:, c, :],
                                                    start=(c == 0), stop=(c == C - 1))
                        last.then_inc(up_full, 1)
                    if not final:
                        transposes()
                    pe.wait_ge(up_free, 2)
                    pe.sem_inc(up_free, -2)
                    pe.sem_inc(up_free, 2)
                    for r in range(2):
                        pe.wait_ge(out_free, 1)
                        pe.sem_inc(out_free, -1)
                        for m in range(M):
                            last = nc.tensor.matmul(psO[r][:, 0:D], hT[:, m, r * P:(r + 1) * P], w2[:, m, :],
                                                    start=(m == 0), stop=(m == M - 1))
                        last.then_inc(out_full, 1)
                transposes()
                with pe.Fori(0, T // 2 - 1) as i:
                    body(False)
                pe.wait_ge(least_ready, 1)
                pe.sem_inc(least_ready, -1)
                nc.tensor.transpose(psL[0:1, 0:P], least[:, :], K.ident[:, :]).then_inc(leastT_full, 1)
                pe.wait_ge(edge_ready, 1)
                pe.sem_inc(edge_ready, -1)
                nc.tensor.matmul(psE[:, 0:1], K.ones[0:1, :], edge[:, :], start=True, stop=True).then_inc(tau_full, 1)
                pe.wait_ge(marks_ready, 1)
                pe.sem_inc(marks_ready, -1)
                nc.tensor.matmul(psM[:, 0:1], K.ones[:, :], both[:, :], start=True, stop=True)
                nc.tensor.matmul(psM[:, 64:64 + T], K.upper[:, :], eq[:, :], start=True, stop=True)
                nc.tensor.matmul(psM[:, 128:128 + T], K.ones[:, :], eq[:, :], start=True, stop=True).then_inc(marks_full, 1)
                body(True)


def normalise(nc, K, ztab):
    fp32, ALU = mybir.dt.float32, mybir.AluOpType
    with ExitStack() as ctx:
        done, stored = K.sem("no_done"), K.sem("no_stored")
        with nc.Block() as block:
            @block.vector
            def _(dve):
                with dve.Fori(0, T // 2) as i:
                    for k in range(2):
                        t = 2 * i + k
                        nc.vector.tensor_scalar(K.Z[:, bass.ds(t, 1), :], K.X[:, bass.ds(t, 1), :], K.mean[:, bass.ds(t, 1)],
                                                K.rstd[:, bass.ds(t, 1)], ALU.subtract, ALU.mult).then_inc(done, 1)

            @block.sync
            def _(sp):
                sp.wait_ge(done, T)
                sp.sem_inc(done, -T)
                sp.dma_start(ztab.rearrange("(t p) n -> p t n", p=P), K.Z[:, :, :]).then_inc(stored, 16)
                sp.wait_ge(stored, 16)


def aggregate(nc, I, K, ztab, stab):
    fp32, i32, ALU, ACT = mybir.dt.float32, mybir.dt.int32, mybir.AluOpType, mybir.ActivationFunctionType
    G = 4
    R = 4
    with ExitStack() as ctx:
        def sb(n, shape, dt=fp32):
            return ctx.enter_context(nc.sbuf_tensor(f"ag_{n}", shape, dt))

        def sem(n):
            return K.sem(f"ag_{n}")
        cur, rows, hot, zero = sb("cur", [P, 2, R * G], i32), sb("rows", [P, R, G, D]), sb("hot", [P, 2, G, P]), sb("zero", [P, P])
        off = sb("off", [P, 2, G, P])
        psA = [ctx.enter_context(nc.psum_tensor(f"ag_psA{k}", [P, 512], fp32)) for k in range(G)]
        chain, pchain, achain, hot_free = sem("chain"), sem("pchain"), sem("achain"), sem("hot_free")
        rows_in, rows_free, passed = [sem(f"rows_in{h}") for h in range(R)], sem("rows_free"), sem("passed")
        hot_ready, acc_full, acc_free, zero_set = sem("hot_ready"), sem("acc_full"), sem("acc_free"), sem("zero_set")
        STAGES = S // G
        wself, bg, xs, ps = sb("wself", [P, C, D]), sb("bg", [P, D]), sb("xs", [P, 2, D + 1]), [
            ctx.enter_context(nc.psum_tensor(f"ag_{n}", [P, 512], fp32)) for n in ("psG0", "psG1", "psT", "psS")]
        xT = sb("xT", [P, 2, D])
        loaded, z_ready, zT_full, zT_ready, s_full = (sem(n) for n in ("loaded", "z_ready", "zT_full", "zT_ready", "s_full"))
        wk, wv, wfc, wq = (sb(n, [P, C, D]) for n in ("wk", "wv", "wfc", "wq"))
        bk, bv, bfc, bq = sb("bk", [1, D]), sb("bv", [1, D]), sb("bfc", [1, D]), sb("bq", [P, C])
        gram, col = sb("gram", [P, C, D + 1]), sb("col", [1, D + 1])
        t1, t1a, kvT, m2, b3 = sb("t1", [P, C, D]), sb("t1a", [1, D]), sb("kvT", [P, C, P]), sb("m2", [P, C * D]), sb("b3", [1, D])
        m_loaded, ready, full = sem("m_loaded"), sem("ready"), sem("full")
        wide_zero, stab_zero = sb("wide_zero", [P, 2, D]), sem("stab_zero")
        wide_zero_set = sem("wide_zero_set")
        with nc.Block() as block:
            @block.sync
            def _(sp):
                sp.dma_start(wself[:, :, :], I["Wself"].rearrange("(c p) n -> p c n", p=P)).then_inc(loaded, 16)
                sp.dma_start(bg[:, :], I["bgnn"].partition_broadcast(P)).then_inc(loaded, 16)
                for a, n in ((wk, "WkT"), (wv, "WvT"), (wfc, "WfcT"), (wq, "Wq")):
                    sp.dma_start(a[:, :, :], I[n].rearrange("(c p) n -> p c n", p=P)).then_inc(m_loaded, 16)
                for a, n in ((bk, "bk"), (bv, "bv"), (bfc, "bfc")):
                    sp.dma_start(a[:, :], I[n].rearrange("(a n) -> a n", a=1)).then_inc(m_loaded, 16)
                sp.dma_start(bq[:, :], I["bq"]).then_inc(m_loaded, 16)
                sp.wait_ge(wide_zero_set, 1)
                sp.sem_inc(wide_zero_set, -1)
                slots = stab[0:ST * P, :].rearrange("(j p r) d -> j p r d", p=P, r=2)
                for j in range(ST // 2):
                    sp.dma_start(slots[j], wide_zero[:, :, :]).then_inc(stab_zero, 16)
                sp.wait_ge(stab_zero, ST // 2 * 16)

            @block.gpsimd
            def _(pool):
                pool.sem_inc(rows_free, R - 1)
                with pool.Fori(0, STAGES // R // 2) as i:
                    for turn in range(2):
                        for h in range(R):
                            pool.wait_ge(rows_free, 1)
                            pool.sem_inc(rows_free, -1)
                            if h == 0:
                                nc.gpsimd.tensor_copy(cur[:, turn, :], K.src_s[:, bass.ds((2 * i + turn) * (R * G), R * G)]).then_inc(pchain, 1)
                                pool.wait_ge(pchain, 1)
                                pool.sem_inc(pchain, -1)
                            for k in range(G):
                                nc.gpsimd.indirect_dma_start(
                                    out=rows[:, h, k, :], out_offset=None, in_=ztab,
                                    in_offset=bass.IndirectOffsetOnAxis(ap=cur[:, turn, h * G + k:h * G + k + 1].bitcast(mybir.dt.uint32), axis=0)
                                ).then_inc(rows_in[h], 16)

            @block.vector
            def _(dve):
                nc.vector.memset(wide_zero[:, :, :], 0.0).then_inc(wide_zero_set, 1)
                nc.vector.memset(zero[:, :], 0.0).then_inc(zero_set, 1)
                nc.vector.memset(K.agg[:, :, :], 0.0).then_inc(chain, 1)
                dve.wait_ge(chain, 1)
                dve.sem_inc(chain, -1)

                def add(ns):
                    for k in range(G):
                        dve.wait_ge(acc_full, 1)
                        dve.sem_inc(acc_full, -1)
                        n = ns[k]
                        nc.vector.tensor_tensor(K.agg[:, bass.ds(n, 1), :], K.agg[:, bass.ds(n, 1), :],
                                                psA[k][:, 0:D].unsqueeze(1), ALU.add).then_inc(chain, 1)
                        dve.wait_ge(chain, 1)
                        dve.sem_inc(chain, -1)
                        dve.sem_inc(acc_free, 1)
                    dve.sem_inc(rows_free, 1)
                    dve.sem_inc(hot_free, 1)

                def rows_of(t, k):
                    nc.vector.tensor_copy(xs[:, k, D:D + 1], K.real[:, bass.ds(t, 1)])
                    return nc.vector.tensor_scalar(xs[:, k, 0:D].unsqueeze(1), K.Z[:, bass.ds(t, 1), :],
                                                   K.real[:, bass.ds(t, 1)], None, ALU.mult)

                def self_part(i):
                    dve.wait_ge(s_full, 1)
                    dve.sem_inc(s_full, -1)
                    nc.vector.tensor_tensor(K.G[:, bass.ds(2 * i, 2), :], ps[3][:, :].rearrange("p (r n) -> p r n", r=2),
                                            bg[:, :].unsqueeze(1).broadcast_to([P, 2, D]), ALU.add)
                dve.wait_ge(loaded, 32)

                def turn_tiles(i):
                    return node_tiles(nc, K, dve, i * (R * G) + SHIFT - G, R * G)

                def attention(step):
                    dve.wait_ge(full, 1)
                    dve.sem_inc(full, -1)
                    if step == 0:
                        for c in range(C):
                            last = nc.vector.tensor_copy(gram[:, c, :], ps[c][:, 0:D + 1])
                    if step == 1:
                        nc.vector.memset(col[:, D:D + 1], float(N))
                        last = nc.vector.tensor_copy(col[:, 0:D], ps[3][0:1, 0:D])
                    if step == 2:
                        for c in range(C):
                            nc.vector.tensor_copy(t1[:, c, :], ps[c][:, 0:D])
                        last = nc.vector.tensor_copy(t1a[:, :], ps[2][0:1, 0:D])
                    if step == 3:
                        for c in range(C):
                            mask = K.blockmask[:, c, 4 * c:4 * c + 4].unsqueeze(2).broadcast_to([P, 4, HD])
                            last = nc.vector.scalar_tensor_tensor(
                                kvT[:, c, :].rearrange("p (h m) -> p h m", m=HD),
                                ps[3][:, c * D + c * P:c * D + (c + 1) * P].rearrange("p (h m) -> p h m", m=HD), 1.0 / N, mask, ALU.mult, ALU.mult)
                    if step == 4:
                        last = nc.vector.tensor_copy(m2[:, :], ps[0][:, :])
                    if step == 5:
                        nc.vector.tensor_copy(K.m3[:, :], ps[2][:, :])
                        last = nc.vector.tensor_copy(b3[:, :], ps[1][0:1, 0:D])
                    if step == 6:
                        last = nc.vector.tensor_copy(K.b3[:, :], ps[3][:, 0:D])
                    last.then_inc(ready, 1)
                with dve.Fori(0, T // 2) as i:
                    ns = turn_tiles(i)
                    rows_of(2 * i, 0)
                    rows_of(2 * i + 1, 1).then_inc(z_ready, 1)
                    for h in range(R):
                        add(ns[h * G:(h + 1) * G])
                    self_part(i)
                for i in (T // 2, T // 2 + 1):
                    ns = turn_tiles(i)
                    for h in range(R):
                        add(ns[h * G:(h + 1) * G])
                        if (i - T // 2) * R + h < 7:
                            attention((i - T // 2) * R + h)
                with dve.Fori(T // 2 + 2, STAGES // R) as i:
                    ns = turn_tiles(i)
                    for h in range(R):
                        add(ns[h * G:(h + 1) * G])
                add(node_tiles(nc, K, dve, STAGES * G + SHIFT - G, G))

            @block.scalar
            def _(act):
                act.sem_inc(hot_free, 1)
                def onehot(i, h):
                    act.wait_ge(hot_free, 1)
                    act.sem_inc(hot_free, -1)
                    for k in range(G):
                        last = nc.scalar.activation(off[:, h % 2, k, :], K.iota[:, 0:P], ACT.Abs, bias=K.base[:, bass.ds((R * i + h) * G + k, 1)])
                    last.then_inc(achain, 1)
                    act.wait_ge(achain, 1)
                    act.sem_inc(achain, -1)
                    nc.scalar.activation(hot[:, h % 2, :, :], off[:, h % 2, :, :], ACT.Relu, bias=K.ones[:, 0:1], scale=-1.0).then_inc(hot_ready, 1)
                with act.Fori(0, T // 2) as i:
                    for h in range(R):
                        if h == 2:
                            act.wait_ge(zT_full, 1)
                            act.sem_inc(zT_full, -1)
                            nc.scalar.activation(K.ZT[:, bass.ds(2 * i, 2), :].rearrange("p t d -> p (t d)"), ps[2][:, :], ACT.Identity)
                            nc.scalar.activation(xT[:, :, :].rearrange("p t d -> p (t d)"), ps[2][:, :], ACT.Identity).then_inc(zT_ready, 1)
                        onehot(i, h)
                with act.Fori(T // 2, STAGES // R) as i:
                    for h in range(R):
                        onehot(i, h)

            @block.tensor
            def _(pe):
                pe.wait_ge(zero_set, 1)
                pe.sem_inc(zero_set, -1)
                for k in range(G):
                    nc.tensor.matmul(psA[k][:, 0:D], zero[:, :], K.iota[:, 0:D], start=True, stop=True).then_inc(acc_full, 1)
                for c in range(C):
                    nc.tensor.matmul(ps[c][:, 0:D + 1], zero[:, :], K.iota[:, 0:D + 1], start=True, stop=False)
                pe.wait_ge(loaded, 32)

                def beside(h):
                    if h == 0:
                        pe.wait_ge(z_ready, 1)
                        pe.sem_inc(z_ready, -1)
                        for r in range(2):
                            for c in range(C):
                                last = nc.tensor.transpose(ps[2][:, (2 * r + c) * P:(2 * r + c + 1) * P], xs[:, r, c * P:(c + 1) * P], K.ident[:, :])
                        last.then_inc(zT_full, 1)
                    if h == 1:
                        for r in range(2):
                            for c in range(C):
                                nc.tensor.matmul(ps[c][:, 0:D + 1], xs[:, r, c * P:(c + 1) * P], xs[:, r, :], start=False, stop=False)
                    if h == 2:
                        pe.wait_ge(zT_ready, 1)
                        pe.sem_inc(zT_ready, -1)
                        for r in range(2):
                            for c in range(C):
                                last = nc.tensor.matmul(ps[3][:, r * D:(r + 1) * D], xT[:, r, c * P:(c + 1) * P], wself[:, c, :],
                                                        start=(c == 0), stop=(c == C - 1))
                        last.then_inc(s_full, 1)

                def attention(step):
                    if step > 0:
                        pe.wait_ge(ready, 1)
                        pe.sem_inc(ready, -1)
                    if step == 0:
                        for c in range(C):
                            last = nc.tensor.matmul(ps[c][:, 0:D + 1], zero[:, :], K.iota[:, 0:D + 1], start=False, stop=True)
                    if step == 1:
                        for c in range(C):
                            last = nc.tensor.transpose(ps[3][0:1, c * P:(c + 1) * P], gram[:, c, D:D + 1], K.ident[:, :])
                    if step == 2:
                        for m in range(C):
                            for c in range(C):
                                nc.tensor.matmul(ps[m][:, 0:D], gram[:, c, m * P:(m + 1) * P], wk[:, c, :], start=(c == 0), stop=False)
                            nc.tensor.matmul(ps[m][:, 0:D], col[:, m * P:(m + 1) * P], bk[:, :], start=False, stop=True)
                        for c in range(C):
                            nc.tensor.matmul(ps[2][0:1, 0:D], gram[:, c, D:D + 1], wk[:, c, :], start=(c == 0), stop=False)
                        last = nc.tensor.matmul(ps[2][0:1, 0:D], col[:, D:D + 1], bk[:, :], start=False, stop=True)
                    if step == 3:
                        for m in range(C):
                            for c in range(C):
                                nc.tensor.matmul(ps[3][:, m * D:(m + 1) * D], wv[:, c, m * P:(m + 1) * P], t1[:, c, :], start=(c == 0), stop=False)
                            last = nc.tensor.matmul(ps[3][:, m * D:(m + 1) * D], bv[:, m * P:(m + 1) * P], t1a[:, :], start=False, stop=True)
                    if step == 4:
                        for c in range(C):
                            last = nc.tensor.matmul(ps[0][:, c * D:(c + 1) * D], kvT[:, c, :], wfc[:, c, :], start=True, stop=True)
                    if step == 5:
                        for m in range(C):
                            for c in range(C):
                                nc.tensor.matmul(ps[2][:, m * D:(m + 1) * D], wq[:, c, m * P:(m + 1) * P], m2[:, c * D:(c + 1) * D],
                                                 start=(c == 0), stop=(c == C - 1))
                        nc.tensor.matmul(ps[1][0:1, 0:D], K.ones[0:1, 0:1], bfc[:, :], start=True, stop=False)
                        for c in range(C):
                            last = nc.tensor.matmul(ps[1][0:1, 0:D], bq[:, c:c + 1], m2[:, c * D:(c + 1) * D], start=False, stop=(c == C - 1))
                    if step == 6:
                        last = nc.tensor.matmul(ps[3][:, 0:D], K.ones[0:1, :], b3[:, :], start=True, stop=True)
                    last.then_inc(full, 1)

                def sums(i, h):
                    pe.wait_ge(hot_ready, 1)
                    pe.sem_inc(hot_ready, -1)
                    pe.wait_ge(rows_in[h], (i + 1) * (16 * G))
                    pe.sem_inc(passed, 1)
                    for j in range(G):
                        pe.wait_ge(acc_free, 1)
                        pe.sem_inc(acc_free, -1)
                        nc.tensor.matmul(psA[j][:, 0:D], hot[:, h % 2, j, :], rows[:, h, j, :],
                                         start=True, stop=True).then_inc(acc_full, 1)
                with pe.Fori(0, T // 2) as i:
                    for h in range(R):
                        sums(i, h)
                        beside(h)
                pe.wait_ge(m_loaded, 16 * 8)
                for i in (T // 2, T // 2 + 1):
                    for h in range(R):
                        sums(i, h)
                        if (i - T // 2) * R + h < 7:
                            attention((i - T // 2) * R + h)
                with pe.Fori(T // 2 + 2, STAGES // R) as i:
                    for h in range(R):
                        sums(i, h)


def combine1(nc, I, K):
    fp32, ALU, ACT = mybir.dt.float32, mybir.AluOpType, mybir.ActivationFunctionType
    with ExitStack() as ctx:
        def sb(n, shape):
            return ctx.enter_context(nc.sbuf_tensor(f"c1_{n}", shape, fp32))

        def sem(n):
            return K.sem(f"c1_{n}")
        wneigh = sb("wneigh", [P, C, D])
        rdeg, ys, zT, yT, g = sb("rdeg", [P, T]), sb("ys", [P, 2, D]), sb("zT", [P, 2, D]), sb("yT", [P, 2, D]), sb("g", [P, 2, D])
        ps = [ctx.enter_context(nc.psum_tensor(f"c1_ps{j}", [P, 512], fp32)) for j in range(8)]
        loaded, chain, b3_added = sem("loaded"), sem("chain"), sem("b3_added")
        ys_ready, yT_full, yT_ready, m_full, g_full, g_ready, relu_ready, m_free = (
            sem(n) for n in ("ys_ready", "yT_full", "yT_ready", "m_full", "g_full", "g_ready", "relu_ready", "m_free"))
        with nc.Block() as block:
            @block.sync
            def _(sp):
                sp.dma_start(wneigh[:, :, :], I["Wneigh"].rearrange("(c p) n -> p c n", p=P)).then_inc(loaded, 16)

            @block.vector
            def _(dve):
                nc.vector.tensor_scalar(rdeg[:, :], K.deg[:, :], 1.0, None, ALU.max).then_inc(chain, 1)
                dve.wait_ge(chain, 1)
                dve.sem_inc(chain, -1)
                nc.vector.reciprocal(rdeg[:, :], rdeg[:, :]).then_inc(chain, 1)
                dve.wait_ge(chain, 1)
                dve.sem_inc(chain, -1)

                def stage(t, k):
                    nc.vector.tensor_scalar(ys[:, k, :].unsqueeze(1), K.agg[:, bass.ds(t, 1), :], rdeg[:, bass.ds(t, 1)],
                                            None, ALU.mult).then_inc(ys_ready, 1)

                def finish(t, k, final):
                    x = K.X[:, bass.ds(t, 1), :]
                    dve.wait_ge(g_full, 1)
                    dve.sem_inc(g_full, -1)
                    nc.vector.tensor_tensor(g[:, k, :].unsqueeze(1), K.G[:, bass.ds(t, 1), :], ps[k][:, 0:D].unsqueeze(1), ALU.add).then_inc(g_ready, 1)
                    if not final:
                        stage(t + 2, k)
                    dve.wait_ge(m_full, 1)
                    dve.sem_inc(m_full, -1)
                    dve.wait_ge(b3_added, 1)
                    dve.sem_inc(b3_added, -1)
                    nc.vector.tensor_tensor(x, x, ps[4 + k][:, 0:D].unsqueeze(1), ALU.add).then_inc(chain, 1)
                    dve.wait_ge(chain, 1)
                    dve.sem_inc(chain, -1)
                    dve.sem_inc(m_free, 1)
                    dve.wait_ge(relu_ready, 1)
                    dve.sem_inc(relu_ready, -1)
                    nc.vector.tensor_tensor(x, x, g[:, k, :].unsqueeze(1), ALU.add).then_inc(chain, 1)
                    dve.wait_ge(chain, 1)
                    dve.sem_inc(chain, -1)
                stage(0, 0)
                stage(1, 1)
                with dve.Fori(0, T // 2 - 1) as i:
                    for k in range(2):
                        finish(2 * i + k, k, False)
                finish(T - 2, 0, True)
                finish(T - 1, 1, True)

            @block.gpsimd
            def _(pool):
                with pool.Fori(0, T) as t:
                    x = K.X[:, bass.ds(t, 1), :]
                    nc.gpsimd.tensor_tensor(x, x, K.b3[:, :].unsqueeze(1), ALU.add).then_inc(b3_added, 1)

            @block.scalar
            def _(act):
                def copies(t, k):
                    act.wait_ge(yT_full, 1)
                    act.sem_inc(yT_full, -1)
                    nc.scalar.activation(yT[:, k, :], ps[6 + k][:, 0:D], ACT.Identity)
                    nc.scalar.activation(zT[:, k, :].unsqueeze(1), K.ZT[:, bass.ds(t, 1), :], ACT.Identity).then_inc(yT_ready, 1)

                def relu(k):
                    act.wait_ge(g_ready, 1)
                    act.sem_inc(g_ready, -1)
                    nc.scalar.activation(g[:, k, :], g[:, k, :], ACT.Relu).then_inc(relu_ready, 1)
                copies(0, 0)
                with act.Fori(0, T // 2 - 1) as i:
                    for k in range(2):
                        copies(2 * i + k + 1, 1 - k)
                        relu(k)
                copies(T - 1, 1)
                relu(0)
                relu(1)

            @block.tensor
            def _(pe):
                pe.wait_ge(loaded, 16)
                pe.sem_inc(m_free, 2)

                def transposes(k):
                    pe.wait_ge(ys_ready, 1)
                    pe.sem_inc(ys_ready, -1)
                    for c in range(C):
                        last = nc.tensor.transpose(ps[6 + k][:, c * P:(c + 1) * P], ys[:, k, c * P:(c + 1) * P], K.ident[:, :])
                    last.then_inc(yT_full, 1)

                def body(final):
                    for k in range(2):
                        pe.wait_ge(yT_ready, 1)
                        pe.sem_inc(yT_ready, -1)
                        if not (final and k == 1):
                            transposes(1 - k)
                        for c in range(C):
                            last = nc.tensor.matmul(ps[k][:, 0:D], yT[:, k, c * P:(c + 1) * P], wneigh[:, c, :], start=(c == 0), stop=(c == C - 1))
                        last.then_inc(g_full, 1)
                        pe.wait_ge(m_free, 1)
                        pe.sem_inc(m_free, -1)
                        for c in range(C):
                            last = nc.tensor.matmul(ps[4 + k][:, 0:D], zT[:, k, c * P:(c + 1) * P], K.m3[:, c * D:(c + 1) * D], start=(c == 0), stop=(c == C - 1))
                        last.then_inc(m_full, 1)
                transposes(0)
                with pe.Fori(0, T // 2 - 1) as i:
                    body(False)
                body(True)


def route(nc, I, K):
    fp32, i32, ALU, ACT = mybir.dt.float32, mybir.dt.int32, mybir.AluOpType, mybir.ActivationFunctionType
    AX = mybir.AxisListType.X
    with ExitStack() as ctx:
        def sb(n, shape, dt=fp32):
            return ctx.enter_context(nc.sbuf_tensor(f"ro_{n}", shape, dt))

        def sem(n):
            return K.sem(f"ro_{n}")
        wr, br, gamma, beta = sb("wr", [P, C, NE]), sb("br", [P, NE]), sb("gamma", [P, C]), sb("beta", [P, C])
        xs, xT, logit = sb("xs", [P, 2, 2, D]), sb("xT", [P, 2, C, 2, P]), sb("logit", [P, T, NE])
        eq, which, left, order = sb("eq", [P, T, NE]), sb("which", [P, T]), sb("left", [P, T, NE]), sb("order", [P, NE])
        one, two = sb("one", [P, T, NE]), sb("two", [P, T, NE])
        top, top2, e = (sb(n, [P, T]) for n in ("top", "top2", "e"))
        marks, before, place, zeros = sb("marks", [P, T, NE]), sb("before", [P, T + 1, NE]), sb("place", [P, T, NE]), sb("zeros", [P, T])
        tiles_i, tiles, ends, start = sb("tiles_i", [P, NE], i32), sb("tiles", [P, NE]), sb("ends", [P, NE + 1]), sb("start", [P, NE])
        slot, spare_i, spare = sb("slot", [P, T, 2]), sb("spare_i", [P, T, 2], i32), sb("spare", [P, T, 2])
        past, expert = sb("past", [P, ST + 4, NE]), sb("expert", [P, ST + 4])
        psT = [ctx.enter_context(nc.psum_tensor(f"ro_psT{j}", [P, 512], fp32)) for j in range(2)]
        psL = [ctx.enter_context(nc.psum_tensor(f"ro_psL{j}", [P, 512], fp32)) for j in range(2)]
        loaded, chain, xs_ready, xT_full, xT_ready, l_full, gap_ready, e_ready = (
            sem(n) for n in ("loaded", "chain", "xs_ready", "xT_full", "xT_ready", "l_full", "gap_ready", "e_ready"))
        marks_ready, ranks_full, spare_ready, l_free, xs_free = sem("marks_ready"), sem("ranks_full"), sem("spare_ready"), sem("l_free"), sem("xs_free")
        with nc.Block() as block:
            @block.gpsimd
            def _(pool):
                pool.iota(spare_i[:, :, :], pattern=[[P, T], [T * P - N, 2]], base=ST * P - N, channel_multiplier=1).then_inc(spare_ready, 1)

            @block.sync
            def _(sp):
                sp.dma_start(wr[:, :, :], I["f1_Wr"].rearrange("(c p) n -> p c n", p=P)).then_inc(loaded, 16)
                sp.dma_start(br[:, :], I["f1_br"].partition_broadcast(P)).then_inc(loaded, 16)
                sp.dma_start(gamma[:, :], I["f1_gamma"]).then_inc(loaded, 16)
                sp.dma_start(beta[:, :], I["f1_beta"]).then_inc(loaded, 16)
                sp.dma_start(K.w1[:, :, :, :], I["f1_W1"].rearrange("e (c p) n -> p e c n", p=P)).then_inc(K.experts_loaded, 16)
                sp.dma_start(K.b1[:, :, :], I["f1_b1"].partition_broadcast(P)).then_inc(K.experts_loaded, 16)
                sp.dma_start(K.w2[:, :, :, :], I["f1_W2"].rearrange("e (m p) n -> p e m n", p=P)).then_inc(K.experts_loaded, 16)
                sp.dma_start(K.b2[:, :, :], I["f1_b2"].partition_broadcast(P)).then_inc(K.experts_loaded, 16)

            @block.vector
            def _(dve):
                def norm(i, k):
                    for r in range(2):
                        t = 2 * i + r
                        last = nc.vector.tensor_scalar(xs[:, k, r, :].unsqueeze(1), K.X[:, bass.ds(t, 1), :], K.mean[:, bass.ds(t, 1)],
                                                       K.rstd[:, bass.ds(t, 1)], ALU.subtract, ALU.mult)
                    last.then_inc(xs_ready, 1)

                def keep(i, k):
                    dve.wait_ge(l_full, 1)
                    dve.sem_inc(l_full, -1)
                    return nc.vector.tensor_tensor(logit[:, bass.ds(2 * i, 2), :], psL[k][:, 0:2 * NE].rearrange("p (r n) -> p r n", r=2),
                                                   br[:, :].unsqueeze(1).broadcast_to([P, 2, NE]), ALU.add)
                norm(0, 0)
                norm(1, 1)
                dve.wait_ge(loaded, 64)
                with dve.Fori(0, T // 4 - 1) as i:
                    for k in range(2):
                        dve.wait_ge(xs_free, 1)
                        dve.sem_inc(xs_free, -1)
                        norm(2 * i + k + 2, k)
                        keep(2 * i + k, k).then_inc(l_free, 1)
                dve.wait_ge(xs_free, 1)
                dve.sem_inc(xs_free, -1)
                norm(T // 2 - 1, 0)
                keep(T // 2 - 3, 0).then_inc(l_free, 1)
                keep(T // 2 - 2, 1)
                keep(T // 2 - 1, 0).then_inc(chain, 1)
                dve.wait_ge(chain, 1)
                dve.sem_inc(chain, -1)
                wide = lambda a: a.unsqueeze(2).broadcast_to([P, T, NE])
                nc.vector.tensor_scalar(order[:, :], K.iota[:, 0:NE], -1.0, float(NE), ALU.mult, ALU.add).then_inc(chain, 1)
                dve.wait_ge(chain, 1)
                dve.sem_inc(chain, -1)

                def first(values, largest, hot):
                    nc.vector.tensor_reduce(largest, values, AX, ALU.max).then_inc(chain, 1)
                    dve.wait_ge(chain, 1)
                    dve.sem_inc(chain, -1)
                    nc.vector.tensor_tensor(eq[:, :, :], values, wide(largest), ALU.is_equal).then_inc(chain, 1)
                    dve.wait_ge(chain, 1)
                    dve.sem_inc(chain, -1)
                    nc.vector.tensor_tensor(eq[:, :, :], eq[:, :, :], order[:, :].unsqueeze(1).broadcast_to([P, T, NE]), ALU.mult).then_inc(chain, 1)
                    dve.wait_ge(chain, 1)
                    dve.sem_inc(chain, -1)
                    nc.vector.tensor_reduce(which[:, :], eq[:, :, :], AX, ALU.max).then_inc(chain, 1)
                    dve.wait_ge(chain, 1)
                    dve.sem_inc(chain, -1)
                    nc.vector.tensor_tensor(hot, eq[:, :, :], wide(which[:, :]), ALU.is_equal).then_inc(chain, 1)
                    dve.wait_ge(chain, 1)
                    dve.sem_inc(chain, -1)
                first(logit[:, :, :], top[:, :], one[:, :, :])
                nc.vector.scalar_tensor_tensor(left[:, :, :], one[:, :, :], -2 * BIG, logit[:, :, :], ALU.mult, ALU.add).then_inc(chain, 1)
                dve.wait_ge(chain, 1)
                dve.sem_inc(chain, -1)
                first(left[:, :, :], top2[:, :], two[:, :, :])
                nc.vector.tensor_tensor(e[:, :], top2[:, :], top[:, :], ALU.subtract).then_inc(gap_ready, 1)
                nc.vector.tensor_tensor(marks[:, :, :], one[:, :, :], two[:, :, :], ALU.add).then_inc(chain, 1)
                dve.wait_ge(chain, 1)
                dve.sem_inc(chain, -1)
                nc.vector.tensor_tensor(marks[:, :, :], marks[:, :, :], wide(K.real[:, :]), ALU.mult).then_inc(marks_ready, 1)
                nc.vector.memset(zeros[:, :], 0.0)
                nc.vector.memset(before[:, 0, :], 0.0)
                nc.vector.memset(ends[:, 0:1], 0.0)
                dve.wait_ge(e_ready, 1)
                dve.sem_inc(e_ready, -1)
                nc.vector.tensor_scalar(top[:, :], e[:, :], 1.0, None, ALU.add).then_inc(chain, 1)
                dve.wait_ge(chain, 1)
                dve.sem_inc(chain, -1)
                nc.vector.reciprocal(K.share[:, :, 0], top[:, :]).then_inc(chain, 1)
                dve.wait_ge(chain, 1)
                dve.sem_inc(chain, -1)
                nc.vector.tensor_tensor(K.share[:, :, 1], K.share[:, :, 0], e[:, :], ALU.mult)
                dve.wait_ge(ranks_full, 1)
                dve.sem_inc(ranks_full, -1)
                for x in range(NE):
                    last = nc.vector.tensor_tensor_scan(before[:, 1:T + 1, x], zeros[:, :],
                                                        psL[1][:, 0:T * NE].rearrange("p (t e) -> p t e", e=NE)[:, :, x], 0.0, ALU.add, ALU.add)
                last.then_inc(chain, 1)
                dve.wait_ge(chain, 1)
                dve.sem_inc(chain, -1)
                nc.vector.tensor_scalar(tiles_i[:, :], before[:, T, :], float(P - 1), None, ALU.add).then_inc(chain, 1)
                dve.wait_ge(chain, 1)
                dve.sem_inc(chain, -1)
                nc.vector.tensor_scalar(tiles_i[:, :], tiles_i[:, :], 7, None, ALU.arith_shift_right).then_inc(chain, 1)
                dve.wait_ge(chain, 1)
                dve.sem_inc(chain, -1)
                nc.vector.tensor_copy(tiles[:, :], tiles_i[:, :]).then_inc(chain, 1)
                dve.wait_ge(chain, 1)
                dve.sem_inc(chain, -1)
                nc.vector.tensor_tensor_scan(ends[:, 1:NE + 1], zeros[:, 0:NE], tiles[:, :], 0.0, ALU.add, ALU.add).then_inc(chain, 1)
                dve.wait_ge(chain, 1)
                dve.sem_inc(chain, -1)
                nc.vector.tensor_tensor(past[:, :, :], K.iota[:, 0:ST + 4].unsqueeze(2).broadcast_to([P, ST + 4, NE]),
                                        ends[:, 1:NE + 1].unsqueeze(1).broadcast_to([P, ST + 4, NE]), ALU.is_ge)
                nc.vector.tensor_scalar(start[:, :], ends[:, 0:NE], float(P), -1.0, ALU.mult, ALU.add).then_inc(chain, 1)
                dve.wait_ge(chain, 1)
                dve.sem_inc(chain, -1)
                nc.vector.tensor_reduce(expert[:, :], past[:, :, :], AX, ALU.add).then_inc(chain, 1)
                dve.wait_ge(chain, 1)
                dve.sem_inc(chain, -1)
                nc.vector.tensor_scalar(K.expert[:, :], expert[:, :], float(NE - 1), None, ALU.min)
                nc.vector.tensor_tensor(place[:, :, :], psL[0][:, 0:T * NE].rearrange("p (t e) -> p t e", e=NE),
                                        before[:, 0:T, :], ALU.add).then_inc(chain, 1)
                dve.wait_ge(chain, 1)
                dve.sem_inc(chain, -1)
                nc.vector.tensor_tensor(place[:, :, :], place[:, :, :], start[:, :].unsqueeze(1).broadcast_to([P, T, NE]), ALU.add).then_inc(chain, 1)
                dve.wait_ge(chain, 1)
                dve.sem_inc(chain, -1)
                nc.vector.tensor_tensor(one[:, :, :], one[:, :, :], place[:, :, :], ALU.mult)
                nc.vector.tensor_tensor(two[:, :, :], two[:, :, :], place[:, :, :], ALU.mult).then_inc(chain, 1)
                dve.wait_ge(chain, 1)
                dve.sem_inc(chain, -1)
                nc.vector.tensor_reduce(slot[:, :, 0], one[:, :, :], AX, ALU.add)
                nc.vector.tensor_reduce(slot[:, :, 1], two[:, :, :], AX, ALU.add).then_inc(chain, 1)
                dve.wait_ge(chain, 1)
                dve.sem_inc(chain, -1)
                dve.wait_ge(spare_ready, 1)
                dve.sem_inc(spare_ready, -1)
                nc.vector.tensor_copy(spare[:, :, :], spare_i[:, :, :]).then_inc(chain, 1)
                dve.wait_ge(chain, 1)
                dve.sem_inc(chain, -1)
                nc.vector.tensor_tensor(slot[:, :, :], slot[:, :, :], spare[:, :, :], ALU.subtract).then_inc(chain, 1)
                dve.wait_ge(chain, 1)
                dve.sem_inc(chain, -1)
                nc.vector.tensor_tensor(slot[:, :, :], slot[:, :, :], K.real[:, :].unsqueeze(2).broadcast_to([P, T, 2]), ALU.mult).then_inc(chain, 1)
                dve.wait_ge(chain, 1)
                dve.sem_inc(chain, -1)
                nc.vector.tensor_tensor(slot[:, :, :], slot[:, :, :], spare[:, :, :], ALU.add).then_inc(chain, 1)
                dve.wait_ge(chain, 1)
                dve.sem_inc(chain, -1)
                nc.vector.tensor_copy(K.slot[:, :, :], slot[:, :, :])
                nc.vector.tensor_scalar(K.back[:, :, :], slot[:, :, :], float(ST * P - 1), None, ALU.min)

            @block.scalar
            def _(act):
                act.wait_ge(loaded, 64)
                def copy(k):
                    act.wait_ge(xT_full, 1)
                    act.sem_inc(xT_full, -1)
                    act.sem_inc(xs_free, 1)
                    for c in range(C):
                        last = nc.scalar.activation(xT[:, k, c, :, :], psT[k][:, c * 2 * P:(c + 1) * 2 * P].rearrange("p (r n) -> p r n", r=2),
                                                    ACT.Identity, bias=beta[:, c:c + 1], scale=gamma[:, c:c + 1])
                    last.then_inc(xT_ready, 1)
                with act.Fori(0, T // 4) as i:
                    for k in range(2):
                        copy(k)
                copy(0)
                act.wait_ge(gap_ready, 1)
                act.sem_inc(gap_ready, -1)
                nc.scalar.activation(e[:, :], e[:, :], ACT.Exp).then_inc(e_ready, 1)

            @block.tensor
            def _(pe):
                pe.wait_ge(loaded, 64)

                def transposes(k):
                    pe.wait_ge(xs_ready, 1)
                    pe.sem_inc(xs_ready, -1)
                    for c in range(C):
                        for r in range(2):
                            last = nc.tensor.transpose(psT[k][:, (2 * c + r) * P:(2 * c + r + 1) * P], xs[:, k, r, c * P:(c + 1) * P], K.ident[:, :])
                    last.then_inc(xT_full, 1)

                def logits(k, final=False):
                    pe.wait_ge(xT_ready, 1)
                    pe.sem_inc(xT_ready, -1)
                    if not final:
                        transposes(1 - k)
                    pe.wait_ge(l_free, 1)
                    pe.sem_inc(l_free, -1)
                    for r in range(2):
                        for c in range(C):
                            last = nc.tensor.matmul(psL[k][:, r * NE:(r + 1) * NE], xT[:, k, c, r, :], wr[:, c, :], start=(c == 0), stop=(c == C - 1))
                    last.then_inc(l_full, 1)
                pe.sem_inc(l_free, 2)
                transposes(0)
                with pe.Fori(0, T // 4) as i:
                    for k in range(2):
                        logits(k)
                logits(0, True)
                pe.wait_ge(marks_ready, 1)
                pe.sem_inc(marks_ready, -1)
                nc.tensor.matmul(psL[0][:, 0:T * NE], K.upper[:, :], marks[:, :, :].rearrange("p t e -> p (t e)"), start=True, stop=True)
                nc.tensor.matmul(psL[1][:, 0:T * NE], K.ones[:, :], marks[:, :, :].rearrange("p t e -> p (t e)"),
                                 start=True, stop=True).then_inc(ranks_full, 1)


def dispatch(nc, K, stab):
    fp32, i32, ALU = mybir.dt.float32, mybir.dt.int32, mybir.AluOpType
    R = 5
    with ExitStack() as ctx:
        def sem(n):
            return K.sem(f"di_{n}")
        xs = ctx.enter_context(nc.sbuf_tensor("di_xs", [P, R, D], fp32))
        cur = ctx.enter_context(nc.sbuf_tensor("di_cur", [P, R, 2], i32))
        xs_ready, passed, sent = sem("xs_ready"), sem("passed"), [sem(f"sent{h}") for h in range(R)]
        with nc.Block() as block:
            @block.vector
            def _(dve):
                def norm(t, h):
                    nc.vector.tensor_copy(cur[:, h, :].unsqueeze(1), K.slot[:, bass.ds(t, 1), :])
                    nc.vector.tensor_scalar(xs[:, h, :].unsqueeze(1), K.X[:, bass.ds(t, 1), :], K.mean[:, bass.ds(t, 1)],
                                            K.rstd[:, bass.ds(t, 1)], ALU.subtract, ALU.mult).then_inc(xs_ready, 1)
                for h in range(R):
                    norm(h, h)
                with dve.Fori(1, TN // R) as i:
                    for h in range(R):
                        dve.wait_ge(sent[h], i * (16 * 2))
                        dve.sem_inc(passed, 1)
                        norm(R * i + h, h)

            @block.gpsimd
            def _(pool):
                with pool.Fori(0, TN // R) as i:
                    for h in range(R):
                        pool.wait_ge(xs_ready, 1)
                        pool.sem_inc(xs_ready, -1)
                        for k in range(2):
                            nc.gpsimd.indirect_dma_start(
                                out=stab, out_offset=bass.IndirectOffsetOnAxis(ap=cur[:, h, k:k + 1].bitcast(mybir.dt.uint32), axis=0),
                                in_=xs[:, h, :], in_offset=None).then_inc(sent[h], 16)
                for h in range(R):
                    pool.wait_ge(sent[h], TN // R * (16 * 2))


def experts(nc, I, K, stab, ytab):
    fp32, ALU, ACT = mybir.dt.float32, mybir.AluOpType, mybir.ActivationFunctionType
    M = FF1 // P
    R = 4
    with ExitStack() as ctx:
        def sb(n, shape):
            return ctx.enter_context(nc.sbuf_tensor(f"ex_{n}", shape, fp32))

        def ps(n):
            return ctx.enter_context(nc.psum_tensor(f"ex_{n}", [P, 512], fp32))

        def sem(n):
            return K.sem(f"ex_{n}")
        w1, b1, w2, b2, loaded = K.w1, K.b1, K.w2, K.b2, K.experts_loaded
        gamma, beta = sb("gamma", [P, C]), sb("beta", [P, C])
        rows, xT, pre, act_h = sb("rows", [P, R, D]), sb("xT", [P, 2, C, P]), sb("pre", [P, 2, FF1]), sb("h", [P, 2, FF1])
        hT, y = sb("hT", [P, 2, FF1]), sb("y", [P, R, D])
        psX, psH, psU, psO = ps("psX"), ps("psH"), [ps("psU0"), ps("psU1")], [ps("psO0"), ps("psO1")]
        rows_in, y_out = [sem(f"rows_in{h}") for h in range(R)], [sem(f"y_out{h}") for h in range(R)]
        rows_free, x_full, xT_ready, u_full, pre_ready, h_ready, hT_full, hT_ready, o_full, y_ready = (
            sem(n) for n in ("rows_free", "x_full", "xT_ready", "u_full", "pre_ready", "h_ready", "hT_full", "hT_ready", "o_full", "y_ready"))
        flat = lambda a: a.rearrange("p a n -> p (a n)")

        def tile_experts(eng, i):
            return nc.values_load_multi_w_load_instructions(
                K.expert[0:1, bass.ds(R * i, R + 1)], [eng.engine], min_val=0, max_val=NE - 1,
                skip_runtime_bounds_check_because="route keeps them below NE")[1]
        with nc.Block() as block:
            @block.sync
            def _(sp):
                sp.dma_start(gamma[:, :], I["f1_gamma"]).then_inc(loaded, 16)
                sp.dma_start(beta[:, :], I["f1_beta"]).then_inc(loaded, 16)

                def load(j, h):
                    sp.dma_start(rows[:, h, :], stab[bass.ds(j * P, P), :]).then_inc(rows_in[h], 16)

                def save(j, h):
                    sp.wait_ge(y_ready, 1)
                    sp.sem_inc(y_ready, -1)
                    sp.dma_start(ytab[bass.ds(j * P, P), :], y[:, h, :]).then_inc(y_out[h], 16)
                for h in range(R):
                    load(h, h)
                with sp.Fori(0, ST // R - 1) as i:
                    for h in range(R):
                        save(R * i + h, h)
                        sp.wait_ge(rows_free, 1)
                        sp.sem_inc(rows_free, -1)
                        load(R * (i + 1) + h, h)
                for h in range(R):
                    save(ST - R + h, h)

            @block.vector
            def _(dve):
                for h in range(R):
                    dve.sem_inc(y_out[h], 16)
                dve.wait_ge(loaded, 96)

                def add_b1(e, h):
                    dve.wait_ge(u_full, 1)
                    dve.sem_inc(u_full, -1)
                    nc.vector.tensor_tensor(pre[:, h, :].unsqueeze(1), psU[h][:, :].unsqueeze(1), b1[:, bass.ds(e, 1), :], ALU.add).then_inc(pre_ready, 1)

                def body(i, final):
                    e = tile_experts(dve, i)
                    for h in range(R):
                        dve.wait_ge(hT_full, 1)
                        dve.sem_inc(hT_full, -1)
                        nc.vector.tensor_copy(hT[:, h % 2, :], psH[:, :]).then_inc(hT_ready, 1)
                        if not (final and h == R - 1):
                            add_b1(e[h + 1], (h + 1) % 2)
                        dve.wait_ge(o_full, 1)
                        dve.sem_inc(o_full, -1)
                        dve.wait_ge(y_out[h], 16)
                        dve.sem_inc(y_out[h], -16)
                        nc.vector.tensor_tensor(y[:, h, :].unsqueeze(1), psO[h % 2][:, 0:D].unsqueeze(1), b2[:, bass.ds(e[h], 1), :], ALU.add).then_inc(y_ready, 1)
                add_b1(tile_experts(dve, 0)[0], 0)
                with dve.Fori(0, ST // R - 1) as i:
                    body(i, False)
                body(ST // R - 1, True)
                for h in range(R):
                    dve.wait_ge(y_out[h], 16)
                    dve.sem_inc(y_out[h], -16)

            @block.scalar
            def _(act):
                act.wait_ge(loaded, 96)

                def turn(h):
                    act.wait_ge(x_full, 1)
                    act.sem_inc(x_full, -1)
                    act.sem_inc(rows_free, 1)
                    for c in range(C):
                        last = nc.scalar.activation(xT[:, h, c, :], psX[:, c * P:(c + 1) * P], ACT.Identity,
                                                    bias=beta[:, c:c + 1], scale=gamma[:, c:c + 1])
                    last.then_inc(xT_ready, 1)

                def gelu(h):
                    act.wait_ge(pre_ready, 1)
                    act.sem_inc(pre_ready, -1)
                    nc.scalar.activation(act_h[:, h, :], pre[:, h, :], ACT.Gelu).then_inc(h_ready, 1)
                turn(0)
                turn(1)
                gelu(0)
                with act.Fori(0, ST // 2 - 1) as i:
                    for h in range(2):
                        turn(h)
                        gelu(1 - h)
                gelu(1)

            @block.tensor
            def _(pe):
                pe.wait_ge(loaded, 96)

                def turn(h):
                    pe.wait_ge(rows_in[h], 16)
                    pe.sem_inc(rows_in[h], -16)
                    for c in range(C):
                        last = nc.tensor.transpose(psX[:, c * P:(c + 1) * P], rows[:, h, c * P:(c + 1) * P], K.ident[:, :])
                    last.then_inc(x_full, 1)

                def up(e, h):
                    pe.wait_ge(xT_ready, 1)
                    pe.sem_inc(xT_ready, -1)
                    for c in range(C):
                        last = nc.tensor.matmul(psU[h][:, :], xT[:, h, c, :], flat(w1[:, bass.ds(e, 1), c, :]), start=(c == 0), stop=(c == C - 1))
                    last.then_inc(u_full, 1)

                def body(i, final):
                    e = tile_experts(pe, i)
                    for h in range(R):
                        pe.wait_ge(h_ready, 1)
                        pe.sem_inc(h_ready, -1)
                        for m in range(M):
                            last = nc.tensor.transpose(psH[:, m * P:(m + 1) * P], act_h[:, h % 2, m * P:(m + 1) * P], K.ident[:, :])
                        last.then_inc(hT_full, 1)
                        if not (final and h == R - 1):
                            up(e[h + 1], (h + 1) % 2)
                        if not (final and h >= R - 2):
                            turn((h + 2) % R)
                        pe.wait_ge(hT_ready, 1)
                        pe.sem_inc(hT_ready, -1)
                        for m in range(M):
                            last = nc.tensor.matmul(psO[h % 2][:, 0:D], hT[:, h % 2, m * P:(m + 1) * P], flat(w2[:, bass.ds(e[h], 1), m, :]),
                                                    start=(m == 0), stop=(m == M - 1))
                        last.then_inc(o_full, 1)
                turn(0)
                up(tile_experts(pe, 0)[0], 0)
                turn(1)
                with pe.Fori(0, ST // R - 1) as i:
                    body(i, False)
                body(ST // R - 1, True)


def collect(nc, K, ytab, out):
    fp32, i32, ALU = mybir.dt.float32, mybir.dt.int32, mybir.AluOpType
    R = 5
    with ExitStack() as ctx:
        def sem(n):
            return K.sem(f"co_{n}")
        y = ctx.enter_context(nc.sbuf_tensor("co_y", [P, R, 2, D], fp32))
        cur = ctx.enter_context(nc.sbuf_tensor("co_cur", [P, R, 2], i32))
        y_in, cur_ready, passed, chain = [sem(f"y_in{h}") for h in range(R)], sem("cur_ready"), sem("passed"), sem("chain")
        x_done, stored = sem("x_done"), sem("stored")
        with nc.Block() as block:
            @block.sync
            def _(sp):
                rows = R * P
                with sp.Fori(0, TN // R - 1) as i:
                    sp.wait_ge(x_done, 1)
                    sp.sem_inc(x_done, -1)
                    sp.dma_start(out[bass.ds(i * rows, rows), :].rearrange("(t p) d -> p t d", p=P), K.X[:, bass.ds(R * i, R), :]).then_inc(stored, 16)
                sp.wait_ge(x_done, 1)
                sp.sem_inc(x_done, -1)
                full = N // P * P
                sp.dma_start(out[(TN - R) * P:full, :].rearrange("(t p) d -> p t d", p=P), K.X[:, TN - R:N // P, :]).then_inc(stored, 16)
                sp.dma_start(out[full:N, :], K.X[0:N - full, N // P, :]).then_inc(stored, 16)
                sp.wait_ge(stored, 16 * (TN // R + 1))

            @block.gpsimd
            def _(pool):
                with pool.Fori(0, TN // R) as i:
                    for h in range(R):
                        pool.wait_ge(cur_ready, 1)
                        pool.sem_inc(cur_ready, -1)
                        for k in range(2):
                            nc.gpsimd.indirect_dma_start(
                                out=y[:, h, k, :], out_offset=None, in_=ytab,
                                in_offset=bass.IndirectOffsetOnAxis(ap=cur[:, h, k:k + 1].bitcast(mybir.dt.uint32), axis=0)
                            ).then_inc(y_in[h], 16)

            @block.vector
            def _(dve):
                def places(t, h):
                    nc.vector.tensor_copy(cur[:, h, :].unsqueeze(1), K.back[:, bass.ds(t, 1), :]).then_inc(cur_ready, 1)

                def turn(i, final):
                    for h in range(R):
                        t = R * i + h
                        x = K.X[:, bass.ds(t, 1), :]
                        dve.wait_ge(y_in[h], (i + 1) * (16 * 2))
                        dve.sem_inc(passed, 1)
                        for k in range(2):
                            nc.vector.scalar_tensor_tensor(
                                x, y[:, h, k, :].unsqueeze(1), K.share[:, bass.ds(t, 1), k:k + 1].rearrange("p a b -> p (a b)"), x,
                                ALU.mult, ALU.add).then_inc(chain, 1)
                            dve.wait_ge(chain, 1)
                            dve.sem_inc(chain, -1)
                        if not final:
                            places(t + R, h)
                    dve.sem_inc(x_done, 1)
                for h in range(R):
                    places(h, h)
                with dve.Fori(0, TN // R - 1) as i:
                    turn(i, False)
                turn(TN // R - 1, True)


class Kept:

    def __init__(self, nc):
        self.nc, self.sems = nc, []

    def sem(self, name):
        self.sems.append(self.nc.alloc_semaphore(name))
        return self.sems[-1]

    def clear(self):
        self.nc.clear_and_free_semaphores(self.sems)
        self.nc.all_engine_barrier()
        self.sems = []


def program(nc, I, out):
    fp32, i32 = mybir.dt.float32, mybir.dt.int32
    htab = nc.dram_tensor("htab", (T * P, TW), fp32, kind="Internal").ap()
    atab = nc.dram_tensor("atab", (T * P, HEADS), fp32, kind="Internal").ap()
    ztab = nc.dram_tensor("ztab", (T * P, D), fp32, kind="Internal").ap()
    wtab = nc.dram_tensor("wtab", (T * P,), fp32, kind="Internal").ap()
    stab = nc.dram_tensor("stab", (ST * P + 2 * (T * P - N), D), fp32, kind="Internal").ap()
    ytab = nc.dram_tensor("ytab", (ST * P, D), fp32, kind="Internal").ap()
    ftab = nc.dram_tensor("ftab", (EP, HEADS), fp32, kind="Internal").ap()
    with ExitStack() as ctx:
        def sb(n, shape, dt=fp32):
            return ctx.enter_context(nc.sbuf_tensor(n, shape, dt))
        K = Kept(nc)
        K.X = sb("X", [P, T, D])
        K.ident, K.upper, K.ones = sb("ident", [P, P]), sb("upper", [P, P]), sb("ones", [P, P])
        K.iota, K.iotai = sb("iota", [P, 512]), sb("iotai", [P, 512], i32)
        K.real, K.blockmask = sb("real", [P, T]), sb("blockmask", [P, C, HEADS])
        K.mean, K.rstd, K.meansq = sb("mean", [P, T]), sb("rstd", [P, T]), sb("meansq", [P, T])
        K.share, K.expert = sb("share", [P, T, 2]), sb("expert", [P, ST + 4], i32)
        K.slot, K.back = sb("slot", [P, T, 2], i32), sb("back", [P, T, 2], i32)
        K.src_s, K.base, K.ns = sb("src_s", [P, S], i32), sb("base", [P, S + 8]), sb("node_tile", [P, S + 10], i32)
        K.src_p, K.cap, K.capall = sb("src_p", [P, ET], i32), sb("cap", [P, ET]), sb("capall", [P, 1])
        K.deg, K.last_edge = sb("deg", [P, T]), sb("last_edge", [P, T], i32)
        setup(nc, I, K)
        K.got_in, K.cur_set, K.passed = [K.sem("got_in0"), K.sem("got_in1")], K.sem("cur_set"), K.sem("passed")
        with ExitStack() as layer:
            K.cur = layer.enter_context(nc.sbuf_tensor("cur", [P, GJ], i32))
            K.got = layer.enter_context(nc.sbuf_tensor("got", [P, GJ, HEADS], fp32))
            K.term = layer.enter_context(nc.sbuf_tensor("term", [P, ET, HEADS], fp32))
            K.wa = layer.enter_context(nc.sbuf_tensor("wa", [P, C, 2 * HEADS], fp32))
            with ExitStack() as first:
                K.w0, K.w0_loaded = first.enter_context(nc.sbuf_tensor("w0", [P, C, D], fp32)), K.sem("w0_loaded")
                K.att = first.enter_context(nc.sbuf_tensor("att", [P, C, 2], fp32))
                row_stats(nc, K, "ln0", lambda sp: load_source_terms(I, K, sp))
                source_terms(nc, I, K, atab)
            K.H = layer.enter_context(nc.sbuf_tensor("H", [P, T, HW], fp32))
            with ExitStack() as mixing:
                K.Q = mixing.enter_context(nc.sbuf_tensor("Q", [P, T, D], fp32))
                K.kvbd = mixing.enter_context(nc.sbuf_tensor("kvbd", [P, C, 2, P], fp32))
                project(nc, I, K, htab, atab)
                mix0(nc, I, K, atab)
            K.node = layer.enter_context(nc.sbuf_tensor("node", [P, T, 2 * HEADS], fp32))
            K.selfw = layer.enter_context(nc.sbuf_tensor("selfw", [P, T, HEADS], fp32))
            edge_tables(nc, I, K, atab)
            K.acc = layer.enter_context(nc.sbuf_tensor("acc", [P, 2, T, TW], fp32))
            softmax_maxima(nc, K, ftab)
            gat(nc, I, K, htab)
        with ExitStack() as layer:
            K.f0_w1 = layer.enter_context(nc.sbuf_tensor("f0_w1", [P, C, FF0], fp32))
            K.f0_b1 = layer.enter_context(nc.sbuf_tensor("f0_b1", [P, FF0 // P], fp32))
            K.f0_w2 = layer.enter_context(nc.sbuf_tensor("f0_w2", [P, FF0 // P, D], fp32))
            K.f0_b2 = layer.enter_context(nc.sbuf_tensor("f0_b2", [P, D], fp32))
            K.f0_loaded = K.sem("f0_loaded")
            row_stats(nc, K, "ln1", lambda sp: load_ffn0(I, K, sp))
            ffn0(nc, I, K, wtab)
        K.clear()
        row_stats(nc, K, "ln2")
        with ExitStack() as layer:
            K.Z = layer.enter_context(nc.sbuf_tensor("Z", [P, T, D], fp32))
            K.ZT = layer.enter_context(nc.sbuf_tensor("ZT", [P, T, D], fp32))
            K.G = layer.enter_context(nc.sbuf_tensor("G", [P, T, D], fp32))
            K.m3 = layer.enter_context(nc.sbuf_tensor("m3", [P, C * D], fp32))
            K.b3 = layer.enter_context(nc.sbuf_tensor("b3", [P, D], fp32))
            K.agg = layer.enter_context(nc.sbuf_tensor("agg", [P, T, D], fp32))
            normalise(nc, K, ztab)
            aggregate(nc, I, K, ztab, stab)
            combine1(nc, I, K)
        row_stats(nc, K, "ln3")
        K.experts_loaded = K.sem("experts_loaded")
        with ExitStack() as layer:
            K.w1 = layer.enter_context(nc.sbuf_tensor("w1", [P, NE, C, FF1], fp32))
            K.b1 = layer.enter_context(nc.sbuf_tensor("b1", [P, NE, FF1], fp32))
            K.w2 = layer.enter_context(nc.sbuf_tensor("w2", [P, NE, FF1 // P, D], fp32))
            K.b2 = layer.enter_context(nc.sbuf_tensor("b2", [P, NE, D], fp32))
            route(nc, I, K)
            dispatch(nc, K, stab)
            experts(nc, I, K, stab, ytab)
        collect(nc, K, ytab, out)


def laid_out(x, src, dst, **w):
    import numpy as np
    f = {k: np.asarray(v) for k, v in w.items()}
    x, src, dst = np.asarray(x), np.asarray(src), np.asarray(dst)
    o = {}
    o["x"] = np.concatenate([x, np.zeros((T * P - N, D), x.dtype)])
    o["src"] = np.concatenate([src, np.zeros(EP - E, src.dtype)])
    o["dst"] = np.concatenate([dst, np.full(EP - E, 4000, dst.dtype)])
    o["W0"], o["W0T"] = f["L0_gnn_W0"], f["L0_gnn_W0"].T
    o["att"] = np.stack([f["L0_gnn_att_src0"].reshape(D), f["L0_gnn_att_dst0"].reshape(D)], axis=1)
    o["b0"] = f["L0_gnn_b0"]
    for n in ("w_qkv", "w_out", "b_out", "w_norm2"):
        o[n] = f["L0_mix_" + n]
    o["w_norm1"] = f["L0_mix_w_norm1"].reshape(C, P).T
    for n in ("wr", "br", "w1", "b1", "w2", "b2"):
        o["f0_" + n] = f["L0_ffn_" + n]
    o["f0_wr"] = o["f0_wr"].reshape(D)
    o["f0_b1"] = o["f0_b1"].reshape(FF0 // P, P).T
    o["Wself"], o["Wneigh"], o["bgnn"] = f["L1_gnn_W_self"], f["L1_gnn_W_neigh"], f["L1_gnn_b"]
    o["Wq"], o["WkT"], o["WvT"], o["WfcT"] = f["L1_mix_Wq"], f["L1_mix_Wk"].T, f["L1_mix_Wv"].T, f["L1_mix_Wfc"].T
    for n in ("bk", "bv", "bfc"):
        o[n] = f["L1_mix_" + n]
    o["bq"] = f["L1_mix_bq"].reshape(C, P).T
    for n in ("gamma", "beta", "Wr", "br", "W1", "b1", "W2", "b2"):
        o["f1_" + n] = f["L1_ffn_" + n]
    o["f1_gamma"], o["f1_beta"] = (o["f1_" + n].reshape(C, P).T for n in ("gamma", "beta"))
    return o


def kernel(**inputs):
    import numpy as _np
    import concourse.bacc as _bacc
    from concourse import mybir as _mybir
    from concourse.bass_utils import run_bass_kernel_spmd as _run

    nc = _bacc.Bacc("TRN2", target_bir_lowering=False, num_devices=1)
    arrays, args = {}, {}
    for name, a in laid_out(**inputs).items():
        a = _np.ascontiguousarray(a)
        arrays[f"in_{name}"] = a
        args[name] = nc.dram_tensor(f"in_{name}", a.shape, _mybir.dt.from_np(a.dtype), kind="ExternalInput").ap()
    out = nc.dram_tensor("out_x", (N, D), _mybir.dt.float32, kind="ExternalOutput").ap()
    program(nc, args, out)
    r = _run(nc, [arrays], core_ids=[0])
    return r.results[0]["out_x"]
```
